# Optimizing a Trainium2 kernel written in Bass

```python
import numpy as np
import jax
import jax.numpy as jnp

def _softmax(x, axis=-1):
    return jax.nn.softmax(x, axis=axis)

def _gelu(x):
    return jax.nn.gelu(x, approximate=True)

def _silu(x):
    return jax.nn.silu(x)

def _sigmoid(x):
    return jax.nn.sigmoid(x)

def _layernorm(x, axis=-1, eps=1e-05):
    m = jnp.mean(x, axis=axis, keepdims=True)
    v = jnp.var(x, axis=axis, keepdims=True)
    return (x - m) / jnp.sqrt(v + eps)

def _scatter_add(tgt, idx, src, axis=0):
    return tgt.at[idx].add(src)

def _segment_sum(src, seg, n):
    return jax.ops.segment_sum(src, seg, n)
kernel_name = 'mk_xattn_ffn_d4_seqx_r8_952048'

def setup_inputs(seed: int=0):
    np.random.seed(seed)
    _w = jnp.asarray

    def _rec_inputs():
        import jax
        import jax.numpy as jnp
        _rk = jax.random.key(seed)
        x = -0.000125 + 0.9999 * jax.random.normal(jax.random.fold_in(_rk, 1), (64, 64, 256), jnp.float32)
        _lenS = 64 - jax.random.randint(jax.random.fold_in(_rk, 7), (64,), 0, max(1, 64 // 4) + 1, jnp.int32)
        _lenS2 = 64 - jax.random.randint(jax.random.fold_in(_rk, 8), (64,), 0, max(1, 64 // 4) + 1, jnp.int32)
        _ctx_2048P = jax.random.normal(jax.random.fold_in(_rk, 11), (64, 16, 256), jnp.float32)
        _ctx_2048c = jax.random.dirichlet(jax.random.fold_in(_rk, 511), 0.3 * jnp.ones((16,), jnp.float32), (64, 64))
        _ctx_2048t = jnp.einsum('bsk,bkd->bsd', _ctx_2048c, _ctx_2048P)
        _ctx_2048t = _ctx_2048t * jax.lax.rsqrt(jnp.mean(jnp.square(_ctx_2048t)) + 1e-12) * 0.953939
        ctx_2048 = -0.000514642 + 1.00011 * (_ctx_2048t + 0.3 * jax.random.normal(jax.random.fold_in(_rk, 611), (64, 64, 256), jnp.float32))
        itok_BxS_0_1023 = jax.random.randint(jax.random.fold_in(_rk, 13), (64, 64), 0, 128, jnp.int32)
        _validS = jnp.arange(64)[None, :] < _lenS[:, None]
        _validS2 = jnp.arange(64)[None, :] < _lenS2[:, None]
        _causal = jnp.tril(jnp.ones((64, 64), dtype=bool))
        mask_BxS2_bk0 = jnp.logical_not(jnp.broadcast_to(_validS2[:, :], (64, 64)))
        return (x, ctx_2048, itok_BxS_0_1023, mask_BxS2_bk0)
    x, ctx_2048, itok_BxS_0_1023, mask_BxS2_bk0 = _rec_inputs()

    def _L0_xattn_setup():
        import jax, jax.numpy as jnp
        import numpy as np
        key = jax.random.key(seed)
        k1, k2, k3 = jax.random.split(key, 3)
        B, S, D, M = (8, 256, 256, 128)
        hidden_states = jax.random.normal(k1, (B, S, D), dtype=jnp.float32)
        memory_tokens = jax.random.normal(k2, (B, M, D), dtype=jnp.float32)
        memory_mask = jax.random.randint(k3, (B, M), 0, 2).astype(jnp.bool_)
        return {'hidden_states': hidden_states, 'memory_tokens': memory_tokens, 'memory_mask': memory_mask}
    _L0_xattn_all = _L0_xattn_setup()
    _L0_xattn_in = {k: v for k, v in _L0_xattn_all.items() if k in ()}
    del _L0_xattn_all

    def _L0_ffn_setup():
        import jax, jax.numpy as jnp
        import numpy as np
        E = 32
        K = 4
        G = 4
        TG = 2
        H = 256
        F = 128
        FS = 256
        SCALE = 2.0
        B, S = (2, 128)
        N = B * S
        CAP = 2 * (N * K // E)

        def _gate(x, gate_w, gate_bias):
            logits = x @ gate_w.T
            scores = jax.nn.sigmoid(logits)
            sc = scores + gate_bias
            n = x.shape[0]
            grp = sc.reshape(n, G, E // G)
            group_scores = jax.lax.top_k(grp, 2)[0].sum(-1)
            _, gidx = jax.lax.top_k(group_scores, TG)
            gmask = jnp.zeros((n, G), sc.dtype).at[jnp.arange(n)[:, None], gidx].set(1.0)
            smask = jnp.repeat(gmask, E // G, axis=1)
            tmp = jnp.where(smask > 0, sc, 0.0)
            _, topk_idx = jax.lax.top_k(tmp, K)
            topk_w = jnp.take_along_axis(scores, topk_idx, axis=1)
            topk_w = topk_w / (topk_w.sum(-1, keepdims=True) + 1e-20)
            return (topk_idx, topk_w * SCALE)

        def _moe(x, topk_idx, topk_w, w1, w2, w3):
            n = x.shape[0]
            flat_e = topk_idx.reshape(-1)
            oh = jax.nn.one_hot(flat_e, E, dtype=jnp.int32)
            pos = (jnp.cumsum(oh, axis=0) * oh).sum(-1) - 1
            keep = pos < CAP
            slot = jnp.where(keep, pos, CAP)
            x_rep = jnp.repeat(x, K, axis=0)
            buf = jnp.zeros((E, CAP, H), x.dtype).at[flat_e, slot].set(x_rep, mode='drop')
            h = jax.nn.silu(jnp.einsum('ech,ehf->ecf', buf, w1)) * jnp.einsum('ech,ehf->ecf', buf, w3)
            ob = jnp.einsum('ecf,efh->ech', h, w2)
            y = ob[flat_e, jnp.minimum(slot, CAP - 1)]
            y = jnp.where(keep[:, None], y, 0.0)
            return (y.reshape(n, K, H) * topk_w[:, :, None]).sum(1)
        key = jax.random.key(seed)
        ks = jax.random.split(key, 9)
        w = 0.02
        return {'hidden_states': jax.random.normal(ks[0], (B, S, H), jnp.float32), 'gate_w': jax.random.normal(ks[1], (E, H), jnp.float32) * w, 'gate_bias': jax.random.normal(ks[2], (E,), jnp.float32) * w, 'w1': jax.random.normal(ks[3], (E, H, F), jnp.float32) * w, 'w2': jax.random.normal(ks[4], (E, F, H), jnp.float32) * w, 'w3': jax.random.normal(ks[5], (E, H, F), jnp.float32) * w, 'shared_gate': jax.random.normal(ks[6], (H, FS), jnp.float32) * w, 'shared_up': jax.random.normal(ks[7], (H, FS), jnp.float32) * w, 'shared_down': jax.random.normal(ks[8], (FS, H), jnp.float32) * w}
    _L0_ffn_all = _L0_ffn_setup()
    _L0_ffn_in = {k: v for k, v in _L0_ffn_all.items() if k in ('gate_w', 'gate_bias', 'w1', 'w2', 'w3', 'shared_gate', 'shared_up', 'shared_down')}
    del _L0_ffn_all

    def _L1_xattn_setup():
        import jax, jax.numpy as jnp
        import numpy as np
        B, S, DIM, HD = (4, 128, 256, 128)
        H = DIM // HD
        GN_EPS = 0.001

        def _decay_masks(n_heads, seq_len):
            gam = 1.0 - 2.0 ** (-5.0 - jnp.arange(n_heads, dtype=jnp.float32))
            idx = jnp.arange(seq_len, dtype=jnp.float32)
            expo = idx[None, :] - idx[:, None]
            D = jnp.where(expo[None, :, :] <= 0, gam[:, None, None] ** expo[None, :, :], 0.0)
            return D / jnp.sqrt(D.sum(axis=-1))[:, None, :]
        key = jax.random.key(seed)
        ks = jax.random.split(key, 8)
        x = jax.random.normal(ks[0], (B, S, DIM), dtype=jnp.float32)
        k = jax.random.normal(ks[1], (B, S, DIM), dtype=jnp.float32)
        v = jax.random.normal(ks[2], (B, S, DIM), dtype=jnp.float32)
        Wh = jax.random.normal(ks[3], (H, HD, HD), dtype=jnp.float32) / np.sqrt(HD)
        wg_w = jax.random.normal(ks[4], (DIM, DIM), dtype=jnp.float32) / np.sqrt(DIM)
        wo_w = jax.random.normal(ks[5], (DIM, DIM), dtype=jnp.float32) / np.sqrt(DIM)
        gn_gamma = jnp.ones((DIM,), dtype=jnp.float32)
        gn_beta = jnp.zeros((DIM,), dtype=jnp.float32)
        return {'x': x, 'k': k, 'v': v, 'Wh': Wh, 'wg_w': wg_w, 'wo_w': wo_w, 'gn_gamma': gn_gamma, 'gn_beta': gn_beta}
    _L1_xattn_all = _L1_xattn_setup()
    _L1_xattn_in = {k: v for k, v in _L1_xattn_all.items() if k in ('Wh', 'wg_w', 'wo_w', 'gn_gamma', 'gn_beta')}
    del _L1_xattn_all

    def _L1_ffn_setup():
        import jax, jax.numpy as jnp
        import numpy as np
        EPS = 1e-06
        K_STEPS = 4
        USE_GATING = True

        def layer_norm(x, gamma, beta):
            mu = jnp.mean(x, axis=-1, keepdims=True)
            var = jnp.mean(jnp.square(x - mu), axis=-1, keepdims=True)
            return (x - mu) * jax.lax.rsqrt(var + EPS) * gamma + beta
        key = jax.random.key(seed)
        B, L, D, H = (4, 512, 256, 1024)
        ks = jax.random.split(key, 16)
        s = 0.02
        return {'x': jax.random.normal(ks[0], (B, L, D), dtype=jnp.float32), 'in_gamma': jnp.ones((D,), jnp.float32), 'in_beta': jnp.zeros((D,), jnp.float32), 'agg_w': jax.random.normal(ks[1], (D, D), jnp.float32) * s, 'agg_b': jnp.zeros((D,), jnp.float32), 'pn_gamma': jnp.ones((D,), jnp.float32), 'pn_beta': jnp.zeros((D,), jnp.float32), 'd1_w': jax.random.normal(ks[2], (D, H), jnp.float32) * s, 'd1_b': jnp.zeros((H,), jnp.float32), 'd2_w': jax.random.normal(ks[3], (H, D), jnp.float32) * s, 'd2_b': jnp.zeros((D,), jnp.float32), 'bc_w': jax.random.normal(ks[4], (D, D), jnp.float32) * s, 'bc_b': jnp.zeros((D,), jnp.float32), 'gate_w': jax.random.normal(ks[5], (D, D), jnp.float32) * s, 'gate_b': jnp.zeros((D,), jnp.float32), 'out_gamma': jnp.ones((D,), jnp.float32), 'out_beta': jnp.zeros((D,), jnp.float32)}
    _L1_ffn_all = _L1_ffn_setup()
    _L1_ffn_in = {k: v for k, v in _L1_ffn_all.items() if k in ('in_gamma', 'in_beta', 'agg_w', 'agg_b', 'pn_gamma', 'pn_beta', 'd1_w', 'd1_b', 'd2_w', 'd2_b', 'bc_w', 'bc_b', 'gate_w', 'gate_b', 'out_gamma', 'out_beta')}
    del _L1_ffn_all

    def _L2_xattn_setup():
        import jax, jax.numpy as jnp
        import numpy as np
        B, Lq, Lk = (2, 512, 128)
        Q_DIM, KV_DIM = (256, 256)
        H, HD = (16, 128)
        KVC, QC, R = (64, 96, 64)
        LOOKBACK = 8
        NEG = -1e+30

        def _rope(x, L):
            half = x.shape[-1] // 2
            inv_freq = 1.0 / 10000.0 ** (jnp.arange(half, dtype=jnp.float32) / half)
            ang = jnp.arange(L, dtype=jnp.float32)[:, None] * inv_freq
            cos, sin = (jnp.cos(ang), jnp.sin(ang))
            x1, x2 = (x[..., :half], x[..., half:])
            return jnp.concatenate([x1 * cos - x2 * sin, x1 * sin + x2 * cos], axis=-1)
        key = jax.random.key(seed)
        ks = jax.random.split(key, 11)

        def w(k, shape, fan_in):
            return jax.random.normal(k, shape, jnp.float32) / np.sqrt(fan_in).astype(np.float32)
        return {'q': jax.random.normal(ks[0], (B, Lq, Q_DIM), jnp.float32), 'kv': jax.random.normal(ks[1], (B, Lk, KV_DIM), jnp.float32), 'seg_id': jnp.sort(jax.random.randint(ks[2], (B, Lq), 0, Lk), axis=-1), 'W_kvc': w(ks[3], (KV_DIM, KVC), KV_DIM), 'W_dq': w(ks[4], (Q_DIM, QC), Q_DIM), 'W_uq': w(ks[5], (QC, H * HD), QC), 'W_qr': w(ks[6], (QC, H * R), QC), 'W_uk': w(ks[7], (KVC, H * HD), KVC), 'W_kr': w(ks[8], (KVC, R), KVC), 'W_uv': w(ks[9], (KVC, H * HD), KVC), 'W_o': w(ks[10], (H * HD, Q_DIM), H * HD)}
    _L2_xattn_all = _L2_xattn_setup()
    _L2_xattn_in = {k: v for k, v in _L2_xattn_all.items() if k in ('W_kvc', 'W_dq', 'W_uq', 'W_qr', 'W_uk', 'W_kr', 'W_uv', 'W_o')}
    del _L2_xattn_all

    def _L2_ffn_setup():
        import jax, jax.numpy as jnp
        import numpy as np
        EPS = 1e-08

        def _quantize(w):
            gamma = jnp.mean(jnp.abs(w))
            return jnp.clip(jnp.round(w / (gamma + EPS)), -1.0, 1.0)

        def _bitlinear(x, w):
            return jnp.matmul(x, _quantize(w).T)
        key = jax.random.key(seed)
        k1, k2, k3, k4 = jax.random.split(key, 4)
        d, h = (256, 704)
        x = jax.random.normal(k1, (4, 256, d), dtype=jnp.float32)
        w1 = jax.random.normal(k2, (h, d), dtype=jnp.float32)
        w2 = jax.random.normal(k3, (h, d), dtype=jnp.float32)
        w3 = jax.random.normal(k4, (d, h), dtype=jnp.float32)
        return {'x': x, 'w1': w1, 'w2': w2, 'w3': w3}
    _L2_ffn_all = _L2_ffn_setup()
    _L2_ffn_in = {k: v for k, v in _L2_ffn_all.items() if k in ('w1', 'w2', 'w3')}
    del _L2_ffn_all

    def _L3_xattn_setup():
        import jax, jax.numpy as jnp
        import numpy as np
        N_HEAD = 8
        key = jax.random.key(seed)
        k1, k2, k3 = jax.random.split(key, 3)
        B, D, L = (4, 128, 256)
        q = jax.random.normal(k1, (B, D, L), dtype=jnp.float32)
        k = jax.random.normal(k2, (B, D, L), dtype=jnp.float32)
        v = jax.random.normal(k3, (B, D, L), dtype=jnp.float32)
        gamma = jnp.ones((), dtype=jnp.float32)
        return {'q': q, 'k': k, 'v': v, 'gamma': gamma}
    _L3_xattn_all = _L3_xattn_setup()
    _L3_xattn_in = {k: v for k, v in _L3_xattn_all.items() if k in ('gamma',)}
    del _L3_xattn_all

    def _L3_ffn_setup():
        import jax, jax.numpy as jnp
        import numpy as np
        B, S, D = (2, 256, 256)
        E, H, TOP_K = (8, 176, 2)
        SH = 176
        ROUTED_SCALE = 2.5
        key = jax.random.key(seed)
        ks = jax.random.split(key, 8)
        std = 0.02
        return {'x': jax.random.normal(ks[0], (B, S, D), jnp.float32), 'gate_w': jax.random.normal(ks[1], (E, D), jnp.float32) * std, 'w1': jax.random.normal(ks[2], (E, D, H), jnp.float32) * std, 'w3': jax.random.normal(ks[3], (E, D, H), jnp.float32) * std, 'w2': jax.random.normal(ks[4], (E, H, D), jnp.float32) * std, 'sw1': jax.random.normal(ks[5], (D, SH), jnp.float32) * std, 'sw3': jax.random.normal(ks[6], (D, SH), jnp.float32) * std, 'sw2': jax.random.normal(ks[7], (SH, D), jnp.float32) * std}
    _L3_ffn_all = _L3_ffn_setup()
    _L3_ffn_in = {k: v for k, v in _L3_ffn_all.items() if k in ('gate_w', 'w1', 'w2', 'w3', 'sw1', 'sw2', 'sw3')}
    del _L3_ffn_all
    return {'x': x, 'ctx_2048': ctx_2048, 'itok_BxS_0_1023': itok_BxS_0_1023, 'mask_BxS2_bk0': mask_BxS2_bk0, 'L0_ffn_gate_w': _L0_ffn_in['gate_w'], 'L0_ffn_gate_bias': _L0_ffn_in['gate_bias'], 'L0_ffn_w1': _L0_ffn_in['w1'], 'L0_ffn_w2': _L0_ffn_in['w2'], 'L0_ffn_w3': _L0_ffn_in['w3'], 'L0_ffn_shared_gate': _L0_ffn_in['shared_gate'], 'L0_ffn_shared_up': _L0_ffn_in['shared_up'], 'L0_ffn_shared_down': _L0_ffn_in['shared_down'], 'L1_xattn_Wh': _L1_xattn_in['Wh'], 'L1_xattn_wg_w': _L1_xattn_in['wg_w'], 'L1_xattn_wo_w': _L1_xattn_in['wo_w'], 'L1_xattn_gn_gamma': _L1_xattn_in['gn_gamma'], 'L1_xattn_gn_beta': _L1_xattn_in['gn_beta'], 'L1_ffn_in_gamma': _L1_ffn_in['in_gamma'], 'L1_ffn_in_beta': _L1_ffn_in['in_beta'], 'L1_ffn_agg_w': _L1_ffn_in['agg_w'], 'L1_ffn_agg_b': _L1_ffn_in['agg_b'], 'L1_ffn_pn_gamma': _L1_ffn_in['pn_gamma'], 'L1_ffn_pn_beta': _L1_ffn_in['pn_beta'], 'L1_ffn_d1_w': _L1_ffn_in['d1_w'], 'L1_ffn_d1_b': _L1_ffn_in['d1_b'], 'L1_ffn_d2_w': _L1_ffn_in['d2_w'], 'L1_ffn_d2_b': _L1_ffn_in['d2_b'], 'L1_ffn_bc_w': _L1_ffn_in['bc_w'], 'L1_ffn_bc_b': _L1_ffn_in['bc_b'], 'L1_ffn_gate_w': _L1_ffn_in['gate_w'], 'L1_ffn_gate_b': _L1_ffn_in['gate_b'], 'L1_ffn_out_gamma': _L1_ffn_in['out_gamma'], 'L1_ffn_out_beta': _L1_ffn_in['out_beta'], 'L2_xattn_W_kvc': _L2_xattn_in['W_kvc'], 'L2_xattn_W_dq': _L2_xattn_in['W_dq'], 'L2_xattn_W_uq': _L2_xattn_in['W_uq'], 'L2_xattn_W_qr': _L2_xattn_in['W_qr'], 'L2_xattn_W_uk': _L2_xattn_in['W_uk'], 'L2_xattn_W_kr': _L2_xattn_in['W_kr'], 'L2_xattn_W_uv': _L2_xattn_in['W_uv'], 'L2_xattn_W_o': _L2_xattn_in['W_o'], 'L2_ffn_w1': _L2_ffn_in['w1'], 'L2_ffn_w2': _L2_ffn_in['w2'], 'L2_ffn_w3': _L2_ffn_in['w3'], 'L3_xattn_gamma': _L3_xattn_in['gamma'], 'L3_ffn_gate_w': _L3_ffn_in['gate_w'], 'L3_ffn_w1': _L3_ffn_in['w1'], 'L3_ffn_w2': _L3_ffn_in['w2'], 'L3_ffn_w3': _L3_ffn_in['w3'], 'L3_ffn_sw1': _L3_ffn_in['sw1'], 'L3_ffn_sw2': _L3_ffn_in['sw2'], 'L3_ffn_sw3': _L3_ffn_in['sw3']}

def reference(x, ctx_2048, itok_BxS_0_1023, mask_BxS2_bk0, L0_ffn_gate_w, L0_ffn_gate_bias, L0_ffn_w1, L0_ffn_w2, L0_ffn_w3, L0_ffn_shared_gate, L0_ffn_shared_up, L0_ffn_shared_down, L1_xattn_Wh, L1_xattn_wg_w, L1_xattn_wo_w, L1_xattn_gn_gamma, L1_xattn_gn_beta, L1_ffn_in_gamma, L1_ffn_in_beta, L1_ffn_agg_w, L1_ffn_agg_b, L1_ffn_pn_gamma, L1_ffn_pn_beta, L1_ffn_d1_w, L1_ffn_d1_b, L1_ffn_d2_w, L1_ffn_d2_b, L1_ffn_bc_w, L1_ffn_bc_b, L1_ffn_gate_w, L1_ffn_gate_b, L1_ffn_out_gamma, L1_ffn_out_beta, L2_xattn_W_kvc, L2_xattn_W_dq, L2_xattn_W_uq, L2_xattn_W_qr, L2_xattn_W_uk, L2_xattn_W_kr, L2_xattn_W_uv, L2_xattn_W_o, L2_ffn_w1, L2_ffn_w2, L2_ffn_w3, L3_xattn_gamma, L3_ffn_gate_w, L3_ffn_w1, L3_ffn_w2, L3_ffn_w3, L3_ffn_sw1, L3_ffn_sw2, L3_ffn_sw3):
    import jax
    import jax.numpy as jnp

    def _L0_xattn_ref(hidden_states, memory_tokens, memory_mask):
        import jax, jax.numpy as jnp
        import numpy as np
        B, S, D = hidden_states.shape
        scale = 1.0 / jnp.sqrt(jnp.asarray(D, hidden_states.dtype))
        scores = jnp.einsum('bsd,bmd->bsm', hidden_states, memory_tokens) * scale
        neg_inf = jnp.asarray(-1e+30, scores.dtype)
        scores = jnp.where(memory_mask[:, None, :], scores, neg_inf)
        attn = jax.nn.softmax(scores, axis=-1)
        readout = jnp.einsum('bsm,bmd->bsd', attn, memory_tokens)
        valid_b = jnp.any(memory_mask, axis=-1)
        out = jnp.where(valid_b[:, None, None], readout, jnp.zeros_like(readout))
        return out

    def _L0_ffn_ref(hidden_states, gate_w, gate_bias, w1, w2, w3, shared_gate, shared_up, shared_down):
        import jax, jax.numpy as jnp
        import numpy as np
        E = 32
        K = 4
        G = 4
        TG = 2
        H = 256
        F = 128
        FS = 256
        SCALE = 2.0
        B, S = (2, 128)
        N = B * S
        CAP = 2 * (N * K // E)

        def _gate(x, gate_w, gate_bias):
            logits = x @ gate_w.T
            scores = jax.nn.sigmoid(logits)
            sc = scores + gate_bias
            n = x.shape[0]
            grp = sc.reshape(n, G, E // G)
            group_scores = jax.lax.top_k(grp, 2)[0].sum(-1)
            _, gidx = jax.lax.top_k(group_scores, TG)
            gmask = jnp.zeros((n, G), sc.dtype).at[jnp.arange(n)[:, None], gidx].set(1.0)
            smask = jnp.repeat(gmask, E // G, axis=1)
            tmp = jnp.where(smask > 0, sc, 0.0)
            _, topk_idx = jax.lax.top_k(tmp, K)
            topk_w = jnp.take_along_axis(scores, topk_idx, axis=1)
            topk_w = topk_w / (topk_w.sum(-1, keepdims=True) + 1e-20)
            return (topk_idx, topk_w * SCALE)

        def _moe(x, topk_idx, topk_w, w1, w2, w3):
            n = x.shape[0]
            flat_e = topk_idx.reshape(-1)
            oh = jax.nn.one_hot(flat_e, E, dtype=jnp.int32)
            pos = (jnp.cumsum(oh, axis=0) * oh).sum(-1) - 1
            keep = pos < CAP
            slot = jnp.where(keep, pos, CAP)
            x_rep = jnp.repeat(x, K, axis=0)
            buf = jnp.zeros((E, CAP, H), x.dtype).at[flat_e, slot].set(x_rep, mode='drop')
            h = jax.nn.silu(jnp.einsum('ech,ehf->ecf', buf, w1)) * jnp.einsum('ech,ehf->ecf', buf, w3)
            ob = jnp.einsum('ecf,efh->ech', h, w2)
            y = ob[flat_e, jnp.minimum(slot, CAP - 1)]
            y = jnp.where(keep[:, None], y, 0.0)
            return (y.reshape(n, K, H) * topk_w[:, :, None]).sum(1)
        b, s, h = hidden_states.shape
        x = hidden_states.reshape(-1, h)
        topk_idx, topk_w = _gate(x, gate_w, gate_bias)
        out = _moe(x, topk_idx, topk_w, w1, w2, w3)
        shared = jax.nn.silu(x @ shared_gate) * (x @ shared_up) @ shared_down
        return (out + shared).reshape(b, s, h)

    def _L1_xattn_ref(x, k, v, Wh, wg_w, wo_w, gn_gamma, gn_beta):
        import jax, jax.numpy as jnp
        import numpy as np
        B, S, DIM, HD = (4, 128, 256, 128)
        H = DIM // HD
        GN_EPS = 0.001

        def _decay_masks(n_heads, seq_len):
            gam = 1.0 - 2.0 ** (-5.0 - jnp.arange(n_heads, dtype=jnp.float32))
            idx = jnp.arange(seq_len, dtype=jnp.float32)
            expo = idx[None, :] - idx[:, None]
            D = jnp.where(expo[None, :, :] <= 0, gam[:, None, None] ** expo[None, :, :], 0.0)
            return D / jnp.sqrt(D.sum(axis=-1))[:, None, :]
        b, s, dim = x.shape
        h, hd, _ = Wh.shape
        xh = x.reshape(b, s, h, hd)
        kh = k.reshape(b, s, h, hd)
        vh = v.reshape(b, s, h, hd)
        Q = jnp.einsum('bshd,hde->bshe', xh, Wh)
        K = jnp.einsum('bshd,hde->bshe', kh, Wh)
        V = jnp.einsum('bshd,hde->bshe', vh, Wh)
        scores = jnp.einsum('bshe,bthe->bhst', Q, K) / jnp.sqrt(jnp.float32(hd))
        Dn = _decay_masks(h, s)
        masked = scores * Dn[None, :, :, :]
        A = jnp.maximum(jnp.abs(masked.sum(axis=0)), 1.0)
        O = jnp.einsum('hst,bthe->bshe', A, V).reshape(b, s, dim)
        mu = O.mean(axis=-1, keepdims=True)
        var = O.var(axis=-1, keepdims=True)
        Y = (O - mu) / jnp.sqrt(var + GN_EPS) * gn_gamma + gn_beta
        W = jax.nn.relu(x @ wg_w)
        return W * Y @ wo_w

    def _L1_ffn_ref(x, in_gamma, in_beta, agg_w, agg_b, pn_gamma, pn_beta, d1_w, d1_b, d2_w, d2_b, bc_w, bc_b, gate_w, gate_b, out_gamma, out_beta):
        import jax, jax.numpy as jnp
        import numpy as np
        EPS = 1e-06
        K_STEPS = 4
        USE_GATING = True

        def layer_norm(x, gamma, beta):
            mu = jnp.mean(x, axis=-1, keepdims=True)
            var = jnp.mean(jnp.square(x - mu), axis=-1, keepdims=True)
            return (x - mu) * jax.lax.rsqrt(var + EPS) * gamma + beta
        x_norm = layer_norm(x, in_gamma, in_beta)
        thought = x_norm[:, -1, :] @ agg_w + agg_b
        for _ in range(K_STEPS):
            t = layer_norm(thought, pn_gamma, pn_beta)
            t = jax.nn.gelu(t @ d1_w + d1_b, approximate=False)
            thought = thought + (t @ d2_w + d2_b)
        broadcast = (thought @ bc_w + bc_b)[:, None, :]
        if USE_GATING:
            gate = jax.nn.sigmoid(x @ gate_w + gate_b)
            out = x + gate * broadcast
        else:
            out = x + broadcast
        return layer_norm(out, out_gamma, out_beta)

    def _L2_xattn_ref(q, kv, seg_id, W_kvc, W_dq, W_uq, W_qr, W_uk, W_kr, W_uv, W_o):
        import jax, jax.numpy as jnp
        import numpy as np
        B, Lq, Lk = (2, 512, 128)
        Q_DIM, KV_DIM = (256, 256)
        H, HD = (16, 128)
        KVC, QC, R = (64, 96, 64)
        LOOKBACK = 8
        NEG = -1e+30

        def _rope(x, L):
            half = x.shape[-1] // 2
            inv_freq = 1.0 / 10000.0 ** (jnp.arange(half, dtype=jnp.float32) / half)
            ang = jnp.arange(L, dtype=jnp.float32)[:, None] * inv_freq
            cos, sin = (jnp.cos(ang), jnp.sin(ang))
            x1, x2 = (x[..., :half], x[..., half:])
            return jnp.concatenate([x1 * cos - x2 * sin, x1 * sin + x2 * cos], axis=-1)
        b, lq, _ = q.shape
        lk = kv.shape[1]
        kv_c = kv @ W_kvc
        q_c = q @ W_dq
        q_nope = (q_c @ W_uq).reshape(b, lq, H, HD).transpose(0, 2, 1, 3)
        q_rope = (q_c @ W_qr).reshape(b, lq, H, R).transpose(0, 2, 1, 3)
        k_nope = (kv_c @ W_uk).reshape(b, lk, H, HD)
        v = (kv_c @ W_uv).reshape(b, lk, H, HD)
        k_rope = kv_c @ W_kr
        q_rope = _rope(q_rope, lq)
        k_rope = _rope(k_rope, lk)
        scale = 1.0 / np.sqrt(HD + R).astype(np.float32)
        scores = (jnp.einsum('bhqd,bkhd->bhqk', q_nope, k_nope) + jnp.einsum('bhqr,bkr->bhqk', q_rope, k_rope)) * scale
        k_ids = jnp.arange(lk)[None, None, :]
        qs = seg_id[:, :, None]
        good = (k_ids <= qs) & (k_ids >= qs - LOOKBACK)
        scores = jnp.where(good[:, None, :, :], scores, NEG)
        attn = jax.nn.softmax(scores, axis=-1)
        out = jnp.einsum('bhqk,bkhd->bqhd', attn, v).reshape(b, lq, H * HD)
        return out @ W_o

    def _L2_ffn_ref(x, w1, w2, w3):
        import jax, jax.numpy as jnp
        import numpy as np
        EPS = 1e-08

        def _quantize(w):
            gamma = jnp.mean(jnp.abs(w))
            return jnp.clip(jnp.round(w / (gamma + EPS)), -1.0, 1.0)

        def _bitlinear(x, w):
            return jnp.matmul(x, _quantize(w).T)
        x1 = _bitlinear(x, w1)
        x2 = _bitlinear(x, w2)
        hidden = jax.nn.sigmoid(x1) * x2
        return _bitlinear(hidden, w3)

    def _L3_xattn_ref(q, k, v, gamma):
        import jax, jax.numpy as jnp
        import numpy as np
        N_HEAD = 8
        B, Dq, Lq = q.shape
        Dv, Lk = (v.shape[-2], v.shape[-1])
        h = N_HEAD
        dq = Dq // h
        dv = Dv // h
        qh = q.reshape(B, h, dq, Lq)
        kh = k.reshape(B, h, dq, Lk)
        vh = v.reshape(B, h, dv, Lk)
        scale = 1.0 / jnp.sqrt(jnp.asarray(dq, dtype=q.dtype))
        qk = jnp.einsum('bhdq,bhdl->bhql', qh, kh) * scale
        sm = jax.nn.softmax(qk, axis=-1)
        ret = jnp.einsum('bhql,bhdl->bhdq', sm, vh)
        ret = ret.reshape(B, Dv, Lq)
        return gamma * ret

    def _L3_ffn_ref(x, gate_w, w1, w2, w3, sw1, sw2, sw3):
        import jax, jax.numpy as jnp
        import numpy as np
        B, S, D = (2, 256, 256)
        E, H, TOP_K = (8, 176, 2)
        SH = 176
        ROUTED_SCALE = 2.5
        b, s, d = x.shape
        xt = x.reshape(b * s, d)
        scores = jax.nn.sigmoid(xt @ gate_w.T)
        top_scores, top_idx = jax.lax.top_k(scores, TOP_K)
        top_scores = top_scores / (jnp.sum(top_scores, axis=-1, keepdims=True) + 1e-20)
        top_scores = top_scores * ROUTED_SCALE
        combine = jnp.sum(jax.nn.one_hot(top_idx, E, dtype=xt.dtype) * top_scores[..., None], axis=1)
        h = jnp.einsum('td,edh->eth', xt, w1)
        u = jnp.einsum('td,edh->eth', xt, w3)
        y = jnp.einsum('eth,ehd->etd', jax.nn.silu(h) * u, w2)
        routed = jnp.einsum('etd,te->td', y, combine)
        shared = jax.nn.silu(xt @ sw1) * (xt @ sw3) @ sw2
        return (routed + shared).reshape(b, s, d)
    x = x + _L0_xattn_ref(_layernorm(x, axis=-1), ctx_2048, mask_BxS2_bk0)
    x = x + _L0_ffn_ref(_layernorm(x, axis=-1), L0_ffn_gate_w, L0_ffn_gate_bias, L0_ffn_w1, L0_ffn_w2, L0_ffn_w3, L0_ffn_shared_gate, L0_ffn_shared_up, L0_ffn_shared_down)
    x = x + _L1_xattn_ref(_layernorm(x, axis=-1), ctx_2048, ctx_2048, L1_xattn_Wh, L1_xattn_wg_w, L1_xattn_wo_w, L1_xattn_gn_gamma, L1_xattn_gn_beta)
    x = x + _L1_ffn_ref(_layernorm(x, axis=-1), L1_ffn_in_gamma, L1_ffn_in_beta, L1_ffn_agg_w, L1_ffn_agg_b, L1_ffn_pn_gamma, L1_ffn_pn_beta, L1_ffn_d1_w, L1_ffn_d1_b, L1_ffn_d2_w, L1_ffn_d2_b, L1_ffn_bc_w, L1_ffn_bc_b, L1_ffn_gate_w, L1_ffn_gate_b, L1_ffn_out_gamma, L1_ffn_out_beta)
    x = x + _L2_xattn_ref(_layernorm(x, axis=-1), ctx_2048, itok_BxS_0_1023, L2_xattn_W_kvc, L2_xattn_W_dq, L2_xattn_W_uq, L2_xattn_W_qr, L2_xattn_W_uk, L2_xattn_W_kr, L2_xattn_W_uv, L2_xattn_W_o)
    x = x + _L2_ffn_ref(_layernorm(x, axis=-1), L2_ffn_w1, L2_ffn_w2, L2_ffn_w3)
    x = x + _L3_xattn_ref(_layernorm(x, axis=-1), ctx_2048, ctx_2048, L3_xattn_gamma)
    x = x + _L3_ffn_ref(_layernorm(x, axis=-1), L3_ffn_gate_w, L3_ffn_w1, L3_ffn_w2, L3_ffn_w3, L3_ffn_sw1, L3_ffn_sw2, L3_ffn_sw3)
    return x

_drawn_inputs = setup_inputs


def setup_inputs(seed=0):
    import zlib

    import numpy as np

    out = dict(_drawn_inputs(seed))
    spreads = {'L1_xattn_gn_gamma': (1.0, 0.2),
     'L1_xattn_gn_beta': (0.0, 0.1),
     'L1_ffn_in_gamma': (1.0, 0.6),
     'L1_ffn_in_beta': (0.0, 0.8),
     'L1_ffn_agg_b': (0.0, 0.365),
     'L1_ffn_pn_gamma': (1.0, 0.6),
     'L1_ffn_pn_beta': (0.0, 0.8),
     'L1_ffn_d1_b': (0.0, 0.446),
     'L1_ffn_d2_b': (0.0, 0.1),
     'L1_ffn_bc_b': (0.0, 0.1),
     'L1_ffn_gate_b': (0.0, 0.8),
     'L1_ffn_out_gamma': (1.0, 0.2),
     'L1_ffn_out_beta': (0.0, 0.1)}
    factors = {'L0_ffn_gate_w': 8.0,
     'L0_ffn_gate_bias': 8.0,
     'L0_ffn_w1': 8.0,
     'L0_ffn_w2': 8.0,
     'L0_ffn_w3': 8.0,
     'L1_ffn_gate_w': 4.239,
     'L3_ffn_gate_w': 8.0,
     'L3_ffn_w1': 8.0,
     'L3_ffn_w2': 8.0,
     'L3_ffn_w3': 8.0,
     'L3_ffn_sw1': 8.0,
     'L3_ffn_sw2': 8.0,
     'L3_ffn_sw3': 8.0}
    for name, (base, spread) in spreads.items():
        noise = np.random.default_rng([zlib.crc32(name.encode()), seed]).standard_normal(out[name].shape)
        drawn = base * np.exp(spread * noise) if base else spread * noise
        out[name] = jnp.asarray(drawn.astype(out[name].dtype))
    for name, factor in factors.items():
        out[name] = (out[name] * factor).astype(out[name].dtype)
    return out
```

```python
from contextlib import ExitStack

import numpy as np

import concourse.bass as bass
from concourse import mybir

ALU = mybir.AluOpType
ACT = mybir.ActivationFunctionType
AX = mybir.AxisListType
F32 = mybir.dt.float32
BF16 = mybir.dt.bfloat16
I32 = mybir.dt.int32
U32 = mybir.dt.uint32
U8 = mybir.dt.uint8

P = 128
B, S, D = 64, 64, 256
N = B * S
NT = N // P
DK = D // P
LN_EPS = 1e-5
NEG = -1e30

E0, TOP0, G0, TG0, F0, FS0, SCALE0 = 32, 4, 4, 2, 128, 256, 2.0
CAP0 = 2 * (256 * TOP0 // E0)
NX = N + CAP0
H1, HD1, GN_EPS = 2, 128, 1e-3
EPS1, STEPS1, HID1 = 1e-6, 4, 1024
H2, HD2, KVC, QC, R2, LOOKBACK = 16, 128, 64, 96, 64, 8
HID2, EPS2 = 704, 1e-8
H3 = 8
DQ3 = S // H3
E3, HID3, TOP3, SCALE3 = 8, 176, 2, 2.5
HH3 = HID3 // 2

LANES = 2
CREDIT = LANES


def ready(t):
    return t + 1 + CREDIT


def freed(t):
    return t + 1


def loaded(i):
    return 16 * i + 16


def stored(i):
    return 16 * i + 32


def store_freed(i):
    return 16 * i + 16


def settle(eng, passed):
    eng.sem_inc(passed, 1)


class Chain:

    def __init__(self, eng, sem, start=0):
        self.eng, self.sem, self.start, self.n = eng, sem, start, 0

    def link(self, ins):
        self.n += 1
        ins.then_inc(self.sem, 1)
        self.eng.wait_ge(self.sem, self.start + self.n)


CONSTS = {}
_at = 0
for _name, _width in (("ident", 128), ("cos", 128), ("sin", 128), ("before", 128), ("iota", 64),
                      ("decay", 128), ("lower", 16), ("one", 128)):
    CONSTS[_name] = (_at, _at + _width)
    _at += _width
CONST_W = _at


def constants():
    c = np.zeros((P, CONST_W), np.float32)

    def put(name, v, rows=slice(0, P)):
        a, b = CONSTS[name]
        c[rows, a:b] = v

    put("ident", np.eye(P, dtype=np.float32))
    half = R2 // 2
    inv_freq = (np.float32(1.0) / np.float32(10000.0) ** (np.arange(half, dtype=np.float32) / np.float32(half))).astype(np.float32)
    ang = (np.arange(S, dtype=np.float32)[:, None] * inv_freq).astype(np.float32)
    cos, sin = (np.tile(f(ang).T.astype(np.float32), (1, 2)) for f in (np.cos, np.sin))
    put("cos", np.concatenate([cos, cos]), slice(64, 128))
    put("sin", np.concatenate([sin, -sin]), slice(64, 128))
    i = np.arange(P)
    put("before", (i[:, None] < i[None, :]).astype(np.float32))
    put("iota", np.arange(64, dtype=np.float32)[None, :])
    gam = (1.0 - 2.0 ** (-5.0 - np.arange(H1, dtype=np.float32))).astype(np.float32)
    expo = np.arange(S, dtype=np.float32)[None, :] - np.arange(S, dtype=np.float32)[:, None]
    dm = np.where(expo[None] <= 0, gam[:, None, None] ** expo[None], 0.0).astype(np.float32)
    dm = dm / np.sqrt(dm.sum(-1))[:, None, :] / np.sqrt(np.float32(HD1))
    put("decay", dm.transpose(1, 0, 2).reshape(S, H1 * S), slice(0, S))
    put("one", 1.0)
    low = (np.arange(G0)[None, :] < np.arange(G0)[:, None]).astype(np.float32)
    put("lower", low.reshape(1, 16))
    return c


class Core:
    pass


HELD = []
OPENED = []


def open_sems(nc, ctx, names):
    OPENED.append(names)
    got = {n: nc.alloc_semaphore(f"{n}_{len(OPENED)}") for n in names.split()}
    HELD.extend(got.values())
    return got


def recycle(nc):
    nc.clear_and_free_semaphores(list(HELD))
    HELD.clear()
    nc.all_engine_barrier()


def give_credit(pool, sems, names, step=1):
    for n in names.split():
        pool.sem_inc(sems[n], CREDIT * step)


def half(ap):
    return ap.rearrange("p (k n) -> p k n", k=DK)


def at_tile(ap, t):
    return ap[:, bass.ds(t, 1), :].rearrange("p a n -> p (a n)")


def finish_stats(nc, c, tag, eps=LN_EPS, src=None, mean=None, rstd=None):
    src, mean, rstd = src or c.bn, mean or c.mean, rstd or c.rstd
    with ExitStack() as ctx:
        s = open_sems(nc, ctx, f"{tag}_chain {tag}_var_ready {tag}_half_set {tag}_rstd_ready")
        block = ctx.enter_context(nc.Block())

        @block.vector
        def _(dve):
            ch = Chain(dve, s[f"{tag}_chain"])
            m_even, m_odd = src[:, :, 1], src[:, :, 4]
            v_even, v_odd = src[:, :, 2], src[:, :, 5]
            nc.vector.tensor_tensor(mean[:, :], m_even, m_odd, ALU.add)
            nc.vector.tensor_tensor(c.small[:, 0, :], m_even, m_odd, ALU.subtract)
            ch.link(nc.vector.tensor_tensor(c.small[:, 1, :], v_even, v_odd, ALU.add))
            nc.vector.tensor_scalar(mean[:, :], mean[:, :], 0.5, None, ALU.mult)
            ch.link(nc.vector.scalar_tensor_tensor(out=c.small[:, 2, :], in0=c.small[:, 0, :], scalar=0.25,
                                                   in1=c.small[:, 0, :], op0=ALU.mult, op1=ALU.mult))
            ch.link(nc.vector.scalar_tensor_tensor(out=c.small[:, 3, :], in0=c.small[:, 1, :], scalar=1.0 / D,
                                                   in1=c.small[:, 2, :], op0=ALU.mult, op1=ALU.add))
            nc.vector.tensor_scalar(c.small[:, 4, :], c.small[:, 3, :], eps, None,
                                    ALU.add).then_inc(s[f"{tag}_var_ready"], 1)

        @block.gpsimd
        def _(pool):
            nc.gpsimd.memset(c.minus_half[:, :], -0.5).then_inc(s[f"{tag}_half_set"], 1)
            pool.wait_ge(s[f"{tag}_half_set"], 1)
            pool.wait_ge(s[f"{tag}_var_ready"], 1)
            nc.gpsimd.tensor_tensor(rstd[:, :], c.small[:, 4, :], c.minus_half[:, :],
                                    ALU.pow).then_inc(s[f"{tag}_rstd_ready"], 1)
            pool.wait_ge(s[f"{tag}_rstd_ready"], 1)


def normalize(nc, c, out, t):
    return nc.vector.tensor_scalar(out, at_tile(c.x, t), c.mean[:, bass.ds(t, 1)], c.rstd[:, bass.ds(t, 1)],
                                   ALU.subtract, ALU.mult)


def transpose_tile(nc, c, bank, src):
    for k in range(DK):
        last = nc.tensor.transpose(bank[:, k * P:(k + 1) * P], src[:, k * P:(k + 1) * P], c.ident)
    return last


def stage_first(nc, c):
    with ExitStack() as ctx:
        s = open_sems(nc, ctx, "consts_loaded x_loaded first_stats")
        block = ctx.enter_context(nc.Block())
        xt = c.d["x"].rearrange("(n p) d -> p n d", p=P)

        @block.sync
        def _(sp):
            sp.dma_start(c.const[:, :], c.d["const"]).then_inc(s["consts_loaded"], 16)
            for n in range(4):
                sp.dma_start(c.x[:, 8 * n:8 * n + 8, :], xt[:, 8 * n:8 * n + 8, :]).then_inc(s["x_loaded"], 16)
            sp.wait_ge(s["consts_loaded"], 16)

        @block.vector
        def _(dve):
            dve.wait_ge(s["x_loaded"], 64)
            with dve.Fori(0, NT) as t:
                nc.vector.bn_stats(at_tile(c.bn, t), at_tile(c.x, t))


def stage_l0_attention(nc, c):
    with ExitStack() as ctx:
        sb = lambda n, sh, dt=F32: ctx.enter_context(nc.sbuf_tensor(n, sh, dt))
        wh = sb("wh", [P, H1, P]); whT = sb("whT", [P, H1, P]); gram = sb("gram", [P, H1, P])
        wkvcT = sb("wkvcT", [KVC, D]); wkr = sb("wkr", [KVC, R2]); wk = sb("wk", [P, DK, P])
        mask8 = sb("mask8", [P, NT, S], U8); keep = sb("keep", [P, NT, S]); drop = sb("drop", [P, NT, S])
        any_valid = sb("any_valid", [P, NT])
        xn = sb("xn_a", [P, LANES, D]); ctx_in = sb("ctx_in", [P, LANES, D]); fT = sb("fT_a", [P, LANES, 4, P])
        sc = sb("scores_a", [P, LANES, S]); prob = sb("prob_a", [P, LANES, P]); probT = sb("probT_a", [P, LANES, P])
        nmax = sb("nmax_a", [P, LANES]); tot = sb("tot_a", [P, LANES]); rec = sb("rec_a", [P, LANES])
        rot = sb("rot_a", [P, LANES, 2, P]); kraw = sb("kraw_a", [P, LANES, P])
        s = open_sems(nc, ctx, "a_weights a_masks a_pe_pre a_gram a_wk a_mask_chain a_mask_ready a_prob_zero "
                      "ctx_loaded0 ctx_loaded1 xn_ready feat_ready feat_copied v_ready v_copied keys_ready key_copied rot_ready "
                      "keys_done scores_ready soft_ready prob_ready probT_ready probT_copied read_ready x_done a_chain")
        block = ctx.enter_context(nc.Block())
        ctx_d = c.d["ctx"]
        ITER_LINKS = 12

        def feat(j): return c.bank[4 * j]
        def vg(j): return c.bank[4 * j + 1]
        def att(j): return c.bank[4 * j + 2]
        def keys(j): return c.bank[4 * j + 3]

        @block.sync
        def _(sp):
            for dst, src in ((wh[:, :, :], c.d["wh"].rearrange("h d e -> d h e")),
                             (whT[:, :, :], c.d["whT"].rearrange("h e d -> e h d")),
                             (wkvcT[:, :], c.d["wkvcT"]), (wkr[:, :], c.d["wkr"]),
                             (wk[:, :, 0:KVC], c.d["wkvc"].rearrange("(k p) n -> p k n", p=P))):
                sp.dma_start(dst, src).then_inc(s["a_weights"], 16)
            for b in range(2):
                src = c.d["mask"].rearrange("(t b) k -> b t k", b=2)[b:b + 1].broadcast_to([64, NT, S // 4])
                sp.dma_start(mask8[64 * b:64 * b + 64, :, :].bitcast(I32), src).then_inc(s["a_masks"], 16)
            with sp.Fori(0, NT // LANES) as i:
                for j in range(LANES):
                    t = i * LANES + j
                    sp.wait_ge(s["x_done"], freed(t))
                    sp.dma_start(ctx_in[:, j, :], ctx_d[bass.ds(t * P, P), :]).then_inc(s[f"ctx_loaded{j}"], 16)

        @block.gpsimd
        def _(pool):
            give_credit(pool, s, "xn_ready feat_ready feat_copied v_ready v_copied keys_ready key_copied rot_ready "
                        "keys_done scores_ready soft_ready prob_ready probT_ready probT_copied read_ready x_done")
            nc.gpsimd.memset(prob[:, :, :], 0.0).then_inc(s["a_prob_zero"], 1)
            with pool.Fori(0, NT // LANES) as i:
                for j in range(LANES):
                    t = i * LANES + j
                    pool.wait_ge(s["rot_ready"], ready(t))
                    nc.gpsimd.tensor_tensor(c.keysT[64:P, bass.ds(t * P, P)], rot[64:P, j, 0, :], rot[64:P, j, 1, :],
                                            ALU.add).then_inc(s["keys_done"], 1)

        @block.tensor
        def _(pe):
            pe.wait_ge(s["a_weights"], 80)
            for h in range(H1):
                nc.tensor.matmul(c.bank[0][:, h * P:(h + 1) * P], whT[:, h, :], whT[:, h, :], start=True, stop=True)
            for k in range(DK):
                last = nc.tensor.matmul(c.bank[1][:, k * R2:(k + 1) * R2], wkvcT[:, k * P:(k + 1) * P], wkr[:, :],
                                        start=True, stop=True)
            last.then_inc(s["a_pe_pre"], 1)
            pe.wait_ge(s["a_gram"], 1)
            pe.wait_ge(s["a_wk"], 1)
            with pe.Fori(0, NT // LANES) as i:
                for j in range(LANES):
                    t = i * LANES + j
                    pe.wait_ge(s["xn_ready"], ready(t))
                    pe.wait_ge(s[f"ctx_loaded{j}"], loaded(i))
                    pe.wait_ge(s["feat_copied"], freed(t))
                    transpose_tile(nc, c, feat(j)[:, 0:D], xn[:, j, :])
                    transpose_tile(nc, c, feat(j)[:, D:2 * D], ctx_in[:, j, :]).then_inc(s["feat_ready"], 1)
                for j in range(LANES):
                    t = i * LANES + j
                    pe.wait_ge(s["feat_copied"], ready(t))
                    pe.wait_ge(s["x_done"], freed(t))
                    for b in range(2):
                        q = slice(64 * b, 64 * b + 64)
                        for k in range(DK):
                            last = nc.tensor.matmul(att(j)[q, 0:S], fT[:, j, k, q], fT[:, j, 2 + k, q],
                                                    start=(k == 0), stop=(k == DK - 1))
                    last.then_inc(s["scores_ready"], 1)
                    pe.wait_ge(s["v_copied"], freed(t))
                    for h in range(H1):
                        nc.tensor.matmul(vg(j)[:, h * P:(h + 1) * P], fT[:, j, 2 + h, :], wh[:, h, :],
                                         start=True, stop=True)
                        last = nc.tensor.matmul(vg(j)[:, D + h * P:D + (h + 1) * P], gram[:, h, :],
                                                fT[:, j, 2 + h, :], start=True, stop=True)
                    last.then_inc(s["v_ready"], 1)
                    pe.wait_ge(s["key_copied"], freed(t))
                    for k in range(DK):
                        nc.tensor.matmul(keys(j)[:, 0:P], wk[:, k, :], fT[:, j, 2 + k, :],
                                         start=(k == 0), stop=(k == DK - 1))
                    for k in range(DK):
                        last = nc.tensor.matmul(keys(j)[:, P:P + KVC], fT[:, j, 2 + k, :], wk[:, k, 0:KVC],
                                                start=(k == 0), stop=(k == DK - 1))
                    last.then_inc(s["keys_ready"], 1)
                for j in range(LANES):
                    t = i * LANES + j
                    pe.wait_ge(s["prob_ready"], ready(t))
                    nc.tensor.transpose(att(j)[:, 0:P], prob[:, j, :], c.ident).then_inc(s["probT_ready"], 1)
                for j in range(LANES):
                    t = i * LANES + j
                    pe.wait_ge(s["probT_copied"], ready(t))
                    nc.tensor.matmul(att(j)[:, 0:D], probT[:, j, :], ctx_in[:, j, :],
                                     start=True, stop=True).then_inc(s["read_ready"], 1)

        @block.scalar
        def _(act):
            act.wait_ge(s["a_pe_pre"], 1)
            act.copy(gram[:, :, :].rearrange("p h n -> p (h n)"), c.bank[0][:, 0:D]).then_inc(s["a_gram"], 1)
            act.wait_ge(s["a_weights"], 80)
            act.copy(wk[:, :, KVC:P], c.bank[1][:, 0:DK * R2].rearrange("p (k n) -> p k n", k=DK)).then_inc(s["a_wk"], 1)
            act.wait_ge(s["a_prob_zero"], 1)
            with act.Fori(0, NT // LANES) as i:
                for j in range(LANES):
                    t = i * LANES + j
                    act.wait_ge(s["feat_ready"], ready(t))
                    act.wait_ge(s["keys_ready"], freed(t))
                    act.copy(fT[:, j, :, :].rearrange("p k n -> p (k n)"), feat(j)[:, :]).then_inc(s["feat_copied"], 1)
                for j in range(LANES):
                    t = i * LANES + j
                    act.wait_ge(s["soft_ready"], ready(t))
                    act.wait_ge(s["probT_ready"], freed(t))
                    act.wait_ge(s["x_done"], freed(t))
                    for b in range(2):
                        q = slice(64 * b, 64 * b + 64)
                        last = nc.scalar.activation(prob[q, j, q], sc[q, j, :], ACT.Exp, bias=nmax[q, j:j + 1],
                                                    accum_out=tot[q, j:j + 1])
                    last.then_inc(s["prob_ready"], 1)
                    act.wait_ge(s["v_ready"], ready(t))
                    act.copy(at_tile(c.v, t), vg(j)[:, 0:D])
                    act.copy(c.gramT[:, :, bass.ds(t * P, P)], vg(j)[:, D:2 * D].rearrange(
                        "p (h n) -> p h n", h=H1)).then_inc(s["v_copied"], 1)
                    act.wait_ge(s["keys_ready"], ready(t))
                    act.wait_ge(s["rot_ready"], freed(t))
                    act.copy(at_tile(c.kvc, t), keys(j)[:, P:P + KVC])
                    act.copy(c.keysT[0:64, bass.ds(t * P, P)], keys(j)[0:64, 0:P])
                    act.copy(kraw[64:P, j, :], keys(j)[64:P, 0:P]).then_inc(s["key_copied"], 1)
                for j in range(LANES):
                    t = i * LANES + j
                    act.wait_ge(s["probT_ready"], ready(t))
                    act.wait_ge(s["read_ready"], freed(t))
                    act.copy(probT[:, j, :], att(j)[:, 0:P]).then_inc(s["probT_copied"], 1)

        @block.vector
        def _(dve):
            ch = Chain(dve, s["a_mask_chain"])
            dve.wait_ge(s["a_masks"], 32)
            ch.link(nc.vector.tensor_copy(keep[:, :, :], mask8[:, :, :]))
            nc.vector.tensor_scalar(drop[:, :, :], keep[:, :, :], 1.0, -NEG, ALU.subtract, ALU.mult)
            ch.link(nc.vector.tensor_reduce(any_valid[:, :], keep[:, :, :], AX.X, ALU.max))
            with dve.Fori(0, NT // LANES) as i:
                ch = Chain(dve, s["a_chain"], i * ITER_LINKS)
                for j in range(LANES):
                    t = i * LANES + j
                    dve.wait_ge(s["feat_ready"], freed(t))
                    normalize(nc, c, xn[:, j, :], t).then_inc(s["xn_ready"], 1)
                for j in range(LANES):
                    t = i * LANES + j
                    dve.wait_ge(s["scores_ready"], ready(t))
                    dve.wait_ge(s["prob_ready"], freed(t))
                    ch.link(nc.vector.scalar_tensor_tensor(out=sc[:, j, :], in0=att(j)[:, 0:S], scalar=D ** -0.5,
                                                           in1=at_tile(keep, t), op0=ALU.mult, op1=ALU.mult))
                    ch.link(nc.vector.tensor_tensor(sc[:, j, :], sc[:, j, :], at_tile(drop, t), ALU.add))
                    nc.vector.tensor_reduce(nmax[:, j:j + 1], sc[:, j, :], AX.X, ALU.max,
                                            negate=True).then_inc(s["soft_ready"], 1)
                for j in range(LANES):
                    t = i * LANES + j
                    dve.wait_ge(s["key_copied"], ready(t))
                    dve.wait_ge(s["keys_done"], freed(t))
                    kr = kraw[:, j, :]
                    nc.vector.tensor_tensor(rot[64:P, j, 0, :], kr[64:P, :], c.cos[64:P, :], ALU.mult)
                    nc.vector.tensor_tensor(rot[96:P, j, 1, :], kr[64:96, :], c.sin[64:96, :], ALU.mult)
                    nc.vector.tensor_tensor(rot[64:96, j, 1, :], kr[96:P, :], c.sin[96:P, :],
                                            ALU.mult).then_inc(s["rot_ready"], 1)
                    dve.wait_ge(s["prob_ready"], ready(t))
                    ch.link(nc.vector.reciprocal(rec[:, j:j + 1], tot[:, j:j + 1]))
                    ch.link(nc.vector.tensor_tensor(rec[:, j:j + 1], rec[:, j:j + 1], any_valid[:, bass.ds(t, 1)], ALU.mult))
                for j in range(LANES):
                    t = i * LANES + j
                    dve.wait_ge(s["read_ready"], ready(t))
                    add_and_stats(nc, c, ch, t, att(j)[:, 0:D], rec[:, j:j + 1], s["x_done"])
                assert ch.n == ITER_LINKS, ch.n


def add_and_stats(nc, c, ch, t, psum, scale, done):
    ch.link(nc.vector.scalar_tensor_tensor(out=at_tile(c.x, t), in0=psum, scalar=scale, in1=at_tile(c.x, t),
                                           op0=ALU.mult, op1=ALU.add))
    ch.link(nc.vector.bn_stats(at_tile(c.bn, t), at_tile(c.x, t)))
    ch.eng.sem_inc(done, 1)


def stage_last(nc, c):
    with ExitStack() as ctx:
        s = open_sems(nc, ctx, "out_stored")
        block = ctx.enter_context(nc.Block())
        ot = c.d["out"].rearrange("(n p) d -> p n d", p=P)

        @block.sync
        def _(sp):
            for n in range(4):
                sp.dma_start(ot[:, 8 * n:8 * n + 8, :], c.x[:, 8 * n:8 * n + 8, :]).then_inc(s["out_stored"], 16)
            sp.wait_ge(s["out_stored"], 64)


def token_loop(i, lanes=LANES):
    return [(j, i * LANES + j) for j in range(lanes)]


def stage_l0_shared(nc, c):
    with ExitStack() as ctx:
        sb = lambda n, sh, dt=F32: ctx.enter_context(nc.sbuf_tensor(n, sh, dt))
        wgu = sb("wgu", [P, DK, 2 * FS0]); wd = sb("wd", [P, FS0 // P, D]); wg = sb("wgate", [P, DK, E0])
        xn = sb("xn_b", [P, LANES, D]); xT = sb("xT_b", [P, LANES, DK, P])
        sig = sb("sig_b", [P, LANES, D]); hT = sb("hT_b", [P, LANES, D]); zero = sb("zero_b", [P, 1024])
        s = open_sems(nc, ctx, "b_weights zero_set zeroed xn_ready feat_ready feat_copied hid_ready sig_ready "
                      "hT_ready logit_ready logit_copied down_ready x_done xn_stored0 xn_stored1 b_chain")
        block = ctx.enter_context(nc.Block())

        def feat(j): return c.bank[4 * j]
        def hid(j): return c.bank[4 * j + 1]
        def logit(j): return c.bank[4 * j + 2]
        def down(j): return c.bank[4 * j + 3]

        @block.sync
        def _(sp):
            for dst, src in ((wg[:, :, :], c.d["g0w"]), (wgu[:, :, 0:FS0], c.d["s0g"]),
                             (wgu[:, :, FS0:2 * FS0], c.d["s0u"]), (wd[:, :, :], c.d["s0d"])):
                sp.dma_start(dst, src.rearrange("(k p) n -> p k n", p=P)).then_inc(s["b_weights"], 16)
            sp.wait_ge(s["zero_set"], 1)
            for n in range(8):
                sp.dma_start(c.moe[512 * n:512 * n + 512, :].rearrange("(p r) d -> p (r d)", r=4),
                             zero[:, :]).then_inc(s["zeroed"], 16)
            sp.dma_start(c.moe[N:NX, :], zero[0:CAP0, 0:D]).then_inc(s["zeroed"], 16)
            sp.dma_start(c.xn_rows[N:NX, :], zero[0:CAP0, 0:D]).then_inc(s["zeroed"], 16)
            with sp.Fori(0, NT // LANES) as i:
                for j, t in token_loop(i):
                    sp.wait_ge(s["xn_ready"], ready(t))
                    sp.dma_start(c.xn_rows[bass.ds(t * P, P), :], xn[:, j, :]).then_inc(s[f"xn_stored{j}"], 16)
            sp.wait_ge(s["zeroed"], 160)
            for j in range(LANES):
                sp.wait_ge(s[f"xn_stored{j}"], 16 * (NT // LANES) + 16)

        @block.gpsimd
        def _(pool):
            nc.gpsimd.memset(zero[:, :], 0.0).then_inc(s["zero_set"], 1)
            give_credit(pool, s, "xn_ready feat_ready feat_copied hid_ready sig_ready hT_ready logit_ready "
                        "logit_copied down_ready x_done")
            for j in range(LANES):
                pool.sem_inc(s[f"xn_stored{j}"], 16)

        @block.tensor
        def _(pe):
            pe.wait_ge(s["b_weights"], 64)
            with pe.Fori(0, NT // LANES) as i:
                for j, t in token_loop(i):
                    pe.wait_ge(s["xn_ready"], ready(t))
                    pe.wait_ge(s["feat_copied"], freed(t))
                    transpose_tile(nc, c, feat(j), xn[:, j, :]).then_inc(s["feat_ready"], 1)
                for j, t in token_loop(i):
                    pe.wait_ge(s["feat_copied"], ready(t))
                    pe.wait_ge(s["hT_ready"], freed(t))
                    for f in range(4):
                        for k in range(DK):
                            last = nc.tensor.matmul(hid(j)[:, f * P:(f + 1) * P], wgu[:, k, f * P:(f + 1) * P],
                                                    xT[:, j, k, :], start=(k == 0), stop=(k == DK - 1))
                    last.then_inc(s["hid_ready"], 1)
                    pe.wait_ge(s["logit_copied"], freed(t))
                    for k in range(DK):
                        last = nc.tensor.matmul(logit(j)[:, 0:E0], xT[:, j, k, :], wg[:, k, :],
                                                start=(k == 0), stop=(k == DK - 1))
                    last.then_inc(s["logit_ready"], 1)
                for j, t in token_loop(i):
                    pe.wait_ge(s["hT_ready"], ready(t))
                    pe.wait_ge(s["x_done"], freed(t))
                    for k in range(DK):
                        last = nc.tensor.matmul(down(j)[:, 0:D], hT[:, j, k * P:(k + 1) * P], wd[:, k, :],
                                                start=(k == 0), stop=(k == DK - 1))
                    last.then_inc(s["down_ready"], 1)

        @block.scalar
        def _(act):
            with act.Fori(0, NT // LANES) as i:
                for j, t in token_loop(i):
                    act.wait_ge(s["feat_ready"], ready(t))
                    act.wait_ge(s["logit_ready"], freed(t))
                    act.copy(xT[:, j, :, :].rearrange("p k n -> p (k n)"), feat(j)[:, 0:D]).then_inc(s["feat_copied"], 1)
                for j, t in token_loop(i):
                    act.wait_ge(s["hid_ready"], ready(t))
                    act.wait_ge(s["hT_ready"], freed(t))
                    nc.scalar.activation(sig[:, j, :], hid(j)[:, 0:D], ACT.Sigmoid).then_inc(s["sig_ready"], 1)
                    act.wait_ge(s["logit_ready"], ready(t))
                    nc.scalar.activation(at_tile(c.score0, t), logit(j)[:, 0:E0],
                                         ACT.Sigmoid).then_inc(s["logit_copied"], 1)

        @block.vector
        def _(dve):
            with dve.Fori(0, NT // LANES) as i:
                ch = Chain(dve, s["b_chain"], i * LANES)
                for j, t in token_loop(i):
                    dve.wait_ge(s["feat_ready"], freed(t))
                    dve.wait_ge(s[f"xn_stored{j}"], store_freed(i))
                    normalize(nc, c, xn[:, j, :], t).then_inc(s["xn_ready"], 1)
                for j, t in token_loop(i):
                    dve.wait_ge(s["sig_ready"], ready(t))
                    dve.wait_ge(s["down_ready"], freed(t))
                    ch.link(nc.vector.tensor_tensor(sig[:, j, :], hid(j)[:, 0:D], sig[:, j, :], ALU.mult))
                    nc.vector.tensor_tensor(hT[:, j, :], hid(j)[:, D:2 * D], sig[:, j, :],
                                            ALU.mult).then_inc(s["hT_ready"], 1)
                for j, t in token_loop(i):
                    dve.wait_ge(s["down_ready"], ready(t))
                    nc.vector.tensor_tensor(at_tile(c.x, t), down(j)[:, 0:D], at_tile(c.x, t),
                                            ALU.add).then_inc(s["x_done"], 1)


BIG = 3e38


def stage_l0_route(nc, c):
    with ExitStack() as ctx:
        sb = lambda n, sh, dt=F32: ctx.enter_context(nc.sbuf_tensor(n, sh, dt))
        NE = NT * E0
        biased = sb("biased", [P, NE]); ta = sb("ta", [P, NE]); tb = sb("tb", [P, NE]); tc_ = sb("tc", [P, NE])
        gs = sb("gs", [P, NT, G0]); gmask = sb("gmask", [P, NT, G0]); bias = sb("gate_bias", [P, E0])
        cand = sb("cand", [P, NT, E0 + 4]); left = sb("left", [P, NT, E0 + 4]); top = sb("top", [P, NT, 8])
        chosen = sb("chosen", [P, NE]); chosen_b = sb("chosen_b", [P, NE], BF16)
        wsum = sb("wsum", [P, NT]); before_b = sb("before_b", [P, P], BF16); ones_b = sb("ones_b", [P, P], BF16)
        wb = sb("wb", [P, NE], BF16); tile_no = sb("tile_no", [P, NE]); row_no = sb("row_no", [P, NE])
        s = open_sems(nc, ctx, "r_bias r_chain r_chosen r_counts r_iota")
        block = ctx.enter_context(nc.Block())

        @block.sync
        def _(sp):
            sp.dma_start(bias[:, :], c.d["g0b"].broadcast_to([P, E0])).then_inc(s["r_bias"], 16)

        @block.gpsimd
        def _(pool):
            nc.gpsimd.iota(tile_no[:, :], pattern=[[1, NT], [0, E0]], base=0, channel_multiplier=0,
                           allow_small_or_imprecise_dtypes=True).then_inc(s["r_iota"], 1)
            nc.gpsimd.iota(row_no[:, :], pattern=[[0, NE]], base=0, channel_multiplier=1,
                           allow_small_or_imprecise_dtypes=True).then_inc(s["r_iota"], 1)
            nc.gpsimd.iota(c.row_col[:, :], pattern=[[0, 1]], base=0, channel_multiplier=1,
                           allow_small_or_imprecise_dtypes=True).then_inc(s["r_iota"], 1)

        @block.tensor
        def _(pe):
            pe.wait_ge(s["r_chosen"], 1)
            for n in range(2):
                cols = slice(512 * n, 512 * n + 512)
                nc.tensor.matmul(c.bank[n][:, :], before_b[:, :], chosen_b[:, cols], start=True, stop=True)
                last = nc.tensor.matmul(c.bank[2 + n][:, :], ones_b[:, :], chosen_b[:, cols], start=True, stop=True)
            last.then_inc(s["r_counts"], 1)

        @block.vector
        def _(dve):
            ch = Chain(dve, s["r_chain"])
            v = nc.vector
            e8 = lambda ap: ap.rearrange("p (g e) -> p g e", e=8)

            def g(ap, a, b): return e8(ap[:, :])[:, :, a:b]
            score = c.score0[:, :, :].rearrange("p t e -> p (t e)")
            te = lambda ap: ap[:, :].rearrange("p (t e) -> p t e", e=E0)
            dve.wait_ge(s["r_bias"], 16)
            ch.link(v.tensor_tensor(te(biased), c.score0[:, :, :],
                                    bias[:, :].unsqueeze(1).broadcast_to([P, NT, E0]), ALU.add))
            v.tensor_tensor(g(ta, 0, 4), g(biased, 0, 4), g(biased, 4, 8), ALU.max)
            ch.link(v.tensor_tensor(g(tb, 0, 4), g(biased, 0, 4), g(biased, 4, 8), ALU.min))
            for w in (2, 1):
                v.tensor_tensor(g(tc_, 0, w), g(ta, 0, w), g(ta, w, 2 * w), ALU.max)
                v.tensor_tensor(g(tc_, 2, 2 + w), g(ta, 0, w), g(ta, w, 2 * w), ALU.min)
                ch.link(v.tensor_tensor(g(tc_, 4, 4 + w), g(tb, 0, w), g(tb, w, 2 * w), ALU.max))
                v.tensor_copy(g(ta, 0, w), g(tc_, 0, w))
                ch.link(v.tensor_tensor(g(tb, 0, w), g(tc_, 2, 2 + w), g(tc_, 4, 4 + w), ALU.max))
            g1 = lambda ap: g(ap, 0, 1).rearrange("p (t g) o -> p t (g o)", g=G0)
            ch.link(v.tensor_tensor(gs[:, :, :], g1(ta), g1(tb), ALU.add))
            rival = gs[:, :, :].unsqueeze(2).broadcast_to([P, NT, G0, G0])
            own = gs[:, :, :].unsqueeze(3).broadcast_to([P, NT, G0, G0])
            sq = lambda ap: ap[:, 0:NT * 16].rearrange("p (t a b) -> p t a b", a=G0, b=G0)
            v.tensor_tensor(sq(ta), rival, own, ALU.is_gt)
            ch.link(v.tensor_tensor(sq(tb), rival, own, ALU.is_equal))
            t16 = lambda ap: ap[:, 0:NT * 16].rearrange("p (t a) -> p t a", a=16)
            ch.link(v.tensor_tensor(t16(tb), t16(tb), c.lower.unsqueeze(1).broadcast_to([P, NT, 16]), ALU.mult))
            ch.link(v.tensor_tensor(ta[:, 0:NT * 16], ta[:, 0:NT * 16], tb[:, 0:NT * 16], ALU.add))
            ch.link(v.tensor_reduce(gmask[:, :, :], sq(ta), AX.X, ALU.add))
            ch.link(v.tensor_scalar(gmask[:, :, :], gmask[:, :, :], float(TG0), None, ALU.is_lt))
            v.memset(cand[:, :, E0:E0 + 4], BIG)
            v.tensor_copy(ones_b[:, :], c.cos_one)
            v.tensor_copy(before_b[:, :], c.before)
            for gi in range(G0):
                last = v.tensor_tensor(cand[:, :, 8 * gi:8 * gi + 8], te(biased)[:, :, 8 * gi:8 * gi + 8],
                                       gmask[:, :, gi:gi + 1].broadcast_to([P, NT, 8]), ALU.mult)
            ch.link(last)
            for t in range(NT):
                last = v.max(top[:, t, :], cand[:, t, 0:E0])
            ch.link(last)
            ch.link(v.memset(top[:, :, TOP0:8], BIG))
            for t in range(NT):
                last = v.match_replace(out=left[:, t, :], in_to_replace=top[:, t, :], in_values=cand[:, t, :],
                                       imm_value=-BIG)
            ch.link(last)
            v.tensor_tensor(te(chosen_b), left[:, :, 0:E0], cand[:, :, 0:E0], ALU.not_equal).then_inc(s["r_chosen"], 1)
            ch.link(v.tensor_tensor(te(chosen), left[:, :, 0:E0], cand[:, :, 0:E0], ALU.not_equal))
            ch.link(v.tensor_tensor(ta[:, :], score, chosen[:, :], ALU.mult))
            ch.link(v.tensor_reduce(wsum[:, :], te(ta), AX.X, ALU.add))
            ch.link(v.tensor_scalar(wsum[:, :], wsum[:, :], 1e-20, None, ALU.add))
            ch.link(v.reciprocal(wsum[:, :], wsum[:, :]))
            ch.link(v.scalar_tensor_tensor(out=te(ta), in0=te(ta), scalar=SCALE0,
                                           in1=wsum[:, :].unsqueeze(2).broadcast_to([P, NT, E0]),
                                           op0=ALU.mult, op1=ALU.mult))
            col = lambda n: c.slot_cols[:, :, :, n].rearrange("p t e -> p (t e)")
            dve.wait_ge(s["r_iota"], 3)
            v.tensor_copy(col(0), chosen[:, :])
            v.tensor_copy(col(1), tile_no[:, :])
            v.tensor_copy(col(2), row_no[:, :])
            for n in (3, 4):
                ch.link(v.tensor_copy(wb[:, :], ta[:, :]))
                v.tensor_copy(col(n), wb[:, :])
                ch.link(v.tensor_tensor(ta[:, :], ta[:, :], wb[:, :], ALU.subtract))
            ch.link(v.tensor_copy(col(5), ta[:, :]))
            dve.wait_ge(s["r_counts"], 1)
            for n in range(2):
                cols = slice(512 * n, 512 * n + 512)
                v.tensor_copy(ta[:, cols], c.bank[2 + n][:, :])
                last = v.tensor_copy(tc_[:, cols], c.bank[n][:, :])
            ch.link(last)
            ch.link(v.tensor_tensor(tc_[:, :], tc_[:, :], ta[:, :], ALU.subtract))
            cur, nxt, step = ta, tb, 1
            while step < NT:
                w = step * E0
                v.tensor_copy(nxt[:, 0:w], cur[:, 0:w])
                ch.link(v.tensor_tensor(nxt[:, w:NE], cur[:, w:NE], cur[:, 0:NE - w], ALU.add))
                cur, nxt, step = nxt, cur, 2 * step
            ch.link(v.tensor_tensor(tc_[:, :], tc_[:, :], cur[:, :], ALU.add))
            ch.link(v.scalar_tensor_tensor(out=chosen[:, :], in0=tc_[:, :], scalar=float(CAP0), in1=chosen[:, :],
                                           op0=ALU.is_lt, op1=ALU.mult))
            ch.link(v.scalar_tensor_tensor(out=tc_[:, :], in0=tc_[:, :], scalar=1.0, in1=chosen[:, :],
                                           op0=ALU.add, op1=ALU.mult))
            ch.link(v.tensor_scalar(c.place[:, :, :].rearrange("p t e -> p (t e)"), tc_[:, :], 1.0, None,
                                    ALU.subtract))


def stage_l0_slots(nc, c):
    with ExitStack() as ctx:
        sb = lambda n, sh, dt=F32: ctx.enter_context(nc.sbuf_tensor(n, sh, dt))
        hot = sb("hot", [P, LANES, E0, CAP0], BF16); cols = sb("cols", [P, LANES, E0 * 6], BF16)
        zeros = sb("zeros_s", [P, E0 * 6], BF16); iota_b = sb("iota_b", [P, CAP0], BF16)
        got = sb("got", [CAP0, E0, 6]); idf = sb("idf", [CAP0, E0]); empty = sb("empty", [CAP0, E0])
        s = open_sems(nc, ctx, "s_zero s_iota hot_ready cols_ready hot_used s_done s_chain")
        block = ctx.enter_context(nc.Block())
        acc = c.bank[0][0:CAP0, 0:E0 * 6]

        @block.gpsimd
        def _(pool):
            give_credit(pool, s, "hot_ready cols_ready hot_used")
            nc.gpsimd.memset(zeros[:, :], 0.0).then_inc(s["s_zero"], 1)

        @block.scalar
        def _(act):
            with act.Fori(0, NT // LANES) as i:
                for j, t in token_loop(i):
                    act.wait_ge(s["hot_used"], freed(t))
                    act.copy(cols[:, j, :], c.slot_cols[:, bass.ds(t, 1), :, :].rearrange(
                        "p a e n -> p (a e n)")).then_inc(s["cols_ready"], 1)

        @block.vector
        def _(dve):
            ch = Chain(dve, s["s_iota"])
            ch.link(nc.vector.tensor_copy(iota_b[:, :], c.iota))
            with dve.Fori(0, NT // LANES) as i:
                for j, t in token_loop(i):
                    dve.wait_ge(s["hot_used"], freed(t))
                    nc.vector.tensor_tensor(hot[:, j, :, :],
                                            at_tile(c.place, t).unsqueeze(2).broadcast_to([P, E0, CAP0]),
                                            iota_b[:, :].unsqueeze(1).broadcast_to([P, E0, CAP0]),
                                            ALU.is_equal).then_inc(s["hot_ready"], 1)
            ch = Chain(dve, s["s_chain"])
            v = nc.vector
            dve.wait_ge(s["s_done"], 1)
            ch.link(v.tensor_copy(got[:, :, :].rearrange("p e n -> p (e n)"), acc))
            row = c.row_col[0:CAP0, :]
            ch.link(v.tensor_scalar(empty[:, :], got[:, :, 0], -1.0, 1.0, ALU.mult, ALU.add))
            v.scalar_tensor_tensor(out=idf[:, :], in0=got[:, :, 1], scalar=float(P), in1=got[:, :, 2],
                                   op0=ALU.mult, op1=ALU.add)
            ch.link(v.tensor_scalar(got[:, :, 0], empty[:, :], row, None, ALU.mult))
            ch.link(v.scalar_tensor_tensor(out=empty[:, :], in0=empty[:, :], scalar=float(N), in1=got[:, :, 0],
                                           op0=ALU.mult, op1=ALU.add))
            v.tensor_tensor(c.slot_token[:, :], idf[:, :], empty[:, :], ALU.add)
            ch.link(v.tensor_tensor(got[:, :, 3], got[:, :, 3], got[:, :, 4], ALU.add))
            ch.link(v.tensor_tensor(c.slot_weight[:, :], got[:, :, 3], got[:, :, 5], ALU.add))

        @block.tensor
        def _(pe):
            pe.wait_ge(s["s_zero"], 1)
            nc.tensor.matmul(acc, zeros[:, 0:CAP0], zeros[:, :], start=True, stop=False, skip_group_check=True)
            with pe.Fori(0, NT // LANES) as i:
                for j, t in token_loop(i):
                    pe.wait_ge(s["hot_ready"], ready(t))
                    pe.wait_ge(s["cols_ready"], ready(t))
                    for e in range(E0):
                        last = nc.tensor.matmul(acc[:, 6 * e:6 * e + 6], hot[:, j, e, :], cols[:, j, 6 * e:6 * e + 6],
                                                start=False, stop=False, skip_group_check=True)
                    last.then_inc(s["hot_used"], 1)
            nc.tensor.matmul(acc, zeros[:, 0:CAP0], zeros[:, :], start=False, stop=True,
                             skip_group_check=True).then_inc(s["s_done"], 1)


def stage_l0_experts(nc, c):
    with ExitStack() as ctx:
        sb = lambda n, sh, dt=F32: ctx.enter_context(nc.sbuf_tensor(n, sh, dt))
        w13 = sb("w13", [P, LANES, 2, DK, F0]); w2 = sb("w2e", [P, LANES, D])
        idx = sb("idx", [CAP0, LANES], I32); xg = sb("xg", [CAP0, LANES, D]); xgT = sb("xgT", [P, LANES, DK * CAP0])
        sig = sb("sig_e", [P, LANES, CAP0]); hT = sb("hT_e", [P, LANES, CAP0]); y = sb("y_e", [CAP0, LANES, D])
        s = open_sems(nc, ctx, "w_loaded0 w_loaded1 idx_ready gathered0 gathered1 feat_ready feat_copied hid_ready "
                      "sig_ready hT_ready down_ready y_ready added0 added1 add_done e_chain pool_passed pe_passed")
        block = ctx.enter_context(nc.Block())

        def feat(j): return c.bank[4 * j]
        def hid(j): return c.bank[4 * j + 1]
        def down(j): return c.bank[4 * j + 2]

        @block.sync
        def _(sp):
            with sp.Fori(0, E0 // LANES) as i:
                for j, e in token_loop(i):
                    sp.wait_ge(s["down_ready"], freed(e))
                    for n, name in enumerate(("e0w1", "e0w3")):
                        sp.dma_start(w13[:, j, n, :, :], c.d[name][bass.ds(e, 1)].rearrange(
                            "a (k p) f -> p (a k) f", p=P)).then_inc(s[f"w_loaded{j}"], 16)
                    sp.dma_start(w2[:, j, :], c.d["e0w2"][bass.ds(e, 1)].rearrange(
                        "a f d -> f (a d)")).then_inc(s[f"w_loaded{j}"], 16)

        @block.gpsimd
        def _(pool):
            give_credit(pool, s, "idx_ready feat_ready feat_copied hid_ready sig_ready hT_ready down_ready y_ready add_done")
            with pool.Fori(0, E0 // LANES) as i:
                for j, e in token_loop(i):
                    pool.wait_ge(s["idx_ready"], ready(e))
                    pool.wait_ge(s["feat_ready"], freed(e))
                    settle(pool, s[f"pool_passed"])
                    nc.gpsimd.indirect_dma_start(
                        out=xg[:, j, :], out_offset=None, in_=c.xn_rows[:, :],
                        in_offset=bass.IndirectOffsetOnAxis(ap=idx[:, j:j + 1], axis=0),
                    ).then_inc(s[f"gathered{j}"], 16)
                for j, e in token_loop(i):
                    pool.wait_ge(s["y_ready"], ready(e))
                    settle(pool, s["pool_passed"])
                    nc.gpsimd.indirect_dma_start(
                        out=c.moe[:, :], out_offset=bass.IndirectOffsetOnAxis(ap=idx[:, j:j + 1], axis=0),
                        in_=y[:, j, :], in_offset=None, compute_op=ALU.add, oob_is_err=True,
                        bounds_check=NX - 1,
                    ).then_inc(s[f"added{j}"], 16)
                    pool.wait_ge(s[f"added{j}"], loaded(i))
                    pool.sem_inc(s["add_done"], 1)

        @block.tensor
        def _(pe):
            with pe.Fori(0, E0 // LANES) as i:
                for j, e in token_loop(i):
                    pe.wait_ge(s[f"gathered{j}"], loaded(i))
                    pe.wait_ge(s["feat_copied"], freed(e))
                    settle(pe, s[f"pe_passed"])
                    for k in range(DK):
                        last = nc.tensor.transpose(feat(j)[:, k * CAP0:(k + 1) * CAP0], xg[:, j, k * P:(k + 1) * P],
                                                   c.ident[0:CAP0, 0:CAP0])
                    last.then_inc(s["feat_ready"], 1)
                for j, e in token_loop(i):
                    pe.wait_ge(s["feat_copied"], ready(e))
                    pe.wait_ge(s[f"w_loaded{j}"], 48 * i + 48)
                    pe.wait_ge(s["hT_ready"], freed(e))
                    for n in range(2):
                        for k in range(DK):
                            last = nc.tensor.matmul(hid(j)[:, n * CAP0:(n + 1) * CAP0], w13[:, j, n, k, :],
                                                    xgT[:, j, k * CAP0:(k + 1) * CAP0],
                                                    start=(k == 0), stop=(k == DK - 1))
                    last.then_inc(s["hid_ready"], 1)
                for j, e in token_loop(i):
                    pe.wait_ge(s["hT_ready"], ready(e))
                    pe.wait_ge(s["y_ready"], freed(e))
                    nc.tensor.matmul(down(j)[0:CAP0, 0:D], hT[:, j, :], w2[:, j, :],
                                     start=True, stop=True).then_inc(s["down_ready"], 1)

        @block.scalar
        def _(act):
            with act.Fori(0, E0 // LANES) as i:
                for j, e in token_loop(i):
                    act.wait_ge(s["feat_ready"], ready(e))
                    act.wait_ge(s["hid_ready"], freed(e))
                    act.copy(xgT[:, j, :], feat(j)[:, 0:DK * CAP0]).then_inc(s["feat_copied"], 1)
                for j, e in token_loop(i):
                    act.wait_ge(s["hid_ready"], ready(e))
                    act.wait_ge(s["hT_ready"], freed(e))
                    nc.scalar.activation(sig[:, j, :], hid(j)[:, 0:CAP0], ACT.Sigmoid).then_inc(s["sig_ready"], 1)

        @block.vector
        def _(dve):
            with dve.Fori(0, E0 // LANES) as i:
                ch = Chain(dve, s["e_chain"], i * LANES)
                for j, e in token_loop(i):
                    dve.wait_ge(s["add_done"], freed(e))
                    nc.vector.tensor_copy(idx[:, j:j + 1], c.slot_token[:, bass.ds(e, 1)]).then_inc(s["idx_ready"], 1)
                for j, e in token_loop(i):
                    dve.wait_ge(s["sig_ready"], ready(e))
                    dve.wait_ge(s["down_ready"], freed(e))
                    ch.link(nc.vector.tensor_tensor(sig[:, j, :], hid(j)[:, 0:CAP0], sig[:, j, :], ALU.mult))
                    nc.vector.tensor_tensor(hT[:, j, :], hid(j)[:, CAP0:2 * CAP0], sig[:, j, :],
                                            ALU.mult).then_inc(s["hT_ready"], 1)
                for j, e in token_loop(i):
                    dve.wait_ge(s["down_ready"], ready(e))
                    nc.vector.tensor_scalar(y[:, j, :], down(j)[0:CAP0, 0:D], c.slot_weight[:, bass.ds(e, 1)], None,
                                            ALU.mult).then_inc(s["y_ready"], 1)


def stage_add_experts(nc, c):
    with ExitStack() as ctx:
        rows = ctx.enter_context(nc.sbuf_tensor("moe_in", [P, NT, D], F32))
        CH = 4
        s = open_sems(nc, ctx, "m_chain " + " ".join(f"m_loaded{n}" for n in range(CH)))
        block = ctx.enter_context(nc.Block())
        src = c.moe[0:N, :].rearrange("(n p) d -> p n d", p=P)
        W = NT // CH

        @block.sync
        def _(sp):
            for n in range(CH):
                sp.dma_start(rows[:, W * n:W * n + W, :], src[:, W * n:W * n + W, :]).then_inc(s[f"m_loaded{n}"], 16)

        @block.vector
        def _(dve):
            for n in range(CH):
                dve.wait_ge(s[f"m_loaded{n}"], 16)
                with dve.Fori(W * n, W * n + W) as t:
                    ch = Chain(dve, s["m_chain"], t)
                    ch.link(nc.vector.tensor_tensor(at_tile(c.x, t), at_tile(c.x, t), at_tile(rows, t), ALU.add))
                    nc.vector.bn_stats(at_tile(c.bn, t), at_tile(c.x, t))


def stage_l1_scores(nc, c):
    with ExitStack() as ctx:
        sb = lambda n, sh, dt=F32: ctx.enter_context(nc.sbuf_tensor(n, sh, dt))
        wg = sb("wg_c", [P, DK, D]); xn = sb("xn_c", [P, LANES, D]); xT = sb("xT_c", [P, LANES, DK, P])
        zeros = sb("zeros_c", [P, P]); padded = sb("padded", [S, H1, 3 * S])
        s = open_sems(nc, ctx, "c_weights c_zero xn_ready feat_ready feat_copied gate_ready gate_copied used_ready "
                      "sum_done c_chain padded_ready mixT_ready")
        block = ctx.enter_context(nc.Block())
        total = c.bank[7][0:S, 0:H1 * S]

        def feat(j): return c.bank[2 * j]
        def gate(j): return c.bank[2 * j + 1]

        @block.sync
        def _(sp):
            sp.dma_start(wg[:, :, :], c.d["wg"].rearrange("(k p) n -> p k n", p=P)).then_inc(s["c_weights"], 16)

        @block.gpsimd
        def _(pool):
            give_credit(pool, s, "xn_ready feat_ready feat_copied gate_ready gate_copied used_ready")
            nc.gpsimd.memset(zeros[:, :], 0.0).then_inc(s["c_zero"], 1)
            nc.gpsimd.memset(padded[:, :, :], 0.0).then_inc(s["c_zero"], 1)

        @block.tensor
        def _(pe):
            pe.wait_ge(s["c_weights"], 16)
            pe.wait_ge(s["c_zero"], 2)
            nc.tensor.matmul(total, zeros[:, 0:S], zeros[:, :], start=True, stop=False, skip_group_check=True)
            with pe.Fori(0, NT // LANES) as i:
                for j, t in token_loop(i):
                    pe.wait_ge(s["xn_ready"], ready(t))
                    pe.wait_ge(s["feat_copied"], freed(t))
                    transpose_tile(nc, c, feat(j), xn[:, j, :]).then_inc(s["feat_ready"], 1)
                for j, t in token_loop(i):
                    pe.wait_ge(s["feat_copied"], ready(t))
                    pe.wait_ge(s["gate_copied"], freed(t))
                    for k in range(DK):
                        last = nc.tensor.matmul(gate(j)[:, 0:D], xT[:, j, k, :], wg[:, k, :],
                                                start=(k == 0), stop=(k == DK - 1))
                    last.then_inc(s["gate_ready"], 1)
                    for h in range(H1):
                        for b in range(2):
                            last = nc.tensor.matmul(total[:, h * S:(h + 1) * S], xT[:, j, h, 64 * b:64 * b + 64],
                                                    c.gramT[:, h, bass.ds(t * P + 64 * b, S)],
                                                    start=False, stop=False, skip_group_check=True)
                    last.then_inc(s["used_ready"], 1)
            nc.tensor.matmul(total, zeros[:, 0:S], zeros[:, :], start=False, stop=True,
                             skip_group_check=True).then_inc(s["sum_done"], 1)
            pe.wait_ge(s["padded_ready"], 1)
            for h in range(H1):
                for b in range(2):
                    last = nc.tensor.transpose(c.bank[0][:, h * P + 64 * b:h * P + 64 * b + 64],
                                               padded[:, h, S * (1 - b):S * (1 - b) + P], c.ident[0:S, 0:S])
            last.then_inc(s["mixT_ready"], 1)

        @block.scalar
        def _(act):
            with act.Fori(0, NT // LANES) as i:
                for j, t in token_loop(i):
                    act.wait_ge(s["feat_ready"], ready(t))
                    act.wait_ge(s["used_ready"], freed(t))
                    act.copy(xT[:, j, :, :].rearrange("p k n -> p (k n)"), feat(j)[:, 0:D]).then_inc(s["feat_copied"], 1)
                for j, t in token_loop(i):
                    act.wait_ge(s["gate_ready"], ready(t))
                    nc.scalar.activation(at_tile(c.gate1, t), gate(j)[:, 0:D], ACT.Relu).then_inc(s["gate_copied"], 1)
            act.wait_ge(s["mixT_ready"], 1)
            act.copy(c.mixT[:, :, :].rearrange("p h n -> p (h n)"), c.bank[0][:, 0:H1 * P])

        @block.vector
        def _(dve):
            with dve.Fori(0, NT // LANES) as i:
                for j, t in token_loop(i):
                    dve.wait_ge(s["feat_ready"], freed(t))
                    normalize(nc, c, xn[:, j, :], t).then_inc(s["xn_ready"], 1)
            ch = Chain(dve, s["c_chain"])
            dve.wait_ge(s["sum_done"], 1)
            mid = padded[:, :, S:2 * S]
            ch.link(nc.vector.tensor_tensor(mid, total.rearrange("p (h n) -> p h n", h=H1),
                                            c.decay[0:S, :].rearrange("p (h n) -> p h n", h=H1), ALU.mult))
            ch.link(nc.vector.scalar_tensor_tensor(out=mid, in0=mid, scalar=-1.0, in1=mid, op0=ALU.mult, op1=ALU.max))
            nc.vector.tensor_scalar(mid, mid, 1.0, None, ALU.max).then_inc(s["padded_ready"], 1)


def stage_l1_mix(nc, c):
    with ExitStack() as ctx:
        sb = lambda n, sh, dt=F32: ctx.enter_context(nc.sbuf_tensor(n, sh, dt))
        wo = sb("wo_m", [P, DK, D]); gamma = sb("gn_gamma", [P, D]); beta = sb("gn_beta", [P, D])
        bn = sb("bn_m", [P, LANES, 6]); mv = sb("mv_m", [P, LANES, 2]); ve = sb("ve_m", [P, LANES]); rs = sb("rs_m", [P, LANES])
        y = sb("y_m", [P, LANES, D]); yT = sb("yT_m", [P, LANES, D])
        s = open_sems(nc, ctx, "m_weights mixed_ready var_ready rstd_ready y_ready yT_ready yT_copied out_ready "
                      "x_done mix_chain dve_passed")
        block = ctx.enter_context(nc.Block())
        LINKS = 12

        def mixed(j): return c.bank[4 * j]
        def turned(j): return c.bank[4 * j + 1]
        def out(j): return c.bank[4 * j + 2]

        @block.sync
        def _(sp):
            sp.dma_start(wo[:, :, :], c.d["wo"].rearrange("(k p) n -> p k n", p=P)).then_inc(s["m_weights"], 16)
            sp.dma_start(gamma[:, :], c.d["gng"].broadcast_to([P, D])).then_inc(s["m_weights"], 16)
            sp.dma_start(beta[:, :], c.d["gnb"].broadcast_to([P, D])).then_inc(s["m_weights"], 16)

        @block.gpsimd
        def _(pool):
            give_credit(pool, s, "mixed_ready var_ready rstd_ready y_ready yT_ready yT_copied out_ready x_done")
            with pool.Fori(0, NT // LANES) as i:
                for j, t in token_loop(i):
                    pool.wait_ge(s["var_ready"], ready(t))
                    nc.gpsimd.tensor_tensor(rs[:, j:j + 1], ve[:, j:j + 1], c.minus_half[:, 0:1],
                                            ALU.pow).then_inc(s["rstd_ready"], 1)

        @block.tensor
        def _(pe):
            pe.wait_ge(s["m_weights"], 48)
            with pe.Fori(0, NT // LANES) as i:
                for j, t in token_loop(i):
                    pe.wait_ge(s["y_ready"], freed(t))
                    for h in range(H1):
                        last = nc.tensor.matmul(mixed(j)[:, h * P:(h + 1) * P], c.mixT[:, h, :],
                                                at_tile(c.v, t)[:, h * P:(h + 1) * P], start=True, stop=True)
                    last.then_inc(s["mixed_ready"], 1)
                for j, t in token_loop(i):
                    pe.wait_ge(s["y_ready"], ready(t))
                    pe.wait_ge(s["yT_copied"], freed(t))
                    transpose_tile(nc, c, turned(j), y[:, j, :]).then_inc(s["yT_ready"], 1)
                for j, t in token_loop(i):
                    pe.wait_ge(s["yT_copied"], ready(t))
                    pe.wait_ge(s["x_done"], freed(t))
                    for k in range(DK):
                        last = nc.tensor.matmul(out(j)[:, 0:D], yT[:, j, k * P:(k + 1) * P], wo[:, k, :],
                                                start=(k == 0), stop=(k == DK - 1))
                    last.then_inc(s["out_ready"], 1)

        @block.scalar
        def _(act):
            with act.Fori(0, NT // LANES) as i:
                for j, t in token_loop(i):
                    act.wait_ge(s["yT_ready"], ready(t))
                    act.wait_ge(s["out_ready"], freed(t))
                    act.copy(yT[:, j, :], turned(j)[:, 0:D]).then_inc(s["yT_copied"], 1)

        @block.vector
        def _(dve):
            dve.wait_ge(s["m_weights"], 48)
            with dve.Fori(0, NT // LANES) as i:
                ch = Chain(dve, s["mix_chain"], i * LINKS)
                for j, t in token_loop(i):
                    dve.wait_ge(s["mixed_ready"], ready(t))
                    ch.link(nc.vector.bn_stats(bn[:, j, :], mixed(j)[:, 0:D]))
                    settle(dve, s["dve_passed"])
                    ch.link(nc.vector.bn_aggr(mv[:, j, :], bn[:, j, :]))
                    nc.vector.tensor_scalar(ve[:, j:j + 1], mv[:, j, 1:2], GN_EPS, None, ALU.add).then_inc(s["var_ready"], 1)
                for j, t in token_loop(i):
                    dve.wait_ge(s["yT_ready"], freed(t))
                    ch.link(nc.vector.scalar_tensor_tensor(out=y[:, j, :], in0=mixed(j)[:, 0:D], scalar=mv[:, j, 0:1],
                                                           in1=gamma[:, :], op0=ALU.subtract, op1=ALU.mult))
                    dve.wait_ge(s["rstd_ready"], ready(t))
                    ch.link(nc.vector.scalar_tensor_tensor(out=y[:, j, :], in0=y[:, j, :], scalar=rs[:, j:j + 1],
                                                           in1=beta[:, :], op0=ALU.mult, op1=ALU.add))
                    nc.vector.tensor_tensor(y[:, j, :], y[:, j, :], at_tile(c.gate1, t), ALU.mult).then_inc(s["y_ready"], 1)
                for j, t in token_loop(i):
                    dve.wait_ge(s["out_ready"], ready(t))
                    add_and_stats(nc, c, ch, t, out(j)[:, 0:D], 1.0, s["x_done"])
                assert ch.n == LINKS, ch.n


def stage_l1_think(nc, c):
    with ExitStack() as ctx:
        sb = lambda n, sh, dt=F32: ctx.enter_context(nc.sbuf_tensor(n, sh, dt))
        M = B
        FT = HID1 // P
        agg = sb("agg_w", [P, DK, D]); d1 = sb("d1_w", [P, DK, HID1]); d2 = sb("d2_w", [P, FT, D]); bcw = sb("bc_w", [P, DK, D])
        row = {n: sb("r_" + n, [M, D]) for n in ("in_gamma", "in_beta", "agg_b", "pn_gamma", "pn_beta", "d2_b", "bc_b")}
        d1b = sb("d1_b", [P, FT])
        last_x = sb("last_x", [M, D]); n1 = sb("n1", [M, D]); th = sb("thought", [M, D])
        bn = sb("bn_t", [M, 6]); mv = sb("mv_t", [M, 2]); ve = sb("ve_t", [M, 1]); rs = sb("rs_t", [M, 1])
        nT = sb("nT", [P, DK * M]); hT = sb("hT_t", [P, FT, M])
        s = open_sems(nc, ctx, "t_loaded t_last t_stored t_chain t_var t_rstd t_normed t_turned t_turn_copied t_up t_gelu "
                      "t_down t_added")
        block = ctx.enter_context(nc.Block())
        NORMS = 2 + STEPS1

        @block.sync
        def _(sp):
            n = 0
            for b in range(2):
                sp.dma_start(last_x[32 * b:32 * b + 32, :], c.x[64 * b + 63:64 * b + 64, :, :]).then_inc(s["t_last"], 16)
            for dst, name in ((agg, "agg_w"), (d1, "d1_w"), (d2, "d2_w"), (bcw, "bc_w")):
                sp.dma_start(dst[:, :, :], c.d["f1_" + name].rearrange("(k p) n -> p k n", p=P)).then_inc(s["t_loaded"], 16)
            for name, dst in row.items():
                sp.dma_start(dst[:, :], c.d["f1_" + name].broadcast_to([M, D])).then_inc(s["t_loaded"], 16)
            sp.dma_start(d1b[:, :], c.d["f1_d1_b"]).then_inc(s["t_loaded"], 16)
            sp.wait_ge(s["t_added"], 2 + STEPS1)
            sp.dma_start(c.think_rows[:, :], n1[:, :]).then_inc(s["t_stored"], 16)
            sp.wait_ge(s["t_stored"], 16)

        @block.gpsimd
        def _(pool):
            for n in range(NORMS):
                pool.wait_ge(s["t_var"], n + 1)
                nc.gpsimd.tensor_tensor(rs[:, :], ve[:, :], c.minus_half[0:M, 0:1], ALU.pow).then_inc(s["t_rstd"], 1)

        @block.tensor
        def _(pe):
            pe.wait_ge(s["t_loaded"], 16 * (5 + len(row)))
            for n in range(2 + STEPS1):
                pe.wait_ge(s["t_normed"], n + 1)
                for k in range(DK):
                    last = nc.tensor.transpose(c.bank[0][:, k * M:(k + 1) * M],
                                               (th if n == 1 + STEPS1 else n1)[:, k * P:(k + 1) * P], c.ident[0:M, 0:M])
                last.then_inc(s["t_turned"], 1)
                pe.wait_ge(s["t_turn_copied"], n + 1)
                if n in (0, 1 + STEPS1):
                    for k in range(DK):
                        last = nc.tensor.matmul(c.bank[1][0:M, 0:D], nT[:, k * M:(k + 1) * M],
                                                (bcw if n else agg)[:, k, :], start=(k == 0), stop=(k == DK - 1))
                    last.then_inc(s["t_down"], 1)
                    continue
                for f in range(FT):
                    for k in range(DK):
                        last = nc.tensor.matmul(c.bank[2][:, f * M:(f + 1) * M], d1[:, k, f * P:(f + 1) * P],
                                                nT[:, k * M:(k + 1) * M], start=(k == 0), stop=(k == DK - 1))
                last.then_inc(s["t_up"], 1)
                pe.wait_ge(s["t_gelu"], n)
                for f in range(FT):
                    last = nc.tensor.matmul(c.bank[1][0:M, 0:D], hT[:, f, :], d2[:, f, :],
                                            start=(f == 0), stop=(f == FT - 1))
                last.then_inc(s["t_down"], 1)

        @block.scalar
        def _(act):
            act.wait_ge(s["t_loaded"], 16 * (5 + len(row)))
            for n in range(2 + STEPS1):
                act.wait_ge(s["t_turned"], n + 1)
                act.copy(nT[:, :], c.bank[0][:, 0:DK * M]).then_inc(s["t_turn_copied"], 1)
                if 1 <= n <= STEPS1:
                    act.wait_ge(s["t_up"], n)
                    for f in range(FT):
                        last = nc.scalar.activation(hT[:, f, :], c.bank[2][:, f * M:(f + 1) * M], ACT.Gelu,
                                                    bias=d1b[:, f:f + 1])
                    last.then_inc(s["t_gelu"], 1)

        @block.vector
        def _(dve):
            ch = Chain(dve, s["t_chain"])
            v = nc.vector

            def norm(n, src, eps, gamma=None, beta=None):
                ch.link(v.bn_stats(bn[:, :], src[:, :]))
                ch.link(v.bn_aggr(mv[:, :], bn[:, :]))
                v.tensor_scalar(ve[:, :], mv[:, 1:2], eps, None, ALU.add).then_inc(s["t_var"], 1)
                dve.wait_ge(s["t_rstd"], n + 1)
                if gamma is None:
                    ch.link(v.tensor_scalar(n1[:, :], src[:, :], mv[:, 0:1], rs[:, :], ALU.subtract, ALU.mult))
                    return
                ch.link(v.scalar_tensor_tensor(out=n1[:, :], in0=src[:, :], scalar=mv[:, 0:1], in1=gamma[:, :],
                                               op0=ALU.subtract, op1=ALU.mult))
                v.scalar_tensor_tensor(out=n1[:, :], in0=n1[:, :], scalar=rs[:, :], in1=beta[:, :],
                                       op0=ALU.mult, op1=ALU.add).then_inc(s["t_normed"], 1)

            dve.wait_ge(s["t_last"], 32)
            dve.wait_ge(s["t_loaded"], 16 * (5 + len(row)))
            norm(0, last_x, LN_EPS)
            norm(1, n1, EPS1, row["in_gamma"], row["in_beta"])
            dve.wait_ge(s["t_down"], 1)
            v.tensor_tensor(th[:, :], c.bank[1][0:M, 0:D], row["agg_b"][:, :], ALU.add).then_inc(s["t_added"], 1)
            for n in range(1, 1 + STEPS1):
                dve.wait_ge(s["t_added"], n)
                norm(1 + n, th, EPS1, row["pn_gamma"], row["pn_beta"])
                dve.wait_ge(s["t_down"], 1 + n)
                ch.link(v.tensor_tensor(th[:, :], c.bank[1][0:M, 0:D], th[:, :], ALU.add))
                v.tensor_tensor(th[:, :], th[:, :], row["d2_b"][:, :], ALU.add).then_inc(s["t_added"], 1)
            dve.wait_ge(s["t_added"], 1 + STEPS1)
            dve.sem_inc(s["t_normed"], 1)
            dve.wait_ge(s["t_down"], 2 + STEPS1)
            v.tensor_tensor(n1[:, :], c.bank[1][0:M, 0:D], row["bc_b"][:, :], ALU.add).then_inc(s["t_added"], 1)


def stage_l1_broadcast(nc, c):
    with ExitStack() as ctx:
        sb = lambda n, sh, dt=F32: ctx.enter_context(nc.sbuf_tensor(n, sh, dt))
        gw = sb("gw_g", [P, DK, D]); row = {n: sb("g_" + n, [P, D]) for n in ("gate_b", "out_gamma", "out_beta")}
        xn = sb("xn_g", [P, LANES, D]); xT = sb("xT_g", [P, LANES, D]); think = sb("think", [P, LANES, D])
        pre = sb("pre_g", [P, LANES, D]); gate = sb("gate_g", [P, LANES, D])
        bn = sb("bn_g", [P, LANES, 6]); mv = sb("mv_g", [P, LANES, 2]); ve = sb("ve_g", [P, LANES]); rs = sb("rs_g", [P, LANES])
        s = open_sems(nc, ctx, "g_weights think_loaded0 think_loaded1 xn_ready feat_ready feat_copied pre_ready "
                      "biased_ready gate_ready mixed_ready var_ready rstd_ready x_done g_chain dve_passed")
        block = ctx.enter_context(nc.Block())
        LINKS = 16

        def feat(j): return c.bank[4 * j]
        def lin(j): return c.bank[4 * j + 1]

        @block.sync
        def _(sp):
            sp.dma_start(gw[:, :, :], c.d["f1_gate_w"].rearrange("(k p) n -> p k n", p=P)).then_inc(s["g_weights"], 16)
            for name, dst in row.items():
                sp.dma_start(dst[:, :], c.d["f1_" + name].broadcast_to([P, D])).then_inc(s["g_weights"], 16)
            with sp.Fori(0, NT // LANES) as i:
                for j, t in token_loop(i):
                    sp.wait_ge(s["mixed_ready"], freed(t))
                    for b in range(2):
                        sp.dma_start(think[64 * b:64 * b + 64, j, :],
                                     c.think_rows[bass.ds(t + NT * b, 1), :].broadcast_to([S, D])
                                     ).then_inc(s[f"think_loaded{j}"], 16)

        @block.gpsimd
        def _(pool):
            give_credit(pool, s, "xn_ready feat_ready feat_copied pre_ready biased_ready gate_ready mixed_ready "
                        "var_ready rstd_ready x_done")
            with pool.Fori(0, NT // LANES) as i:
                for j, t in token_loop(i):
                    pool.wait_ge(s["var_ready"], ready(t))
                    nc.gpsimd.tensor_tensor(rs[:, j:j + 1], ve[:, j:j + 1], c.minus_half[:, 0:1],
                                            ALU.pow).then_inc(s["rstd_ready"], 1)

        @block.tensor
        def _(pe):
            pe.wait_ge(s["g_weights"], 64)
            with pe.Fori(0, NT // LANES) as i:
                for j, t in token_loop(i):
                    pe.wait_ge(s["xn_ready"], ready(t))
                    pe.wait_ge(s["feat_copied"], freed(t))
                    transpose_tile(nc, c, feat(j), xn[:, j, :]).then_inc(s["feat_ready"], 1)
                for j, t in token_loop(i):
                    pe.wait_ge(s["feat_copied"], ready(t))
                    pe.wait_ge(s["biased_ready"], freed(t))
                    for k in range(DK):
                        last = nc.tensor.matmul(lin(j)[:, 0:D], xT[:, j, k * P:(k + 1) * P], gw[:, k, :],
                                                start=(k == 0), stop=(k == DK - 1))
                    last.then_inc(s["pre_ready"], 1)

        @block.scalar
        def _(act):
            with act.Fori(0, NT // LANES) as i:
                for j, t in token_loop(i):
                    act.wait_ge(s["feat_ready"], ready(t))
                    act.wait_ge(s["pre_ready"], freed(t))
                    act.copy(xT[:, j, :], feat(j)[:, 0:D]).then_inc(s["feat_copied"], 1)
                for j, t in token_loop(i):
                    act.wait_ge(s["biased_ready"], ready(t))
                    act.wait_ge(s["x_done"], freed(t))
                    nc.scalar.activation(gate[:, j, :], pre[:, j, :], ACT.Sigmoid).then_inc(s["gate_ready"], 1)

        @block.vector
        def _(dve):
            dve.wait_ge(s["g_weights"], 64)
            v = nc.vector
            with dve.Fori(0, NT // LANES) as i:
                ch = Chain(dve, s["g_chain"], i * LINKS)
                for j, t in token_loop(i):
                    dve.wait_ge(s["feat_ready"], freed(t))
                    normalize(nc, c, xn[:, j, :], t).then_inc(s["xn_ready"], 1)
                for j, t in token_loop(i):
                    dve.wait_ge(s["pre_ready"], ready(t))
                    dve.wait_ge(s["gate_ready"], freed(t))
                    v.tensor_tensor(pre[:, j, :], lin(j)[:, 0:D], row["gate_b"][:, :], ALU.add).then_inc(s["biased_ready"], 1)
                for j, t in token_loop(i):
                    dve.wait_ge(s["gate_ready"], ready(t))
                    dve.wait_ge(s[f"think_loaded{j}"], 32 * i + 32)
                    ch.link(v.tensor_tensor(gate[:, j, :], gate[:, j, :], think[:, j, :], ALU.mult))
                    ins = v.tensor_tensor(gate[:, j, :], gate[:, j, :], xn[:, j, :], ALU.add)
                    ch.link(ins)
                    dve.sem_inc(s["mixed_ready"], 1)
                    ch.link(v.bn_stats(bn[:, j, :], gate[:, j, :]))
                    settle(dve, s["dve_passed"])
                    ch.link(v.bn_aggr(mv[:, j, :], bn[:, j, :]))
                    v.tensor_scalar(ve[:, j:j + 1], mv[:, j, 1:2], EPS1, None, ALU.add).then_inc(s["var_ready"], 1)
                for j, t in token_loop(i):
                    ch.link(v.scalar_tensor_tensor(out=gate[:, j, :], in0=gate[:, j, :], scalar=mv[:, j, 0:1],
                                                   in1=row["out_gamma"][:, :], op0=ALU.subtract, op1=ALU.mult))
                    dve.wait_ge(s["rstd_ready"], ready(t))
                    ch.link(v.scalar_tensor_tensor(out=gate[:, j, :], in0=gate[:, j, :], scalar=rs[:, j:j + 1],
                                                   in1=row["out_beta"][:, :], op0=ALU.mult, op1=ALU.add))
                    ch.link(v.tensor_tensor(at_tile(c.x, t), gate[:, j, :], at_tile(c.x, t), ALU.add))
                    ch.link(v.bn_stats(at_tile(c.bn, t), at_tile(c.x, t)))
                    dve.sem_inc(s["x_done"], 1)
                assert ch.n == LINKS, ch.n


def stage_l2_attention(nc, c):
    with ExitStack() as ctx:
        sb = lambda n, sh, dt=F32: ctx.enter_context(nc.sbuf_tensor(n, sh, dt))
        HP = H2 // 2
        SC = H2 * S
        wdq = sb("wdq", [P, DK, QC]); wq = sb("wq_abs", [QC, H2, P]); wvo = sb("wvo", [P, HP, D])
        seg_i = sb("seg_i", [P, NT], I32); seg = sb("seg", [P, NT]); seg_lo = sb("seg_lo", [P, NT])
        xn = sb("xn_l", [P, LANES, D]); xT = sb("xT_l", [P, LANES, D]); qcT = sb("qcT", [QC, LANES, P])
        q = sb("q_l", [P, LANES, H2, P]); rot = sb("rot_l", [P, H2, P])
        key = sb("key_l", [P, LANES, P]); kv2 = sb("kv2", [P, LANES, 2, P])
        drop = sb("drop_l", [P, LANES, S]); sc = sb("sc_l", [P, LANES, H2, S]); scT = sb("scT_l", [P, LANES, HP, P])
        mx = sb("mx_l", [P, LANES, H2]); sm = sb("sm_l", [P, LANES, H2])
        rd = sb("rd_l", [P, LANES, HP, P])
        s = open_sems(nc, ctx, "l_weights l_zero l_pre l_folded l_seg xn_ready feat_ready feat_copied qc_ready qc_copied q_ready "
                      "nope_copied rope_done kv_ready key_ready scores_ready shifted_ready exp_ready prob_ready turned_ready "
                      "turned_copied read_ready read_copied out_ready x_done l_chain seg_chain")
        scale = float(np.float32(1.0) / np.sqrt(np.float32(HD2 + R2)))
        LINKS = 22

        def bank(j, n): return c.bank[4 * j + n]

        with ExitStack() as pre:
            wt = lambda n, sh: pre.enter_context(nc.sbuf_tensor(n, sh, F32))
            wuqT = wt("wuqT", [P, H2, QC]); wukT = wt("wukT", [P, H2, KVC]); wuvT = wt("wuvT", [P, H2, KVC])
            wqr = wt("wqr", [QC, H2, R2]); wo = wt("wo_l", [P, H2, D])
            block = pre.enter_context(nc.Block())

            @block.sync
            def _(sp):
                for dst, src in ((wdq[:, :, :], c.d["wdq"].rearrange("(k p) n -> p k n", p=P)), (wuqT[:, :, :], c.d["wuqT"]),
                                 (wukT[:, :, :], c.d["wukT"]), (wuvT[:, :, :], c.d["wuvT"]), (wqr[:, :, :], c.d["wqr"]),
                                 (wo[:, :, :], c.d["wo2"]), (seg_i[:, :], c.d["seg"])):
                    sp.dma_start(dst, src).then_inc(s["l_weights"], 16)
                sp.wait_ge(s["l_weights"], 112)

            @block.tensor
            def _(pe):
                pe.wait_ge(s["l_weights"], 112)
                for h in range(H2):
                    last = nc.tensor.matmul(c.bank[h // 8][0:QC, (h % 8) * KVC:(h % 8 + 1) * KVC], wuqT[:, h, :],
                                            wukT[:, h, :], start=True, stop=True)
                for h in range(H2):
                    r = slice(64 * (h % 2), 64 * (h % 2) + 64)
                    hp = h // 2
                    last = nc.tensor.matmul(c.bank[2 + hp // 2][r, (hp % 2) * D:(hp % 2 + 1) * D], wuvT[:, h, :],
                                            wo[:, h, :], start=True, stop=True)
                last.then_inc(s["l_pre"], 1)

            @block.scalar
            def _(act):
                act.wait_ge(s["l_weights"], 112)
                act.mul(wq[:, :, KVC:P], wqr[:, :, :], scale)
                act.wait_ge(s["l_pre"], 1)
                for n in range(2):
                    act.mul(wq[:, 8 * n:8 * n + 8, 0:KVC],
                            c.bank[n][0:QC, :].rearrange("p (h n) -> p h n", h=8), scale)
                for n in range(4):
                    act.copy(wvo[:, 2 * n:2 * n + 2, :].rearrange("p h n -> p (h n)"), c.bank[2 + n][:, :])

            @block.vector
            def _(dve):
                ch = Chain(dve, s["seg_chain"])
                dve.wait_ge(s["l_weights"], 112)
                ch.link(nc.vector.tensor_copy(seg[:, :], seg_i[:, :]))
                nc.vector.tensor_scalar(seg_lo[:, :], seg[:, :], float(LOOKBACK), None, ALU.subtract)

        block = ctx.enter_context(nc.Block())

        @block.gpsimd
        def _(pool):
            give_credit(pool, s, "xn_ready feat_ready feat_copied qc_ready qc_copied q_ready nope_copied rope_done "
                        "kv_ready key_ready scores_ready shifted_ready exp_ready prob_ready turned_ready turned_copied read_ready "
                        "read_copied out_ready x_done")
            nc.gpsimd.memset(kv2[:, :, :, :], 0.0).then_inc(s["l_zero"], 1)
            with pool.Fori(0, NT // LANES) as i:
                for j, t in token_loop(i):
                    pool.wait_ge(s["scores_ready"], freed(t))
                    nc.gpsimd.tensor_copy(key[:, j, :], c.keysT[:, bass.ds(t * P, P)]).then_inc(s["key_ready"], 1)

        @block.tensor
        def _(pe):
            with pe.Fori(0, NT // LANES) as i:
                for j, t in token_loop(i):
                    pe.wait_ge(s["xn_ready"], ready(t))
                    pe.wait_ge(s["read_copied"], freed(t))
                    transpose_tile(nc, c, bank(j, 0), xn[:, j, :]).then_inc(s["feat_ready"], 1)
                for j, t in token_loop(i):
                    pe.wait_ge(s["feat_copied"], ready(t))
                    for k in range(DK):
                        last = nc.tensor.matmul(bank(j, 1)[0:QC, 0:P], wdq[:, k, :], xT[:, j, k * P:(k + 1) * P],
                                                start=(k == 0), stop=(k == DK - 1))
                    last.then_inc(s["qc_ready"], 1)
                for j, t in token_loop(i):
                    pe.wait_ge(s["qc_copied"], ready(t))
                    pe.wait_ge(s["x_done"], freed(t))
                    for h in range(H2):
                        last = nc.tensor.matmul(bank(j, h // 4)[:, (h % 4) * P:(h % 4 + 1) * P], wq[:, h, :],
                                                qcT[:, j, :], start=True, stop=True)
                    last.then_inc(s["q_ready"], 1)
                for j, t in token_loop(i):
                    pe.wait_ge(s["nope_copied"], ready(t))
                    pe.wait_ge(s["rope_done"], ready(t))
                    pe.wait_ge(s["key_ready"], ready(t))
                    for b in range(2):
                        r = slice(64 * b, 64 * b + 64)
                        for h in range(H2):
                            last = nc.tensor.matmul(bank(j, h // 8)[r, (h % 8) * S:(h % 8 + 1) * S],
                                                    q[:, j, h, r], key[:, j, r], start=True, stop=True)
                    last.then_inc(s["scores_ready"], 1)
                for j, t in token_loop(i):
                    pe.wait_ge(s["prob_ready"], ready(t))
                    for hp in range(HP):
                        last = nc.tensor.transpose(bank(j, 2 + hp // 4)[:, (hp % 4) * P:(hp % 4 + 1) * P],
                                                   sc[:, j, 2 * hp:2 * hp + 2, :].rearrange("p h n -> p (h n)"), c.ident)
                    last.then_inc(s["turned_ready"], 1)
                for j, t in token_loop(i):
                    pe.wait_ge(s["turned_copied"], ready(t))
                    pe.wait_ge(s["kv_ready"], ready(t))
                    for b in range(2):
                        last = nc.tensor.matmul(bank(j, b)[:, :].rearrange("p (h q) -> p h q", h=HP), kv2[:, j, b, :],
                                                scT[:, j, :, 64 * b:64 * b + 64], start=True, stop=True)
                    last.then_inc(s["read_ready"], 1)
                for j, t in token_loop(i):
                    pe.wait_ge(s["read_copied"], ready(t))
                    for hp in range(HP):
                        last = nc.tensor.matmul(bank(j, 2)[:, 0:D], rd[:, j, hp, :], wvo[:, hp, :],
                                                start=(hp == 0), stop=(hp == HP - 1))
                    last.then_inc(s["out_ready"], 1)

        @block.scalar
        def _(act):
            act.wait_ge(s["l_zero"], 1)
            with act.Fori(0, NT // LANES) as i:
                for j, t in token_loop(i):
                    act.wait_ge(s["feat_ready"], ready(t))
                    act.wait_ge(s["qc_ready"], freed(t))
                    act.copy(xT[:, j, :], bank(j, 0)[:, 0:D]).then_inc(s["feat_copied"], 1)
                for j, t in token_loop(i):
                    act.wait_ge(s["qc_ready"], ready(t))
                    act.wait_ge(s["q_ready"], freed(t))
                    act.copy(qcT[:, j, :], bank(j, 1)[0:QC, 0:P]).then_inc(s["qc_copied"], 1)
                for j, t in token_loop(i):
                    act.wait_ge(s["q_ready"], ready(t))
                    act.wait_ge(s["scores_ready"], freed(t))
                    for n in range(4):
                        last = act.copy(q[0:64, j, 4 * n:4 * n + 4, :].rearrange("p h n -> p (h n)"), bank(j, n)[0:64, :])
                    last.then_inc(s["nope_copied"], 1)
                for j, t in token_loop(i):
                    act.wait_ge(s["read_ready"], freed(t))
                    for b in range(2):
                        for r in range(2):
                            last = act.copy(kv2[64 * r:64 * r + 64, j, b, 64 * r:64 * r + 64],
                                            at_tile(c.kvc, t)[64 * b:64 * b + 64, :])
                    last.then_inc(s["kv_ready"], 1)
                for j, t in token_loop(i):
                    act.wait_ge(s["shifted_ready"], ready(t))
                    nc.scalar.activation(sc[:, j, :, :], sc[:, j, :, :], ACT.Exp).then_inc(s["exp_ready"], 1)
                for j, t in token_loop(i):
                    act.wait_ge(s["turned_ready"], ready(t))
                    act.wait_ge(s["read_ready"], freed(t))
                    for n in range(2):
                        last = act.copy(scT[:, j, 4 * n:4 * n + 4, :].rearrange("p h n -> p (h n)"), bank(j, 2 + n)[:, :])
                    last.then_inc(s["turned_copied"], 1)
                for j, t in token_loop(i):
                    act.wait_ge(s["read_ready"], ready(t))
                    act.wait_ge(s["out_ready"], freed(t))
                    for b in range(2):
                        last = act.copy(rd[:, j, :, 64 * b:64 * b + 64],
                                        bank(j, b)[:, :].rearrange("p (h q) -> p h q", h=HP))
                    last.then_inc(s["read_copied"], 1)

        @block.vector
        def _(dve):
            v = nc.vector
            with dve.Fori(0, NT // LANES) as i:
                ch = Chain(dve, s["l_chain"], i * LINKS)
                for j, t in token_loop(i):
                    dve.wait_ge(s["feat_ready"], freed(t))
                    normalize(nc, c, xn[:, j, :], t).then_inc(s["xn_ready"], 1)
                    ch.link(v.tensor_scalar(drop[:, j, :], c.iota, seg[:, bass.ds(t, 1)], None, ALU.is_le))
                    ch.link(v.scalar_tensor_tensor(out=drop[:, j, :], in0=c.iota, scalar=seg_lo[:, bass.ds(t, 1)],
                                                   in1=drop[:, j, :], op0=ALU.is_ge, op1=ALU.mult))
                    ch.link(v.tensor_scalar(drop[:, j, :], drop[:, j, :], 1.0, -NEG, ALU.subtract, ALU.mult))
                for j, t in token_loop(i):
                    dve.wait_ge(s["q_ready"], ready(t))
                    dve.wait_ge(s["scores_ready"], freed(t))
                    for n in range(4):
                        hs = slice(4 * n, 4 * n + 4)
                        raw = bank(j, n)[:, :].rearrange("p (h n) -> p h n", h=4)
                        tab = lambda ap, a, b: ap[a:b, :].unsqueeze(1).broadcast_to([b - a, 4, P])
                        v.tensor_tensor(q[64:P, j, hs, :], raw[64:P], tab(c.cos, 64, P), ALU.mult)
                        v.tensor_tensor(rot[96:P, hs, :], raw[64:96], tab(c.sin, 64, 96), ALU.mult)
                        last = v.tensor_tensor(rot[64:96, hs, :], raw[96:P], tab(c.sin, 96, P), ALU.mult)
                    ch.link(last)
                    ch.link(v.tensor_tensor(q[64:P, j, :, :], q[64:P, j, :, :], rot[64:P, :, :], ALU.add))
                    dve.sem_inc(s["rope_done"], 1)
                for j, t in token_loop(i):
                    dve.wait_ge(s["scores_ready"], ready(t))
                    dve.wait_ge(s["turned_ready"], freed(t))
                    for n in range(2):
                        last = v.tensor_tensor(sc[:, j, 8 * n:8 * n + 8, :], bank(j, n)[:, :].rearrange("p (h n) -> p h n", h=8),
                                               drop[:, j, :].unsqueeze(1).broadcast_to([P, 8, S]), ALU.add)
                    ch.link(last)
                    ch.link(v.tensor_reduce(mx[:, j, :], sc[:, j, :, :], AX.X, ALU.max))
                    v.tensor_tensor(sc[:, j, :, :], sc[:, j, :, :], mx[:, j, :].unsqueeze(2).broadcast_to([P, H2, S]),
                                    ALU.subtract).then_inc(s["shifted_ready"], 1)
                for j, t in token_loop(i):
                    dve.wait_ge(s["exp_ready"], ready(t))
                    ch.link(v.tensor_reduce(sm[:, j, :], sc[:, j, :, :], AX.X, ALU.add))
                    ch.link(v.reciprocal(sm[:, j, :], sm[:, j, :]))
                    v.tensor_tensor(sc[:, j, :, :], sc[:, j, :, :], sm[:, j, :].unsqueeze(2).broadcast_to([P, H2, S]),
                                    ALU.mult).then_inc(s["prob_ready"], 1)
                for j, t in token_loop(i):
                    dve.wait_ge(s["out_ready"], ready(t))
                    add_and_stats(nc, c, ch, t, bank(j, 2)[:, 0:D], 1.0, s["x_done"])
                assert ch.n == LINKS, ch.n


FT2 = -(-HID2 // P)


def stage_l2_ternary(nc, c):
    with ExitStack() as ctx:
        sb = lambda n, sh, dt=F32: ctx.enter_context(nc.sbuf_tensor(n, sh, dt))
        HW = FT2 * P
        w12 = sb("w12", [P, DK, 2, HW], BF16); w3 = sb("w3q", [P, FT2, D], BF16)
        xn = sb("xn_t", [P, LANES, D]); xp = sb("xp", [P, LANES, 3, D], BF16); rest = sb("rest_t", [P, LANES, D])
        sig = sb("sig_t", [P, LANES, HW]); hp = sb("hp", [P, LANES, 3, HW], BF16)
        s = open_sems(nc, ctx, "q_loaded q_zero q_sums q_total q_chain xn_ready feat_ready part1_ready rest_ready "
                      "part2_ready xp_ready up_ready sig_ready h_ready hpart1_ready hrest_ready hpart2_ready hp_ready "
                      "down_ready x_done t2_chain")
        LINKS = 4
        with ExitStack() as pre:
            wt = lambda n, sh: pre.enter_context(nc.sbuf_tensor(n, sh, F32))
            raw12 = wt("raw12", [P, DK, 2, HW]); raw3 = wt("raw3", [P, FT2, D]); tmp = wt("tmp_q", [P, DK * 2 * HW])
            ab = wt("abs_sums", [P, 3]); ones = wt("ones_q", [P, P]); inv = wt("inv_q", [P, 3])
            block = pre.enter_context(nc.Block())

            @block.sync
            def _(sp):
                sp.wait_ge(s["q_zero"], 3)
                for n, name in enumerate(("t1", "t2")):
                    sp.dma_start(raw12[:, :, n, 0:HID2], c.d[name].rearrange("(k p) n -> p k n", p=P)).then_inc(s["q_loaded"], 16)
                full = HID2 // P
                sp.dma_start(raw3[:, 0:full, :], c.d["t3"][0:full * P, :].rearrange("(k p) n -> p k n", p=P)).then_inc(s["q_loaded"], 16)
                sp.dma_start(raw3[0:HID2 - full * P, full, :], c.d["t3"][full * P:HID2, :]).then_inc(s["q_loaded"], 16)

            @block.gpsimd
            def _(pool):
                nc.gpsimd.memset(raw12[:, :, :, HID2:HW], 0.0).then_inc(s["q_zero"], 1)
                nc.gpsimd.memset(raw3[:, FT2 - 1, :], 0.0).then_inc(s["q_zero"], 1)
                nc.gpsimd.memset(ones[:, :], 1.0).then_inc(s["q_zero"], 1)

            @block.tensor
            def _(pe):
                pe.wait_ge(s["q_zero"], 3)
                pe.wait_ge(s["q_sums"], 3)
                nc.tensor.matmul(c.bank[0][:, 0:3], ones[:, :], ab[:, :], start=True, stop=True).then_inc(s["q_total"], 1)

            @block.vector
            def _(dve):
                v = nc.vector
                ch = Chain(dve, s["q_chain"])
                dve.wait_ge(s["q_loaded"], 64)
                for n in range(2):
                    v.tensor_reduce(ab[:, n:n + 1], raw12[:, :, n, :], AX.XY, ALU.add,
                                    apply_absolute_value=True).then_inc(s["q_sums"], 1)
                v.tensor_reduce(ab[:, 2:3], raw3[:, :, :], AX.XY, ALU.add,
                                apply_absolute_value=True).then_inc(s["q_sums"], 1)
                dve.wait_ge(s["q_total"], 1)
                ch.link(v.tensor_scalar(inv[:, :], c.bank[0][:, 0:3], 1.0 / (HID2 * D), EPS2, ALU.mult, ALU.add))
                ch.link(v.reciprocal(inv[:, :], inv[:, :]))
                for n in range(3):
                    src = raw12[:, :, n, :] if n < 2 else raw3[:, :, :]
                    dst = w12[:, :, n, :] if n < 2 else w3[:, :, :]
                    a, b = (DK, HW) if n < 2 else (FT2, D)
                    t3 = tmp[:, 0:a * b].rearrange("p (a b) -> p a b", a=a)
                    ch.link(v.tensor_scalar(t3, src, inv[:, n:n + 1], -0.5, ALU.mult, ALU.is_lt))
                    ch.link(v.tensor_scalar(src, src, inv[:, n:n + 1], 0.5, ALU.mult, ALU.is_gt))
                    ch.link(v.tensor_tensor(dst, src, t3, ALU.subtract))

        block = ctx.enter_context(nc.Block())

        def up(j, n, f):
            at = n * FT2 + f
            return c.bank[4 * j + 1 + at // 4][:, (at % 4) * P:(at % 4 + 1) * P]

        def feat(j): return c.bank[4 * j]

        @block.gpsimd
        def _(pool):
            give_credit(pool, s, "xn_ready feat_ready part1_ready rest_ready part2_ready xp_ready up_ready sig_ready "
                        "h_ready hpart1_ready hrest_ready hpart2_ready hp_ready down_ready x_done")
            with pool.Fori(0, NT // LANES) as i:
                for j, t in token_loop(i):
                    pool.wait_ge(s["part2_ready"], ready(t))
                    nc.gpsimd.tensor_tensor(xp[:, j, 2, :], rest[:, j, :], xp[:, j, 1, :],
                                            ALU.subtract).then_inc(s["xp_ready"], 1)
                for j, t in token_loop(i):
                    pool.wait_ge(s["hpart2_ready"], ready(t))
                    nc.gpsimd.tensor_tensor(hp[:, j, 2, :], sig[:, j, :], hp[:, j, 1, :],
                                            ALU.subtract).then_inc(s["hp_ready"], 1)

        @block.tensor
        def _(pe):
            with pe.Fori(0, NT // LANES) as i:
                for j, t in token_loop(i):
                    pe.wait_ge(s["xn_ready"], ready(t))
                    pe.wait_ge(s["x_done"], freed(t))
                    transpose_tile(nc, c, feat(j), xn[:, j, :]).then_inc(s["feat_ready"], 1)
                for j, t in token_loop(i):
                    pe.wait_ge(s["xp_ready"], ready(t))
                    pe.wait_ge(s["h_ready"], freed(t))
                    for n in range(2):
                        for f in range(FT2):
                            for k in range(DK):
                                for part in range(3):
                                    last = nc.tensor.matmul(up(j, n, f), w12[:, k, n, f * P:(f + 1) * P],
                                                            xp[:, j, part, k * P:(k + 1) * P],
                                                            start=(k == 0 and part == 0), stop=(k == DK - 1 and part == 2))
                    last.then_inc(s["up_ready"], 1)
                for j, t in token_loop(i):
                    pe.wait_ge(s["hp_ready"], ready(t))
                    for part in range(3):
                        for f in range(FT2):
                            last = nc.tensor.matmul(feat(j)[:, 0:D], hp[:, j, part, f * P:(f + 1) * P], w3[:, f, :],
                                                    start=(part == 0 and f == 0), stop=(part == 2 and f == FT2 - 1))
                    last.then_inc(s["down_ready"], 1)

        @block.scalar
        def _(act):
            with act.Fori(0, NT // LANES) as i:
                for j, t in token_loop(i):
                    act.wait_ge(s["feat_ready"], ready(t))
                    act.wait_ge(s["up_ready"], freed(t))
                    act.copy(xp[:, j, 0, :], feat(j)[:, 0:D]).then_inc(s["part1_ready"], 1)
                for j, t in token_loop(i):
                    act.wait_ge(s["rest_ready"], ready(t))
                    act.copy(xp[:, j, 1, :], rest[:, j, :]).then_inc(s["part2_ready"], 1)
                for j, t in token_loop(i):
                    act.wait_ge(s["up_ready"], ready(t))
                    act.wait_ge(s["hp_ready"], freed(t))
                    nc.scalar.activation(sig[:, j, 0:4 * P], c.bank[4 * j + 1][:, :], ACT.Sigmoid)
                    nc.scalar.activation(sig[:, j, 4 * P:HW], c.bank[4 * j + 2][:, 0:(FT2 - 4) * P],
                                         ACT.Sigmoid).then_inc(s["sig_ready"], 1)
                for j, t in token_loop(i):
                    act.wait_ge(s["h_ready"], ready(t))
                    act.wait_ge(s["down_ready"], freed(t))
                    act.copy(hp[:, j, 0, :], sig[:, j, :]).then_inc(s["hpart1_ready"], 1)
                for j, t in token_loop(i):
                    act.wait_ge(s["hrest_ready"], ready(t))
                    act.copy(hp[:, j, 1, :], sig[:, j, :]).then_inc(s["hpart2_ready"], 1)

        @block.vector
        def _(dve):
            v = nc.vector
            with dve.Fori(0, NT // LANES) as i:
                ch = Chain(dve, s["t2_chain"], i * LINKS)
                for j, t in token_loop(i):
                    dve.wait_ge(s["feat_ready"], freed(t))
                    normalize(nc, c, xn[:, j, :], t).then_inc(s["xn_ready"], 1)
                for j, t in token_loop(i):
                    dve.wait_ge(s["part1_ready"], ready(t))
                    dve.wait_ge(s["xp_ready"], freed(t))
                    v.tensor_tensor(rest[:, j, :], feat(j)[:, 0:D], xp[:, j, 0, :], ALU.subtract).then_inc(s["rest_ready"], 1)
                for j, t in token_loop(i):
                    dve.wait_ge(s["sig_ready"], ready(t))
                    lo = (8 - FT2) * P
                    v.tensor_tensor(sig[:, j, 0:lo], c.bank[4 * j + 2][:, (FT2 - 4) * P:4 * P], sig[:, j, 0:lo], ALU.mult)
                    v.tensor_tensor(sig[:, j, lo:HW], c.bank[4 * j + 3][:, :], sig[:, j, lo:HW],
                                    ALU.mult).then_inc(s["h_ready"], 1)
                for j, t in token_loop(i):
                    dve.wait_ge(s["hpart1_ready"], ready(t))
                    v.tensor_tensor(sig[:, j, :], sig[:, j, :], hp[:, j, 0, :], ALU.subtract).then_inc(s["hrest_ready"], 1)
                for j, t in token_loop(i):
                    dve.wait_ge(s["down_ready"], ready(t))
                    add_and_stats(nc, c, ch, t, feat(j)[:, 0:D], 1.0, s["x_done"])
                assert ch.n == LINKS, ch.n


def stage_l3_split(nc, c):
    with ExitStack() as ctx:
        sb = lambda n, sh, dt=F32: ctx.enter_context(nc.sbuf_tensor(n, sh, dt))
        src = sb("src_s", [P, LANES, 2, D]); parts = sb("parts_s", [P, LANES, 2, 3, D], BF16)
        s = open_sems(nc, ctx, "scaled ctx_loaded0 ctx_loaded1 xn_ready part1_ready rest_ready part2_ready parts_ready "
                      "turned_ready turned_copied stored0 stored1")
        block = ctx.enter_context(nc.Block())

        @block.sync
        def _(sp):
            with sp.Fori(0, NT // LANES) as i:
                for j, t in token_loop(i):
                    sp.wait_ge(s["parts_ready"], freed(t))
                    sp.wait_ge(s["turned_ready"], freed(t))
                    sp.dma_start(src[:, j, 1, :], c.d["ctx"][bass.ds(t * P, P), :]).then_inc(s[f"ctx_loaded{j}"], 16)
                for j, t in token_loop(i):
                    sp.wait_ge(s["parts_ready"], ready(t))
                    for n, dst in enumerate((c.q_parts, c.k_parts)):
                        for a in range(3):
                            sp.dma_start(dst[a, :, bass.ds(t * 2 * H3, 2 * H3), :].rearrange("c h l -> h c l"),
                                         parts[:, j, n, a, :]).then_inc(s[f"stored{j}"], 16)
            for j in range(LANES):
                sp.wait_ge(s[f"stored{j}"], 96 * (NT // LANES) + 96)

        @block.gpsimd
        def _(pool):
            give_credit(pool, s, "xn_ready part1_ready rest_ready part2_ready parts_ready turned_ready turned_copied")
            for j in range(LANES):
                pool.sem_inc(s[f"stored{j}"], 96)

        @block.tensor
        def _(pe):
            with pe.Fori(0, NT // LANES) as i:
                for j, t in token_loop(i):
                    pe.wait_ge(s[f"ctx_loaded{j}"], loaded(i))
                    pe.wait_ge(s["turned_copied"], freed(t))
                    transpose_tile(nc, c, c.bank[j], src[:, j, 1, :]).then_inc(s["turned_ready"], 1)

        @block.scalar
        def _(act):
            with act.Fori(0, NT // LANES) as i:
                for j, t in token_loop(i):
                    act.wait_ge(s["turned_ready"], ready(t))
                    act.copy(c.vT[:, :, bass.ds(t * P, P)], half(c.bank[j][:, 0:D])).then_inc(s["turned_copied"], 1)
                for j, t in token_loop(i):
                    act.wait_ge(s["xn_ready"], ready(t))
                    act.wait_ge(s[f"ctx_loaded{j}"], loaded(i))
                    act.wait_ge(s[f"stored{j}"], 96 * i + 96)
                    act.copy(parts[:, j, :, 0, :], src[:, j, :, :]).then_inc(s["part1_ready"], 1)
                for j, t in token_loop(i):
                    act.wait_ge(s["rest_ready"], ready(t))
                    act.copy(parts[:, j, :, 1, :], src[:, j, :, :]).then_inc(s["part2_ready"], 1)

        @block.vector
        def _(dve):
            v = nc.vector
            v.tensor_scalar(c.rstd[:, :], c.rstd[:, :], float(np.float32(DQ3) ** np.float32(-0.5)), None,
                            ALU.mult).then_inc(s["scaled"], 1)
            dve.wait_ge(s["scaled"], 1)
            with dve.Fori(0, NT // LANES) as i:
                for j, t in token_loop(i):
                    dve.wait_ge(s["parts_ready"], freed(t))
                    normalize(nc, c, src[:, j, 0, :], t).then_inc(s["xn_ready"], 1)
                for j, t in token_loop(i):
                    dve.wait_ge(s["part1_ready"], ready(t))
                    dve.wait_ge(s["turned_ready"], ready(t))
                    v.tensor_tensor(src[:, j, :, :], src[:, j, :, :], parts[:, j, :, 0, :],
                                    ALU.subtract).then_inc(s["rest_ready"], 1)
                for j, t in token_loop(i):
                    dve.wait_ge(s["part2_ready"], ready(t))
                    v.tensor_tensor(parts[:, j, :, 2, :], src[:, j, :, :], parts[:, j, :, 1, :],
                                    ALU.subtract).then_inc(s["parts_ready"], 1)


def stage_l3_attention(nc, c):
    with ExitStack() as ctx:
        sb = lambda n, sh, dt=F32: ctx.enter_context(nc.sbuf_tensor(n, sh, dt))
        R = 9 * DQ3
        U = 2 * H3
        AH = DQ3 + 1
        NA, NB = 4, 2
        q = sb("q_3", [R, 2, H3 * D], BF16); k = sb("k_3", [R, 2, H3 * D], BF16)
        val = sb("val_3", [P, 2, DK, H3, AH]); nmax = sb("nmax_3", [P, NA, 2])
        e = sb("e_3", [P, NA, 2, D]); eT = sb("eT_3", [P, NA, DK, D])
        rec = sb("rec_3", [P, 2 * H3]); on = sb("on_3", [P, 2, 2, S]); gam = sb("gam_3", [P, 1])
        s = open_sems(nc, ctx, "gamma_loaded ones_set qk_loaded0 qk_loaded1 val_ready scores_ready max_ready exp_ready "
                      "turned_ready eT_ready used_ready batch_read tile_turned x_done n_chain")
        block = ctx.enter_context(nc.Block())
        scores = lambda u: c.bank[u % NA]
        turned = lambda u: c.bank[NA + u % NB]
        readout = c.bank[6][:, 0:2 * H3 * AH]
        final = c.bank[7][:, 0:D]
        LINKS = 6

        def unit(t, u):
            return t * U + u

        def unit_ready(t, u):
            return unit(t, u) + 1 + NA

        def unit_freed(t, u, banks=NA):
            return unit(t, u) + 1 + NA - banks

        def by_scalar(u):
            return u % 8 in (1, 4, 7)

        @block.sync
        def _(sp):
            sp.dma_start(gam[:, :], c.d["gamma3"].broadcast_to([P, 1])).then_inc(s["gamma_loaded"], 16)

            def load(t, first=False):
                for b in range(2):
                    if not first:
                        sp.wait_ge(s["scores_ready"], unit_ready(t - 1, b * H3 + H3 - 1))
                    cols = bass.ds((t * 2 + b) * H3, H3)
                    k_rows = c.k_parts[:, :, cols, :].rearrange("a c h l -> (a c) (h l)")
                    for i in range(3):
                        rows = slice(24 * i, 24 * i + 24)
                        q_rows = c.q_parts[i, :, cols, :].rearrange("c h l -> c (h l)").unsqueeze(0)
                        sp.dma_start(q[rows, b, :], q_rows.broadcast_to([3, DQ3, H3 * D])).then_inc(s[f"qk_loaded{b}"], 16)
                        sp.dma_start(k[rows, b, :], k_rows).then_inc(s[f"qk_loaded{b}"], 16)

            load(0, first=True)
            with sp.Fori(1, NT) as t:
                load(t)

        @block.gpsimd
        def _(pool):
            nc.gpsimd.memset(val[:, :, :, :, :], 1.0).then_inc(s["ones_set"], 1)
            pool.wait_ge(s["ones_set"], 1)
            give_credit(pool, s, "val_ready batch_read tile_turned x_done")
            for n in ("scores_ready", "max_ready", "exp_ready", "turned_ready", "eT_ready", "used_ready"):
                pool.sem_inc(s[n], NA)

            def values(t, first=False):
                for b in range(2):
                    nb = 2 * t + b
                    if not first:
                        pool.wait_ge(s["used_ready"], unit_ready(t - 1, b * H3 + H3 - 1))
                    for lt in range(DK):
                        last = nc.gpsimd.tensor_copy(val[:, b, lt, :, 0:DQ3], c.vT[:, lt, bass.ds(nb * S, S)].rearrange(
                            "p (h c) -> p h c", h=H3))
                    last.then_inc(s["val_ready"], 1)

            values(0, first=True)
            with pool.Fori(1, NT) as t:
                values(t)

        @block.tensor
        def _(pe):
            def score(t, u):
                b, h = divmod(u, H3)
                if h == 0:
                    pe.wait_ge(s[f"qk_loaded{b}"], 96 * t + 96)
                pe.wait_ge(s["exp_ready"], unit_freed(t, u))
                for qt in range(2):
                    last = nc.tensor.matmul(scores(u)[:, qt * D:(qt + 1) * D], q[:, b, h * D + qt * P:h * D + qt * P + P],
                                            k[:, b, h * D:(h + 1) * D], start=True, stop=True)
                last.then_inc(s["scores_ready"], 1)

            def turn(t, u):
                pe.wait_ge(s["exp_ready"], unit_ready(t, u))
                pe.wait_ge(s["eT_ready"], unit_freed(t, u, NB))
                for lt in range(DK):
                    for qt in range(2):
                        last = nc.tensor.transpose(turned(u)[:, lt * D + qt * P:lt * D + qt * P + P],
                                                   e[:, u % NA, qt, lt * P:(lt + 1) * P], c.ident)
                last.then_inc(s["turned_ready"], 1)

            def read(t, u):
                b, h = divmod(u, H3)
                pe.wait_ge(s["eT_ready"], unit_ready(t, u))
                if h == 0:
                    pe.wait_ge(s["val_ready"], ready(2 * t + b))
                    pe.wait_ge(s["batch_read"], 2 * t + b + CREDIT)
                for qt in range(2):
                    out = readout[:, (qt * H3 + h) * AH:(qt * H3 + h + 1) * AH]
                    for lt in range(DK):
                        last = nc.tensor.matmul(out, eT[:, u % NA, lt, qt * P:(qt + 1) * P], val[:, b, lt, h, :],
                                                start=(lt == 0), stop=(lt == DK - 1))
                last.then_inc(s["used_ready"], 1)

            def finish(t):
                pe.wait_ge(s["batch_read"], 2 * t + 2 + CREDIT)
                pe.wait_ge(s["x_done"], t + CREDIT)
                for qt in range(2):
                    last = nc.tensor.transpose(final[:, qt * P:(qt + 1) * P],
                                               on[:, qt, :, :].rearrange("p b n -> p (b n)"), c.ident)
                last.then_inc(s["tile_turned"], 1)

            def tile(t, first=False, last=False):
                for u in range(U):
                    if u < U - 1:
                        score(t, u + 1)
                    elif not last:
                        score(t + 1, 0)
                    turn(t, u)
                    if u > 0:
                        read(t, u - 1)
                    elif not first:
                        read(t - 1, U - 1)
                    if u == 3 and not first:
                        finish(t - 1)

            score(0, 0)
            tile(0, first=True)
            with pe.Fori(1, NT - 1) as t:
                tile(t)
            tile(NT - 1, last=True)
            read(NT - 1, U - 1)
            finish(NT - 1)

        @block.scalar
        def _(act):
            with act.Fori(0, NT) as t:
                for u in range(U):
                    act.wait_ge(s["max_ready"], unit_ready(t, u))
                    act.wait_ge(s["turned_ready"], unit_freed(t, u))
                    for qt in range(2):
                        last = nc.scalar.activation(e[:, u % NA, qt, :], scores(u)[:, qt * D:(qt + 1) * D], ACT.Exp,
                                                    bias=nmax[:, u % NA, qt:qt + 1])
                    last.then_inc(s["exp_ready"], 1)
                    if by_scalar(u):
                        act.wait_ge(s["turned_ready"], unit_ready(t, u))
                        act.wait_ge(s["used_ready"], unit_freed(t, u))
                        act.wait_ge(s["eT_ready"], unit_freed(t, u, 1))
                        act.copy(eT[:, u % NA, :, :].rearrange("p k n -> p (k n)"), turned(u)[:, :]).then_inc(s["eT_ready"], 1)

        @block.vector
        def _(dve):
            v = nc.vector
            ch = None

            def maxima(t, u):
                dve.wait_ge(s["scores_ready"], unit_ready(t, u))
                v.tensor_reduce(nmax[:, u % NA, :], scores(u)[:, :].rearrange("p (a n) -> p a n", a=2), AX.X, ALU.max,
                                negate=True).then_inc(s["max_ready"], 1)

            def copy(t, u):
                dve.wait_ge(s["turned_ready"], unit_ready(t, u))
                dve.wait_ge(s["used_ready"], unit_freed(t, u))
                dve.wait_ge(s["eT_ready"], unit_freed(t, u, 1))
                v.tensor_copy(eT[:, u % NA, :, :].rearrange("p k n -> p (k n)"), turned(u)[:, :]).then_inc(s["eT_ready"], 1)

            def batch(t, b, ch):
                dve.wait_ge(s["used_ready"], unit_ready(t, b * H3 + H3 - 1))
                if b == 0:
                    dve.wait_ge(s["tile_turned"], t + CREDIT)
                r3 = readout.rearrange("p (n a) -> p n a", a=AH)
                ch.link(v.reciprocal(rec[:, :], r3[:, :, DQ3]))
                ch.link(v.tensor_scalar(rec[:, :], rec[:, :], gam[:, 0:1], None, ALU.mult))
                for qt in range(2):
                    last = v.tensor_tensor(on[:, qt, b, :].rearrange("p (h c) -> p h c", h=H3),
                                           r3[:, qt * H3:(qt + 1) * H3, 0:DQ3],
                                           rec[:, qt * H3:(qt + 1) * H3].unsqueeze(2).broadcast_to([P, H3, DQ3]), ALU.mult)
                last.then_inc(s["batch_read"], 1)

            def finish(t, ch):
                dve.wait_ge(s["tile_turned"], t + 1 + CREDIT)
                add_and_stats(nc, c, ch, t, final, 1.0, s["x_done"])

            def tile(t, first=False, last=False):
                ch = Chain(dve, s["n_chain"], 0 if first else t * LINKS - 4)
                for u in range(U):
                    maxima(t, u)
                    if u >= 2 and not by_scalar(u - 2):
                        copy(t, u - 2)
                    elif u == 0 and not first and not by_scalar(U - 2):
                        copy(t - 1, U - 2)
                    elif u == 1 and not first and not by_scalar(U - 1):
                        copy(t - 1, U - 1)
                    if u == 2 and not first:
                        batch(t - 1, 1, ch)
                    if u == 7 and not first:
                        finish(t - 1, ch)
                    if u == H3 + 2:
                        batch(t, 0, ch)
                if last:
                    for u in (U - 2, U - 1):
                        if not by_scalar(u):
                            copy(t, u)
                    batch(t, 1, ch)
                    finish(t, ch)

            dve.wait_ge(s["gamma_loaded"], 16)
            tile(0, first=True)
            with dve.Fori(1, NT - 1) as t:
                tile(t)
            tile(NT - 1, last=True)


def stage_l3_gate(nc, c):
    with ExitStack() as ctx:
        sb = lambda n, sh, dt=F32: ctx.enter_context(nc.sbuf_tensor(n, sh, dt))
        wg = sb("wg_3", [P, DK, E3]); xn = sb("xn_g3", [P, LANES, D]); xT = sb("xT_g3", [P, LANES, D])
        s = open_sems(nc, ctx, "g3_loaded xn_ready feat_ready feat_copied logit_ready logit_copied")
        block = ctx.enter_context(nc.Block())

        @block.sync
        def _(sp):
            sp.dma_start(wg[:, :, :], c.d["g3w"].rearrange("(k p) n -> p k n", p=P)).then_inc(s["g3_loaded"], 16)

        @block.gpsimd
        def _(pool):
            give_credit(pool, s, "xn_ready feat_ready feat_copied logit_ready logit_copied")

        @block.tensor
        def _(pe):
            pe.wait_ge(s["g3_loaded"], 16)
            with pe.Fori(0, NT // LANES) as i:
                for j, t in token_loop(i):
                    pe.wait_ge(s["xn_ready"], ready(t))
                    pe.wait_ge(s["feat_copied"], freed(t))
                    transpose_tile(nc, c, c.bank[j], xn[:, j, :]).then_inc(s["feat_ready"], 1)
                for j, t in token_loop(i):
                    pe.wait_ge(s["feat_copied"], ready(t))
                    pe.wait_ge(s["logit_copied"], freed(t))
                    for k in range(DK):
                        last = nc.tensor.matmul(c.bank[2 + j][:, 0:E3], xT[:, j, k * P:(k + 1) * P], wg[:, k, :],
                                                start=(k == 0), stop=(k == DK - 1))
                    last.then_inc(s["logit_ready"], 1)

        @block.scalar
        def _(act):
            with act.Fori(0, NT // LANES) as i:
                for j, t in token_loop(i):
                    act.wait_ge(s["logit_ready"], ready(t))
                    nc.scalar.activation(at_tile(c.score3, t), c.bank[2 + j][:, 0:E3],
                                         ACT.Sigmoid).then_inc(s["logit_copied"], 1)

        @block.vector
        def _(dve):
            with dve.Fori(0, NT // LANES) as i:
                for j, t in token_loop(i):
                    dve.wait_ge(s["feat_ready"], freed(t))
                    normalize(nc, c, xn[:, j, :], t).then_inc(s["xn_ready"], 1)
                for j, t in token_loop(i):
                    dve.wait_ge(s["feat_ready"], ready(t))
                    dve.wait_ge(s["logit_ready"], freed(t))
                    nc.vector.tensor_copy(xT[:, j, :], c.bank[j][:, 0:D]).then_inc(s["feat_copied"], 1)


def stage_l3_route(nc, c):
    with ExitStack() as ctx:
        sb = lambda n, sh, dt=F32: ctx.enter_context(nc.sbuf_tensor(n, sh, dt))
        pad = 8 - TOP3
        cand = sb("cand_3", [P, NT, E3 + pad]); left = sb("left_3", [P, NT, E3 + pad]); top = sb("top_3", [P, NT, 8])
        total = sb("total_3", [P, NT])
        s = open_sems(nc, ctx, "r3_chain")
        block = ctx.enter_context(nc.Block())

        @block.vector
        def _(dve):
            ch = Chain(dve, s["r3_chain"])
            v = nc.vector
            v.memset(cand[:, :, E3:E3 + pad], BIG)
            ch.link(v.tensor_copy(cand[:, :, 0:E3], c.score3[:, :, :]))
            for t in range(NT):
                last = v.max(top[:, t, :], cand[:, t, 0:E3])
            ch.link(last)
            ch.link(v.memset(top[:, :, TOP3:8], BIG))
            for t in range(NT):
                last = v.match_replace(out=left[:, t, :], in_to_replace=top[:, t, :], in_values=cand[:, t, :],
                                       imm_value=-BIG)
            ch.link(last)
            ch.link(v.tensor_tensor(left[:, :, 0:E3], left[:, :, 0:E3], cand[:, :, 0:E3], ALU.not_equal))
            ch.link(v.tensor_tensor(left[:, :, 0:E3], left[:, :, 0:E3], cand[:, :, 0:E3], ALU.mult))
            ch.link(v.tensor_reduce(total[:, :], left[:, :, 0:E3], AX.X, ALU.add))
            ch.link(v.tensor_scalar(total[:, :], total[:, :], 1e-20, None, ALU.add))
            ch.link(v.reciprocal(total[:, :], total[:, :]))
            comb = c.comb[:, :].rearrange("p (t e) -> p t e", e=E3 + 1)
            v.memset(comb[:, :, E3:E3 + 1], 1.0)
            ch.link(v.scalar_tensor_tensor(out=comb[:, :, 0:E3], in0=left[:, :, 0:E3], scalar=SCALE3,
                                           in1=total[:, :].unsqueeze(2).broadcast_to([P, NT, E3]),
                                           op0=ALU.mult, op1=ALU.mult))


def stage_l3_experts(nc, c):
    with ExitStack() as ctx:
        sb = lambda n, sh, dt=F32: ctx.enter_context(nc.sbuf_tensor(n, sh, dt))
        U = E3 + 1
        HW = U * HID3
        CH = -(-HW // P)
        NA, NB, NG = 3, 2, 4
        groups = [range(0, 4), range(4, 7), range(7, 10), range(10, CH)]
        w13 = sb("w13_3", [P, DK, U * 2 * HID3]); w2 = sb("w2_3", [P, CH, D])
        xn = sb("xn_3", [P, D]); xT = sb("xT_3", [P, 2, D]); sig = sb("sig_3", [P, NA, HID3])
        hid = sb("hid_3", [P, 2, HW]); hT = sb("hT_3", [P, CH, P])
        s = open_sems(nc, ctx, "w_loaded xn_ready feat_ready xT_ready hid_ready sig_ready prod_ready turned_ready "
                      "hT_ready down_ready x_done e3_chain")
        LINKS = U
        block = ctx.enter_context(nc.Block())
        feat = c.bank[0][:, 0:D]
        gates = lambda e: c.bank[1 + e % NA]
        turned = lambda g: c.bank[1 + NA + g % NB]
        out = lambda j: c.bank[1 + NA + NB + j][:, 0:D]
        width = lambda ch: min(P, HW - ch * P)

        def unit_ready(t, e):
            return t * U + e + 1 + NA

        def group_ready(t, g):
            return t * NG + g + 1 + NG

        @block.sync
        def _(sp):
            loads = []
            for k in range(DK):
                rows = slice(k * P, (k + 1) * P)
                view = w13[:, k, :].rearrange("p (e n) -> p e n", e=U)
                for n, (routed, shared) in enumerate((("e3w1", "s3w1"), ("e3w3", "s3w3"))):
                    cols = slice(n * HID3, (n + 1) * HID3)
                    loads.append((view[:, 0:E3, cols], c.d[routed][:, rows, :].rearrange("e p n -> p e n")))
                    loads.append((view[:, E3, cols], c.d[shared][rows, :]))
            full = E3 * HID3 // P
            loads.append((w2[:, 0:full, :], c.d["e3w2"].rearrange("e h n -> (e h) n").rearrange("(c p) n -> p c n", p=P)))
            loads.append((w2[:, full, :], c.d["s3w2"][0:P, :]))
            loads.append((w2[0:HID3 - P, full + 1, :], c.d["s3w2"][P:HID3, :]))
            assert len(loads) == 11
            for dst, src in loads:
                sp.dma_start(dst, src).then_inc(s["w_loaded"], 16)

        @block.gpsimd
        def _(pool):
            for names, credit in (("hid_ready sig_ready prod_ready", NA), ("turned_ready hT_ready down_ready", NG),
                                  ("xn_ready feat_ready xT_ready x_done", CREDIT)):
                for n in names.split():
                    pool.sem_inc(s[n], credit)

        def schedule(first, last, hidden, hidden_turn, down, features):
            for e in range(U):
                hidden(0, e)
                if not first and e in (0, 1):
                    hidden_turn(-1, 2 + e)
                if e == 3:
                    hidden_turn(0, 0)
                if e == 7:
                    hidden_turn(0, 1)
                if not first and e in (2, 3):
                    down(-1, e)
                if e == 5:
                    down(0, 0)
                if e == 8:
                    down(0, 1)
                if e == 6 and not last:
                    features(1)
            if last:
                for g in (2, 3):
                    hidden_turn(0, g)
                for g in (2, 3):
                    down(0, g)

        @block.tensor
        def _(pe):
            def features(t):
                pe.wait_ge(s["xn_ready"], ready(t))
                transpose_tile(nc, c, feat, xn[:, :]).then_inc(s["feat_ready"], 1)

            def tile(t, j, first=False, last=False):
                def hidden(dt, e):
                    if e == 0:
                        pe.wait_ge(s["xT_ready"], ready(t))
                    pe.wait_ge(s["prod_ready"], unit_ready(t, e) - NA)
                    for k in range(DK):
                        op = nc.tensor.matmul(gates(e)[:, 0:2 * HID3], xT[:, j, k * P:(k + 1) * P],
                                              w13[:, k, e * 2 * HID3:(e + 1) * 2 * HID3], start=(k == 0), stop=(k == DK - 1))
                    op.then_inc(s["hid_ready"], 1)

                def turn(dt, g):
                    upto = groups[g][-1] * P + width(groups[g][-1])
                    pe.wait_ge(s["prod_ready"], unit_ready(t + dt, (upto - 1) // HID3))
                    pe.wait_ge(s["hT_ready"], group_ready(t + dt, g) - NB)
                    for n, ck in enumerate(groups[g]):
                        w = width(ck)
                        op = nc.tensor.transpose(turned(g)[0:w, n * P:(n + 1) * P],
                                                 hid[:, (j + dt) % 2, ck * P:ck * P + w], c.ident)
                    op.then_inc(s["turned_ready"], 1)

                def down(dt, g):
                    pe.wait_ge(s["hT_ready"], group_ready(t + dt, g))
                    if g == 0:
                        pe.wait_ge(s["x_done"], freed(t))
                    for ck in groups[g]:
                        w = width(ck)
                        op = nc.tensor.matmul(out((j + dt) % 2), hT[0:w, ck, :], w2[0:w, ck, :],
                                              start=(ck == 0), stop=(ck == CH - 1))
                    op.then_inc(s["down_ready"], 1)

                schedule(first, last, hidden, turn, down, lambda dt: features(t + dt))

            pe.wait_ge(s["w_loaded"], 176)
            features(0)
            tile(0, 0, first=True)
            with pe.Fori(0, (NT - 2) // 2) as i:
                tile(2 * i + 1, 1)
                tile(2 * i + 2, 0)
            tile(NT - 1, 1, last=True)

        @block.scalar
        def _(act):
            def features(t, j):
                act.wait_ge(s["feat_ready"], ready(t))
                act.copy(xT[:, j, :], feat).then_inc(s["xT_ready"], 1)

            def tile(t, j, first=False, last=False):
                def hidden(dt, e):
                    act.wait_ge(s["hid_ready"], unit_ready(t, e))
                    act.wait_ge(s["prod_ready"], unit_ready(t, e) - NA)
                    nc.scalar.activation(sig[:, e % NA, :], gates(e)[:, 0:HID3], ACT.Sigmoid).then_inc(s["sig_ready"], 1)

                def copy(dt, g):
                    act.wait_ge(s["turned_ready"], group_ready(t + dt, g))
                    act.wait_ge(s["down_ready"], group_ready(t + dt, g) - NG)
                    n, at = len(groups[g]), groups[g][0]
                    full = n if width(at + n - 1) == P else n - 1
                    op = act.copy(hT[:, at:at + full, :].rearrange("p c n -> p (c n)"), turned(g)[:, 0:full * P])
                    if full < n:
                        w = width(at + n - 1)
                        op = act.copy(hT[0:w, at + full, :], turned(g)[0:w, full * P:n * P])
                    op.then_inc(s["hT_ready"], 1)

                schedule(first, last, hidden, copy, lambda dt, g: None, lambda dt: features(t + dt, (j + dt) % 2))

            features(0, 0)
            tile(0, 0, first=True)
            with act.Fori(0, (NT - 2) // 2) as i:
                tile(2 * i + 1, 1)
                tile(2 * i + 2, 0)
            tile(NT - 1, 1, last=True)

        @block.vector
        def _(dve):
            v = nc.vector

            def features(t):
                dve.wait_ge(s["feat_ready"], t + CREDIT)
                normalize(nc, c, xn[:, :], t).then_inc(s["xn_ready"], 1)

            def add(t, j):
                dve.wait_ge(s["down_ready"], group_ready(t, NG - 1))
                v.tensor_tensor(at_tile(c.x, t), out(j), at_tile(c.x, t), ALU.add).then_inc(s["x_done"], 1)

            def tile(t, j, first=False, last=False):
                ch = Chain(dve, s["e3_chain"], t * LINKS)
                for e in range(U):
                    dve.wait_ge(s["sig_ready"], unit_ready(t, e))
                    ch.link(v.tensor_tensor(sig[:, e % NA, :], gates(e)[:, 0:HID3], sig[:, e % NA, :], ALU.mult))
                    v.scalar_tensor_tensor(out=hid[:, j, e * HID3:(e + 1) * HID3], in0=gates(e)[:, HID3:2 * HID3],
                                           scalar=c.comb[:, bass.ds(t * U + e, 1)], in1=sig[:, e % NA, :],
                                           op0=ALU.mult, op1=ALU.mult).then_inc(s["prod_ready"], 1)
                    if e == 3 and not last:
                        features(t + 1)
                    if e == 5 and not first:
                        add(t - 1, 1 - j)
                if last:
                    add(t, j)
                assert ch.n == LINKS, ch.n

            features(0)
            tile(0, 0, first=True)
            with dve.Fori(0, (NT - 2) // 2) as i:
                tile(2 * i + 1, 1)
                tile(2 * i + 2, 0)
            tile(NT - 1, 1, last=True)


def layers(nc, c):
    with ExitStack() as keys:
        c.keysT = keys.enter_context(nc.sbuf_tensor("keysT", [P, N], F32))
        c.kvc = keys.enter_context(nc.sbuf_tensor("kvc", [P, NT, KVC], F32))
        with ExitStack() as kv:
            res = lambda n, sh, dt=F32: kv.enter_context(nc.sbuf_tensor(n, sh, dt))
            c.v = res("v_all", [P, NT, D])
            c.gramT = res("gramT", [P, H1, N])
            finish_stats(nc, c, "st0")
            stage_l0_attention(nc, c)
            finish_stats(nc, c, "st1")
            with ExitStack() as moe:
                l0 = lambda n, sh, dt=F32: moe.enter_context(nc.sbuf_tensor(n, sh, dt))
                c.score0 = l0("score0", [P, NT, E0]); c.row_col = l0("row_col", [P, 1])
                c.slot_token = l0("slot_token", [CAP0, E0], I32); c.slot_weight = l0("slot_weight", [CAP0, E0])
                c.place = l0("place", [P, NT, E0], BF16)
                stage_l0_shared(nc, c)
                with ExitStack() as sl:
                    c.slot_cols = sl.enter_context(nc.sbuf_tensor("slot_cols", [P, NT, E0, 6], BF16))
                    stage_l0_route(nc, c)
                    stage_l0_slots(nc, c)
                stage_l0_experts(nc, c)
            stage_add_experts(nc, c)
            c.gate1 = res("gate1", [P, NT, D])
            c.mixT = res("mixT", [P, H1, P])
            finish_stats(nc, c, "st2")
            stage_l1_scores(nc, c)
            stage_l1_mix(nc, c)
        finish_stats(nc, c, "st3")
        stage_l1_think(nc, c)
        stage_l1_broadcast(nc, c)
        recycle(nc)
        finish_stats(nc, c, "st4")
        stage_l2_attention(nc, c)
    finish_stats(nc, c, "st5")
    stage_l2_ternary(nc, c)
    recycle(nc)
    finish_stats(nc, c, "st6")
    with ExitStack() as l3:
        c.vT = l3.enter_context(nc.sbuf_tensor("vT", [P, DK, N], F32))
        stage_l3_split(nc, c)
        stage_l3_attention(nc, c)
    finish_stats(nc, c, "st7")
    with ExitStack() as moe:
        l3 = lambda n, sh, dt=F32: moe.enter_context(nc.sbuf_tensor(n, sh, dt))
        c.score3 = l3("score3", [P, NT, E3]); c.comb = l3("comb", [P, NT * (E3 + 1)])
        stage_l3_gate(nc, c)
        stage_l3_route(nc, c)
        stage_l3_experts(nc, c)



def build_program(nc, d):
    c = Core()
    HELD.clear()
    OPENED.clear()
    c.d = d
    with ExitStack() as ctx:
        sb = lambda n, sh, dt=F32: ctx.enter_context(nc.sbuf_tensor(n, sh, dt))
        c.bank = [ctx.enter_context(nc.psum_tensor(f"bank{k}", [P, 512], F32)) for k in range(8)]
        c.x = sb("x_all", [P, NT, D])
        c.bn = sb("bn_all", [P, NT, 6])
        c.mean = sb("mean_all", [P, NT])
        c.rstd = sb("rstd_all", [P, NT])
        c.small = sb("small", [P, 5, NT])
        c.minus_half = sb("minus_half", [P, NT])
        c.const = sb("const_sb", [P, CONST_W])
        part = lambda n: c.const[:, CONSTS[n][0]:CONSTS[n][1]]
        c.ident, c.cos, c.sin, c.before, c.iota = (part(n) for n in ("ident", "cos", "sin", "before", "iota"))
        c.moe = nc.dram_tensor("moe_rows", (NX, D), F32, kind="Internal").ap()
        c.think_rows = nc.dram_tensor("think_rows", (B, D), F32, kind="Internal").ap()
        c.xn_rows = nc.dram_tensor("xn_rows", (NX, D), F32, kind="Internal").ap()
        c.q_parts, c.k_parts = (nc.dram_tensor(n, (3, DQ3, B * H3, D), BF16, kind="Internal").ap()
                                for n in ("q_parts", "k_parts"))
        c.decay, c.lower = part("decay"), part("lower")
        c.cos_one = part("one")
        stage_first(nc, c)
        layers(nc, c)
        stage_last(nc, c)


def lay_out(inputs):
    f = {k: np.asarray(v) for k, v in inputs.items()}
    a = {
        "x": f["x"].reshape(N, D),
        "ctx": f["ctx_2048"].reshape(N, D),
        "mask": f["mask_BxS2_bk0"].view(np.int32),
        "seg": f["itok_BxS_0_1023"].reshape(NT, P).T,
        "const": constants(),
        "wh": f["L1_xattn_Wh"],
        "whT": f["L1_xattn_Wh"].transpose(0, 2, 1),
        "wkvc": f["L2_xattn_W_kvc"],
        "wkvcT": f["L2_xattn_W_kvc"].T,
        "wkr": f["L2_xattn_W_kr"],
        "g0w": f["L0_ffn_gate_w"].T,
        "g0b": f["L0_ffn_gate_bias"].reshape(1, E0),
        "e0w1": f["L0_ffn_w1"], "e0w2": f["L0_ffn_w2"], "e0w3": f["L0_ffn_w3"],
        "s0g": f["L0_ffn_shared_gate"], "s0u": f["L0_ffn_shared_up"], "s0d": f["L0_ffn_shared_down"],
        "wg": f["L1_xattn_wg_w"], "wo": f["L1_xattn_wo_w"],
        "gng": f["L1_xattn_gn_gamma"].reshape(1, D), "gnb": f["L1_xattn_gn_beta"].reshape(1, D),
    }
    for n in ("in_gamma", "in_beta", "agg_b", "pn_gamma", "pn_beta", "d1_b", "d2_b", "bc_b", "gate_b",
              "out_gamma", "out_beta"):
        a["f1_" + n] = f["L1_ffn_" + n].reshape(1, -1)
    a["f1_d1_b"] = f["L1_ffn_d1_b"].reshape(HID1 // P, P).T
    for n in ("agg_w", "d1_w", "d2_w", "bc_w", "gate_w"):
        a["f1_" + n] = f["L1_ffn_" + n]
    a.update({
        "wdq": f["L2_xattn_W_dq"],
        "wuqT": f["L2_xattn_W_uq"].reshape(QC, H2, HD2).transpose(2, 1, 0),
        "wukT": f["L2_xattn_W_uk"].reshape(KVC, H2, HD2).transpose(2, 1, 0),
        "wuvT": f["L2_xattn_W_uv"].reshape(KVC, H2, HD2).transpose(2, 1, 0),
        "wqr": f["L2_xattn_W_qr"].reshape(QC, H2, R2),
        "wo2": f["L2_xattn_W_o"].reshape(H2, HD2, D).transpose(1, 0, 2),
        "t1": f["L2_ffn_w1"].T, "t2": f["L2_ffn_w2"].T, "t3": f["L2_ffn_w3"].T,
        "gamma3": f["L3_xattn_gamma"].reshape(1, 1),
        "g3w": f["L3_ffn_gate_w"].T,
        "e3w1": f["L3_ffn_w1"], "e3w2": f["L3_ffn_w2"], "e3w3": f["L3_ffn_w3"],
        "s3w1": f["L3_ffn_sw1"], "s3w2": f["L3_ffn_sw2"], "s3w3": f["L3_ffn_sw3"],
    })
    return {k: np.ascontiguousarray(v) for k, v in a.items()}


def kernel(**inputs):
    import concourse.bacc as bacc
    from concourse.bass_utils import run_bass_kernel_spmd

    nc = bacc.Bacc("TRN2", target_bir_lowering=False, num_devices=1)
    arrays = {"in_" + k: v for k, v in lay_out(inputs).items()}
    d = {k[3:]: nc.dram_tensor(k, v.shape, mybir.dt.from_np(v.dtype), kind="ExternalInput").ap()
         for k, v in arrays.items()}
    d["out"] = nc.dram_tensor("out_x", (N, D), F32, kind="ExternalOutput").ap()
    build_program(nc, d)
    r = run_bass_kernel_spmd(nc, [arrays], core_ids=[0])
    return r.results[0]["out_x"].reshape(B, S, D)
```

```python
from contextlib import ExitStack

import numpy as np

import concourse.bass as bass
from concourse import mybir

ALU = mybir.AluOpType
ACT = mybir.ActivationFunctionType
AX = mybir.AxisListType
F32 = mybir.dt.float32
BF16 = mybir.dt.bfloat16
I32 = mybir.dt.int32
U32 = mybir.dt.uint32
U8 = mybir.dt.uint8

P = 128
B, S, D = 64, 64, 256
N = B * S
NT = N // P
DK = D // P
LN_EPS = 1e-5
NEG = -1e30

E0, TOP0, G0, TG0, F0, FS0, SCALE0 = 32, 4, 4, 2, 128, 256, 2.0
CAP0 = 2 * (256 * TOP0 // E0)
NX = N + CAP0
H1, HD1, GN_EPS = 2, 128, 1e-3
EPS1, STEPS1, HID1 = 1e-6, 4, 1024
H2, HD2, KVC, QC, R2, LOOKBACK = 16, 128, 64, 96, 64, 8
HID2, EPS2 = 704, 1e-8
H3 = 8
DQ3 = S // H3
E3, HID3, TOP3, SCALE3 = 8, 176, 2, 2.5
HH3 = HID3 // 2

LANES = 2
CREDIT = LANES


def ready(t):
    return t + 1 + CREDIT


def freed(t):
    return t + 1


def loaded(i):
    return 16 * i + 16


def stored(i):
    return 16 * i + 32


def store_freed(i):
    return 16 * i + 16


def settle(eng, passed):
    eng.sem_inc(passed, 1)


class Chain:

    def __init__(self, eng, sem, start=0):
        self.eng, self.sem, self.start, self.n = eng, sem, start, 0

    def link(self, ins):
        self.n += 1
        ins.then_inc(self.sem, 1)
        self.eng.wait_ge(self.sem, self.start + self.n)


CONSTS = {}
_at = 0
for _name, _width in (("ident", 128), ("cos", 128), ("sin", 128), ("before", 128), ("iota", 64),
                      ("decay", 128), ("lower", 16), ("one", 128)):
    CONSTS[_name] = (_at, _at + _width)
    _at += _width
CONST_W = _at


def constants():
    c = np.zeros((P, CONST_W), np.float32)

    def put(name, v, rows=slice(0, P)):
        a, b = CONSTS[name]
        c[rows, a:b] = v

    put("ident", np.eye(P, dtype=np.float32))
    half = R2 // 2
    inv_freq = (np.float32(1.0) / np.float32(10000.0) ** (np.arange(half, dtype=np.float32) / np.float32(half))).astype(np.float32)
    ang = (np.arange(S, dtype=np.float32)[:, None] * inv_freq).astype(np.float32)
    cos, sin = (np.tile(f(ang).T.astype(np.float32), (1, 2)) for f in (np.cos, np.sin))
    put("cos", np.concatenate([cos, cos]), slice(64, 128))
    put("sin", np.concatenate([sin, -sin]), slice(64, 128))
    i = np.arange(P)
    put("before", (i[:, None] < i[None, :]).astype(np.float32))
    put("iota", np.arange(64, dtype=np.float32)[None, :])
    gam = (1.0 - 2.0 ** (-5.0 - np.arange(H1, dtype=np.float32))).astype(np.float32)
    expo = np.arange(S, dtype=np.float32)[None, :] - np.arange(S, dtype=np.float32)[:, None]
    dm = np.where(expo[None] <= 0, gam[:, None, None] ** expo[None], 0.0).astype(np.float32)
    dm = dm / np.sqrt(dm.sum(-1))[:, None, :] / np.sqrt(np.float32(HD1))
    put("decay", dm.transpose(1, 0, 2).reshape(S, H1 * S), slice(0, S))
    put("one", 1.0)
    low = (np.arange(G0)[None, :] < np.arange(G0)[:, None]).astype(np.float32)
    put("lower", low.reshape(1, 16))
    return c


class Core:
    pass


HELD = []
OPENED = []


def open_sems(nc, ctx, names):
    OPENED.append(names)
    got = {n: nc.alloc_semaphore(f"{n}_{len(OPENED)}") for n in names.split()}
    HELD.extend(got.values())
    return got


def recycle(nc):
    nc.clear_and_free_semaphores(list(HELD))
    HELD.clear()
    nc.all_engine_barrier()


def give_credit(pool, sems, names, step=1):
    for n in names.split():
        pool.sem_inc(sems[n], CREDIT * step)


def half(ap):
    return ap.rearrange("p (k n) -> p k n", k=DK)


def at_tile(ap, t):
    return ap[:, bass.ds(t, 1), :].rearrange("p a n -> p (a n)")


def finish_stats(nc, c, tag, eps=LN_EPS, src=None, mean=None, rstd=None):
    src, mean, rstd = src or c.bn, mean or c.mean, rstd or c.rstd
    with ExitStack() as ctx:
        s = open_sems(nc, ctx, f"{tag}_chain {tag}_var_ready {tag}_half_set {tag}_rstd_ready")
        block = ctx.enter_context(nc.Block())

        @block.vector
        def _(dve):
            ch = Chain(dve, s[f"{tag}_chain"])
            m_even, m_odd = src[:, :, 1], src[:, :, 4]
            v_even, v_odd = src[:, :, 2], src[:, :, 5]
            nc.vector.tensor_tensor(mean[:, :], m_even, m_odd, ALU.add)
            nc.vector.tensor_tensor(c.small[:, 0, :], m_even, m_odd, ALU.subtract)
            ch.link(nc.vector.tensor_tensor(c.small[:, 1, :], v_even, v_odd, ALU.add))
            nc.vector.tensor_scalar(mean[:, :], mean[:, :], 0.5, None, ALU.mult)
            ch.link(nc.vector.scalar_tensor_tensor(out=c.small[:, 2, :], in0=c.small[:, 0, :], scalar=0.25,
                                                   in1=c.small[:, 0, :], op0=ALU.mult, op1=ALU.mult))
            ch.link(nc.vector.scalar_tensor_tensor(out=c.small[:, 3, :], in0=c.small[:, 1, :], scalar=1.0 / D,
                                                   in1=c.small[:, 2, :], op0=ALU.mult, op1=ALU.add))
            nc.vector.tensor_scalar(c.small[:, 4, :], c.small[:, 3, :], eps, None,
                                    ALU.add).then_inc(s[f"{tag}_var_ready"], 1)

        @block.gpsimd
        def _(pool):
            nc.gpsimd.memset(c.minus_half[:, :], -0.5).then_inc(s[f"{tag}_half_set"], 1)
            pool.wait_ge(s[f"{tag}_half_set"], 1)
            pool.wait_ge(s[f"{tag}_var_ready"], 1)
            nc.gpsimd.tensor_tensor(rstd[:, :], c.small[:, 4, :], c.minus_half[:, :],
                                    ALU.pow).then_inc(s[f"{tag}_rstd_ready"], 1)
            pool.wait_ge(s[f"{tag}_rstd_ready"], 1)


def normalize(nc, c, out, t):
    return nc.vector.tensor_scalar(out, at_tile(c.x, t), c.mean[:, bass.ds(t, 1)], c.rstd[:, bass.ds(t, 1)],
                                   ALU.subtract, ALU.mult)


def transpose_tile(nc, c, bank, src):
    for k in range(DK):
        last = nc.tensor.transpose(bank[:, k * P:(k + 1) * P], src[:, k * P:(k + 1) * P], c.ident)
    return last


def stage_first(nc, c):
    with ExitStack() as ctx:
        s = open_sems(nc, ctx, "consts_loaded x_loaded first_stats")
        block = ctx.enter_context(nc.Block())
        xt = c.d["x"].rearrange("(n p) d -> p n d", p=P)

        @block.sync
        def _(sp):
            sp.dma_start(c.const[:, :], c.d["const"]).then_inc(s["consts_loaded"], 16)
            for n in range(4):
                sp.dma_start(c.x[:, 8 * n:8 * n + 8, :], xt[:, 8 * n:8 * n + 8, :]).then_inc(s["x_loaded"], 16)
            sp.wait_ge(s["consts_loaded"], 16)

        @block.vector
        def _(dve):
            dve.wait_ge(s["x_loaded"], 64)
            with dve.Fori(0, NT) as t:
                nc.vector.bn_stats(at_tile(c.bn, t), at_tile(c.x, t))


def stage_l0_attention(nc, c):
    with ExitStack() as ctx:
        sb = lambda n, sh, dt=F32: ctx.enter_context(nc.sbuf_tensor(n, sh, dt))
        wh = sb("wh", [P, H1, P]); whT = sb("whT", [P, H1, P]); gram = sb("gram", [P, H1, P])
        wkvcT = sb("wkvcT", [KVC, D]); wkr = sb("wkr", [KVC, R2]); wk = sb("wk", [P, DK, P])
        mask8 = sb("mask8", [P, NT, S], U8); keep = sb("keep", [P, NT, S]); drop = sb("drop", [P, NT, S])
        any_valid = sb("any_valid", [P, NT])
        xn = sb("xn_a", [P, LANES, D]); ctx_in = sb("ctx_in", [P, LANES, D]); fT = sb("fT_a", [P, LANES, 4, P])
        sc = sb("scores_a", [P, LANES, S]); prob = sb("prob_a", [P, LANES, P]); probT = sb("probT_a", [P, LANES, P])
        nmax = sb("nmax_a", [P, LANES]); tot = sb("tot_a", [P, LANES]); rec = sb("rec_a", [P, LANES])
        rot = sb("rot_a", [P, LANES, 2, P]); kraw = sb("kraw_a", [P, LANES, P])
        s = open_sems(nc, ctx, "a_weights a_masks a_pe_pre a_gram a_wk a_mask_chain a_mask_ready a_prob_zero "
                      "ctx_loaded0 ctx_loaded1 xn_ready feat_ready feat_copied v_ready v_copied keys_ready key_copied rot_ready "
                      "keys_done scores_ready soft_ready prob_ready probT_ready probT_copied read_ready x_done a_chain")
        block = ctx.enter_context(nc.Block())
        ctx_d = c.d["ctx"]
        ITER_LINKS = 12

        def feat(j): return c.bank[4 * j]
        def vg(j): return c.bank[4 * j + 1]
        def att(j): return c.bank[4 * j + 2]
        def keys(j): return c.bank[4 * j + 3]

        @block.sync
        def _(sp):
            for dst, src in ((wh[:, :, :], c.d["wh"].rearrange("h d e -> d h e")),
                             (whT[:, :, :], c.d["whT"].rearrange("h e d -> e h d")),
                             (wkvcT[:, :], c.d["wkvcT"]), (wkr[:, :], c.d["wkr"]),
                             (wk[:, :, 0:KVC], c.d["wkvc"].rearrange("(k p) n -> p k n", p=P))):
                sp.dma_start(dst, src).then_inc(s["a_weights"], 16)
            for b in range(2):
                src = c.d["mask"].rearrange("(t b) k -> b t k", b=2)[b:b + 1].broadcast_to([64, NT, S // 4])
                sp.dma_start(mask8[64 * b:64 * b + 64, :, :].bitcast(I32), src).then_inc(s["a_masks"], 16)
            with sp.Fori(0, NT // LANES) as i:
                for j in range(LANES):
                    t = i * LANES + j
                    sp.wait_ge(s["x_done"], freed(t))
                    sp.dma_start(ctx_in[:, j, :], ctx_d[bass.ds(t * P, P), :]).then_inc(s[f"ctx_loaded{j}"], 16)

        @block.gpsimd
        def _(pool):
            give_credit(pool, s, "xn_ready feat_ready feat_copied v_ready v_copied keys_ready key_copied rot_ready "
                        "keys_done scores_ready soft_ready prob_ready probT_ready probT_copied read_ready x_done")
            nc.gpsimd.memset(prob[:, :, :], 0.0).then_inc(s["a_prob_zero"], 1)
            with pool.Fori(0, NT // LANES) as i:
                for j in range(LANES):
                    t = i * LANES + j
                    pool.wait_ge(s["rot_ready"], ready(t))
                    nc.gpsimd.tensor_tensor(c.keysT[64:P, bass.ds(t * P, P)], rot[64:P, j, 0, :], rot[64:P, j, 1, :],
                                            ALU.add).then_inc(s["keys_done"], 1)

        @block.tensor
        def _(pe):
            pe.wait_ge(s["a_weights"], 80)
            for h in range(H1):
                nc.tensor.matmul(c.bank[0][:, h * P:(h + 1) * P], whT[:, h, :], whT[:, h, :], start=True, stop=True)
            for k in range(DK):
                last = nc.tensor.matmul(c.bank[1][:, k * R2:(k + 1) * R2], wkvcT[:, k * P:(k + 1) * P], wkr[:, :],
                                        start=True, stop=True)
            last.then_inc(s["a_pe_pre"], 1)
            pe.wait_ge(s["a_gram"], 1)
            pe.wait_ge(s["a_wk"], 1)
            with pe.Fori(0, NT // LANES) as i:
                for j in range(LANES):
                    t = i * LANES + j
                    pe.wait_ge(s["xn_ready"], ready(t))
                    pe.wait_ge(s[f"ctx_loaded{j}"], loaded(i))
                    pe.wait_ge(s["feat_copied"], freed(t))
                    transpose_tile(nc, c, feat(j)[:, 0:D], xn[:, j, :])
                    transpose_tile(nc, c, feat(j)[:, D:2 * D], ctx_in[:, j, :]).then_inc(s["feat_ready"], 1)
                for j in range(LANES):
                    t = i * LANES + j
                    pe.wait_ge(s["feat_copied"], ready(t))
                    pe.wait_ge(s["x_done"], freed(t))
                    for b in range(2):
                        q = slice(64 * b, 64 * b + 64)
                        for k in range(DK):
                            last = nc.tensor.matmul(att(j)[q, 0:S], fT[:, j, k, q], fT[:, j, 2 + k, q],
                                                    start=(k == 0), stop=(k == DK - 1))
                    last.then_inc(s["scores_ready"], 1)
                    pe.wait_ge(s["v_copied"], freed(t))
                    for h in range(H1):
                        nc.tensor.matmul(vg(j)[:, h * P:(h + 1) * P], fT[:, j, 2 + h, :], wh[:, h, :],
                                         start=True, stop=True)
                        last = nc.tensor.matmul(vg(j)[:, D + h * P:D + (h + 1) * P], gram[:, h, :],
                                                fT[:, j, 2 + h, :], start=True, stop=True)
                    last.then_inc(s["v_ready"], 1)
                    pe.wait_ge(s["key_copied"], freed(t))
                    for k in range(DK):
                        nc.tensor.matmul(keys(j)[:, 0:P], wk[:, k, :], fT[:, j, 2 + k, :],
                                         start=(k == 0), stop=(k == DK - 1))
                    for k in range(DK):
                        last = nc.tensor.matmul(keys(j)[:, P:P + KVC], fT[:, j, 2 + k, :], wk[:, k, 0:KVC],
                                                start=(k == 0), stop=(k == DK - 1))
                    last.then_inc(s["keys_ready"], 1)
                for j in range(LANES):
                    t = i * LANES + j
                    pe.wait_ge(s["prob_ready"], ready(t))
                    nc.tensor.transpose(att(j)[:, 0:P], prob[:, j, :], c.ident).then_inc(s["probT_ready"], 1)
                for j in range(LANES):
                    t = i * LANES + j
                    pe.wait_ge(s["probT_copied"], ready(t))
                    nc.tensor.matmul(att(j)[:, 0:D], probT[:, j, :], ctx_in[:, j, :],
                                     start=True, stop=True).then_inc(s["read_ready"], 1)

        @block.scalar
        def _(act):
            act.wait_ge(s["a_pe_pre"], 1)
            act.copy(gram[:, :, :].rearrange("p h n -> p (h n)"), c.bank[0][:, 0:D]).then_inc(s["a_gram"], 1)
            act.wait_ge(s["a_weights"], 80)
            act.copy(wk[:, :, KVC:P], c.bank[1][:, 0:DK * R2].rearrange("p (k n) -> p k n", k=DK)).then_inc(s["a_wk"], 1)
            act.wait_ge(s["a_prob_zero"], 1)
            with act.Fori(0, NT // LANES) as i:
                for j in range(LANES):
                    t = i * LANES + j
                    act.wait_ge(s["feat_ready"], ready(t))
                    act.wait_ge(s["keys_ready"], freed(t))
                    act.copy(fT[:, j, :, :].rearrange("p k n -> p (k n)"), feat(j)[:, :]).then_inc(s["feat_copied"], 1)
                for j in range(LANES):
                    t = i * LANES + j
                    act.wait_ge(s["soft_ready"], ready(t))
                    act.wait_ge(s["probT_ready"], freed(t))
                    act.wait_ge(s["x_done"], freed(t))
                    for b in range(2):
                        q = slice(64 * b, 64 * b + 64)
                        last = nc.scalar.activation(prob[q, j, q], sc[q, j, :], ACT.Exp, bias=nmax[q, j:j + 1],
                                                    accum_out=tot[q, j:j + 1])
                    last.then_inc(s["prob_ready"], 1)
                    act.wait_ge(s["v_ready"], ready(t))
                    act.copy(at_tile(c.v, t), vg(j)[:, 0:D])
                    act.copy(c.gramT[:, :, bass.ds(t * P, P)], vg(j)[:, D:2 * D].rearrange(
                        "p (h n) -> p h n", h=H1)).then_inc(s["v_copied"], 1)
                    act.wait_ge(s["keys_ready"], ready(t))
                    act.wait_ge(s["rot_ready"], freed(t))
                    act.copy(at_tile(c.kvc, t), keys(j)[:, P:P + KVC])
                    act.copy(c.keysT[0:64, bass.ds(t * P, P)], keys(j)[0:64, 0:P])
                    act.copy(kraw[64:P, j, :], keys(j)[64:P, 0:P]).then_inc(s["key_copied"], 1)
                for j in range(LANES):
                    t = i * LANES + j
                    act.wait_ge(s["probT_ready"], ready(t))
                    act.wait_ge(s["read_ready"], freed(t))
                    act.copy(probT[:, j, :], att(j)[:, 0:P]).then_inc(s["probT_copied"], 1)

        @block.vector
        def _(dve):
            ch = Chain(dve, s["a_mask_chain"])
            dve.wait_ge(s["a_masks"], 32)
            ch.link(nc.vector.tensor_copy(keep[:, :, :], mask8[:, :, :]))
            nc.vector.tensor_scalar(drop[:, :, :], keep[:, :, :], 1.0, -NEG, ALU.subtract, ALU.mult)
            ch.link(nc.vector.tensor_reduce(any_valid[:, :], keep[:, :, :], AX.X, ALU.max))
            with dve.Fori(0, NT // LANES) as i:
                ch = Chain(dve, s["a_chain"], i * ITER_LINKS)
                for j in range(LANES):
                    t = i * LANES + j
                    dve.wait_ge(s["feat_ready"], freed(t))
                    normalize(nc, c, xn[:, j, :], t).then_inc(s["xn_ready"], 1)
                for j in range(LANES):
                    t = i * LANES + j
                    dve.wait_ge(s["scores_ready"], ready(t))
                    dve.wait_ge(s["prob_ready"], freed(t))
                    ch.link(nc.vector.scalar_tensor_tensor(out=sc[:, j, :], in0=att(j)[:, 0:S], scalar=D ** -0.5,
                                                           in1=at_tile(keep, t), op0=ALU.mult, op1=ALU.mult))
                    ch.link(nc.vector.tensor_tensor(sc[:, j, :], sc[:, j, :], at_tile(drop, t), ALU.add))
                    nc.vector.tensor_reduce(nmax[:, j:j + 1], sc[:, j, :], AX.X, ALU.max,
                                            negate=True).then_inc(s["soft_ready"], 1)
                for j in range(LANES):
                    t = i * LANES + j
                    dve.wait_ge(s["key_copied"], ready(t))
                    dve.wait_ge(s["keys_done"], freed(t))
                    kr = kraw[:, j, :]
                    nc.vector.tensor_tensor(rot[64:P, j, 0, :], kr[64:P, :], c.cos[64:P, :], ALU.mult)
                    nc.vector.tensor_tensor(rot[96:P, j, 1, :], kr[64:96, :], c.sin[64:96, :], ALU.mult)
                    nc.vector.tensor_tensor(rot[64:96, j, 1, :], kr[96:P, :], c.sin[96:P, :],
                                            ALU.mult).then_inc(s["rot_ready"], 1)
                    dve.wait_ge(s["prob_ready"], ready(t))
                    ch.link(nc.vector.reciprocal(rec[:, j:j + 1], tot[:, j:j + 1]))
                    ch.link(nc.vector.tensor_tensor(rec[:, j:j + 1], rec[:, j:j + 1], any_valid[:, bass.ds(t, 1)], ALU.mult))
                for j in range(LANES):
                    t = i * LANES + j
                    dve.wait_ge(s["read_ready"], ready(t))
                    add_and_stats(nc, c, ch, t, att(j)[:, 0:D], rec[:, j:j + 1], s["x_done"])
                assert ch.n == ITER_LINKS, ch.n


def add_and_stats(nc, c, ch, t, psum, scale, done):
    ch.link(nc.vector.scalar_tensor_tensor(out=at_tile(c.x, t), in0=psum, scalar=scale, in1=at_tile(c.x, t),
                                           op0=ALU.mult, op1=ALU.add))
    ch.link(nc.vector.bn_stats(at_tile(c.bn, t), at_tile(c.x, t)))
    ch.eng.sem_inc(done, 1)


def stage_last(nc, c):
    with ExitStack() as ctx:
        s = open_sems(nc, ctx, "out_stored")
        block = ctx.enter_context(nc.Block())
        ot = c.d["out"].rearrange("(n p) d -> p n d", p=P)

        @block.sync
        def _(sp):
            for n in range(4):
                sp.dma_start(ot[:, 8 * n:8 * n + 8, :], c.x[:, 8 * n:8 * n + 8, :]).then_inc(s["out_stored"], 16)
            sp.wait_ge(s["out_stored"], 64)


def token_loop(i, lanes=LANES):
    return [(j, i * LANES + j) for j in range(lanes)]


def stage_l0_shared(nc, c):
    with ExitStack() as ctx:
        sb = lambda n, sh, dt=F32: ctx.enter_context(nc.sbuf_tensor(n, sh, dt))
        wgu = sb("wgu", [P, DK, 2 * FS0]); wd = sb("wd", [P, FS0 // P, D]); wg = sb("wgate", [P, DK, E0])
        xn = sb("xn_b", [P, LANES, D]); xT = sb("xT_b", [P, LANES, DK, P])
        sig = sb("sig_b", [P, LANES, D]); hT = sb("hT_b", [P, LANES, D]); zero = sb("zero_b", [P, 1024])
        s = open_sems(nc, ctx, "b_weights zero_set zeroed xn_ready feat_ready feat_copied hid_ready sig_ready "
                      "hT_ready logit_ready logit_copied down_ready x_done xn_stored0 xn_stored1 b_chain")
        block = ctx.enter_context(nc.Block())

        def feat(j): return c.bank[4 * j]
        def hid(j): return c.bank[4 * j + 1]
        def logit(j): return c.bank[4 * j + 2]
        def down(j): return c.bank[4 * j + 3]

        @block.sync
        def _(sp):
            for dst, src in ((wg[:, :, :], c.d["g0w"]), (wgu[:, :, 0:FS0], c.d["s0g"]),
                             (wgu[:, :, FS0:2 * FS0], c.d["s0u"]), (wd[:, :, :], c.d["s0d"])):
                sp.dma_start(dst, src.rearrange("(k p) n -> p k n", p=P)).then_inc(s["b_weights"], 16)
            sp.wait_ge(s["zero_set"], 1)
            for n in range(8):
                sp.dma_start(c.moe[512 * n:512 * n + 512, :].rearrange("(p r) d -> p (r d)", r=4),
                             zero[:, :]).then_inc(s["zeroed"], 16)
            sp.dma_start(c.moe[N:NX, :], zero[0:CAP0, 0:D]).then_inc(s["zeroed"], 16)
            sp.dma_start(c.xn_rows[N:NX, :], zero[0:CAP0, 0:D]).then_inc(s["zeroed"], 16)
            with sp.Fori(0, NT // LANES) as i:
                for j, t in token_loop(i):
                    sp.wait_ge(s["xn_ready"], ready(t))
                    sp.dma_start(c.xn_rows[bass.ds(t * P, P), :], xn[:, j, :]).then_inc(s[f"xn_stored{j}"], 16)
            sp.wait_ge(s["zeroed"], 160)
            for j in range(LANES):
                sp.wait_ge(s[f"xn_stored{j}"], 16 * (NT // LANES) + 16)

        @block.gpsimd
        def _(pool):
            nc.gpsimd.memset(zero[:, :], 0.0).then_inc(s["zero_set"], 1)
            give_credit(pool, s, "xn_ready feat_ready feat_copied hid_ready sig_ready hT_ready logit_ready "
                        "logit_copied down_ready x_done")
            for j in range(LANES):
                pool.sem_inc(s[f"xn_stored{j}"], 16)

        @block.tensor
        def _(pe):
            pe.wait_ge(s["b_weights"], 64)
            with pe.Fori(0, NT // LANES) as i:
                for j, t in token_loop(i):
                    pe.wait_ge(s["xn_ready"], ready(t))
                    pe.wait_ge(s["feat_copied"], freed(t))
                    transpose_tile(nc, c, feat(j), xn[:, j, :]).then_inc(s["feat_ready"], 1)
                for j, t in token_loop(i):
                    pe.wait_ge(s["feat_copied"], ready(t))
                    pe.wait_ge(s["hT_ready"], freed(t))
                    for f in range(4):
                        for k in range(DK):
                            last = nc.tensor.matmul(hid(j)[:, f * P:(f + 1) * P], wgu[:, k, f * P:(f + 1) * P],
                                                    xT[:, j, k, :], start=(k == 0), stop=(k == DK - 1))
                    last.then_inc(s["hid_ready"], 1)
                    pe.wait_ge(s["logit_copied"], freed(t))
                    for k in range(DK):
                        last = nc.tensor.matmul(logit(j)[:, 0:E0], xT[:, j, k, :], wg[:, k, :],
                                                start=(k == 0), stop=(k == DK - 1))
                    last.then_inc(s["logit_ready"], 1)
                for j, t in token_loop(i):
                    pe.wait_ge(s["hT_ready"], ready(t))
                    pe.wait_ge(s["x_done"], freed(t))
                    for k in range(DK):
                        last = nc.tensor.matmul(down(j)[:, 0:D], hT[:, j, k * P:(k + 1) * P], wd[:, k, :],
                                                start=(k == 0), stop=(k == DK - 1))
                    last.then_inc(s["down_ready"], 1)

        @block.scalar
        def _(act):
            with act.Fori(0, NT // LANES) as i:
                for j, t in token_loop(i):
                    act.wait_ge(s["feat_ready"], ready(t))
                    act.wait_ge(s["logit_ready"], freed(t))
                    act.copy(xT[:, j, :, :].rearrange("p k n -> p (k n)"), feat(j)[:, 0:D]).then_inc(s["feat_copied"], 1)
                for j, t in token_loop(i):
                    act.wait_ge(s["hid_ready"], ready(t))
                    act.wait_ge(s["hT_ready"], freed(t))
                    nc.scalar.activation(sig[:, j, :], hid(j)[:, 0:D], ACT.Sigmoid).then_inc(s["sig_ready"], 1)
                    act.wait_ge(s["logit_ready"], ready(t))
                    nc.scalar.activation(at_tile(c.score0, t), logit(j)[:, 0:E0],
                                         ACT.Sigmoid).then_inc(s["logit_copied"], 1)

        @block.vector
        def _(dve):
            with dve.Fori(0, NT // LANES) as i:
                ch = Chain(dve, s["b_chain"], i * LANES)
                for j, t in token_loop(i):
                    dve.wait_ge(s["feat_ready"], freed(t))
                    dve.wait_ge(s[f"xn_stored{j}"], store_freed(i))
                    normalize(nc, c, xn[:, j, :], t).then_inc(s["xn_ready"], 1)
                for j, t in token_loop(i):
                    dve.wait_ge(s["sig_ready"], ready(t))
                    dve.wait_ge(s["down_ready"], freed(t))
                    ch.link(nc.vector.tensor_tensor(sig[:, j, :], hid(j)[:, 0:D], sig[:, j, :], ALU.mult))
                    nc.vector.tensor_tensor(hT[:, j, :], hid(j)[:, D:2 * D], sig[:, j, :],
                                            ALU.mult).then_inc(s["hT_ready"], 1)
                for j, t in token_loop(i):
                    dve.wait_ge(s["down_ready"], ready(t))
                    nc.vector.tensor_tensor(at_tile(c.x, t), down(j)[:, 0:D], at_tile(c.x, t),
                                            ALU.add).then_inc(s["x_done"], 1)


BIG = 3e38


def stage_l0_route(nc, c):
    with ExitStack() as ctx:
        sb = lambda n, sh, dt=F32: ctx.enter_context(nc.sbuf_tensor(n, sh, dt))
        NE = NT * E0
        biased = sb("biased", [P, NE]); ta = sb("ta", [P, NE]); tb = sb("tb", [P, NE]); tc_ = sb("tc", [P, NE])
        gs = sb("gs", [P, NT, G0]); gmask = sb("gmask", [P, NT, G0]); bias = sb("gate_bias", [P, E0])
        cand = sb("cand", [P, NT, E0 + 4]); left = sb("left", [P, NT, E0 + 4]); top = sb("top", [P, NT, 8])
        chosen = sb("chosen", [P, NE]); chosen_b = sb("chosen_b", [P, NE], BF16)
        wsum = sb("wsum", [P, NT]); before_b = sb("before_b", [P, P], BF16); ones_b = sb("ones_b", [P, P], BF16)
        wb = sb("wb", [P, NE], BF16); tile_no = sb("tile_no", [P, NE]); row_no = sb("row_no", [P, NE])
        s = open_sems(nc, ctx, "r_bias r_chain r_chosen r_counts r_iota")
        block = ctx.enter_context(nc.Block())

        @block.sync
        def _(sp):
            sp.dma_start(bias[:, :], c.d["g0b"].broadcast_to([P, E0])).then_inc(s["r_bias"], 16)

        @block.gpsimd
        def _(pool):
            nc.gpsimd.iota(tile_no[:, :], pattern=[[1, NT], [0, E0]], base=0, channel_multiplier=0,
                           allow_small_or_imprecise_dtypes=True).then_inc(s["r_iota"], 1)
            nc.gpsimd.iota(row_no[:, :], pattern=[[0, NE]], base=0, channel_multiplier=1,
                           allow_small_or_imprecise_dtypes=True).then_inc(s["r_iota"], 1)
            nc.gpsimd.iota(c.row_col[:, :], pattern=[[0, 1]], base=0, channel_multiplier=1,
                           allow_small_or_imprecise_dtypes=True).then_inc(s["r_iota"], 1)

        @block.tensor
        def _(pe):
            pe.wait_ge(s["r_chosen"], 1)
            for n in range(2):
                cols = slice(512 * n, 512 * n + 512)
                nc.tensor.matmul(c.bank[n][:, :], before_b[:, :], chosen_b[:, cols], start=True, stop=True)
                last = nc.tensor.matmul(c.bank[2 + n][:, :], ones_b[:, :], chosen_b[:, cols], start=True, stop=True)
            last.then_inc(s["r_counts"], 1)

        @block.vector
        def _(dve):
            ch = Chain(dve, s["r_chain"])
            v = nc.vector
            e8 = lambda ap: ap.rearrange("p (g e) -> p g e", e=8)

            def g(ap, a, b): return e8(ap[:, :])[:, :, a:b]
            score = c.score0[:, :, :].rearrange("p t e -> p (t e)")
            te = lambda ap: ap[:, :].rearrange("p (t e) -> p t e", e=E0)
            dve.wait_ge(s["r_bias"], 16)
            ch.link(v.tensor_tensor(te(biased), c.score0[:, :, :],
                                    bias[:, :].unsqueeze(1).broadcast_to([P, NT, E0]), ALU.add))
            v.tensor_tensor(g(ta, 0, 4), g(biased, 0, 4), g(biased, 4, 8), ALU.max)
            ch.link(v.tensor_tensor(g(tb, 0, 4), g(biased, 0, 4), g(biased, 4, 8), ALU.min))
            for w in (2, 1):
                v.tensor_tensor(g(tc_, 0, w), g(ta, 0, w), g(ta, w, 2 * w), ALU.max)
                v.tensor_tensor(g(tc_, 2, 2 + w), g(ta, 0, w), g(ta, w, 2 * w), ALU.min)
                ch.link(v.tensor_tensor(g(tc_, 4, 4 + w), g(tb, 0, w), g(tb, w, 2 * w), ALU.max))
                v.tensor_copy(g(ta, 0, w), g(tc_, 0, w))
                ch.link(v.tensor_tensor(g(tb, 0, w), g(tc_, 2, 2 + w), g(tc_, 4, 4 + w), ALU.max))
            g1 = lambda ap: g(ap, 0, 1).rearrange("p (t g) o -> p t (g o)", g=G0)
            ch.link(v.tensor_tensor(gs[:, :, :], g1(ta), g1(tb), ALU.add))
            rival = gs[:, :, :].unsqueeze(2).broadcast_to([P, NT, G0, G0])
            own = gs[:, :, :].unsqueeze(3).broadcast_to([P, NT, G0, G0])
            sq = lambda ap: ap[:, 0:NT * 16].rearrange("p (t a b) -> p t a b", a=G0, b=G0)
            v.tensor_tensor(sq(ta), rival, own, ALU.is_gt)
            ch.link(v.tensor_tensor(sq(tb), rival, own, ALU.is_equal))
            t16 = lambda ap: ap[:, 0:NT * 16].rearrange("p (t a) -> p t a", a=16)
            ch.link(v.tensor_tensor(t16(tb), t16(tb), c.lower.unsqueeze(1).broadcast_to([P, NT, 16]), ALU.mult))
            ch.link(v.tensor_tensor(ta[:, 0:NT * 16], ta[:, 0:NT * 16], tb[:, 0:NT * 16], ALU.add))
            ch.link(v.tensor_reduce(gmask[:, :, :], sq(ta), AX.X, ALU.add))
            ch.link(v.tensor_scalar(gmask[:, :, :], gmask[:, :, :], float(TG0), None, ALU.is_lt))
            v.memset(cand[:, :, E0:E0 + 4], BIG)
            v.tensor_copy(ones_b[:, :], c.cos_one)
            v.tensor_copy(before_b[:, :], c.before)
            for gi in range(G0):
                last = v.tensor_tensor(cand[:, :, 8 * gi:8 * gi + 8], te(biased)[:, :, 8 * gi:8 * gi + 8],
                                       gmask[:, :, gi:gi + 1].broadcast_to([P, NT, 8]), ALU.mult)
            ch.link(last)
            for t in range(NT):
                last = v.max(top[:, t, :], cand[:, t, 0:E0])
            ch.link(last)
            ch.link(v.memset(top[:, :, TOP0:8], BIG))
            for t in range(NT):
                last = v.match_replace(out=left[:, t, :], in_to_replace=top[:, t, :], in_values=cand[:, t, :],
                                       imm_value=-BIG)
            ch.link(last)
            v.tensor_tensor(te(chosen_b), left[:, :, 0:E0], cand[:, :, 0:E0], ALU.not_equal).then_inc(s["r_chosen"], 1)
            ch.link(v.tensor_tensor(te(chosen), left[:, :, 0:E0], cand[:, :, 0:E0], ALU.not_equal))
            ch.link(v.tensor_tensor(ta[:, :], score, chosen[:, :], ALU.mult))
            ch.link(v.tensor_reduce(wsum[:, :], te(ta), AX.X, ALU.add))
            ch.link(v.tensor_scalar(wsum[:, :], wsum[:, :], 1e-20, None, ALU.add))
            ch.link(v.reciprocal(wsum[:, :], wsum[:, :]))
            ch.link(v.scalar_tensor_tensor(out=te(ta), in0=te(ta), scalar=SCALE0,
                                           in1=wsum[:, :].unsqueeze(2).broadcast_to([P, NT, E0]),
                                           op0=ALU.mult, op1=ALU.mult))
            col = lambda n: c.slot_cols[:, :, :, n].rearrange("p t e -> p (t e)")
            dve.wait_ge(s["r_iota"], 3)
            v.tensor_copy(col(0), chosen[:, :])
            v.tensor_copy(col(1), tile_no[:, :])
            v.tensor_copy(col(2), row_no[:, :])
            for n in (3, 4):
                ch.link(v.tensor_copy(wb[:, :], ta[:, :]))
                v.tensor_copy(col(n), wb[:, :])
                ch.link(v.tensor_tensor(ta[:, :], ta[:, :], wb[:, :], ALU.subtract))
            ch.link(v.tensor_copy(col(5), ta[:, :]))
            dve.wait_ge(s["r_counts"], 1)
            for n in range(2):
                cols = slice(512 * n, 512 * n + 512)
                v.tensor_copy(ta[:, cols], c.bank[2 + n][:, :])
                last = v.tensor_copy(tc_[:, cols], c.bank[n][:, :])
            ch.link(last)
            ch.link(v.tensor_tensor(tc_[:, :], tc_[:, :], ta[:, :], ALU.subtract))
            cur, nxt, step = ta, tb, 1
            while step < NT:
                w = step * E0
                v.tensor_copy(nxt[:, 0:w], cur[:, 0:w])
                ch.link(v.tensor_tensor(nxt[:, w:NE], cur[:, w:NE], cur[:, 0:NE - w], ALU.add))
                cur, nxt, step = nxt, cur, 2 * step
            ch.link(v.tensor_tensor(tc_[:, :], tc_[:, :], cur[:, :], ALU.add))
            ch.link(v.scalar_tensor_tensor(out=chosen[:, :], in0=tc_[:, :], scalar=float(CAP0), in1=chosen[:, :],
                                           op0=ALU.is_lt, op1=ALU.mult))
            ch.link(v.scalar_tensor_tensor(out=tc_[:, :], in0=tc_[:, :], scalar=1.0, in1=chosen[:, :],
                                           op0=ALU.add, op1=ALU.mult))
            ch.link(v.tensor_scalar(c.place[:, :, :].rearrange("p t e -> p (t e)"), tc_[:, :], 1.0, None,
                                    ALU.subtract))


def stage_l0_slots(nc, c):
    with ExitStack() as ctx:
        sb = lambda n, sh, dt=F32: ctx.enter_context(nc.sbuf_tensor(n, sh, dt))
        hot = sb("hot", [P, LANES, E0, CAP0], BF16); cols = sb("cols", [P, LANES, E0 * 6], BF16)
        zeros = sb("zeros_s", [P, E0 * 6], BF16); iota_b = sb("iota_b", [P, CAP0], BF16)
        got = sb("got", [CAP0, E0, 6]); idf = sb("idf", [CAP0, E0]); empty = sb("empty", [CAP0, E0])
        s = open_sems(nc, ctx, "s_zero s_iota hot_ready cols_ready hot_used s_done s_chain")
        block = ctx.enter_context(nc.Block())
        acc = c.bank[0][0:CAP0, 0:E0 * 6]

        @block.gpsimd
        def _(pool):
            give_credit(pool, s, "hot_ready cols_ready hot_used")
            nc.gpsimd.memset(zeros[:, :], 0.0).then_inc(s["s_zero"], 1)

        @block.scalar
        def _(act):
            with act.Fori(0, NT // LANES) as i:
                for j, t in token_loop(i):
                    act.wait_ge(s["hot_used"], freed(t))
                    act.copy(cols[:, j, :], c.slot_cols[:, bass.ds(t, 1), :, :].rearrange(
                        "p a e n -> p (a e n)")).then_inc(s["cols_ready"], 1)

        @block.vector
        def _(dve):
            ch = Chain(dve, s["s_iota"])
            ch.link(nc.vector.tensor_copy(iota_b[:, :], c.iota))
            with dve.Fori(0, NT // LANES) as i:
                for j, t in token_loop(i):
                    dve.wait_ge(s["hot_used"], freed(t))
                    nc.vector.tensor_tensor(hot[:, j, :, :],
                                            at_tile(c.place, t).unsqueeze(2).broadcast_to([P, E0, CAP0]),
                                            iota_b[:, :].unsqueeze(1).broadcast_to([P, E0, CAP0]),
                                            ALU.is_equal).then_inc(s["hot_ready"], 1)
            ch = Chain(dve, s["s_chain"])
            v = nc.vector
            dve.wait_ge(s["s_done"], 1)
            ch.link(v.tensor_copy(got[:, :, :].rearrange("p e n -> p (e n)"), acc))
            row = c.row_col[0:CAP0, :]
            ch.link(v.tensor_scalar(empty[:, :], got[:, :, 0], -1.0, 1.0, ALU.mult, ALU.add))
            v.scalar_tensor_tensor(out=idf[:, :], in0=got[:, :, 1], scalar=float(P), in1=got[:, :, 2],
                                   op0=ALU.mult, op1=ALU.add)
            ch.link(v.tensor_scalar(got[:, :, 0], empty[:, :], row, None, ALU.mult))
            ch.link(v.scalar_tensor_tensor(out=empty[:, :], in0=empty[:, :], scalar=float(N), in1=got[:, :, 0],
                                           op0=ALU.mult, op1=ALU.add))
            v.tensor_tensor(c.slot_token[:, :], idf[:, :], empty[:, :], ALU.add)
            ch.link(v.tensor_tensor(got[:, :, 3], got[:, :, 3], got[:, :, 4], ALU.add))
            ch.link(v.tensor_tensor(c.slot_weight[:, :], got[:, :, 3], got[:, :, 5], ALU.add))

        @block.tensor
        def _(pe):
            pe.wait_ge(s["s_zero"], 1)
            nc.tensor.matmul(acc, zeros[:, 0:CAP0], zeros[:, :], start=True, stop=False, skip_group_check=True)
            with pe.Fori(0, NT // LANES) as i:
                for j, t in token_loop(i):
                    pe.wait_ge(s["hot_ready"], ready(t))
                    pe.wait_ge(s["cols_ready"], ready(t))
                    for e in range(E0):
                        last = nc.tensor.matmul(acc[:, 6 * e:6 * e + 6], hot[:, j, e, :], cols[:, j, 6 * e:6 * e + 6],
                                                start=False, stop=False, skip_group_check=True)
                    last.then_inc(s["hot_used"], 1)
            nc.tensor.matmul(acc, zeros[:, 0:CAP0], zeros[:, :], start=False, stop=True,
                             skip_group_check=True).then_inc(s["s_done"], 1)


def stage_l0_experts(nc, c):
    with ExitStack() as ctx:
        sb = lambda n, sh, dt=F32: ctx.enter_context(nc.sbuf_tensor(n, sh, dt))
        w13 = sb("w13", [P, LANES, 2, DK, F0]); w2 = sb("w2e", [P, LANES, D])
        idx = sb("idx", [CAP0, LANES], I32); xg = sb("xg", [CAP0, LANES, D]); xgT = sb("xgT", [P, LANES, DK * CAP0])
        sig = sb("sig_e", [P, LANES, CAP0]); hT = sb("hT_e", [P, LANES, CAP0]); y = sb("y_e", [CAP0, LANES, D])
        s = open_sems(nc, ctx, "w_loaded0 w_loaded1 idx_ready gathered0 gathered1 feat_ready feat_copied hid_ready "
                      "sig_ready hT_ready down_ready y_ready added0 added1 add_done e_chain pool_passed pe_passed")
        block = ctx.enter_context(nc.Block())

        def feat(j): return c.bank[4 * j]
        def hid(j): return c.bank[4 * j + 1]
        def down(j): return c.bank[4 * j + 2]

        @block.sync
        def _(sp):
            with sp.Fori(0, E0 // LANES) as i:
                for j, e in token_loop(i):
                    sp.wait_ge(s["down_ready"], freed(e))
                    for n, name in enumerate(("e0w1", "e0w3")):
                        sp.dma_start(w13[:, j, n, :, :], c.d[name][bass.ds(e, 1)].rearrange(
                            "a (k p) f -> p (a k) f", p=P)).then_inc(s[f"w_loaded{j}"], 16)
                    sp.dma_start(w2[:, j, :], c.d["e0w2"][bass.ds(e, 1)].rearrange(
                        "a f d -> f (a d)")).then_inc(s[f"w_loaded{j}"], 16)

        @block.gpsimd
        def _(pool):
            give_credit(pool, s, "idx_ready feat_ready feat_copied hid_ready sig_ready hT_ready down_ready y_ready add_done")
            with pool.Fori(0, E0 // LANES) as i:
                for j, e in token_loop(i):
                    pool.wait_ge(s["idx_ready"], ready(e))
                    pool.wait_ge(s["feat_ready"], freed(e))
                    settle(pool, s[f"pool_passed"])
                    nc.gpsimd.indirect_dma_start(
                        out=xg[:, j, :], out_offset=None, in_=c.xn_rows[:, :],
                        in_offset=bass.IndirectOffsetOnAxis(ap=idx[:, j:j + 1], axis=0),
                    ).then_inc(s[f"gathered{j}"], 16)
                for j, e in token_loop(i):
                    pool.wait_ge(s["y_ready"], ready(e))
                    settle(pool, s["pool_passed"])
                    nc.gpsimd.indirect_dma_start(
                        out=c.moe[:, :], out_offset=bass.IndirectOffsetOnAxis(ap=idx[:, j:j + 1], axis=0),
                        in_=y[:, j, :], in_offset=None, compute_op=ALU.add, oob_is_err=True,
                        bounds_check=NX - 1,
                    ).then_inc(s[f"added{j}"], 16)
                    pool.wait_ge(s[f"added{j}"], loaded(i))
                    pool.sem_inc(s["add_done"], 1)

        @block.tensor
        def _(pe):
            with pe.Fori(0, E0 // LANES) as i:
                for j, e in token_loop(i):
                    pe.wait_ge(s[f"gathered{j}"], loaded(i))
                    pe.wait_ge(s["feat_copied"], freed(e))
                    settle(pe, s[f"pe_passed"])
                    for k in range(DK):
                        last = nc.tensor.transpose(feat(j)[:, k * CAP0:(k + 1) * CAP0], xg[:, j, k * P:(k + 1) * P],
                                                   c.ident[0:CAP0, 0:CAP0])
                    last.then_inc(s["feat_ready"], 1)
                for j, e in token_loop(i):
                    pe.wait_ge(s["feat_copied"], ready(e))
                    pe.wait_ge(s[f"w_loaded{j}"], 48 * i + 48)
                    pe.wait_ge(s["hT_ready"], freed(e))
                    for n in range(2):
                        for k in range(DK):
                            last = nc.tensor.matmul(hid(j)[:, n * CAP0:(n + 1) * CAP0], w13[:, j, n, k, :],
                                                    xgT[:, j, k * CAP0:(k + 1) * CAP0],
                                                    start=(k == 0), stop=(k == DK - 1))
                    last.then_inc(s["hid_ready"], 1)
                for j, e in token_loop(i):
                    pe.wait_ge(s["hT_ready"], ready(e))
                    pe.wait_ge(s["y_ready"], freed(e))
                    nc.tensor.matmul(down(j)[0:CAP0, 0:D], hT[:, j, :], w2[:, j, :],
                                     start=True, stop=True).then_inc(s["down_ready"], 1)

        @block.scalar
        def _(act):
            with act.Fori(0, E0 // LANES) as i:
                for j, e in token_loop(i):
                    act.wait_ge(s["feat_ready"], ready(e))
                    act.wait_ge(s["hid_ready"], freed(e))
                    act.copy(xgT[:, j, :], feat(j)[:, 0:DK * CAP0]).then_inc(s["feat_copied"], 1)
                for j, e in token_loop(i):
                    act.wait_ge(s["hid_ready"], ready(e))
                    act.wait_ge(s["hT_ready"], freed(e))
                    nc.scalar.activation(sig[:, j, :], hid(j)[:, 0:CAP0], ACT.Sigmoid).then_inc(s["sig_ready"], 1)

        @block.vector
        def _(dve):
            with dve.Fori(0, E0 // LANES) as i:
                ch = Chain(dve, s["e_chain"], i * LANES)
                for j, e in token_loop(i):
                    dve.wait_ge(s["add_done"], freed(e))
                    nc.vector.tensor_copy(idx[:, j:j + 1], c.slot_token[:, bass.ds(e, 1)]).then_inc(s["idx_ready"], 1)
                for j, e in token_loop(i):
                    dve.wait_ge(s["sig_ready"], ready(e))
                    dve.wait_ge(s["down_ready"], freed(e))
                    ch.link(nc.vector.tensor_tensor(sig[:, j, :], hid(j)[:, 0:CAP0], sig[:, j, :], ALU.mult))
                    nc.vector.tensor_tensor(hT[:, j, :], hid(j)[:, CAP0:2 * CAP0], sig[:, j, :],
                                            ALU.mult).then_inc(s["hT_ready"], 1)
                for j, e in token_loop(i):
                    dve.wait_ge(s["down_ready"], ready(e))
                    nc.vector.tensor_scalar(y[:, j, :], down(j)[0:CAP0, 0:D], c.slot_weight[:, bass.ds(e, 1)], None,
                                            ALU.mult).then_inc(s["y_ready"], 1)


def stage_add_experts(nc, c):
    with ExitStack() as ctx:
        rows = ctx.enter_context(nc.sbuf_tensor("moe_in", [P, NT, D], F32))
        CH = 4
        s = open_sems(nc, ctx, "m_chain " + " ".join(f"m_loaded{n}" for n in range(CH)))
        block = ctx.enter_context(nc.Block())
        src = c.moe[0:N, :].rearrange("(n p) d -> p n d", p=P)
        W = NT // CH

        @block.sync
        def _(sp):
            for n in range(CH):
                sp.dma_start(rows[:, W * n:W * n + W, :], src[:, W * n:W * n + W, :]).then_inc(s[f"m_loaded{n}"], 16)

        @block.vector
        def _(dve):
            for n in range(CH):
                dve.wait_ge(s[f"m_loaded{n}"], 16)
                with dve.Fori(W * n, W * n + W) as t:
                    ch = Chain(dve, s["m_chain"], t)
                    ch.link(nc.vector.tensor_tensor(at_tile(c.x, t), at_tile(c.x, t), at_tile(rows, t), ALU.add))
                    nc.vector.bn_stats(at_tile(c.bn, t), at_tile(c.x, t))


def stage_l1_scores(nc, c):
    with ExitStack() as ctx:
        sb = lambda n, sh, dt=F32: ctx.enter_context(nc.sbuf_tensor(n, sh, dt))
        wg = sb("wg_c", [P, DK, D]); xn = sb("xn_c", [P, LANES, D]); xT = sb("xT_c", [P, LANES, DK, P])
        zeros = sb("zeros_c", [P, P]); padded = sb("padded", [S, H1, 3 * S])
        s = open_sems(nc, ctx, "c_weights c_zero xn_ready feat_ready feat_copied gate_ready gate_copied used_ready "
                      "sum_done c_chain padded_ready mixT_ready")
        block = ctx.enter_context(nc.Block())
        total = c.bank[7][0:S, 0:H1 * S]

        def feat(j): return c.bank[2 * j]
        def gate(j): return c.bank[2 * j + 1]

        @block.sync
        def _(sp):
            sp.dma_start(wg[:, :, :], c.d["wg"].rearrange("(k p) n -> p k n", p=P)).then_inc(s["c_weights"], 16)

        @block.gpsimd
        def _(pool):
            give_credit(pool, s, "xn_ready feat_ready feat_copied gate_ready gate_copied used_ready")
            nc.gpsimd.memset(zeros[:, :], 0.0).then_inc(s["c_zero"], 1)
            nc.gpsimd.memset(padded[:, :, :], 0.0).then_inc(s["c_zero"], 1)

        @block.tensor
        def _(pe):
            pe.wait_ge(s["c_weights"], 16)
            pe.wait_ge(s["c_zero"], 2)
            nc.tensor.matmul(total, zeros[:, 0:S], zeros[:, :], start=True, stop=False, skip_group_check=True)
            with pe.Fori(0, NT // LANES) as i:
                for j, t in token_loop(i):
                    pe.wait_ge(s["xn_ready"], ready(t))
                    pe.wait_ge(s["feat_copied"], freed(t))
                    transpose_tile(nc, c, feat(j), xn[:, j, :]).then_inc(s["feat_ready"], 1)
                for j, t in token_loop(i):
                    pe.wait_ge(s["feat_copied"], ready(t))
                    pe.wait_ge(s["gate_copied"], freed(t))
                    for k in range(DK):
                        last = nc.tensor.matmul(gate(j)[:, 0:D], xT[:, j, k, :], wg[:, k, :],
                                                start=(k == 0), stop=(k == DK - 1))
                    last.then_inc(s["gate_ready"], 1)
                    for h in range(H1):
                        for b in range(2):
                            last = nc.tensor.matmul(total[:, h * S:(h + 1) * S], xT[:, j, h, 64 * b:64 * b + 64],
                                                    c.gramT[:, h, bass.ds(t * P + 64 * b, S)],
                                                    start=False, stop=False, skip_group_check=True)
                    last.then_inc(s["used_ready"], 1)
            nc.tensor.matmul(total, zeros[:, 0:S], zeros[:, :], start=False, stop=True,
                             skip_group_check=True).then_inc(s["sum_done"], 1)
            pe.wait_ge(s["padded_ready"], 1)
            for h in range(H1):
                for b in range(2):
                    last = nc.tensor.transpose(c.bank[0][:, h * P + 64 * b:h * P + 64 * b + 64],
                                               padded[:, h, S * (1 - b):S * (1 - b) + P], c.ident[0:S, 0:S])
            last.then_inc(s["mixT_ready"], 1)

        @block.scalar
        def _(act):
            with act.Fori(0, NT // LANES) as i:
                for j, t in token_loop(i):
                    act.wait_ge(s["feat_ready"], ready(t))
                    act.wait_ge(s["used_ready"], freed(t))
                    act.copy(xT[:, j, :, :].rearrange("p k n -> p (k n)"), feat(j)[:, 0:D]).then_inc(s["feat_copied"], 1)
                for j, t in token_loop(i):
                    act.wait_ge(s["gate_ready"], ready(t))
                    nc.scalar.activation(at_tile(c.gate1, t), gate(j)[:, 0:D], ACT.Relu).then_inc(s["gate_copied"], 1)
            act.wait_ge(s["mixT_ready"], 1)
            act.copy(c.mixT[:, :, :].rearrange("p h n -> p (h n)"), c.bank[0][:, 0:H1 * P])

        @block.vector
        def _(dve):
            with dve.Fori(0, NT // LANES) as i:
                for j, t in token_loop(i):
                    dve.wait_ge(s["feat_ready"], freed(t))
                    normalize(nc, c, xn[:, j, :], t).then_inc(s["xn_ready"], 1)
            ch = Chain(dve, s["c_chain"])
            dve.wait_ge(s["sum_done"], 1)
            mid = padded[:, :, S:2 * S]
            ch.link(nc.vector.tensor_tensor(mid, total.rearrange("p (h n) -> p h n", h=H1),
                                            c.decay[0:S, :].rearrange("p (h n) -> p h n", h=H1), ALU.mult))
            ch.link(nc.vector.scalar_tensor_tensor(out=mid, in0=mid, scalar=-1.0, in1=mid, op0=ALU.mult, op1=ALU.max))
            nc.vector.tensor_scalar(mid, mid, 1.0, None, ALU.max).then_inc(s["padded_ready"], 1)


def stage_l1_mix(nc, c):
    with ExitStack() as ctx:
        sb = lambda n, sh, dt=F32: ctx.enter_context(nc.sbuf_tensor(n, sh, dt))
        wo = sb("wo_m", [P, DK, D]); gamma = sb("gn_gamma", [P, D]); beta = sb("gn_beta", [P, D])
        bn = sb("bn_m", [P, LANES, 6]); mv = sb("mv_m", [P, LANES, 2]); ve = sb("ve_m", [P, LANES]); rs = sb("rs_m", [P, LANES])
        y = sb("y_m", [P, LANES, D]); yT = sb("yT_m", [P, LANES, D])
        s = open_sems(nc, ctx, "m_weights mixed_ready var_ready rstd_ready y_ready yT_ready yT_copied out_ready "
                      "x_done mix_chain dve_passed")
        block = ctx.enter_context(nc.Block())
        LINKS = 12

        def mixed(j): return c.bank[4 * j]
        def turned(j): return c.bank[4 * j + 1]
        def out(j): return c.bank[4 * j + 2]

        @block.sync
        def _(sp):
            sp.dma_start(wo[:, :, :], c.d["wo"].rearrange("(k p) n -> p k n", p=P)).then_inc(s["m_weights"], 16)
            sp.dma_start(gamma[:, :], c.d["gng"].broadcast_to([P, D])).then_inc(s["m_weights"], 16)
            sp.dma_start(beta[:, :], c.d["gnb"].broadcast_to([P, D])).then_inc(s["m_weights"], 16)

        @block.gpsimd
        def _(pool):
            give_credit(pool, s, "mixed_ready var_ready rstd_ready y_ready yT_ready yT_copied out_ready x_done")
            with pool.Fori(0, NT // LANES) as i:
                for j, t in token_loop(i):
                    pool.wait_ge(s["var_ready"], ready(t))
                    nc.gpsimd.tensor_tensor(rs[:, j:j + 1], ve[:, j:j + 1], c.minus_half[:, 0:1],
                                            ALU.pow).then_inc(s["rstd_ready"], 1)

        @block.tensor
        def _(pe):
            pe.wait_ge(s["m_weights"], 48)
            with pe.Fori(0, NT // LANES) as i:
                for j, t in token_loop(i):
                    pe.wait_ge(s["y_ready"], freed(t))
                    for h in range(H1):
                        last = nc.tensor.matmul(mixed(j)[:, h * P:(h + 1) * P], c.mixT[:, h, :],
                                                at_tile(c.v, t)[:, h * P:(h + 1) * P], start=True, stop=True)
                    last.then_inc(s["mixed_ready"], 1)
                for j, t in token_loop(i):
                    pe.wait_ge(s["y_ready"], ready(t))
                    pe.wait_ge(s["yT_copied"], freed(t))
                    transpose_tile(nc, c, turned(j), y[:, j, :]).then_inc(s["yT_ready"], 1)
                for j, t in token_loop(i):
                    pe.wait_ge(s["yT_copied"], ready(t))
                    pe.wait_ge(s["x_done"], freed(t))
                    for k in range(DK):
                        last = nc.tensor.matmul(out(j)[:, 0:D], yT[:, j, k * P:(k + 1) * P], wo[:, k, :],
                                                start=(k == 0), stop=(k == DK - 1))
                    last.then_inc(s["out_ready"], 1)

        @block.scalar
        def _(act):
            with act.Fori(0, NT // LANES) as i:
                for j, t in token_loop(i):
                    act.wait_ge(s["yT_ready"], ready(t))
                    act.wait_ge(s["out_ready"], freed(t))
                    act.copy(yT[:, j, :], turned(j)[:, 0:D]).then_inc(s["yT_copied"], 1)

        @block.vector
        def _(dve):
            dve.wait_ge(s["m_weights"], 48)
            with dve.Fori(0, NT // LANES) as i:
                ch = Chain(dve, s["mix_chain"], i * LINKS)
                for j, t in token_loop(i):
                    dve.wait_ge(s["mixed_ready"], ready(t))
                    ch.link(nc.vector.bn_stats(bn[:, j, :], mixed(j)[:, 0:D]))
                    settle(dve, s["dve_passed"])
                    ch.link(nc.vector.bn_aggr(mv[:, j, :], bn[:, j, :]))
                    nc.vector.tensor_scalar(ve[:, j:j + 1], mv[:, j, 1:2], GN_EPS, None, ALU.add).then_inc(s["var_ready"], 1)
                for j, t in token_loop(i):
                    dve.wait_ge(s["yT_ready"], freed(t))
                    ch.link(nc.vector.scalar_tensor_tensor(out=y[:, j, :], in0=mixed(j)[:, 0:D], scalar=mv[:, j, 0:1],
                                                           in1=gamma[:, :], op0=ALU.subtract, op1=ALU.mult))
                    dve.wait_ge(s["rstd_ready"], ready(t))
                    ch.link(nc.vector.scalar_tensor_tensor(out=y[:, j, :], in0=y[:, j, :], scalar=rs[:, j:j + 1],
                                                           in1=beta[:, :], op0=ALU.mult, op1=ALU.add))
                    nc.vector.tensor_tensor(y[:, j, :], y[:, j, :], at_tile(c.gate1, t), ALU.mult).then_inc(s["y_ready"], 1)
                for j, t in token_loop(i):
                    dve.wait_ge(s["out_ready"], ready(t))
                    add_and_stats(nc, c, ch, t, out(j)[:, 0:D], 1.0, s["x_done"])
                assert ch.n == LINKS, ch.n


def stage_l1_think(nc, c):
    with ExitStack() as ctx:
        sb = lambda n, sh, dt=F32: ctx.enter_context(nc.sbuf_tensor(n, sh, dt))
        M = B
        FT = HID1 // P
        agg = sb("agg_w", [P, DK, D]); d1 = sb("d1_w", [P, DK, HID1]); d2 = sb("d2_w", [P, FT, D]); bcw = sb("bc_w", [P, DK, D])
        row = {n: sb("r_" + n, [M, D]) for n in ("in_gamma", "in_beta", "agg_b", "pn_gamma", "pn_beta", "d2_b", "bc_b")}
        d1b = sb("d1_b", [P, FT])
        last_x = sb("last_x", [M, D]); n1 = sb("n1", [M, D]); th = sb("thought", [M, D])
        bn = sb("bn_t", [M, 6]); mv = sb("mv_t", [M, 2]); ve = sb("ve_t", [M, 1]); rs = sb("rs_t", [M, 1])
        nT = sb("nT", [P, DK * M]); hT = sb("hT_t", [P, FT, M])
        s = open_sems(nc, ctx, "t_loaded t_last t_stored t_chain t_var t_rstd t_normed t_turned t_turn_copied t_up t_gelu "
                      "t_down t_added")
        block = ctx.enter_context(nc.Block())
        NORMS = 2 + STEPS1

        @block.sync
        def _(sp):
            n = 0
            for b in range(2):
                sp.dma_start(last_x[32 * b:32 * b + 32, :], c.x[64 * b + 63:64 * b + 64, :, :]).then_inc(s["t_last"], 16)
            for dst, name in ((agg, "agg_w"), (d1, "d1_w"), (d2, "d2_w"), (bcw, "bc_w")):
                sp.dma_start(dst[:, :, :], c.d["f1_" + name].rearrange("(k p) n -> p k n", p=P)).then_inc(s["t_loaded"], 16)
            for name, dst in row.items():
                sp.dma_start(dst[:, :], c.d["f1_" + name].broadcast_to([M, D])).then_inc(s["t_loaded"], 16)
            sp.dma_start(d1b[:, :], c.d["f1_d1_b"]).then_inc(s["t_loaded"], 16)
            sp.wait_ge(s["t_added"], 2 + STEPS1)
            sp.dma_start(c.think_rows[:, :], n1[:, :]).then_inc(s["t_stored"], 16)
            sp.wait_ge(s["t_stored"], 16)

        @block.gpsimd
        def _(pool):
            for n in range(NORMS):
                pool.wait_ge(s["t_var"], n + 1)
                nc.gpsimd.tensor_tensor(rs[:, :], ve[:, :], c.minus_half[0:M, 0:1], ALU.pow).then_inc(s["t_rstd"], 1)

        @block.tensor
        def _(pe):
            pe.wait_ge(s["t_loaded"], 16 * (5 + len(row)))
            for n in range(2 + STEPS1):
                pe.wait_ge(s["t_normed"], n + 1)
                for k in range(DK):
                    last = nc.tensor.transpose(c.bank[0][:, k * M:(k + 1) * M],
                                               (th if n == 1 + STEPS1 else n1)[:, k * P:(k + 1) * P], c.ident[0:M, 0:M])
                last.then_inc(s["t_turned"], 1)
                pe.wait_ge(s["t_turn_copied"], n + 1)
                if n in (0, 1 + STEPS1):
                    for k in range(DK):
                        last = nc.tensor.matmul(c.bank[1][0:M, 0:D], nT[:, k * M:(k + 1) * M],
                                                (bcw if n else agg)[:, k, :], start=(k == 0), stop=(k == DK - 1))
                    last.then_inc(s["t_down"], 1)
                    continue
                for f in range(FT):
                    for k in range(DK):
                        last = nc.tensor.matmul(c.bank[2][:, f * M:(f + 1) * M], d1[:, k, f * P:(f + 1) * P],
                                                nT[:, k * M:(k + 1) * M], start=(k == 0), stop=(k == DK - 1))
                last.then_inc(s["t_up"], 1)
                pe.wait_ge(s["t_gelu"], n)
                for f in range(FT):
                    last = nc.tensor.matmul(c.bank[1][0:M, 0:D], hT[:, f, :], d2[:, f, :],
                                            start=(f == 0), stop=(f == FT - 1))
                last.then_inc(s["t_down"], 1)

        @block.scalar
        def _(act):
            act.wait_ge(s["t_loaded"], 16 * (5 + len(row)))
            for n in range(2 + STEPS1):
                act.wait_ge(s["t_turned"], n + 1)
                act.copy(nT[:, :], c.bank[0][:, 0:DK * M]).then_inc(s["t_turn_copied"], 1)
                if 1 <= n <= STEPS1:
                    act.wait_ge(s["t_up"], n)
                    for f in range(FT):
                        last = nc.scalar.activation(hT[:, f, :], c.bank[2][:, f * M:(f + 1) * M], ACT.Gelu,
                                                    bias=d1b[:, f:f + 1])
                    last.then_inc(s["t_gelu"], 1)

        @block.vector
        def _(dve):
            ch = Chain(dve, s["t_chain"])
            v = nc.vector

            def norm(n, src, eps, gamma=None, beta=None):
                ch.link(v.bn_stats(bn[:, :], src[:, :]))
                ch.link(v.bn_aggr(mv[:, :], bn[:, :]))
                v.tensor_scalar(ve[:, :], mv[:, 1:2], eps, None, ALU.add).then_inc(s["t_var"], 1)
                dve.wait_ge(s["t_rstd"], n + 1)
                if gamma is None:
                    ch.link(v.tensor_scalar(n1[:, :], src[:, :], mv[:, 0:1], rs[:, :], ALU.subtract, ALU.mult))
                    return
                ch.link(v.scalar_tensor_tensor(out=n1[:, :], in0=src[:, :], scalar=mv[:, 0:1], in1=gamma[:, :],
                                               op0=ALU.subtract, op1=ALU.mult))
                v.scalar_tensor_tensor(out=n1[:, :], in0=n1[:, :], scalar=rs[:, :], in1=beta[:, :],
                                       op0=ALU.mult, op1=ALU.add).then_inc(s["t_normed"], 1)

            dve.wait_ge(s["t_last"], 32)
            dve.wait_ge(s["t_loaded"], 16 * (5 + len(row)))
            norm(0, last_x, LN_EPS)
            norm(1, n1, EPS1, row["in_gamma"], row["in_beta"])
            dve.wait_ge(s["t_down"], 1)
            v.tensor_tensor(th[:, :], c.bank[1][0:M, 0:D], row["agg_b"][:, :], ALU.add).then_inc(s["t_added"], 1)
            for n in range(1, 1 + STEPS1):
                dve.wait_ge(s["t_added"], n)
                norm(1 + n, th, EPS1, row["pn_gamma"], row["pn_beta"])
                dve.wait_ge(s["t_down"], 1 + n)
                ch.link(v.tensor_tensor(th[:, :], c.bank[1][0:M, 0:D], th[:, :], ALU.add))
                v.tensor_tensor(th[:, :], th[:, :], row["d2_b"][:, :], ALU.add).then_inc(s["t_added"], 1)
            dve.wait_ge(s["t_added"], 1 + STEPS1)
            dve.sem_inc(s["t_normed"], 1)
            dve.wait_ge(s["t_down"], 2 + STEPS1)
            v.tensor_tensor(n1[:, :], c.bank[1][0:M, 0:D], row["bc_b"][:, :], ALU.add).then_inc(s["t_added"], 1)


def stage_l1_broadcast(nc, c):
    with ExitStack() as ctx:
        sb = lambda n, sh, dt=F32: ctx.enter_context(nc.sbuf_tensor(n, sh, dt))
        gw = sb("gw_g", [P, DK, D]); row = {n: sb("g_" + n, [P, D]) for n in ("gate_b", "out_gamma", "out_beta")}
        xn = sb("xn_g", [P, LANES, D]); xT = sb("xT_g", [P, LANES, D]); think = sb("think", [P, LANES, D])
        pre = sb("pre_g", [P, LANES, D]); gate = sb("gate_g", [P, LANES, D])
        bn = sb("bn_g", [P, LANES, 6]); mv = sb("mv_g", [P, LANES, 2]); ve = sb("ve_g", [P, LANES]); rs = sb("rs_g", [P, LANES])
        s = open_sems(nc, ctx, "g_weights think_loaded0 think_loaded1 xn_ready feat_ready feat_copied pre_ready "
                      "biased_ready gate_ready mixed_ready var_ready rstd_ready x_done g_chain dve_passed")
        block = ctx.enter_context(nc.Block())
        LINKS = 16

        def feat(j): return c.bank[4 * j]
        def lin(j): return c.bank[4 * j + 1]

        @block.sync
        def _(sp):
            sp.dma_start(gw[:, :, :], c.d["f1_gate_w"].rearrange("(k p) n -> p k n", p=P)).then_inc(s["g_weights"], 16)
            for name, dst in row.items():
                sp.dma_start(dst[:, :], c.d["f1_" + name].broadcast_to([P, D])).then_inc(s["g_weights"], 16)
            with sp.Fori(0, NT // LANES) as i:
                for j, t in token_loop(i):
                    sp.wait_ge(s["mixed_ready"], freed(t))
                    for b in range(2):
                        sp.dma_start(think[64 * b:64 * b + 64, j, :],
                                     c.think_rows[bass.ds(t + NT * b, 1), :].broadcast_to([S, D])
                                     ).then_inc(s[f"think_loaded{j}"], 16)

        @block.gpsimd
        def _(pool):
            give_credit(pool, s, "xn_ready feat_ready feat_copied pre_ready biased_ready gate_ready mixed_ready "
                        "var_ready rstd_ready x_done")
            with pool.Fori(0, NT // LANES) as i:
                for j, t in token_loop(i):
                    pool.wait_ge(s["var_ready"], ready(t))
                    nc.gpsimd.tensor_tensor(rs[:, j:j + 1], ve[:, j:j + 1], c.minus_half[:, 0:1],
                                            ALU.pow).then_inc(s["rstd_ready"], 1)

        @block.tensor
        def _(pe):
            pe.wait_ge(s["g_weights"], 64)
            with pe.Fori(0, NT // LANES) as i:
                for j, t in token_loop(i):
                    pe.wait_ge(s["xn_ready"], ready(t))
                    pe.wait_ge(s["feat_copied"], freed(t))
                    transpose_tile(nc, c, feat(j), xn[:, j, :]).then_inc(s["feat_ready"], 1)
                for j, t in token_loop(i):
                    pe.wait_ge(s["feat_copied"], ready(t))
                    pe.wait_ge(s["biased_ready"], freed(t))
                    for k in range(DK):
                        last = nc.tensor.matmul(lin(j)[:, 0:D], xT[:, j, k * P:(k + 1) * P], gw[:, k, :],
                                                start=(k == 0), stop=(k == DK - 1))
                    last.then_inc(s["pre_ready"], 1)

        @block.scalar
        def _(act):
            with act.Fori(0, NT // LANES) as i:
                for j, t in token_loop(i):
                    act.wait_ge(s["feat_ready"], ready(t))
                    act.wait_ge(s["pre_ready"], freed(t))
                    act.copy(xT[:, j, :], feat(j)[:, 0:D]).then_inc(s["feat_copied"], 1)
                for j, t in token_loop(i):
                    act.wait_ge(s["biased_ready"], ready(t))
                    act.wait_ge(s["x_done"], freed(t))
                    nc.scalar.activation(gate[:, j, :], pre[:, j, :], ACT.Sigmoid).then_inc(s["gate_ready"], 1)

        @block.vector
        def _(dve):
            dve.wait_ge(s["g_weights"], 64)
            v = nc.vector
            with dve.Fori(0, NT // LANES) as i:
                ch = Chain(dve, s["g_chain"], i * LINKS)
                for j, t in token_loop(i):
                    dve.wait_ge(s["feat_ready"], freed(t))
                    normalize(nc, c, xn[:, j, :], t).then_inc(s["xn_ready"], 1)
                for j, t in token_loop(i):
                    dve.wait_ge(s["pre_ready"], ready(t))
                    dve.wait_ge(s["gate_ready"], freed(t))
                    v.tensor_tensor(pre[:, j, :], lin(j)[:, 0:D], row["gate_b"][:, :], ALU.add).then_inc(s["biased_ready"], 1)
                for j, t in token_loop(i):
                    dve.wait_ge(s["gate_ready"], ready(t))
                    dve.wait_ge(s[f"think_loaded{j}"], 32 * i + 32)
                    ch.link(v.tensor_tensor(gate[:, j, :], gate[:, j, :], think[:, j, :], ALU.mult))
                    ins = v.tensor_tensor(gate[:, j, :], gate[:, j, :], xn[:, j, :], ALU.add)
                    ch.link(ins)
                    dve.sem_inc(s["mixed_ready"], 1)
                    ch.link(v.bn_stats(bn[:, j, :], gate[:, j, :]))
                    settle(dve, s["dve_passed"])
                    ch.link(v.bn_aggr(mv[:, j, :], bn[:, j, :]))
                    v.tensor_scalar(ve[:, j:j + 1], mv[:, j, 1:2], EPS1, None, ALU.add).then_inc(s["var_ready"], 1)
                for j, t in token_loop(i):
                    ch.link(v.scalar_tensor_tensor(out=gate[:, j, :], in0=gate[:, j, :], scalar=mv[:, j, 0:1],
                                                   in1=row["out_gamma"][:, :], op0=ALU.subtract, op1=ALU.mult))
                    dve.wait_ge(s["rstd_ready"], ready(t))
                    ch.link(v.scalar_tensor_tensor(out=gate[:, j, :], in0=gate[:, j, :], scalar=rs[:, j:j + 1],
                                                   in1=row["out_beta"][:, :], op0=ALU.mult, op1=ALU.add))
                    ch.link(v.tensor_tensor(at_tile(c.x, t), gate[:, j, :], at_tile(c.x, t), ALU.add))
                    ch.link(v.bn_stats(at_tile(c.bn, t), at_tile(c.x, t)))
                    dve.sem_inc(s["x_done"], 1)
                assert ch.n == LINKS, ch.n


def stage_l2_attention(nc, c):
    with ExitStack() as ctx:
        sb = lambda n, sh, dt=F32: ctx.enter_context(nc.sbuf_tensor(n, sh, dt))
        HP = H2 // 2
        SC = H2 * S
        wdq = sb("wdq", [P, DK, QC]); wq = sb("wq_abs", [QC, H2, P]); wvo = sb("wvo", [P, HP, D])
        seg_i = sb("seg_i", [P, NT], I32); seg = sb("seg", [P, NT]); seg_lo = sb("seg_lo", [P, NT])
        xn = sb("xn_l", [P, LANES, D]); xT = sb("xT_l", [P, LANES, D]); qcT = sb("qcT", [QC, LANES, P])
        q = sb("q_l", [P, LANES, H2, P]); rot = sb("rot_l", [P, LANES, H2, P])
        key = sb("key_l", [P, LANES, P]); kv2 = sb("kv2", [P, LANES, 2, P])
        drop = sb("drop_l", [P, LANES, S]); sc = sb("sc_l", [P, LANES, H2, S]); scT = sb("scT_l", [P, LANES, HP, P])
        mx = sb("mx_l", [P, LANES, H2]); sm = sb("sm_l", [P, LANES, H2])
        rd = sb("rd_l", [P, LANES, HP, P])
        s = open_sems(nc, ctx, "l_weights l_zero l_pre l_folded l_seg xn_ready feat_ready feat_copied qc_ready qc_copied q_ready "
                      "nope_copied rope_done rope_added kv_ready key_ready scores_ready max_ready shifted_ready exp_ready sum_ready prob_ready turned_ready "
                      "turned_copied read_ready read_copied out_ready x_done drop_chain masked summed add_chain seg_chain")
        scale = float(np.float32(1.0) / np.sqrt(np.float32(HD2 + R2)))

        def bank(j, n): return c.bank[4 * j + n]

        with ExitStack() as pre:
            wt = lambda n, sh: pre.enter_context(nc.sbuf_tensor(n, sh, F32))
            wuqT = wt("wuqT", [P, H2, QC]); wukT = wt("wukT", [P, H2, KVC]); wuvT = wt("wuvT", [P, H2, KVC])
            wqr = wt("wqr", [QC, H2, R2]); wo = wt("wo_l", [P, H2, D])
            block = pre.enter_context(nc.Block())

            @block.sync
            def _(sp):
                for dst, src in ((wdq[:, :, :], c.d["wdq"].rearrange("(k p) n -> p k n", p=P)), (wuqT[:, :, :], c.d["wuqT"]),
                                 (wukT[:, :, :], c.d["wukT"]), (wuvT[:, :, :], c.d["wuvT"]), (wqr[:, :, :], c.d["wqr"]),
                                 (wo[:, :, :], c.d["wo2"]), (seg_i[:, :], c.d["seg"])):
                    sp.dma_start(dst, src).then_inc(s["l_weights"], 16)
                sp.wait_ge(s["l_weights"], 112)

            @block.tensor
            def _(pe):
                pe.wait_ge(s["l_weights"], 112)
                for h in range(H2):
                    last = nc.tensor.matmul(c.bank[h // 8][0:QC, (h % 8) * KVC:(h % 8 + 1) * KVC], wuqT[:, h, :],
                                            wukT[:, h, :], start=True, stop=True)
                for h in range(H2):
                    r = slice(64 * (h % 2), 64 * (h % 2) + 64)
                    hp = h // 2
                    last = nc.tensor.matmul(c.bank[2 + hp // 2][r, (hp % 2) * D:(hp % 2 + 1) * D], wuvT[:, h, :],
                                            wo[:, h, :], start=True, stop=True)
                last.then_inc(s["l_pre"], 1)

            @block.scalar
            def _(act):
                act.wait_ge(s["l_weights"], 112)
                act.mul(wq[:, :, KVC:P], wqr[:, :, :], scale)
                act.wait_ge(s["l_pre"], 1)
                for n in range(2):
                    act.mul(wq[:, 8 * n:8 * n + 8, 0:KVC],
                            c.bank[n][0:QC, :].rearrange("p (h n) -> p h n", h=8), scale)
                for n in range(4):
                    act.copy(wvo[:, 2 * n:2 * n + 2, :].rearrange("p h n -> p (h n)"), c.bank[2 + n][:, :])

            @block.vector
            def _(dve):
                ch = Chain(dve, s["seg_chain"])
                dve.wait_ge(s["l_weights"], 112)
                ch.link(nc.vector.tensor_copy(seg[:, :], seg_i[:, :]))
                nc.vector.tensor_scalar(seg_lo[:, :], seg[:, :], float(LOOKBACK), None, ALU.subtract)

        block = ctx.enter_context(nc.Block())

        def run(eng, ahead, behind, after=lambda t, j: None):
            ahead(0, 0)
            after(0, 0)
            with eng.Fori(0, NT // 2 - 1) as i:
                for j in range(2):
                    ahead(2 * i + j + 1, 1 - j)
                    behind(2 * i + j, j)
                    after(2 * i + j + 1, 1 - j)
            ahead(NT - 1, 1)
            behind(NT - 2, 0)
            after(NT - 1, 1)
            behind(NT - 1, 1)

        def halves(t, n):
            return 2 * t + n + 1 + 2 * CREDIT

        @block.gpsimd
        def _(pool):
            give_credit(pool, s, "xn_ready feat_ready feat_copied qc_ready qc_copied q_ready nope_copied "
                        "kv_ready key_ready scores_ready max_ready shifted_ready exp_ready sum_ready prob_ready "
                        "turned_ready turned_copied read_ready read_copied out_ready x_done")
            give_credit(pool, s, "rope_done rope_added", 2)
            nc.gpsimd.memset(kv2[:, :, :, :], 0.0).then_inc(s["l_zero"], 1)
            flat = lambda ap: ap.rearrange("p h n -> p (h n)")

            def key_copy(t, j):
                pool.wait_ge(s["rope_added"], halves(t - 1, 1))
                pool.wait_ge(s["scores_ready"], freed(t))
                nc.gpsimd.tensor_copy(key[:, j, :], c.keysT[:, bass.ds(t * P, P)]).then_inc(s["key_ready"], 1)

            def softmax(t, j):
                pool.wait_ge(s["max_ready"], ready(t))
                nc.gpsimd.tensor_tensor(sc[:, j, :, :], sc[:, j, :, :], mx[:, j, :].unsqueeze(2).broadcast_to([P, H2, S]),
                                        ALU.subtract).then_inc(s["shifted_ready"], 1)
                pool.wait_ge(s["sum_ready"], ready(t))
                nc.gpsimd.tensor_tensor(sc[:, j, :, :], sc[:, j, :, :], sm[:, j, :].unsqueeze(2).broadcast_to([P, H2, S]),
                                        ALU.mult).then_inc(s["prob_ready"], 1)

            def rope_add(t, j):
                pool.wait_ge(s["key_ready"], ready(t))
                pool.wait_ge(s["prob_ready"], ready(t) - 1)
                for n in range(2):
                    pool.wait_ge(s["rope_done"], halves(t, n))
                    hs = slice(8 * n, 8 * n + 8)
                    nc.gpsimd.tensor_tensor(q[64:P, j, hs, :], q[64:P, j, hs, :], rot[64:P, j, hs, :],
                                            ALU.add).then_inc(s["rope_added"], 1)

            run(pool, key_copy, softmax, rope_add)

        @block.tensor
        def _(pe):
            def front(t, j):
                pe.wait_ge(s["xn_ready"], ready(t))
                pe.wait_ge(s["read_copied"], freed(t))
                transpose_tile(nc, c, bank(j, 0), xn[:, j, :]).then_inc(s["feat_ready"], 1)
                pe.wait_ge(s["feat_copied"], ready(t))
                for k in range(DK):
                    last = nc.tensor.matmul(bank(j, 1)[0:QC, 0:P], wdq[:, k, :], xT[:, j, k * P:(k + 1) * P],
                                            start=(k == 0), stop=(k == DK - 1))
                last.then_inc(s["qc_ready"], 1)
                pe.wait_ge(s["qc_copied"], ready(t))
                pe.wait_ge(s["x_done"], freed(t))
                for h in range(H2):
                    last = nc.tensor.matmul(bank(j, h // 4)[:, (h % 4) * P:(h % 4 + 1) * P], wq[:, h, :],
                                            qcT[:, j, :], start=True, stop=True)
                last.then_inc(s["q_ready"], 1)

            def back(t, j):
                pe.wait_ge(s["prob_ready"], ready(t))
                for hp in range(HP):
                    last = nc.tensor.transpose(bank(j, 2 + hp // 4)[:, (hp % 4) * P:(hp % 4 + 1) * P],
                                               sc[:, j, 2 * hp:2 * hp + 2, :].rearrange("p h n -> p (h n)"), c.ident)
                last.then_inc(s["turned_ready"], 1)
                pe.wait_ge(s["turned_copied"], ready(t))
                pe.wait_ge(s["kv_ready"], ready(t))
                for b in range(2):
                    last = nc.tensor.matmul(bank(j, b)[:, :].rearrange("p (h q) -> p h q", h=HP), kv2[:, j, b, :],
                                            scT[:, j, :, 64 * b:64 * b + 64], start=True, stop=True)
                last.then_inc(s["read_ready"], 1)
                pe.wait_ge(s["read_copied"], ready(t))
                for hp in range(HP):
                    last = nc.tensor.matmul(bank(j, 2)[:, 0:D], rd[:, j, hp, :], wvo[:, hp, :],
                                            start=(hp == 0), stop=(hp == HP - 1))
                last.then_inc(s["out_ready"], 1)

            def scores(t, j):
                pe.wait_ge(s["nope_copied"], ready(t))
                pe.wait_ge(s["rope_done"], halves(t, 1))
                pe.wait_ge(s["key_ready"], ready(t))
                for h in range(H2):
                    if h % 8 == 0:
                        pe.wait_ge(s["rope_added"], halves(t, h // 8))
                    for b in range(2):
                        r = slice(64 * b, 64 * b + 64)
                        last = nc.tensor.matmul(bank(j, h // 8)[r, (h % 8) * S:(h % 8 + 1) * S],
                                                q[:, j, h, r], key[:, j, r], start=True, stop=True)
                last.then_inc(s["scores_ready"], 1)

            run(pe, front, back, scores)

        @block.scalar
        def _(act):
            def front(t, j):
                act.wait_ge(s["feat_ready"], ready(t))
                act.wait_ge(s["qc_ready"], freed(t))
                act.copy(xT[:, j, :], bank(j, 0)[:, 0:D]).then_inc(s["feat_copied"], 1)
                act.wait_ge(s["qc_ready"], ready(t))
                act.wait_ge(s["q_ready"], freed(t))
                act.copy(qcT[:, j, :], bank(j, 1)[0:QC, 0:P]).then_inc(s["qc_copied"], 1)

            def exponent(t, j):
                act.wait_ge(s["shifted_ready"], ready(t))
                nc.scalar.activation(sc[:, j, :, :], sc[:, j, :, :], ACT.Exp).then_inc(s["exp_ready"], 1)

            def nope(t, j):
                act.wait_ge(s["q_ready"], ready(t))
                act.wait_ge(s["scores_ready"], freed(t))
                for n in range(4):
                    last = act.copy(q[0:64, j, 4 * n:4 * n + 4, :].rearrange("p h n -> p (h n)"), bank(j, n)[0:64, :])
                last.then_inc(s["nope_copied"], 1)
                act.wait_ge(s["read_ready"], freed(t))
                for b in range(2):
                    for r in range(2):
                        last = act.copy(kv2[64 * r:64 * r + 64, j, b, 64 * r:64 * r + 64],
                                        at_tile(c.kvc, t)[64 * b:64 * b + 64, :])
                last.then_inc(s["kv_ready"], 1)

            def back(t, j):
                act.wait_ge(s["turned_ready"], ready(t))
                act.wait_ge(s["read_ready"], freed(t))
                for n in range(2):
                    last = act.copy(scT[:, j, 4 * n:4 * n + 4, :].rearrange("p h n -> p (h n)"), bank(j, 2 + n)[:, :])
                last.then_inc(s["turned_copied"], 1)
                act.wait_ge(s["read_ready"], ready(t))
                act.wait_ge(s["out_ready"], freed(t))
                for b in range(2):
                    last = act.copy(rd[:, j, :, 64 * b:64 * b + 64],
                                    bank(j, b)[:, :].rearrange("p (h q) -> p h q", h=HP))
                last.then_inc(s["read_copied"], 1)

            act.wait_ge(s["l_zero"], 1)
            front(0, 0)
            nope(0, 0)
            with act.Fori(0, NT // 2 - 1) as i:
                for j in range(2):
                    front(2 * i + j + 1, 1 - j)
                    exponent(2 * i + j, j)
                    nope(2 * i + j + 1, 1 - j)
                    back(2 * i + j, j)
            front(NT - 1, 1)
            exponent(NT - 2, 0)
            nope(NT - 1, 1)
            back(NT - 2, 0)
            exponent(NT - 1, 1)
            back(NT - 1, 1)

        @block.vector
        def _(dve):
            v = nc.vector

            def front(t, j):
                ch = Chain(dve, s["drop_chain"], 3 * t)
                dve.wait_ge(s["feat_ready"], freed(t))
                normalize(nc, c, xn[:, j, :], t).then_inc(s["xn_ready"], 1)
                ch.link(v.tensor_scalar(drop[:, j, :], c.iota, seg[:, bass.ds(t, 1)], None, ALU.is_le))
                ch.link(v.scalar_tensor_tensor(out=drop[:, j, :], in0=c.iota, scalar=seg_lo[:, bass.ds(t, 1)],
                                               in1=drop[:, j, :], op0=ALU.is_ge, op1=ALU.mult))
                ch.link(v.tensor_scalar(drop[:, j, :], drop[:, j, :], 1.0, -NEG, ALU.subtract, ALU.mult))

            def rope(t, j, n):
                if n == 0:
                    dve.wait_ge(s["q_ready"], ready(t))
                    dve.wait_ge(s["scores_ready"], freed(t))
                for m in (2 * n, 2 * n + 1):
                    hs = slice(4 * m, 4 * m + 4)
                    raw = bank(j, m)[:, :].rearrange("p (h n) -> p h n", h=4)
                    tab = lambda ap, a, b: ap[a:b, :].unsqueeze(1).broadcast_to([b - a, 4, P])
                    v.tensor_tensor(q[64:P, j, hs, :], raw[64:P], tab(c.cos, 64, P), ALU.mult)
                    v.tensor_tensor(rot[96:P, j, hs, :], raw[64:96], tab(c.sin, 64, 96), ALU.mult)
                    last = v.tensor_tensor(rot[64:96, j, hs, :], raw[96:P], tab(c.sin, 96, P), ALU.mult)
                last.then_inc(s["rope_done"], 1)

            def maxima(t, j):
                ch = Chain(dve, s["masked"], t)
                dve.wait_ge(s["scores_ready"], ready(t))
                dve.wait_ge(s["turned_ready"], freed(t))
                for n in range(2):
                    last = v.tensor_tensor(sc[:, j, 8 * n:8 * n + 8, :], bank(j, n)[:, :].rearrange("p (h n) -> p h n", h=8),
                                           drop[:, j, :].unsqueeze(1).broadcast_to([P, 8, S]), ALU.add)
                ch.link(last)
                v.tensor_reduce(mx[:, j, :], sc[:, j, :, :], AX.X, ALU.max).then_inc(s["max_ready"], 1)

            def sums(t, j):
                ch = Chain(dve, s["summed"], t)
                dve.wait_ge(s["exp_ready"], ready(t))
                ch.link(v.tensor_reduce(sm[:, j, :], sc[:, j, :, :], AX.X, ALU.add))
                v.reciprocal(sm[:, j, :], sm[:, j, :]).then_inc(s["sum_ready"], 1)

            def back(t, j):
                dve.wait_ge(s["out_ready"], ready(t))
                add_and_stats(nc, c, Chain(dve, s["add_chain"], 2 * t), t, bank(j, 2)[:, 0:D], 1.0, s["x_done"])

            def step(t, j):
                front(t + 1, 1 - j)
                maxima(t, j)
                rope(t + 1, 1 - j, 0)
                sums(t, j)
                rope(t + 1, 1 - j, 1)
                back(t, j)

            front(0, 0)
            rope(0, 0, 0)
            rope(0, 0, 1)
            with dve.Fori(0, NT // 2 - 1) as i:
                step(2 * i, 0)
                step(2 * i + 1, 1)
            step(NT - 2, 0)
            maxima(NT - 1, 1)
            sums(NT - 1, 1)
            back(NT - 1, 1)


FT2 = -(-HID2 // P)


def stage_l2_ternary(nc, c):
    with ExitStack() as ctx:
        sb = lambda n, sh, dt=F32: ctx.enter_context(nc.sbuf_tensor(n, sh, dt))
        HW = FT2 * P
        w12 = sb("w12", [P, DK, 2, HW], BF16); w3 = sb("w3q", [P, FT2, D], BF16)
        xn = sb("xn_t", [P, LANES, D]); xp = sb("xp", [P, LANES, 3, D], BF16); rest = sb("rest_t", [P, LANES, D])
        sig = sb("sig_t", [P, LANES, HW]); hp = sb("hp", [P, LANES, 3, HW], BF16)
        s = open_sems(nc, ctx, "q_loaded q_zero q_sums q_total q_chain xn_ready feat_ready part1_ready rest_ready "
                      "part2_ready xp_ready up_ready sig_ready h_ready hpart1_ready hrest_ready hpart2_ready hp_ready "
                      "down_ready x_done t2_chain")
        LINKS = 4
        with ExitStack() as pre:
            wt = lambda n, sh: pre.enter_context(nc.sbuf_tensor(n, sh, F32))
            raw12 = wt("raw12", [P, DK, 2, HW]); raw3 = wt("raw3", [P, FT2, D]); tmp = wt("tmp_q", [P, DK * 2 * HW])
            ab = wt("abs_sums", [P, 3]); ones = wt("ones_q", [P, P]); inv = wt("inv_q", [P, 3])
            block = pre.enter_context(nc.Block())

            @block.sync
            def _(sp):
                sp.wait_ge(s["q_zero"], 3)
                for n, name in enumerate(("t1", "t2")):
                    sp.dma_start(raw12[:, :, n, 0:HID2], c.d[name].rearrange("(k p) n -> p k n", p=P)).then_inc(s["q_loaded"], 16)
                full = HID2 // P
                sp.dma_start(raw3[:, 0:full, :], c.d["t3"][0:full * P, :].rearrange("(k p) n -> p k n", p=P)).then_inc(s["q_loaded"], 16)
                sp.dma_start(raw3[0:HID2 - full * P, full, :], c.d["t3"][full * P:HID2, :]).then_inc(s["q_loaded"], 16)

            @block.gpsimd
            def _(pool):
                nc.gpsimd.memset(raw12[:, :, :, HID2:HW], 0.0).then_inc(s["q_zero"], 1)
                nc.gpsimd.memset(raw3[:, FT2 - 1, :], 0.0).then_inc(s["q_zero"], 1)
                nc.gpsimd.memset(ones[:, :], 1.0).then_inc(s["q_zero"], 1)

            @block.tensor
            def _(pe):
                pe.wait_ge(s["q_zero"], 3)
                pe.wait_ge(s["q_sums"], 3)
                nc.tensor.matmul(c.bank[0][:, 0:3], ones[:, :], ab[:, :], start=True, stop=True).then_inc(s["q_total"], 1)

            @block.vector
            def _(dve):
                v = nc.vector
                ch = Chain(dve, s["q_chain"])
                dve.wait_ge(s["q_loaded"], 64)
                for n in range(2):
                    v.tensor_reduce(ab[:, n:n + 1], raw12[:, :, n, :], AX.XY, ALU.add,
                                    apply_absolute_value=True).then_inc(s["q_sums"], 1)
                v.tensor_reduce(ab[:, 2:3], raw3[:, :, :], AX.XY, ALU.add,
                                apply_absolute_value=True).then_inc(s["q_sums"], 1)
                dve.wait_ge(s["q_total"], 1)
                ch.link(v.tensor_scalar(inv[:, :], c.bank[0][:, 0:3], 1.0 / (HID2 * D), EPS2, ALU.mult, ALU.add))
                ch.link(v.reciprocal(inv[:, :], inv[:, :]))
                for n in range(3):
                    src = raw12[:, :, n, :] if n < 2 else raw3[:, :, :]
                    dst = w12[:, :, n, :] if n < 2 else w3[:, :, :]
                    a, b = (DK, HW) if n < 2 else (FT2, D)
                    t3 = tmp[:, 0:a * b].rearrange("p (a b) -> p a b", a=a)
                    ch.link(v.tensor_scalar(t3, src, inv[:, n:n + 1], -0.5, ALU.mult, ALU.is_lt))
                    ch.link(v.tensor_scalar(src, src, inv[:, n:n + 1], 0.5, ALU.mult, ALU.is_gt))
                    ch.link(v.tensor_tensor(dst, src, t3, ALU.subtract))

        block = ctx.enter_context(nc.Block())

        def up(j, n, f):
            at = n * FT2 + f
            return c.bank[4 * j + 1 + at // 4][:, (at % 4) * P:(at % 4 + 1) * P]

        def feat(j): return c.bank[4 * j]

        @block.gpsimd
        def _(pool):
            give_credit(pool, s, "xn_ready feat_ready part1_ready rest_ready part2_ready xp_ready up_ready sig_ready "
                        "h_ready hpart1_ready hrest_ready hpart2_ready hp_ready down_ready x_done")
            with pool.Fori(0, NT // LANES) as i:
                for j, t in token_loop(i):
                    pool.wait_ge(s["part2_ready"], ready(t))
                    nc.gpsimd.tensor_tensor(xp[:, j, 2, :], rest[:, j, :], xp[:, j, 1, :],
                                            ALU.subtract).then_inc(s["xp_ready"], 1)
                for j, t in token_loop(i):
                    pool.wait_ge(s["hpart2_ready"], ready(t))
                    nc.gpsimd.tensor_tensor(hp[:, j, 2, :], sig[:, j, :], hp[:, j, 1, :],
                                            ALU.subtract).then_inc(s["hp_ready"], 1)

        @block.tensor
        def _(pe):
            with pe.Fori(0, NT // LANES) as i:
                for j, t in token_loop(i):
                    pe.wait_ge(s["xn_ready"], ready(t))
                    pe.wait_ge(s["x_done"], freed(t))
                    transpose_tile(nc, c, feat(j), xn[:, j, :]).then_inc(s["feat_ready"], 1)
                for j, t in token_loop(i):
                    pe.wait_ge(s["xp_ready"], ready(t))
                    pe.wait_ge(s["h_ready"], freed(t))
                    for n in range(2):
                        for f in range(FT2):
                            for k in range(DK):
                                for part in range(3):
                                    last = nc.tensor.matmul(up(j, n, f), w12[:, k, n, f * P:(f + 1) * P],
                                                            xp[:, j, part, k * P:(k + 1) * P],
                                                            start=(k == 0 and part == 0), stop=(k == DK - 1 and part == 2))
                    last.then_inc(s["up_ready"], 1)
                for j, t in token_loop(i):
                    pe.wait_ge(s["hp_ready"], ready(t))
                    for part in range(3):
                        for f in range(FT2):
                            last = nc.tensor.matmul(feat(j)[:, 0:D], hp[:, j, part, f * P:(f + 1) * P], w3[:, f, :],
                                                    start=(part == 0 and f == 0), stop=(part == 2 and f == FT2 - 1))
                    last.then_inc(s["down_ready"], 1)

        @block.scalar
        def _(act):
            with act.Fori(0, NT // LANES) as i:
                for j, t in token_loop(i):
                    act.wait_ge(s["feat_ready"], ready(t))
                    act.wait_ge(s["up_ready"], freed(t))
                    act.copy(xp[:, j, 0, :], feat(j)[:, 0:D]).then_inc(s["part1_ready"], 1)
                for j, t in token_loop(i):
                    act.wait_ge(s["rest_ready"], ready(t))
                    act.copy(xp[:, j, 1, :], rest[:, j, :]).then_inc(s["part2_ready"], 1)
                for j, t in token_loop(i):
                    act.wait_ge(s["up_ready"], ready(t))
                    act.wait_ge(s["hp_ready"], freed(t))
                    nc.scalar.activation(sig[:, j, 0:4 * P], c.bank[4 * j + 1][:, :], ACT.Sigmoid)
                    nc.scalar.activation(sig[:, j, 4 * P:HW], c.bank[4 * j + 2][:, 0:(FT2 - 4) * P],
                                         ACT.Sigmoid).then_inc(s["sig_ready"], 1)
                for j, t in token_loop(i):
                    act.wait_ge(s["h_ready"], ready(t))
                    act.wait_ge(s["down_ready"], freed(t))
                    act.copy(hp[:, j, 0, :], sig[:, j, :]).then_inc(s["hpart1_ready"], 1)
                for j, t in token_loop(i):
                    act.wait_ge(s["hrest_ready"], ready(t))
                    act.copy(hp[:, j, 1, :], sig[:, j, :]).then_inc(s["hpart2_ready"], 1)

        @block.vector
        def _(dve):
            v = nc.vector
            with dve.Fori(0, NT // LANES) as i:
                ch = Chain(dve, s["t2_chain"], i * LINKS)
                for j, t in token_loop(i):
                    dve.wait_ge(s["feat_ready"], freed(t))
                    normalize(nc, c, xn[:, j, :], t).then_inc(s["xn_ready"], 1)
                for j, t in token_loop(i):
                    dve.wait_ge(s["part1_ready"], ready(t))
                    dve.wait_ge(s["xp_ready"], freed(t))
                    v.tensor_tensor(rest[:, j, :], feat(j)[:, 0:D], xp[:, j, 0, :], ALU.subtract).then_inc(s["rest_ready"], 1)
                for j, t in token_loop(i):
                    dve.wait_ge(s["sig_ready"], ready(t))
                    lo = (8 - FT2) * P
                    v.tensor_tensor(sig[:, j, 0:lo], c.bank[4 * j + 2][:, (FT2 - 4) * P:4 * P], sig[:, j, 0:lo], ALU.mult)
                    v.tensor_tensor(sig[:, j, lo:HW], c.bank[4 * j + 3][:, :], sig[:, j, lo:HW],
                                    ALU.mult).then_inc(s["h_ready"], 1)
                for j, t in token_loop(i):
                    dve.wait_ge(s["hpart1_ready"], ready(t))
                    v.tensor_tensor(sig[:, j, :], sig[:, j, :], hp[:, j, 0, :], ALU.subtract).then_inc(s["hrest_ready"], 1)
                for j, t in token_loop(i):
                    dve.wait_ge(s["down_ready"], ready(t))
                    add_and_stats(nc, c, ch, t, feat(j)[:, 0:D], 1.0, s["x_done"])
                assert ch.n == LINKS, ch.n


def upper(ap):
    return ap.bitcast(BF16)[:, 1::2]


def stage_l3_split(nc, c):
    with ExitStack() as ctx:
        sb = lambda n, sh, dt=F32: ctx.enter_context(nc.sbuf_tensor(n, sh, dt))
        L = 4
        src = sb("src_s", [P, L, 2 * D]); rest = sb("rest_s", [P, L, 2 * D])
        parts = sb("parts_s", [P, L, 3, 2 * D], BF16)
        ctx_loaded = [f"ctx_loaded{j}" for j in range(L)]
        stored = [f"stored{j}" for j in range(L)]
        s = open_sems(nc, ctx, "scaled xn_ready high_ready rest_ready mid_ready low_ready turned_ready turned_copied "
                      + " ".join(ctx_loaded + stored))
        block = ctx.enter_context(nc.Block())

        def done(t):
            return t + 1 + L

        def before(t):
            return t + 1

        def lanes(i):
            return [(j, i * L + j) for j in range(L)]

        @block.sync
        def _(sp):
            def load(t, j):
                sp.dma_start(src[:, j, D:2 * D], c.d["ctx"][bass.ds(t * P, P), :]).then_inc(s[ctx_loaded[j]], 16)

            def step(i, last=False):
                for j, t in lanes(i):
                    sp.wait_ge(s["mid_ready"], done(t))
                    sp.wait_ge(s["low_ready"], done(t))
                    if not last:
                        sp.wait_ge(s["turned_ready"], done(t))
                        load(t + L, j)
                    for n, dst in enumerate((c.q_parts, c.k_parts)):
                        for a in range(3):
                            sp.dma_start(dst[a, :, bass.ds(t * 2 * H3, 2 * H3), :].rearrange("c h l -> h c l"),
                                         parts[:, j, a, n * D:(n + 1) * D]).then_inc(s[stored[j]], 16)

            for j in range(L):
                load(j, j)
            with sp.Fori(0, NT // L - 1) as i:
                step(i)
            step(NT // L - 1, last=True)
            for j in range(L):
                sp.wait_ge(s[stored[j]], 96 * (NT // L) + 96)

        @block.gpsimd
        def _(pool):
            for name in ("xn_ready", "high_ready", "rest_ready", "mid_ready", "low_ready", "turned_ready", "turned_copied"):
                pool.sem_inc(s[name], L)
            for name in stored:
                pool.sem_inc(s[name], 96)
            with pool.Fori(0, NT // L) as i:
                for j, t in lanes(i):
                    pool.wait_ge(s["rest_ready"], done(t))
                    pool.wait_ge(s[stored[j]], 96 * i + 96)
                    nc.gpsimd.tensor_tensor(parts[:, j, 2, :], rest[:, j, :], upper(rest[:, j, :]),
                                            ALU.subtract).then_inc(s["low_ready"], 1)

        @block.tensor
        def _(pe):
            with pe.Fori(0, NT // L) as i:
                for j, t in lanes(i):
                    pe.wait_ge(s[ctx_loaded[j]], loaded(i))
                    pe.wait_ge(s["turned_copied"], before(t))
                    transpose_tile(nc, c, c.bank[j], src[:, j, D:2 * D]).then_inc(s["turned_ready"], 1)

        @block.scalar
        def _(act):
            with act.Fori(0, NT // L) as i:
                for j, t in lanes(i):
                    act.wait_ge(s["turned_ready"], done(t))
                    act.copy(c.vT[:, :, bass.ds(t * P, P)], half(c.bank[j][:, 0:D])).then_inc(s["turned_copied"], 1)
                    act.wait_ge(s["xn_ready"], done(t))
                    act.wait_ge(s[ctx_loaded[j]], loaded(i))
                    act.wait_ge(s[stored[j]], 96 * i + 96)
                    act.copy(parts[:, j, 0, :], upper(src[:, j, :])).then_inc(s["high_ready"], 1)
                for j, t in lanes(i):
                    act.wait_ge(s["rest_ready"], done(t))
                    act.copy(parts[:, j, 1, :], upper(rest[:, j, :])).then_inc(s["mid_ready"], 1)

        @block.vector
        def _(dve):
            v = nc.vector
            v.tensor_scalar(c.rstd[:, :], c.rstd[:, :], float(np.float32(DQ3) ** np.float32(-0.5)), None,
                            ALU.mult).then_inc(s["scaled"], 1)
            dve.wait_ge(s["scaled"], 1)
            with dve.Fori(0, NT // L) as i:
                for j, t in lanes(i):
                    dve.wait_ge(s["high_ready"], before(t))
                    dve.wait_ge(s["rest_ready"], before(t))
                    normalize(nc, c, src[:, j, 0:D], t).then_inc(s["xn_ready"], 1)
                for j, t in lanes(i):
                    dve.wait_ge(s["xn_ready"], done(t))
                    dve.wait_ge(s[ctx_loaded[j]], loaded(i))
                    dve.wait_ge(s["mid_ready"], before(t))
                    dve.wait_ge(s["low_ready"], before(t))
                    v.tensor_tensor(rest[:, j, :], src[:, j, :], upper(src[:, j, :]),
                                    ALU.subtract).then_inc(s["rest_ready"], 1)


def stage_l3_attention(nc, c):
    with ExitStack() as ctx:
        sb = lambda n, sh, dt=F32: ctx.enter_context(nc.sbuf_tensor(n, sh, dt))
        R = 9 * DQ3
        AH = DQ3 + 1
        BUF = 4
        LEAD = 2
        LAG = 4
        NS, NT_, NE = 2, 2, 8
        UC = NE
        q = sb("q_3", [R + 2, BUF, H3 * D], BF16); k = sb("k_3", [R + 2, BUF, H3 * D], BF16)
        val = sb("val_3", [P, BUF, DK, H3, 3, AH], BF16); vrest = sb("vrest_3", [P, 2, DK, H3, DQ3])
        nmax = sb("nmax_3", [P, BUF, 2 * H3])
        rows = sb("rows_3", [2 * H3, BUF, 2, P], BF16)
        eT = sb("eT_3", [P, NE, DK, D]); rest = sb("rest_3", [P, NE, DK, D]); low = sb("low_3", [P, NE, DK, D], BF16)
        total = sb("total_r3", [P, 2, 2 * H3, AH])
        rec = sb("rec_3", [P, 2, 2 * H3]); on = sb("on_3", [P, 2, 2, S]); gam = sb("gam_3", [P, 1])
        qk_loaded = [f"qk_loaded{b}" for b in range(BUF)]
        rows_loaded = [f"rows_loaded{b}" for b in range(BUF)]
        s = open_sems(nc, ctx, "gamma_loaded ones_set val_ready scores_ready max_ready max_turned max_split turned_ready "
                      "exp_ready rest_ready low_ready val_rest val_low used_ready batch_read tile_turned x_done split_chain norm_chain add_chain " + " ".join(qk_loaded + rows_loaded))
        block = ctx.enter_context(nc.Block())
        scores = lambda h: c.bank[h % NS]
        scoresT = lambda h: c.bank[NS + h % NT_]
        readout = lambda b: c.bank[NS + NT_ + b % 2][:, 0:2 * H3 * 3 * AH]
        final = c.bank[6][:, 0:D]
        max_rows = c.bank[7][0:2 * H3, 0:P]

        def unit_ready(g, b, h):
            return (g * BUF + b) * H3 + h + 1 + UC

        def batch_ready(g, b):
            return ready(g * BUF + b)

        def at(g, b, ahead=0):
            return g + (b + ahead) // BUF, (b + ahead) % BUF

        def exists(g, b, ahead=0):
            return not isinstance(g, int) or 0 <= g * BUF + b + ahead < B

        def run(eng, batch):
            for b in range(BUF):
                batch(0, b)
            with eng.Fori(1, B // BUF - 1) as g:
                for b in range(BUF):
                    batch(g, b)
            for b in range(BUF):
                batch(B // BUF - 1, b)

        @block.sync
        def _(sp):
            sp.dma_start(gam[:, :], c.d["gamma3"].broadcast_to([P, 1])).then_inc(s["gamma_loaded"], 16)
            sp.wait_ge(s["ones_set"], 3)

            def load(g, b):
                cols = bass.ds((g * BUF + b) * H3, H3)
                k_rows = c.k_parts[:, :, cols, :].rearrange("a c h l -> (a c) (h l)")
                for i in range(3):
                    part = slice(3 * DQ3 * i, 3 * DQ3 * (i + 1))
                    q_rows = c.q_parts[i, :, cols, :].rearrange("c h l -> c (h l)").unsqueeze(0)
                    sp.dma_start(q[part, b, :], q_rows.broadcast_to([3, DQ3, H3 * D])).then_inc(s[qk_loaded[b]], 16)
                    sp.dma_start(k[part, b, :], k_rows).then_inc(s[qk_loaded[b]], 16)

            def lay_rows(g, b):
                sp.wait_ge(s["max_split"], batch_ready(g, b))
                for a in range(2):
                    sp.dma_start(q[R + a:R + a + 1, b, :], rows[:, b, a, :]).then_inc(s[rows_loaded[b]], 16)

            def batch(g, b):
                if exists(g, b, 3):
                    if exists(g, b, -1):
                        sp.wait_ge(s["turned_ready"], unit_ready(*at(g, b, -1), H3 - 1))
                    load(*at(g, b, 3))
                if exists(g, b, 1):
                    lay_rows(*at(g, b, 1))

            for b in range(3):
                load(0, b)
            lay_rows(0, 0)
            run(sp, batch)

        @block.gpsimd
        def _(pool):
            nc.gpsimd.memset(val[:, :, :, :, :, :], 0.0).then_inc(s["ones_set"], 1)
            pool.wait_ge(s["ones_set"], 1)
            nc.gpsimd.memset(val[:, :, :, :, 0, DQ3:AH], 1.0).then_inc(s["ones_set"], 1)
            pool.wait_ge(s["ones_set"], 2)
            nc.gpsimd.memset(k[64:R + 2, :, :], 1.0).then_inc(s["ones_set"], 1)
            pool.wait_ge(s["ones_set"], 3)
            give_credit(pool, s, "val_ready max_turned max_split batch_read tile_turned x_done")
            for name in ("scores_ready", "max_ready", "turned_ready", "exp_ready", "rest_ready", "low_ready", "used_ready"):
                pool.sem_inc(s[name], UC)

            def values(g, b):
                if exists(g, b, -BUF):
                    pool.wait_ge(s["used_ready"], unit_ready(g - 1, b, H3 - 1))
                n = g * BUF + b
                for lt in range(DK):
                    src = c.vT[:, lt, bass.ds(n * S, S)]
                    hi = upper(src).rearrange("p (h c) -> p h c", h=H3)
                    nc.gpsimd.tensor_tensor(vrest[:, b % 2, lt, :, :], src.rearrange("p (h c) -> p h c", h=H3),
                                            hi, ALU.subtract)
                    last = nc.gpsimd.tensor_copy(val[:, b, lt, :, 0, 0:DQ3], hi)
                last.then_inc(s["val_rest"], 1)
                pool.wait_ge(s["val_rest"], n + 1)
                rest_all = vrest[:, b % 2, :, :, :].rearrange("p k h c -> p (k h c)")
                hi = upper(rest_all).rearrange("p (n c) -> p n c", c=DQ3)
                flat = val[:, b, :, :, :, :].rearrange("p k h n a -> p (k h) n a")
                nc.gpsimd.tensor_tensor(flat[:, :, 2, 0:DQ3], rest_all.rearrange("p (n c) -> p n c", c=DQ3), hi,
                                        ALU.subtract)
                nc.gpsimd.tensor_copy(flat[:, :, 1, 0:DQ3], hi).then_inc(s["val_ready"], 1)

            def batch(g, b):
                for h in range(H3):
                    pool.wait_ge(s["rest_ready"], unit_ready(g, b, h))
                    r2 = rest[:, h, :, :].rearrange("p k n -> p (k n)")
                    nc.gpsimd.tensor_tensor(low[:, h, :, :].rearrange("p k n -> p (k n)"), r2, upper(r2),
                                            ALU.subtract).then_inc(s["low_ready"], 1)
                    if h == 3 and exists(g, b, 1):
                        values(*at(g, b, 1))

            values(0, 0)
            run(pool, batch)

        @block.tensor
        def _(pe):
            def score(g, b, h):
                if h == 0:
                    pe.wait_ge(s[qk_loaded[b]], 96 * g + 96)
                pe.wait_ge(s["max_ready"], unit_ready(g, b, h) - NS)
                for qt in range(2):
                    last = nc.tensor.matmul(scores(h)[:, qt * D:(qt + 1) * D],
                                            q[0:R, b, h * D + qt * P:h * D + qt * P + P],
                                            k[0:R, b, h * D:(h + 1) * D], start=True, stop=True)
                last.then_inc(s["scores_ready"], 1)

            def turn_max(g, b):
                pe.wait_ge(s["max_ready"], unit_ready(g, b, H3 - 1))
                pe.wait_ge(s["max_split"], batch_ready(g, b) - 1)
                nc.tensor.transpose(max_rows, nmax[:, b, :], c.ident).then_inc(s["max_turned"], 1)

            def score_turned(g, b, h):
                if h == 0:
                    pe.wait_ge(s[rows_loaded[b]], 32 * g + 32)
                pe.wait_ge(s["exp_ready"], unit_ready(g, b, h) - NT_)
                for lt in range(DK):
                    last = nc.tensor.matmul(scoresT(h)[:, lt * D:(lt + 1) * D],
                                            k[:, b, h * D + lt * P:h * D + lt * P + P],
                                            q[:, b, h * D:(h + 1) * D], start=True, stop=True)
                last.then_inc(s["turned_ready"], 1)

            def read(g, b, h):
                pe.wait_ge(s["low_ready"], unit_ready(g, b, h))
                if h == 0:
                    pe.wait_ge(s["val_ready"], batch_ready(g, b))
                    pe.wait_ge(s["batch_read"], batch_ready(g, b) - 2)
                for qt in range(2):
                    out = readout(b)[:, (qt * H3 + h) * 3 * AH:(qt * H3 + h + 1) * 3 * AH]
                    for n, part in enumerate((lambda ap: upper(ap), lambda ap: upper(ap), lambda ap: ap)):
                        src = (eT, rest, low)[n]
                        for lt in range(DK):
                            last = nc.tensor.matmul(out, part(src[:, h % NE, lt, qt * P:(qt + 1) * P]),
                                                    val[:, b, lt, h, :, :].rearrange("p n a -> p (n a)"),
                                                    start=(n == 0 and lt == 0), stop=(n == 2 and lt == DK - 1))
                last.then_inc(s["used_ready"], 1)

            def finish(g, b):
                pe.wait_ge(s["batch_read"], batch_ready(g, b))
                pe.wait_ge(s["x_done"], ready(2 * g + b // 2) - 1)
                for qt in range(2):
                    last = nc.tensor.transpose(final[:, qt * P:(qt + 1) * P],
                                               on[:, qt, :, :].rearrange("p b n -> p (b n)"), c.ident)
                last.then_inc(s["tile_turned"], 1)

            def batch(g, b):
                for h in range(H3):
                    if exists(g, b, LEAD):
                        score(*at(g, b, LEAD), h)
                    if h == 1 and exists(g, b, 1):
                        turn_max(*at(g, b, 1))
                    score_turned(g, b, h)
                    if h >= LAG:
                        read(g, b, h - LAG)
                    elif exists(g, b, -1):
                        read(*at(g, b, -1), H3 + h - LAG)
                    if h == 7 and b % 2 == 0 and exists(g, b, -1):
                        finish(*at(g, b, -1))

            for h in range(H3):
                score(0, 0, h)
            turn_max(0, 0)
            for h in range(H3):
                score(0, 1, h)
            run(pe, batch)
            for h in range(H3 - LAG, H3):
                read(B // BUF - 1, BUF - 1, h)
            finish(B // BUF - 1, BUF - 1)

        @block.scalar
        def _(act):
            def batch(g, b):
                for h in range(H3):
                    act.wait_ge(s["turned_ready"], unit_ready(g, b, h))
                    act.wait_ge(s["used_ready"], unit_ready(g, b, h) - NE)
                    nc.scalar.activation(eT[:, h % NE, :, :].rearrange("p k n -> p (k n)"), scoresT(h)[:, :],
                                         ACT.Exp).then_inc(s["exp_ready"], 1)

            run(act, batch)

        @block.vector
        def _(dve):
            v = nc.vector

            def maxima(g, b, h):
                dve.wait_ge(s["scores_ready"], unit_ready(g, b, h))
                v.tensor_reduce(nmax[:, b, 2 * h:2 * h + 2], scores(h)[:, :].rearrange("p (a n) -> p a n", a=2), AX.X,
                                ALU.max, negate=True).then_inc(s["max_ready"], 1)

            def split_max(g, b):
                ch = Chain(dve, s["split_chain"], g * BUF + b)
                dve.wait_ge(s["max_turned"], batch_ready(g, b))
                ch.link(v.tensor_scalar(rows[:, b, 0, :], max_rows, 1.0, None, ALU.mult))
                v.tensor_tensor(rows[:, b, 1, :], max_rows, rows[:, b, 0, :], ALU.subtract).then_inc(s["max_split"], 1)

            def normalized(g, b):
                ch = Chain(dve, s["norm_chain"], (g * BUF + b) * 3)
                dve.wait_ge(s["used_ready"], unit_ready(g, b, H3 - 1))
                if b % 2 == 0:
                    dve.wait_ge(s["tile_turned"], ready(2 * g + b // 2) - 1)
                r3 = total[:, b % 2, :, :]
                ch.link(v.tensor_reduce(r3, readout(b).rearrange("p (n i a) -> p n a i", i=3, a=AH), AX.X, ALU.add))
                ch.link(v.reciprocal(rec[:, b % 2, :], r3[:, :, DQ3]))
                ch.link(v.tensor_scalar(rec[:, b % 2, :], rec[:, b % 2, :], gam[:, 0:1], None, ALU.mult))
                for qt in range(2):
                    last = v.tensor_tensor(on[:, qt, b % 2, :].rearrange("p (h c) -> p h c", h=H3),
                                           r3[:, qt * H3:(qt + 1) * H3, 0:DQ3],
                                           rec[:, b % 2, qt * H3:(qt + 1) * H3].unsqueeze(2).broadcast_to([P, H3, DQ3]), ALU.mult)
                last.then_inc(s["batch_read"], 1)

            def finish(g, b):
                t = 2 * g + b // 2
                dve.wait_ge(s["tile_turned"], ready(t))
                add_and_stats(nc, c, Chain(dve, s["add_chain"], 2 * t), t, final, 1.0, s["x_done"])

            def remainder(g, b, h):
                dve.wait_ge(s["exp_ready"], unit_ready(g, b, h))
                e2 = eT[:, h, :, :].rearrange("p k n -> p (k n)")
                v.tensor_tensor(rest[:, h, :, :].rearrange("p k n -> p (k n)"), e2, upper(e2),
                                ALU.subtract).then_inc(s["rest_ready"], 1)

            def batch(g, b):
                for h in range(H3):
                    if exists(g, b, LEAD):
                        maxima(*at(g, b, LEAD), h)
                    if h > 0:
                        remainder(g, b, h - 1)
                    elif exists(g, b, -1):
                        remainder(*at(g, b, -1), H3 - 1)
                    if h == 2 and exists(g, b, 1):
                        split_max(*at(g, b, 1))
                    if h == 5 and exists(g, b, -1):
                        normalized(*at(g, b, -1))
                    if h == 1 and b % 2 == 1 and exists(g, b, -2):
                        finish(*at(g, b, -2))

            dve.wait_ge(s["gamma_loaded"], 16)
            for h in range(H3):
                maxima(0, 0, h)
            split_max(0, 0)
            for h in range(H3):
                maxima(0, 1, h)
            run(dve, batch)
            remainder(B // BUF - 1, BUF - 1, H3 - 1)
            normalized(B // BUF - 1, BUF - 1)
            finish(B // BUF - 1, BUF - 1)


def stage_l3_gate(nc, c):
    with ExitStack() as ctx:
        sb = lambda n, sh, dt=F32: ctx.enter_context(nc.sbuf_tensor(n, sh, dt))
        wg = sb("wg_3", [P, DK, E3]); xn = sb("xn_g3", [P, LANES, D]); xT = sb("xT_g3", [P, LANES, D])
        s = open_sems(nc, ctx, "g3_loaded xn_ready feat_ready feat_copied logit_ready logit_copied")
        block = ctx.enter_context(nc.Block())

        @block.sync
        def _(sp):
            sp.dma_start(wg[:, :, :], c.d["g3w"].rearrange("(k p) n -> p k n", p=P)).then_inc(s["g3_loaded"], 16)

        @block.gpsimd
        def _(pool):
            give_credit(pool, s, "xn_ready feat_ready feat_copied logit_ready logit_copied")

        @block.tensor
        def _(pe):
            pe.wait_ge(s["g3_loaded"], 16)
            with pe.Fori(0, NT // LANES) as i:
                for j, t in token_loop(i):
                    pe.wait_ge(s["xn_ready"], ready(t))
                    pe.wait_ge(s["feat_copied"], freed(t))
                    transpose_tile(nc, c, c.bank[j], xn[:, j, :]).then_inc(s["feat_ready"], 1)
                for j, t in token_loop(i):
                    pe.wait_ge(s["feat_copied"], ready(t))
                    pe.wait_ge(s["logit_copied"], freed(t))
                    for k in range(DK):
                        last = nc.tensor.matmul(c.bank[2 + j][:, 0:E3], xT[:, j, k * P:(k + 1) * P], wg[:, k, :],
                                                start=(k == 0), stop=(k == DK - 1))
                    last.then_inc(s["logit_ready"], 1)

        @block.scalar
        def _(act):
            with act.Fori(0, NT // LANES) as i:
                for j, t in token_loop(i):
                    act.wait_ge(s["logit_ready"], ready(t))
                    nc.scalar.activation(at_tile(c.score3, t), c.bank[2 + j][:, 0:E3],
                                         ACT.Sigmoid).then_inc(s["logit_copied"], 1)

        @block.vector
        def _(dve):
            with dve.Fori(0, NT // LANES) as i:
                for j, t in token_loop(i):
                    dve.wait_ge(s["feat_ready"], freed(t))
                    normalize(nc, c, xn[:, j, :], t).then_inc(s["xn_ready"], 1)
                for j, t in token_loop(i):
                    dve.wait_ge(s["feat_ready"], ready(t))
                    dve.wait_ge(s["logit_ready"], freed(t))
                    nc.vector.tensor_copy(xT[:, j, :], c.bank[j][:, 0:D]).then_inc(s["feat_copied"], 1)


def stage_l3_route(nc, c):
    with ExitStack() as ctx:
        sb = lambda n, sh, dt=F32: ctx.enter_context(nc.sbuf_tensor(n, sh, dt))
        pad = 8 - TOP3
        cand = sb("cand_3", [P, NT, E3 + pad]); left = sb("left_3", [P, NT, E3 + pad]); top = sb("top_3", [P, NT, 8])
        total = sb("total_3", [P, NT])
        s = open_sems(nc, ctx, "r3_chain")
        block = ctx.enter_context(nc.Block())

        @block.vector
        def _(dve):
            ch = Chain(dve, s["r3_chain"])
            v = nc.vector
            v.memset(cand[:, :, E3:E3 + pad], BIG)
            ch.link(v.tensor_copy(cand[:, :, 0:E3], c.score3[:, :, :]))
            for t in range(NT):
                last = v.max(top[:, t, :], cand[:, t, 0:E3])
            ch.link(last)
            ch.link(v.memset(top[:, :, TOP3:8], BIG))
            for t in range(NT):
                last = v.match_replace(out=left[:, t, :], in_to_replace=top[:, t, :], in_values=cand[:, t, :],
                                       imm_value=-BIG)
            ch.link(last)
            ch.link(v.tensor_tensor(left[:, :, 0:E3], left[:, :, 0:E3], cand[:, :, 0:E3], ALU.not_equal))
            ch.link(v.tensor_tensor(left[:, :, 0:E3], left[:, :, 0:E3], cand[:, :, 0:E3], ALU.mult))
            ch.link(v.tensor_reduce(total[:, :], left[:, :, 0:E3], AX.X, ALU.add))
            ch.link(v.tensor_scalar(total[:, :], total[:, :], 1e-20, None, ALU.add))
            ch.link(v.reciprocal(total[:, :], total[:, :]))
            comb = c.comb[:, :].rearrange("p (t e) -> p t e", e=E3 + 1)
            v.memset(comb[:, :, E3:E3 + 1], 1.0)
            ch.link(v.scalar_tensor_tensor(out=comb[:, :, 0:E3], in0=left[:, :, 0:E3], scalar=SCALE3,
                                           in1=total[:, :].unsqueeze(2).broadcast_to([P, NT, E3]),
                                           op0=ALU.mult, op1=ALU.mult))


def stage_l3_experts(nc, c):
    with ExitStack() as ctx:
        sb = lambda n, sh, dt=F32: ctx.enter_context(nc.sbuf_tensor(n, sh, dt))
        U = E3 + 1
        HW = U * HID3
        CH = -(-HW // P)
        NA, NB, NG = 3, 2, 4
        groups = [range(0, 4), range(4, 7), range(7, 10), range(10, CH)]
        w13 = sb("w13_3", [P, DK, U * 2 * HID3]); w2 = sb("w2_3", [P, CH, D])
        xn = sb("xn_3", [P, D]); xT = sb("xT_3", [P, 2, D]); sig = sb("sig_3", [P, NA, HID3])
        hid = sb("hid_3", [P, 2, HW]); hT = sb("hT_3", [P, CH, P])
        s = open_sems(nc, ctx, "w_loaded xn_ready feat_ready xT_ready hid_ready sig_ready prod_ready turned_ready "
                      "hT_ready down_ready x_done e3_chain")
        LINKS = U
        block = ctx.enter_context(nc.Block())
        feat = c.bank[0][:, 0:D]
        gates = lambda e: c.bank[1 + e % NA]
        turned = lambda g: c.bank[1 + NA + g % NB]
        out = lambda j: c.bank[1 + NA + NB + j][:, 0:D]
        width = lambda ch: min(P, HW - ch * P)

        def unit_ready(t, e):
            return t * U + e + 1 + NA

        def group_ready(t, g):
            return t * NG + g + 1 + NG

        @block.sync
        def _(sp):
            loads = []
            for k in range(DK):
                rows = slice(k * P, (k + 1) * P)
                view = w13[:, k, :].rearrange("p (e n) -> p e n", e=U)
                for n, (routed, shared) in enumerate((("e3w1", "s3w1"), ("e3w3", "s3w3"))):
                    cols = slice(n * HID3, (n + 1) * HID3)
                    loads.append((view[:, 0:E3, cols], c.d[routed][:, rows, :].rearrange("e p n -> p e n")))
                    loads.append((view[:, E3, cols], c.d[shared][rows, :]))
            full = E3 * HID3 // P
            loads.append((w2[:, 0:full, :], c.d["e3w2"].rearrange("e h n -> (e h) n").rearrange("(c p) n -> p c n", p=P)))
            loads.append((w2[:, full, :], c.d["s3w2"][0:P, :]))
            loads.append((w2[0:HID3 - P, full + 1, :], c.d["s3w2"][P:HID3, :]))
            assert len(loads) == 11
            for dst, src in loads:
                sp.dma_start(dst, src).then_inc(s["w_loaded"], 16)

        @block.gpsimd
        def _(pool):
            for names, credit in (("hid_ready sig_ready prod_ready", NA), ("turned_ready hT_ready down_ready", NG),
                                  ("xn_ready feat_ready xT_ready x_done", CREDIT)):
                for n in names.split():
                    pool.sem_inc(s[n], credit)

        def schedule(first, last, hidden, hidden_turn, down, features):
            for e in range(U):
                hidden(0, e)
                if not first and e in (0, 1):
                    hidden_turn(-1, 2 + e)
                if e == 3:
                    hidden_turn(0, 0)
                if e == 7:
                    hidden_turn(0, 1)
                if not first and e in (2, 3):
                    down(-1, e)
                if e == 5:
                    down(0, 0)
                if e == 8:
                    down(0, 1)
                if e == 6 and not last:
                    features(1)
            if last:
                for g in (2, 3):
                    hidden_turn(0, g)
                for g in (2, 3):
                    down(0, g)

        @block.tensor
        def _(pe):
            def features(t):
                pe.wait_ge(s["xn_ready"], ready(t))
                transpose_tile(nc, c, feat, xn[:, :]).then_inc(s["feat_ready"], 1)

            def tile(t, j, first=False, last=False):
                def hidden(dt, e):
                    if e == 0:
                        pe.wait_ge(s["xT_ready"], ready(t))
                    pe.wait_ge(s["prod_ready"], unit_ready(t, e) - NA)
                    for k in range(DK):
                        op = nc.tensor.matmul(gates(e)[:, 0:2 * HID3], xT[:, j, k * P:(k + 1) * P],
                                              w13[:, k, e * 2 * HID3:(e + 1) * 2 * HID3], start=(k == 0), stop=(k == DK - 1))
                    op.then_inc(s["hid_ready"], 1)

                def turn(dt, g):
                    upto = groups[g][-1] * P + width(groups[g][-1])
                    pe.wait_ge(s["prod_ready"], unit_ready(t + dt, (upto - 1) // HID3))
                    pe.wait_ge(s["hT_ready"], group_ready(t + dt, g) - NB)
                    for n, ck in enumerate(groups[g]):
                        w = width(ck)
                        op = nc.tensor.transpose(turned(g)[0:w, n * P:(n + 1) * P],
                                                 hid[:, (j + dt) % 2, ck * P:ck * P + w], c.ident)
                    op.then_inc(s["turned_ready"], 1)

                def down(dt, g):
                    pe.wait_ge(s["hT_ready"], group_ready(t + dt, g))
                    if g == 0:
                        pe.wait_ge(s["x_done"], freed(t))
                    for ck in groups[g]:
                        w = width(ck)
                        op = nc.tensor.matmul(out((j + dt) % 2), hT[0:w, ck, :], w2[0:w, ck, :],
                                              start=(ck == 0), stop=(ck == CH - 1))
                    op.then_inc(s["down_ready"], 1)

                schedule(first, last, hidden, turn, down, lambda dt: features(t + dt))

            pe.wait_ge(s["w_loaded"], 176)
            features(0)
            tile(0, 0, first=True)
            with pe.Fori(0, (NT - 2) // 2) as i:
                tile(2 * i + 1, 1)
                tile(2 * i + 2, 0)
            tile(NT - 1, 1, last=True)

        @block.scalar
        def _(act):
            def features(t, j):
                act.wait_ge(s["feat_ready"], ready(t))
                act.copy(xT[:, j, :], feat).then_inc(s["xT_ready"], 1)

            def tile(t, j, first=False, last=False):
                def hidden(dt, e):
                    act.wait_ge(s["hid_ready"], unit_ready(t, e))
                    act.wait_ge(s["prod_ready"], unit_ready(t, e) - NA)
                    nc.scalar.activation(sig[:, e % NA, :], gates(e)[:, 0:HID3], ACT.Sigmoid).then_inc(s["sig_ready"], 1)

                def copy(dt, g):
                    act.wait_ge(s["turned_ready"], group_ready(t + dt, g))
                    act.wait_ge(s["down_ready"], group_ready(t + dt, g) - NG)
                    n, at = len(groups[g]), groups[g][0]
                    full = n if width(at + n - 1) == P else n - 1
                    op = act.copy(hT[:, at:at + full, :].rearrange("p c n -> p (c n)"), turned(g)[:, 0:full * P])
                    if full < n:
                        w = width(at + n - 1)
                        op = act.copy(hT[0:w, at + full, :], turned(g)[0:w, full * P:n * P])
                    op.then_inc(s["hT_ready"], 1)

                schedule(first, last, hidden, copy, lambda dt, g: None, lambda dt: features(t + dt, (j + dt) % 2))

            features(0, 0)
            tile(0, 0, first=True)
            with act.Fori(0, (NT - 2) // 2) as i:
                tile(2 * i + 1, 1)
                tile(2 * i + 2, 0)
            tile(NT - 1, 1, last=True)

        @block.vector
        def _(dve):
            v = nc.vector

            def features(t):
                dve.wait_ge(s["feat_ready"], t + CREDIT)
                normalize(nc, c, xn[:, :], t).then_inc(s["xn_ready"], 1)

            def add(t, j):
                dve.wait_ge(s["down_ready"], group_ready(t, NG - 1))
                v.tensor_tensor(at_tile(c.x, t), out(j), at_tile(c.x, t), ALU.add).then_inc(s["x_done"], 1)

            def tile(t, j, first=False, last=False):
                ch = Chain(dve, s["e3_chain"], t * LINKS)
                for e in range(U):
                    dve.wait_ge(s["sig_ready"], unit_ready(t, e))
                    ch.link(v.tensor_tensor(sig[:, e % NA, :], gates(e)[:, 0:HID3], sig[:, e % NA, :], ALU.mult))
                    v.scalar_tensor_tensor(out=hid[:, j, e * HID3:(e + 1) * HID3], in0=gates(e)[:, HID3:2 * HID3],
                                           scalar=c.comb[:, bass.ds(t * U + e, 1)], in1=sig[:, e % NA, :],
                                           op0=ALU.mult, op1=ALU.mult).then_inc(s["prod_ready"], 1)
                    if e == 3 and not last:
                        features(t + 1)
                    if e == 5 and not first:
                        add(t - 1, 1 - j)
                if last:
                    add(t, j)
                assert ch.n == LINKS, ch.n

            features(0)
            tile(0, 0, first=True)
            with dve.Fori(0, (NT - 2) // 2) as i:
                tile(2 * i + 1, 1)
                tile(2 * i + 2, 0)
            tile(NT - 1, 1, last=True)


def layers(nc, c):
    with ExitStack() as keys:
        c.keysT = keys.enter_context(nc.sbuf_tensor("keysT", [P, N], F32))
        c.kvc = keys.enter_context(nc.sbuf_tensor("kvc", [P, NT, KVC], F32))
        with ExitStack() as kv:
            res = lambda n, sh, dt=F32: kv.enter_context(nc.sbuf_tensor(n, sh, dt))
            c.v = res("v_all", [P, NT, D])
            c.gramT = res("gramT", [P, H1, N])
            finish_stats(nc, c, "st0")
            stage_l0_attention(nc, c)
            finish_stats(nc, c, "st1")
            with ExitStack() as moe:
                l0 = lambda n, sh, dt=F32: moe.enter_context(nc.sbuf_tensor(n, sh, dt))
                c.score0 = l0("score0", [P, NT, E0]); c.row_col = l0("row_col", [P, 1])
                c.slot_token = l0("slot_token", [CAP0, E0], I32); c.slot_weight = l0("slot_weight", [CAP0, E0])
                c.place = l0("place", [P, NT, E0], BF16)
                stage_l0_shared(nc, c)
                with ExitStack() as sl:
                    c.slot_cols = sl.enter_context(nc.sbuf_tensor("slot_cols", [P, NT, E0, 6], BF16))
                    stage_l0_route(nc, c)
                    stage_l0_slots(nc, c)
                stage_l0_experts(nc, c)
            stage_add_experts(nc, c)
            c.gate1 = res("gate1", [P, NT, D])
            c.mixT = res("mixT", [P, H1, P])
            finish_stats(nc, c, "st2")
            stage_l1_scores(nc, c)
            stage_l1_mix(nc, c)
        finish_stats(nc, c, "st3")
        stage_l1_think(nc, c)
        stage_l1_broadcast(nc, c)
        recycle(nc)
        finish_stats(nc, c, "st4")
        stage_l2_attention(nc, c)
    finish_stats(nc, c, "st5")
    stage_l2_ternary(nc, c)
    recycle(nc)
    finish_stats(nc, c, "st6")
    with ExitStack() as l3:
        c.vT = l3.enter_context(nc.sbuf_tensor("vT", [P, DK, N], F32))
        stage_l3_split(nc, c)
        stage_l3_attention(nc, c)
    finish_stats(nc, c, "st7")
    with ExitStack() as moe:
        l3 = lambda n, sh, dt=F32: moe.enter_context(nc.sbuf_tensor(n, sh, dt))
        c.score3 = l3("score3", [P, NT, E3]); c.comb = l3("comb", [P, NT * (E3 + 1)])
        stage_l3_gate(nc, c)
        stage_l3_route(nc, c)
        stage_l3_experts(nc, c)



def build_program(nc, d):
    c = Core()
    HELD.clear()
    OPENED.clear()
    c.d = d
    with ExitStack() as ctx:
        sb = lambda n, sh, dt=F32: ctx.enter_context(nc.sbuf_tensor(n, sh, dt))
        c.bank = [ctx.enter_context(nc.psum_tensor(f"bank{k}", [P, 512], F32)) for k in range(8)]
        c.x = sb("x_all", [P, NT, D])
        c.bn = sb("bn_all", [P, NT, 6])
        c.mean = sb("mean_all", [P, NT])
        c.rstd = sb("rstd_all", [P, NT])
        c.small = sb("small", [P, 5, NT])
        c.minus_half = sb("minus_half", [P, NT])
        c.const = sb("const_sb", [P, CONST_W])
        part = lambda n: c.const[:, CONSTS[n][0]:CONSTS[n][1]]
        c.ident, c.cos, c.sin, c.before, c.iota = (part(n) for n in ("ident", "cos", "sin", "before", "iota"))
        c.moe = nc.dram_tensor("moe_rows", (NX, D), F32, kind="Internal").ap()
        c.think_rows = nc.dram_tensor("think_rows", (B, D), F32, kind="Internal").ap()
        c.xn_rows = nc.dram_tensor("xn_rows", (NX, D), F32, kind="Internal").ap()
        c.q_parts, c.k_parts = (nc.dram_tensor(n, (3, DQ3, B * H3, D), BF16, kind="Internal").ap()
                                for n in ("q_parts", "k_parts"))
        c.decay, c.lower = part("decay"), part("lower")
        c.cos_one = part("one")
        stage_first(nc, c)
        layers(nc, c)
        stage_last(nc, c)


def lay_out(inputs):
    f = {k: np.asarray(v) for k, v in inputs.items()}
    a = {
        "x": f["x"].reshape(N, D),
        "ctx": f["ctx_2048"].reshape(N, D),
        "mask": f["mask_BxS2_bk0"].view(np.int32),
        "seg": f["itok_BxS_0_1023"].reshape(NT, P).T,
        "const": constants(),
        "wh": f["L1_xattn_Wh"],
        "whT": f["L1_xattn_Wh"].transpose(0, 2, 1),
        "wkvc": f["L2_xattn_W_kvc"],
        "wkvcT": f["L2_xattn_W_kvc"].T,
        "wkr": f["L2_xattn_W_kr"],
        "g0w": f["L0_ffn_gate_w"].T,
        "g0b": f["L0_ffn_gate_bias"].reshape(1, E0),
        "e0w1": f["L0_ffn_w1"], "e0w2": f["L0_ffn_w2"], "e0w3": f["L0_ffn_w3"],
        "s0g": f["L0_ffn_shared_gate"], "s0u": f["L0_ffn_shared_up"], "s0d": f["L0_ffn_shared_down"],
        "wg": f["L1_xattn_wg_w"], "wo": f["L1_xattn_wo_w"],
        "gng": f["L1_xattn_gn_gamma"].reshape(1, D), "gnb": f["L1_xattn_gn_beta"].reshape(1, D),
    }
    for n in ("in_gamma", "in_beta", "agg_b", "pn_gamma", "pn_beta", "d1_b", "d2_b", "bc_b", "gate_b",
              "out_gamma", "out_beta"):
        a["f1_" + n] = f["L1_ffn_" + n].reshape(1, -1)
    a["f1_d1_b"] = f["L1_ffn_d1_b"].reshape(HID1 // P, P).T
    for n in ("agg_w", "d1_w", "d2_w", "bc_w", "gate_w"):
        a["f1_" + n] = f["L1_ffn_" + n]
    a.update({
        "wdq": f["L2_xattn_W_dq"],
        "wuqT": f["L2_xattn_W_uq"].reshape(QC, H2, HD2).transpose(2, 1, 0),
        "wukT": f["L2_xattn_W_uk"].reshape(KVC, H2, HD2).transpose(2, 1, 0),
        "wuvT": f["L2_xattn_W_uv"].reshape(KVC, H2, HD2).transpose(2, 1, 0),
        "wqr": f["L2_xattn_W_qr"].reshape(QC, H2, R2),
        "wo2": f["L2_xattn_W_o"].reshape(H2, HD2, D).transpose(1, 0, 2),
        "t1": f["L2_ffn_w1"].T, "t2": f["L2_ffn_w2"].T, "t3": f["L2_ffn_w3"].T,
        "gamma3": f["L3_xattn_gamma"].reshape(1, 1),
        "g3w": f["L3_ffn_gate_w"].T,
        "e3w1": f["L3_ffn_w1"], "e3w2": f["L3_ffn_w2"], "e3w3": f["L3_ffn_w3"],
        "s3w1": f["L3_ffn_sw1"], "s3w2": f["L3_ffn_sw2"], "s3w3": f["L3_ffn_sw3"],
    })
    return {k: np.ascontiguousarray(v) for k, v in a.items()}


def kernel(**inputs):
    import concourse.bacc as bacc
    from concourse.bass_utils import run_bass_kernel_spmd

    nc = bacc.Bacc("TRN2", target_bir_lowering=False, num_devices=1)
    arrays = {"in_" + k: v for k, v in lay_out(inputs).items()}
    d = {k[3:]: nc.dram_tensor(k, v.shape, mybir.dt.from_np(v.dtype), kind="ExternalInput").ap()
         for k, v in arrays.items()}
    d["out"] = nc.dram_tensor("out_x", (N, D), F32, kind="ExternalOutput").ap()
    build_program(nc, d)
    r = run_bass_kernel_spmd(nc, [arrays], core_ids=[0])
    return r.results[0]["out_x"].reshape(B, S, D)
```

```python
from contextlib import ExitStack

import numpy as np

import concourse.bass as bass
from concourse import mybir

ALU = mybir.AluOpType
ACT = mybir.ActivationFunctionType
AX = mybir.AxisListType
F32 = mybir.dt.float32
BF16 = mybir.dt.bfloat16
I32 = mybir.dt.int32
U32 = mybir.dt.uint32
U8 = mybir.dt.uint8

P = 128
B, S, D = 64, 64, 256
N = B * S
NT = N // P
DK = D // P
LN_EPS = 1e-5
NEG = -1e30

E0, TOP0, G0, TG0, F0, FS0, SCALE0 = 32, 4, 4, 2, 128, 256, 2.0
CAP0 = 2 * (256 * TOP0 // E0)
NX = N + CAP0
H1, HD1, GN_EPS = 2, 128, 1e-3
EPS1, STEPS1, HID1 = 1e-6, 4, 1024
H2, HD2, KVC, QC, R2, LOOKBACK = 16, 128, 64, 96, 64, 8
HID2, EPS2 = 704, 1e-8
H3 = 8
DQ3 = S // H3
E3, HID3, TOP3, SCALE3 = 8, 176, 2, 2.5
HH3 = HID3 // 2

LANES = 2
CREDIT = LANES
WIDE = 4


def ready(t, lanes=LANES):
    return t + 1 + lanes


def freed(t):
    return t + 1


def loaded(i):
    return 16 * i + 16


def stored(i):
    return 16 * i + 32


def store_freed(i):
    return 16 * i + 16


def settle(eng, passed):
    eng.sem_inc(passed, 1)


class Chain:

    def __init__(self, eng, sem, start=0):
        self.eng, self.sem, self.start, self.n = eng, sem, start, 0

    def link(self, ins):
        self.n += 1
        ins.then_inc(self.sem, 1)
        self.eng.wait_ge(self.sem, self.start + self.n)


CONSTS = {}
_at = 0
for _name, _width in (("ident", 128), ("cos", 128), ("sin", 128), ("before", 128), ("iota", 64),
                      ("decay", 128), ("lower", 16), ("one", 128)):
    CONSTS[_name] = (_at, _at + _width)
    _at += _width
CONST_W = _at


def constants():
    c = np.zeros((P, CONST_W), np.float32)

    def put(name, v, rows=slice(0, P)):
        a, b = CONSTS[name]
        c[rows, a:b] = v

    put("ident", np.eye(P, dtype=np.float32))
    half = R2 // 2
    inv_freq = (np.float32(1.0) / np.float32(10000.0) ** (np.arange(half, dtype=np.float32) / np.float32(half))).astype(np.float32)
    ang = (np.arange(S, dtype=np.float32)[:, None] * inv_freq).astype(np.float32)
    cos, sin = (np.tile(f(ang).T.astype(np.float32), (1, 2)) for f in (np.cos, np.sin))
    put("cos", np.concatenate([cos, cos]), slice(64, 128))
    put("sin", np.concatenate([sin, -sin]), slice(64, 128))
    i = np.arange(P)
    put("before", (i[:, None] < i[None, :]).astype(np.float32))
    put("iota", np.arange(64, dtype=np.float32)[None, :])
    gam = (1.0 - 2.0 ** (-5.0 - np.arange(H1, dtype=np.float32))).astype(np.float32)
    expo = np.arange(S, dtype=np.float32)[None, :] - np.arange(S, dtype=np.float32)[:, None]
    dm = np.where(expo[None] <= 0, gam[:, None, None] ** expo[None], 0.0).astype(np.float32)
    dm = dm / np.sqrt(dm.sum(-1))[:, None, :] / np.sqrt(np.float32(HD1))
    put("decay", dm.transpose(1, 0, 2).reshape(S, H1 * S), slice(0, S))
    put("one", 1.0)
    low = (np.arange(G0)[None, :] < np.arange(G0)[:, None]).astype(np.float32)
    put("lower", low.reshape(1, 16))
    return c


class Core:
    pass


HELD = []
OPENED = []


def open_sems(nc, ctx, names):
    OPENED.append(names)
    got = {n: nc.alloc_semaphore(f"{n}_{len(OPENED)}") for n in names.split()}
    HELD.extend(got.values())
    return got


def recycle(nc):
    nc.clear_and_free_semaphores(list(HELD))
    HELD.clear()
    nc.all_engine_barrier()


def give_credit(pool, sems, names, step=1):
    for n in names.split():
        pool.sem_inc(sems[n], CREDIT * step)


def half(ap):
    return ap.rearrange("p (k n) -> p k n", k=DK)


def upper(ap):
    return ap.bitcast(BF16)[:, 1::2]


def at_tile(ap, t):
    return ap[:, bass.ds(t, 1), :].rearrange("p a n -> p (a n)")


def finish_stats(nc, c, tag, eps=LN_EPS, src=None, mean=None, rstd=None):
    src, mean, rstd = src or c.bn, mean or c.mean, rstd or c.rstd
    with ExitStack() as ctx:
        s = open_sems(nc, ctx, f"{tag}_chain {tag}_var_ready {tag}_half_set {tag}_rstd_ready")
        block = ctx.enter_context(nc.Block())

        @block.vector
        def _(dve):
            ch = Chain(dve, s[f"{tag}_chain"])
            m_even, m_odd = src[:, :, 1], src[:, :, 4]
            v_even, v_odd = src[:, :, 2], src[:, :, 5]
            nc.vector.tensor_tensor(mean[:, :], m_even, m_odd, ALU.add)
            nc.vector.tensor_tensor(c.small[:, 0, :], m_even, m_odd, ALU.subtract)
            ch.link(nc.vector.tensor_tensor(c.small[:, 1, :], v_even, v_odd, ALU.add))
            nc.vector.tensor_scalar(mean[:, :], mean[:, :], 0.5, None, ALU.mult)
            ch.link(nc.vector.scalar_tensor_tensor(out=c.small[:, 2, :], in0=c.small[:, 0, :], scalar=0.25,
                                                   in1=c.small[:, 0, :], op0=ALU.mult, op1=ALU.mult))
            ch.link(nc.vector.scalar_tensor_tensor(out=c.small[:, 3, :], in0=c.small[:, 1, :], scalar=1.0 / D,
                                                   in1=c.small[:, 2, :], op0=ALU.mult, op1=ALU.add))
            nc.vector.tensor_scalar(c.small[:, 4, :], c.small[:, 3, :], eps, None,
                                    ALU.add).then_inc(s[f"{tag}_var_ready"], 1)

        @block.gpsimd
        def _(pool):
            nc.gpsimd.memset(c.minus_half[:, :], -0.5).then_inc(s[f"{tag}_half_set"], 1)
            pool.wait_ge(s[f"{tag}_half_set"], 1)
            pool.wait_ge(s[f"{tag}_var_ready"], 1)
            nc.gpsimd.tensor_tensor(rstd[:, :], c.small[:, 4, :], c.minus_half[:, :],
                                    ALU.pow).then_inc(s[f"{tag}_rstd_ready"], 1)
            pool.wait_ge(s[f"{tag}_rstd_ready"], 1)


def normalize(nc, c, out, t):
    return nc.vector.tensor_scalar(out, at_tile(c.x, t), c.mean[:, bass.ds(t, 1)], c.rstd[:, bass.ds(t, 1)],
                                   ALU.subtract, ALU.mult)


def transpose_tile(nc, c, bank, src):
    for k in range(DK):
        last = nc.tensor.transpose(bank[:, k * P:(k + 1) * P], src[:, k * P:(k + 1) * P], c.ident)
    return last


def stage_first(nc, c):
    with ExitStack() as ctx:
        CH = 4
        s = open_sems(nc, ctx, "consts_loaded " + " ".join(f"x_loaded{n}" for n in range(CH)))
        block = ctx.enter_context(nc.Block())
        xt = c.d["x"].rearrange("(n p) d -> p n d", p=P)

        @block.sync
        def _(sp):
            for n in range(CH):
                sp.dma_start(c.x[:, 8 * n:8 * n + 8, :], xt[:, 8 * n:8 * n + 8, :]).then_inc(s[f"x_loaded{n}"], 16)
            sp.dma_start(c.const[:, :], c.d["const"]).then_inc(s["consts_loaded"], 16)
            sp.wait_ge(s["consts_loaded"], 16)

        @block.vector
        def _(dve):
            for n in range(CH):
                dve.wait_ge(s[f"x_loaded{n}"], 16)
                for t in range(8 * n, 8 * n + 8):
                    nc.vector.bn_stats(c.bn[:, t, :], c.x[:, t, :])


def stage_l0_attention(nc, c):
    with ExitStack() as ctx:
        sb = lambda n, sh, dt=F32: ctx.enter_context(nc.sbuf_tensor(n, sh, dt))
        wh = sb("wh", [P, H1, P]); whT = sb("whT", [P, H1, P]); gram = sb("gram", [P, H1, P])
        wkvcT = sb("wkvcT", [KVC, D]); wkr = sb("wkr", [KVC, R2]); wk = sb("wk", [P, DK, P])
        mask8 = sb("mask8", [P, NT, S], U8); keep = sb("keep", [P, NT, S]); drop = sb("drop", [P, NT, S])
        any_valid = sb("any_valid", [P, NT])
        xn = sb("xn_a", [P, WIDE, D]); ctx_in = sb("ctx_in", [P, WIDE, D]); fT = sb("fT_a", [P, WIDE, 4, P])
        sc = sb("scores_a", [P, WIDE, S]); prob = sb("prob_a", [P, WIDE, P]); probT = sb("probT_a", [P, WIDE, P])
        nmax = sb("nmax_a", [P, WIDE]); tot = sb("tot_a", [P, WIDE]); rec = sb("rec_a", [P, WIDE])
        rot = sb("rot_a", [P, WIDE, 2, P]); kraw = sb("kraw_a", [P, WIDE, P])
        s = open_sems(nc, ctx, "a_weights a_masks a_pe_pre a_gram a_wk a_mask_chain a_mask_ready a_prob_zero "
                      "xn_ready feat_ready feat_copied v_ready v_copied keys_ready key_copied rot_ready "
                      "keys_done scores_ready soft_ready prob_ready probT_ready probT_copied read_ready x_done a_chain "
                      + " ".join(f"ctx_loaded{j}" for j in range(WIDE)))
        block = ctx.enter_context(nc.Block())
        ctx_d = c.d["ctx"]
        ITER_LINKS = 6 * WIDE

        def feat(j): return c.bank[2 * j]
        def vg(j): return c.bank[2 * j]
        def att(j): return c.bank[2 * j + 1]
        def keys(j): return c.bank[2 * j + 1]

        @block.sync
        def _(sp):
            for dst, src in ((wh[:, :, :], c.d["wh"].rearrange("h d e -> d h e")),
                             (whT[:, :, :], c.d["whT"].rearrange("h e d -> e h d")),
                             (wkvcT[:, :], c.d["wkvcT"]), (wkr[:, :], c.d["wkr"]),
                             (wk[:, :, 0:KVC], c.d["wkvc"].rearrange("(k p) n -> p k n", p=P))):
                sp.dma_start(dst, src).then_inc(s["a_weights"], 16)
            for b in range(2):
                src = c.d["mask"].rearrange("(t b) k -> b t k", b=2)[b:b + 1].broadcast_to([64, NT, S // 4])
                sp.dma_start(mask8[64 * b:64 * b + 64, :, :].bitcast(I32), src).then_inc(s["a_masks"], 16)
            with sp.Fori(0, NT // WIDE) as i:
                for j in range(WIDE):
                    t = i * WIDE + j
                    sp.wait_ge(s["x_done"], freed(t))
                    sp.dma_start(ctx_in[:, j, :], ctx_d[bass.ds(t * P, P), :]).then_inc(s[f"ctx_loaded{j}"], 16)

        @block.gpsimd
        def _(pool):
            give_credit(pool, s, "xn_ready feat_ready feat_copied v_ready v_copied keys_ready key_copied rot_ready "
                        "keys_done scores_ready soft_ready prob_ready probT_ready probT_copied read_ready x_done", WIDE // CREDIT)
            nc.gpsimd.memset(prob[:, :, :], 0.0).then_inc(s["a_prob_zero"], 1)
            with pool.Fori(0, NT // WIDE) as i:
                for j in range(WIDE):
                    t = i * WIDE + j
                    pool.wait_ge(s["rot_ready"], ready(t, WIDE))
                    nc.gpsimd.tensor_tensor(c.keysT[64:P, bass.ds(t * P, P)], rot[64:P, j, 0, :], rot[64:P, j, 1, :],
                                            ALU.add).then_inc(s["keys_done"], 1)

        @block.tensor
        def _(pe):
            pe.wait_ge(s["a_weights"], 80)
            for h in range(H1):
                nc.tensor.matmul(c.bank[0][:, h * P:(h + 1) * P], whT[:, h, :], whT[:, h, :], start=True, stop=True)
            for k in range(DK):
                last = nc.tensor.matmul(c.bank[1][:, k * R2:(k + 1) * R2], wkvcT[:, k * P:(k + 1) * P], wkr[:, :],
                                        start=True, stop=True)
            last.then_inc(s["a_pe_pre"], 1)
            pe.wait_ge(s["a_gram"], 1)
            pe.wait_ge(s["a_wk"], 1)
            with pe.Fori(0, NT // WIDE) as i:
                for j in range(WIDE):
                    t = i * WIDE + j
                    pe.wait_ge(s["xn_ready"], ready(t, WIDE))
                    pe.wait_ge(s[f"ctx_loaded{j}"], loaded(i))
                    pe.wait_ge(s["v_copied"], freed(t))
                    transpose_tile(nc, c, feat(j)[:, 0:D], xn[:, j, :])
                    transpose_tile(nc, c, feat(j)[:, D:2 * D], ctx_in[:, j, :]).then_inc(s["feat_ready"], 1)
                for j in range(WIDE):
                    t = i * WIDE + j
                    pe.wait_ge(s["feat_copied"], ready(t, WIDE))
                    pe.wait_ge(s["x_done"], freed(t))
                    for k in range(DK):
                        nc.tensor.matmul(keys(j)[:, 0:P], wk[:, k, :], fT[:, j, 2 + k, :],
                                         start=(k == 0), stop=(k == DK - 1))
                    for k in range(DK):
                        last = nc.tensor.matmul(keys(j)[:, P:P + KVC], fT[:, j, 2 + k, :], wk[:, k, 0:KVC],
                                                start=(k == 0), stop=(k == DK - 1))
                    last.then_inc(s["keys_ready"], 1)
                    for h in range(H1):
                        nc.tensor.matmul(vg(j)[:, h * P:(h + 1) * P], fT[:, j, 2 + h, :], wh[:, h, :],
                                         start=True, stop=True)
                        last = nc.tensor.matmul(vg(j)[:, D + h * P:D + (h + 1) * P], gram[:, h, :],
                                                fT[:, j, 2 + h, :], start=True, stop=True)
                    last.then_inc(s["v_ready"], 1)
                for j in range(WIDE):
                    t = i * WIDE + j
                    pe.wait_ge(s["key_copied"], ready(t, WIDE))
                    for b in range(2):
                        q = slice(64 * b, 64 * b + 64)
                        for k in range(DK):
                            last = nc.tensor.matmul(att(j)[q, 0:S], fT[:, j, k, q], fT[:, j, 2 + k, q],
                                                    start=(k == 0), stop=(k == DK - 1))
                    last.then_inc(s["scores_ready"], 1)
                for j in range(WIDE):
                    t = i * WIDE + j
                    pe.wait_ge(s["prob_ready"], ready(t, WIDE))
                    nc.tensor.transpose(att(j)[:, 0:P], prob[:, j, :], c.ident).then_inc(s["probT_ready"], 1)
                for j in range(WIDE):
                    t = i * WIDE + j
                    pe.wait_ge(s["probT_copied"], ready(t, WIDE))
                    nc.tensor.matmul(att(j)[:, 0:D], probT[:, j, :], ctx_in[:, j, :],
                                     start=True, stop=True).then_inc(s["read_ready"], 1)

        @block.scalar
        def _(act):
            act.wait_ge(s["a_pe_pre"], 1)
            act.copy(gram[:, :, :].rearrange("p h n -> p (h n)"), c.bank[0][:, 0:D]).then_inc(s["a_gram"], 1)
            act.wait_ge(s["a_weights"], 80)
            act.copy(wk[:, :, KVC:P], c.bank[1][:, 0:DK * R2].rearrange("p (k n) -> p k n", k=DK)).then_inc(s["a_wk"], 1)
            act.wait_ge(s["a_prob_zero"], 1)
            with act.Fori(0, NT // WIDE) as i:
                for j in range(WIDE):
                    t = i * WIDE + j
                    act.wait_ge(s["feat_ready"], ready(t, WIDE))
                    act.wait_ge(s["scores_ready"], freed(t))
                    act.copy(fT[:, j, :, :].rearrange("p k n -> p (k n)"), feat(j)[:, :]).then_inc(s["feat_copied"], 1)
                for j in range(WIDE):
                    t = i * WIDE + j
                    act.wait_ge(s["keys_ready"], ready(t, WIDE))
                    act.wait_ge(s["rot_ready"], freed(t))
                    act.copy(at_tile(c.kvc, t), keys(j)[:, P:P + KVC])
                    act.copy(c.keysT[0:64, bass.ds(t * P, P)], keys(j)[0:64, 0:P])
                    act.copy(kraw[64:P, j, :], keys(j)[64:P, 0:P]).then_inc(s["key_copied"], 1)
                for j in range(WIDE):
                    t = i * WIDE + j
                    act.wait_ge(s["v_ready"], ready(t, WIDE))
                    act.copy(at_tile(c.v, t), vg(j)[:, 0:D])
                    act.copy(c.gramT[:, :, bass.ds(t * P, P)], vg(j)[:, D:2 * D].rearrange(
                        "p (h n) -> p h n", h=H1)).then_inc(s["v_copied"], 1)
                for j in range(WIDE):
                    t = i * WIDE + j
                    act.wait_ge(s["soft_ready"], ready(t, WIDE))
                    act.wait_ge(s["probT_ready"], freed(t))
                    act.wait_ge(s["x_done"], freed(t))
                    for b in range(2):
                        q = slice(64 * b, 64 * b + 64)
                        last = nc.scalar.activation(prob[q, j, q], sc[q, j, :], ACT.Exp, bias=nmax[q, j:j + 1],
                                                    accum_out=tot[q, j:j + 1])
                    last.then_inc(s["prob_ready"], 1)
                for j in range(WIDE):
                    t = i * WIDE + j
                    act.wait_ge(s["probT_ready"], ready(t, WIDE))
                    act.wait_ge(s["read_ready"], freed(t))
                    act.copy(probT[:, j, :], att(j)[:, 0:P]).then_inc(s["probT_copied"], 1)

        @block.vector
        def _(dve):
            ch = Chain(dve, s["a_mask_chain"])
            dve.wait_ge(s["a_masks"], 32)
            ch.link(nc.vector.tensor_copy(keep[:, :, :], mask8[:, :, :]))
            nc.vector.tensor_scalar(drop[:, :, :], keep[:, :, :], 1.0, -NEG, ALU.subtract, ALU.mult)
            ch.link(nc.vector.tensor_reduce(any_valid[:, :], keep[:, :, :], AX.X, ALU.max))
            with dve.Fori(0, NT // WIDE) as i:
                ch = Chain(dve, s["a_chain"], i * ITER_LINKS)
                for j in range(WIDE):
                    t = i * WIDE + j
                    dve.wait_ge(s["feat_ready"], freed(t))
                    normalize(nc, c, xn[:, j, :], t).then_inc(s["xn_ready"], 1)
                for j in range(WIDE):
                    t = i * WIDE + j
                    dve.wait_ge(s["key_copied"], ready(t, WIDE))
                    dve.wait_ge(s["keys_done"], freed(t))
                    kr = kraw[:, j, :]
                    nc.vector.tensor_tensor(rot[64:P, j, 0, :], kr[64:P, :], c.cos[64:P, :], ALU.mult)
                    nc.vector.tensor_tensor(rot[96:P, j, 1, :], kr[64:96, :], c.sin[64:96, :], ALU.mult)
                    nc.vector.tensor_tensor(rot[64:96, j, 1, :], kr[96:P, :], c.sin[96:P, :],
                                            ALU.mult).then_inc(s["rot_ready"], 1)
                for j in range(WIDE):
                    t = i * WIDE + j
                    dve.wait_ge(s["scores_ready"], ready(t, WIDE))
                    dve.wait_ge(s["prob_ready"], freed(t))
                    ch.link(nc.vector.scalar_tensor_tensor(out=sc[:, j, :], in0=att(j)[:, 0:S], scalar=D ** -0.5,
                                                           in1=at_tile(keep, t), op0=ALU.mult, op1=ALU.mult))
                    ch.link(nc.vector.tensor_tensor(sc[:, j, :], sc[:, j, :], at_tile(drop, t), ALU.add))
                    nc.vector.tensor_reduce(nmax[:, j:j + 1], sc[:, j, :], AX.X, ALU.max,
                                            negate=True).then_inc(s["soft_ready"], 1)
                for j in range(WIDE):
                    t = i * WIDE + j
                    dve.wait_ge(s["prob_ready"], ready(t, WIDE))
                    ch.link(nc.vector.reciprocal(rec[:, j:j + 1], tot[:, j:j + 1]))
                    ch.link(nc.vector.tensor_tensor(rec[:, j:j + 1], rec[:, j:j + 1], any_valid[:, bass.ds(t, 1)], ALU.mult))
                for j in range(WIDE):
                    t = i * WIDE + j
                    dve.wait_ge(s["read_ready"], ready(t, WIDE))
                    add_and_stats(nc, c, ch, t, att(j)[:, 0:D], rec[:, j:j + 1], s["x_done"])
                assert ch.n == ITER_LINKS, ch.n


def add_and_stats(nc, c, ch, t, psum, scale, done):
    ch.link(nc.vector.scalar_tensor_tensor(out=at_tile(c.x, t), in0=psum, scalar=scale, in1=at_tile(c.x, t),
                                           op0=ALU.mult, op1=ALU.add))
    ch.link(nc.vector.bn_stats(at_tile(c.bn, t), at_tile(c.x, t)))
    ch.eng.sem_inc(done, 1)


def stage_last(nc, c):
    with ExitStack() as ctx:
        s = open_sems(nc, ctx, "out_stored")
        block = ctx.enter_context(nc.Block())
        ot = c.d["out"].rearrange("(n p) d -> p n d", p=P)

        @block.sync
        def _(sp):
            for n in range(4):
                sp.dma_start(ot[:, 8 * n:8 * n + 8, :], c.x[:, 8 * n:8 * n + 8, :]).then_inc(s["out_stored"], 16)
            sp.wait_ge(s["out_stored"], 64)


def token_loop(i, lanes=LANES):
    return [(j, i * lanes + j) for j in range(lanes)]


def stage_l0_shared(nc, c):
    with ExitStack() as ctx:
        sb = lambda n, sh, dt=F32: ctx.enter_context(nc.sbuf_tensor(n, sh, dt))
        wgu = sb("wgu", [P, DK, 2 * FS0]); wd = sb("wd", [P, FS0 // P, D]); wg = sb("wgate", [P, DK, E0])
        xn = sb("xn_b", [P, WIDE, D]); xT = sb("xT_b", [P, WIDE, DK, P])
        sig = sb("sig_b", [P, WIDE, D]); hT = sb("hT_b", [P, WIDE, D]); zero = sb("zero_b", [P, 1024])
        s = open_sems(nc, ctx, "b_weights zero_set zeroed xn_ready feat_ready feat_copied hid_ready sig_ready "
                      "hT_ready logit_ready logit_copied down_ready x_done b_chain "
                      + " ".join(f"xn_stored{j}" for j in range(WIDE)))
        block = ctx.enter_context(nc.Block())

        def hid(j): return c.bank[2 * j]
        def feat(j): return c.bank[2 * j + 1][:, 0:D]
        def logit(j): return c.bank[2 * j + 1][:, 0:E0]
        def down(j): return c.bank[2 * j + 1][:, D:2 * D]

        @block.sync
        def _(sp):
            for dst, src in ((wg[:, :, :], c.d["g0w"]), (wgu[:, :, 0:FS0], c.d["s0g"]),
                             (wgu[:, :, FS0:2 * FS0], c.d["s0u"]), (wd[:, :, :], c.d["s0d"])):
                sp.dma_start(dst, src.rearrange("(k p) n -> p k n", p=P)).then_inc(s["b_weights"], 16)
            sp.wait_ge(s["zero_set"], 1)
            for n in range(8):
                sp.dma_start(c.moe[512 * n:512 * n + 512, :].rearrange("(p r) d -> p (r d)", r=4),
                             zero[:, :]).then_inc(s["zeroed"], 16)
            sp.dma_start(c.moe[N:NX, :], zero[0:CAP0, 0:D]).then_inc(s["zeroed"], 16)
            sp.dma_start(c.xn_rows[N:NX, :], zero[0:CAP0, 0:D]).then_inc(s["zeroed"], 16)
            with sp.Fori(0, NT // WIDE) as i:
                for j, t in token_loop(i, WIDE):
                    sp.wait_ge(s["xn_ready"], ready(t, WIDE))
                    sp.dma_start(c.xn_rows[bass.ds(t * P, P), :], xn[:, j, :]).then_inc(s[f"xn_stored{j}"], 16)
            sp.wait_ge(s["zeroed"], 160)
            for j in range(WIDE):
                sp.wait_ge(s[f"xn_stored{j}"], 16 * (NT // WIDE) + 16)

        @block.gpsimd
        def _(pool):
            nc.gpsimd.memset(zero[:, :], 0.0).then_inc(s["zero_set"], 1)
            give_credit(pool, s, "xn_ready feat_ready feat_copied hid_ready sig_ready hT_ready logit_ready "
                        "logit_copied down_ready x_done", WIDE // CREDIT)
            for j in range(WIDE):
                pool.sem_inc(s[f"xn_stored{j}"], 16)

        @block.tensor
        def _(pe):
            pe.wait_ge(s["b_weights"], 64)
            with pe.Fori(0, NT // WIDE) as i:
                for j, t in token_loop(i, WIDE):
                    pe.wait_ge(s["xn_ready"], ready(t, WIDE))
                    pe.wait_ge(s["x_done"], freed(t))
                    transpose_tile(nc, c, feat(j), xn[:, j, :]).then_inc(s["feat_ready"], 1)
                for j, t in token_loop(i, WIDE):
                    pe.wait_ge(s["feat_copied"], ready(t, WIDE))
                    pe.wait_ge(s["hT_ready"], freed(t))
                    for f in range(4):
                        for k in range(DK):
                            last = nc.tensor.matmul(hid(j)[:, f * P:(f + 1) * P], wgu[:, k, f * P:(f + 1) * P],
                                                    xT[:, j, k, :], start=(k == 0), stop=(k == DK - 1))
                    last.then_inc(s["hid_ready"], 1)
                    for k in range(DK):
                        last = nc.tensor.matmul(logit(j)[:, 0:E0], xT[:, j, k, :], wg[:, k, :],
                                                start=(k == 0), stop=(k == DK - 1))
                    last.then_inc(s["logit_ready"], 1)
                for j, t in token_loop(i, WIDE):
                    pe.wait_ge(s["hT_ready"], ready(t, WIDE))
                    pe.wait_ge(s["logit_copied"], ready(t, WIDE))
                    for k in range(DK):
                        last = nc.tensor.matmul(down(j)[:, 0:D], hT[:, j, k * P:(k + 1) * P], wd[:, k, :],
                                                start=(k == 0), stop=(k == DK - 1))
                    last.then_inc(s["down_ready"], 1)

        @block.scalar
        def _(act):
            with act.Fori(0, NT // WIDE) as i:
                for j, t in token_loop(i, WIDE):
                    act.wait_ge(s["feat_ready"], ready(t, WIDE))
                    act.wait_ge(s["logit_ready"], freed(t))
                    act.copy(xT[:, j, :, :].rearrange("p k n -> p (k n)"), feat(j)[:, 0:D]).then_inc(s["feat_copied"], 1)
                for j, t in token_loop(i, WIDE):
                    act.wait_ge(s["hid_ready"], ready(t, WIDE))
                    act.wait_ge(s["hT_ready"], freed(t))
                    nc.scalar.activation(sig[:, j, :], hid(j)[:, 0:D], ACT.Sigmoid).then_inc(s["sig_ready"], 1)
                    act.wait_ge(s["logit_ready"], ready(t, WIDE))
                    nc.scalar.activation(at_tile(c.score0, t), logit(j)[:, 0:E0],
                                         ACT.Sigmoid).then_inc(s["logit_copied"], 1)

        @block.vector
        def _(dve):
            with dve.Fori(0, NT // WIDE) as i:
                ch = Chain(dve, s["b_chain"], i * WIDE)
                for j, t in token_loop(i, WIDE):
                    dve.wait_ge(s["feat_ready"], freed(t))
                    dve.wait_ge(s[f"xn_stored{j}"], store_freed(i))
                    normalize(nc, c, xn[:, j, :], t).then_inc(s["xn_ready"], 1)
                for j, t in token_loop(i, WIDE):
                    dve.wait_ge(s["sig_ready"], ready(t, WIDE))
                    dve.wait_ge(s["down_ready"], freed(t))
                    ch.link(nc.vector.tensor_tensor(sig[:, j, :], hid(j)[:, 0:D], sig[:, j, :], ALU.mult))
                    nc.vector.tensor_tensor(hT[:, j, :], hid(j)[:, D:2 * D], sig[:, j, :],
                                            ALU.mult).then_inc(s["hT_ready"], 1)
                for j, t in token_loop(i, WIDE):
                    dve.wait_ge(s["down_ready"], ready(t, WIDE))
                    nc.vector.tensor_tensor(at_tile(c.x, t), down(j)[:, 0:D], at_tile(c.x, t),
                                            ALU.add).then_inc(s["x_done"], 1)


BIG = 3e38


def stage_l0_route(nc, c):
    with ExitStack() as ctx:
        sb = lambda n, sh, dt=F32: ctx.enter_context(nc.sbuf_tensor(n, sh, dt))
        NE = NT * E0
        biased = sb("biased", [P, NE]); ta = sb("ta", [P, NE]); tb = sb("tb", [P, NE]); tc_ = sb("tc", [P, NE])
        gs = sb("gs", [P, NT, G0]); gmask = sb("gmask", [P, NT, G0]); bias = sb("gate_bias", [P, E0])
        cand = sb("cand", [P, NT, E0 + 4]); left = sb("left", [P, NT, E0 + 4]); top = sb("top", [P, NT, 8])
        chosen = sb("chosen", [P, NE]); chosen_b = sb("chosen_b", [P, NE], BF16)
        wsum = sb("wsum", [P, NT]); before_b = sb("before_b", [P, P], BF16); ones_b = sb("ones_b", [P, P], BF16)
        wb = sb("wb", [P, NE], BF16); tile_no = sb("tile_no", [P, NE]); row_no = sb("row_no", [P, NE])
        s = open_sems(nc, ctx, "r_bias r_chain r_chosen r_counts r_iota")
        block = ctx.enter_context(nc.Block())

        @block.sync
        def _(sp):
            sp.dma_start(bias[:, :], c.d["g0b"].broadcast_to([P, E0])).then_inc(s["r_bias"], 16)

        @block.gpsimd
        def _(pool):
            nc.gpsimd.iota(tile_no[:, :], pattern=[[1, NT], [0, E0]], base=0, channel_multiplier=0,
                           allow_small_or_imprecise_dtypes=True).then_inc(s["r_iota"], 1)
            nc.gpsimd.iota(row_no[:, :], pattern=[[0, NE]], base=0, channel_multiplier=1,
                           allow_small_or_imprecise_dtypes=True).then_inc(s["r_iota"], 1)
            nc.gpsimd.iota(c.row_col[:, :], pattern=[[0, 1]], base=0, channel_multiplier=1,
                           allow_small_or_imprecise_dtypes=True).then_inc(s["r_iota"], 1)

        @block.tensor
        def _(pe):
            pe.wait_ge(s["r_chosen"], 1)
            for n in range(2):
                cols = slice(512 * n, 512 * n + 512)
                nc.tensor.matmul(c.bank[n][:, :], before_b[:, :], chosen_b[:, cols], start=True, stop=True)
                last = nc.tensor.matmul(c.bank[2 + n][:, :], ones_b[:, :], chosen_b[:, cols], start=True, stop=True)
            last.then_inc(s["r_counts"], 1)

        @block.vector
        def _(dve):
            ch = Chain(dve, s["r_chain"])
            v = nc.vector
            e8 = lambda ap: ap.rearrange("p (g e) -> p g e", e=8)

            def g(ap, a, b): return e8(ap[:, :])[:, :, a:b]
            score = c.score0[:, :, :].rearrange("p t e -> p (t e)")
            te = lambda ap: ap[:, :].rearrange("p (t e) -> p t e", e=E0)
            dve.wait_ge(s["r_bias"], 16)
            ch.link(v.tensor_tensor(te(biased), c.score0[:, :, :],
                                    bias[:, :].unsqueeze(1).broadcast_to([P, NT, E0]), ALU.add))
            v.tensor_tensor(g(ta, 0, 4), g(biased, 0, 4), g(biased, 4, 8), ALU.max)
            ch.link(v.tensor_tensor(g(tb, 0, 4), g(biased, 0, 4), g(biased, 4, 8), ALU.min))
            for w in (2, 1):
                v.tensor_tensor(g(tc_, 0, w), g(ta, 0, w), g(ta, w, 2 * w), ALU.max)
                v.tensor_tensor(g(tc_, 2, 2 + w), g(ta, 0, w), g(ta, w, 2 * w), ALU.min)
                ch.link(v.tensor_tensor(g(tc_, 4, 4 + w), g(tb, 0, w), g(tb, w, 2 * w), ALU.max))
                v.tensor_copy(g(ta, 0, w), g(tc_, 0, w))
                ch.link(v.tensor_tensor(g(tb, 0, w), g(tc_, 2, 2 + w), g(tc_, 4, 4 + w), ALU.max))
            g1 = lambda ap: g(ap, 0, 1).rearrange("p (t g) o -> p t (g o)", g=G0)
            ch.link(v.tensor_tensor(gs[:, :, :], g1(ta), g1(tb), ALU.add))
            rival = gs[:, :, :].unsqueeze(2).broadcast_to([P, NT, G0, G0])
            own = gs[:, :, :].unsqueeze(3).broadcast_to([P, NT, G0, G0])
            sq = lambda ap: ap[:, 0:NT * 16].rearrange("p (t a b) -> p t a b", a=G0, b=G0)
            v.tensor_tensor(sq(ta), rival, own, ALU.is_gt)
            ch.link(v.tensor_tensor(sq(tb), rival, own, ALU.is_equal))
            t16 = lambda ap: ap[:, 0:NT * 16].rearrange("p (t a) -> p t a", a=16)
            ch.link(v.tensor_tensor(t16(tb), t16(tb), c.lower.unsqueeze(1).broadcast_to([P, NT, 16]), ALU.mult))
            ch.link(v.tensor_tensor(ta[:, 0:NT * 16], ta[:, 0:NT * 16], tb[:, 0:NT * 16], ALU.add))
            ch.link(v.tensor_reduce(gmask[:, :, :], sq(ta), AX.X, ALU.add))
            ch.link(v.tensor_scalar(gmask[:, :, :], gmask[:, :, :], float(TG0), None, ALU.is_lt))
            v.memset(cand[:, :, E0:E0 + 4], BIG)
            v.tensor_copy(ones_b[:, :], c.cos_one)
            v.tensor_copy(before_b[:, :], c.before)
            for gi in range(G0):
                last = v.tensor_tensor(cand[:, :, 8 * gi:8 * gi + 8], te(biased)[:, :, 8 * gi:8 * gi + 8],
                                       gmask[:, :, gi:gi + 1].broadcast_to([P, NT, 8]), ALU.mult)
            ch.link(last)
            for t in range(NT):
                last = v.max(top[:, t, :], cand[:, t, 0:E0])
            ch.link(last)
            ch.link(v.memset(top[:, :, TOP0:8], BIG))
            for t in range(NT):
                last = v.match_replace(out=left[:, t, :], in_to_replace=top[:, t, :], in_values=cand[:, t, :],
                                       imm_value=-BIG)
            ch.link(last)
            v.tensor_tensor(te(chosen_b), left[:, :, 0:E0], cand[:, :, 0:E0], ALU.not_equal).then_inc(s["r_chosen"], 1)
            ch.link(v.tensor_tensor(te(chosen), left[:, :, 0:E0], cand[:, :, 0:E0], ALU.not_equal))
            ch.link(v.tensor_tensor(ta[:, :], score, chosen[:, :], ALU.mult))
            ch.link(v.tensor_reduce(wsum[:, :], te(ta), AX.X, ALU.add))
            ch.link(v.tensor_scalar(wsum[:, :], wsum[:, :], 1e-20, None, ALU.add))
            ch.link(v.reciprocal(wsum[:, :], wsum[:, :]))
            ch.link(v.scalar_tensor_tensor(out=te(ta), in0=te(ta), scalar=SCALE0,
                                           in1=wsum[:, :].unsqueeze(2).broadcast_to([P, NT, E0]),
                                           op0=ALU.mult, op1=ALU.mult))
            col = lambda n: c.slot_cols[:, :, :, n].rearrange("p t e -> p (t e)")
            dve.wait_ge(s["r_iota"], 3)
            v.tensor_copy(col(0), chosen[:, :])
            v.tensor_copy(col(1), tile_no[:, :])
            v.tensor_copy(col(2), row_no[:, :])
            for n in (3, 4):
                ch.link(v.tensor_copy(wb[:, :], ta[:, :]))
                v.tensor_copy(col(n), wb[:, :])
                ch.link(v.tensor_tensor(ta[:, :], ta[:, :], wb[:, :], ALU.subtract))
            ch.link(v.tensor_copy(col(5), ta[:, :]))
            dve.wait_ge(s["r_counts"], 1)
            for n in range(2):
                cols = slice(512 * n, 512 * n + 512)
                v.tensor_copy(ta[:, cols], c.bank[2 + n][:, :])
                last = v.tensor_copy(tc_[:, cols], c.bank[n][:, :])
            ch.link(last)
            ch.link(v.tensor_tensor(tc_[:, :], tc_[:, :], ta[:, :], ALU.subtract))
            cur, nxt, step = ta, tb, 1
            while step < NT:
                w = step * E0
                v.tensor_copy(nxt[:, 0:w], cur[:, 0:w])
                ch.link(v.tensor_tensor(nxt[:, w:NE], cur[:, w:NE], cur[:, 0:NE - w], ALU.add))
                cur, nxt, step = nxt, cur, 2 * step
            ch.link(v.tensor_tensor(tc_[:, :], tc_[:, :], cur[:, :], ALU.add))
            ch.link(v.scalar_tensor_tensor(out=chosen[:, :], in0=tc_[:, :], scalar=float(CAP0), in1=chosen[:, :],
                                           op0=ALU.is_lt, op1=ALU.mult))
            ch.link(v.scalar_tensor_tensor(out=tc_[:, :], in0=tc_[:, :], scalar=1.0, in1=chosen[:, :],
                                           op0=ALU.add, op1=ALU.mult))
            ch.link(v.tensor_scalar(c.place[:, :, :].rearrange("p t e -> p (t e)"), tc_[:, :], 1.0, None,
                                    ALU.subtract))


def stage_l0_slots(nc, c):
    with ExitStack() as ctx:
        sb = lambda n, sh, dt=F32: ctx.enter_context(nc.sbuf_tensor(n, sh, dt))
        hot = sb("hot", [P, LANES, E0, CAP0], BF16); cols = sb("cols", [P, LANES, E0 * 6], BF16)
        zeros = sb("zeros_s", [P, E0 * 6], BF16); iota_b = sb("iota_b", [P, CAP0], BF16)
        got = sb("got", [CAP0, E0, 6]); idf = sb("idf", [CAP0, E0]); empty = sb("empty", [CAP0, E0])
        s = open_sems(nc, ctx, "s_zero s_iota hot_ready cols_ready hot_used s_done s_chain")
        block = ctx.enter_context(nc.Block())
        acc = c.bank[0][0:CAP0, 0:E0 * 6]

        @block.gpsimd
        def _(pool):
            give_credit(pool, s, "hot_ready cols_ready hot_used")
            nc.gpsimd.memset(zeros[:, :], 0.0).then_inc(s["s_zero"], 1)

        @block.scalar
        def _(act):
            with act.Fori(0, NT // LANES) as i:
                for j, t in token_loop(i):
                    act.wait_ge(s["hot_used"], freed(t))
                    act.copy(cols[:, j, :], c.slot_cols[:, bass.ds(t, 1), :, :].rearrange(
                        "p a e n -> p (a e n)")).then_inc(s["cols_ready"], 1)

        @block.vector
        def _(dve):
            ch = Chain(dve, s["s_iota"])
            ch.link(nc.vector.tensor_copy(iota_b[:, :], c.iota))
            with dve.Fori(0, NT // LANES) as i:
                for j, t in token_loop(i):
                    dve.wait_ge(s["hot_used"], freed(t))
                    nc.vector.tensor_tensor(hot[:, j, :, :],
                                            at_tile(c.place, t).unsqueeze(2).broadcast_to([P, E0, CAP0]),
                                            iota_b[:, :].unsqueeze(1).broadcast_to([P, E0, CAP0]),
                                            ALU.is_equal).then_inc(s["hot_ready"], 1)
            ch = Chain(dve, s["s_chain"])
            v = nc.vector
            dve.wait_ge(s["s_done"], 1)
            ch.link(v.tensor_copy(got[:, :, :].rearrange("p e n -> p (e n)"), acc))
            row = c.row_col[0:CAP0, :]
            ch.link(v.tensor_scalar(empty[:, :], got[:, :, 0], -1.0, 1.0, ALU.mult, ALU.add))
            v.scalar_tensor_tensor(out=idf[:, :], in0=got[:, :, 1], scalar=float(P), in1=got[:, :, 2],
                                   op0=ALU.mult, op1=ALU.add)
            ch.link(v.tensor_scalar(got[:, :, 0], empty[:, :], row, None, ALU.mult))
            ch.link(v.scalar_tensor_tensor(out=empty[:, :], in0=empty[:, :], scalar=float(N), in1=got[:, :, 0],
                                           op0=ALU.mult, op1=ALU.add))
            v.tensor_tensor(c.slot_token[:, :], idf[:, :], empty[:, :], ALU.add)
            ch.link(v.tensor_tensor(got[:, :, 3], got[:, :, 3], got[:, :, 4], ALU.add))
            ch.link(v.tensor_tensor(c.slot_weight[:, :], got[:, :, 3], got[:, :, 5], ALU.add))

        @block.tensor
        def _(pe):
            pe.wait_ge(s["s_zero"], 1)
            nc.tensor.matmul(acc, zeros[:, 0:CAP0], zeros[:, :], start=True, stop=False, skip_group_check=True)
            with pe.Fori(0, NT // LANES) as i:
                for j, t in token_loop(i):
                    pe.wait_ge(s["hot_ready"], ready(t))
                    pe.wait_ge(s["cols_ready"], ready(t))
                    for e in range(E0):
                        last = nc.tensor.matmul(acc[:, 6 * e:6 * e + 6], hot[:, j, e, :], cols[:, j, 6 * e:6 * e + 6],
                                                start=False, stop=False, skip_group_check=True)
                    last.then_inc(s["hot_used"], 1)
            nc.tensor.matmul(acc, zeros[:, 0:CAP0], zeros[:, :], start=False, stop=True,
                             skip_group_check=True).then_inc(s["s_done"], 1)


def stage_l0_experts(nc, c):
    with ExitStack() as ctx:
        sb = lambda n, sh, dt=F32: ctx.enter_context(nc.sbuf_tensor(n, sh, dt))
        L = 4
        w13 = sb("w13", [P, L, 2, DK, F0]); w2 = sb("w2e", [P, L, D])
        idx = sb("idx", [CAP0, L], I32); xg = sb("xg", [CAP0, L, D]); xgT = sb("xgT", [P, L, DK * CAP0])
        sig = sb("sig_e", [P, L, CAP0]); hT = sb("hT_e", [P, L, CAP0]); y = sb("y_e", [CAP0, L, D])
        lane_sems = {n: [f"{n}{j}" for j in range(L)] for n in ("w_loaded", "gathered", "added")}
        s = open_sems(nc, ctx, "idx_ready feat_ready feat_copied hid_ready sig_ready hT_ready down_ready y_ready add_done "
                      "e_chain pool_passed pe_passed " + " ".join(sum(lane_sems.values(), [])))
        block = ctx.enter_context(nc.Block())

        def feat(j): return c.bank[4 * (j % 2)]
        def hid(j): return c.bank[4 * (j % 2) + 1]
        def down(j): return c.bank[4 * (j % 2) + 2]

        def done(e):
            return e + 1 + L

        def reusable(e, lanes=L):
            return e + 1 + L - lanes

        def pairs(i):
            return [[(j, i * L + j) for j in (first, first + 1)] for first in range(0, L, 2)]

        @block.sync
        def _(sp):
            with sp.Fori(0, E0 // L) as i:
                for pair in pairs(i):
                    for j, e in pair:
                        sp.wait_ge(s["down_ready"], reusable(e))
                        for n, name in enumerate(("e0w1", "e0w3")):
                            sp.dma_start(w13[:, j, n, :, :], c.d[name][bass.ds(e, 1)].rearrange(
                                "a (k p) f -> p (a k) f", p=P)).then_inc(s[f"w_loaded{j}"], 16)
                        sp.dma_start(w2[:, j, :], c.d["e0w2"][bass.ds(e, 1)].rearrange(
                            "a f d -> f (a d)")).then_inc(s[f"w_loaded{j}"], 16)

        @block.gpsimd
        def _(pool):
            for n in ("idx_ready", "feat_ready", "feat_copied", "hid_ready", "sig_ready", "hT_ready", "down_ready",
                      "y_ready", "add_done"):
                pool.sem_inc(s[n], L)

            def gather(pair):
                for j, e in pair:
                    pool.wait_ge(s["idx_ready"], done(e))
                    pool.wait_ge(s["feat_ready"], reusable(e))
                    settle(pool, s["pool_passed"])
                    nc.gpsimd.indirect_dma_start(
                        out=xg[:, j, :], out_offset=None, in_=c.xn_rows[:, :],
                        in_offset=bass.IndirectOffsetOnAxis(ap=idx[:, j:j + 1], axis=0),
                    ).then_inc(s[f"gathered{j}"], 16)

            def add(pair, i):
                for j, e in pair:
                    pool.wait_ge(s["y_ready"], done(e))
                    settle(pool, s["pool_passed"])
                    nc.gpsimd.indirect_dma_start(
                        out=c.moe[:, :], out_offset=bass.IndirectOffsetOnAxis(ap=idx[:, j:j + 1], axis=0),
                        in_=y[:, j, :], in_offset=None, compute_op=ALU.add, oob_is_err=True,
                        bounds_check=NX - 1,
                    ).then_inc(s[f"added{j}"], 16)
                    pool.wait_ge(s[f"added{j}"], loaded(i))
                    pool.sem_inc(s["add_done"], 1)

            last = E0 // L - 1
            gather(pairs(0)[0])
            with pool.Fori(0, last) as i:
                gather(pairs(i)[1])
                add(pairs(i)[0], i)
                gather(pairs(i + 1)[0])
                add(pairs(i)[1], i)
            gather(pairs(last)[1])
            add(pairs(last)[0], last)
            add(pairs(last)[1], last)

        @block.tensor
        def _(pe):
            def turn(pair, i):
                for j, e in pair:
                    pe.wait_ge(s[f"gathered{j}"], loaded(i))
                    pe.wait_ge(s["feat_copied"], reusable(e, 2))
                    settle(pe, s["pe_passed"])
                    for k in range(DK):
                        last = nc.tensor.transpose(feat(j)[:, k * CAP0:(k + 1) * CAP0], xg[:, j, k * P:(k + 1) * P],
                                                   c.ident[0:CAP0, 0:CAP0])
                    last.then_inc(s["feat_ready"], 1)

            def products(pair, i):
                for j, e in pair:
                    pe.wait_ge(s["feat_copied"], done(e))
                    pe.wait_ge(s[f"w_loaded{j}"], 48 * i + 48)
                    pe.wait_ge(s["hT_ready"], reusable(e, 2))
                    for n in range(2):
                        for k in range(DK):
                            last = nc.tensor.matmul(hid(j)[:, n * CAP0:(n + 1) * CAP0], w13[:, j, n, k, :],
                                                    xgT[:, j, k * CAP0:(k + 1) * CAP0],
                                                    start=(k == 0), stop=(k == DK - 1))
                    last.then_inc(s["hid_ready"], 1)
                for j, e in pair:
                    pe.wait_ge(s["hT_ready"], done(e))
                    pe.wait_ge(s["y_ready"], reusable(e, 2))
                    nc.tensor.matmul(down(j)[0:CAP0, 0:D], hT[:, j, :], w2[:, j, :],
                                     start=True, stop=True).then_inc(s["down_ready"], 1)

            with pe.Fori(0, E0 // L) as i:
                for pair in pairs(i):
                    turn(pair, i)
                    products(pair, i)

        @block.scalar
        def _(act):
            with act.Fori(0, E0 // L) as i:
                for pair in pairs(i):
                    for j, e in pair:
                        act.wait_ge(s["feat_ready"], done(e))
                        act.wait_ge(s["hid_ready"], reusable(e))
                        act.copy(xgT[:, j, :], feat(j)[:, 0:DK * CAP0]).then_inc(s["feat_copied"], 1)
                    for j, e in pair:
                        act.wait_ge(s["hid_ready"], done(e))
                        act.wait_ge(s["hT_ready"], reusable(e))
                        nc.scalar.activation(sig[:, j, :], hid(j)[:, 0:CAP0], ACT.Sigmoid).then_inc(s["sig_ready"], 1)

        @block.vector
        def _(dve):
            def indices(pair):
                for j, e in pair:
                    dve.wait_ge(s["add_done"], reusable(e))
                    nc.vector.tensor_copy(idx[:, j:j + 1], c.slot_token[:, bass.ds(e, 1)]).then_inc(s["idx_ready"], 1)

            def compute(pair):
                for j, e in pair:
                    ch = Chain(dve, s["e_chain"], e)
                    dve.wait_ge(s["sig_ready"], done(e))
                    dve.wait_ge(s["down_ready"], reusable(e))
                    ch.link(nc.vector.tensor_tensor(sig[:, j, :], hid(j)[:, 0:CAP0], sig[:, j, :], ALU.mult))
                    nc.vector.tensor_tensor(hT[:, j, :], hid(j)[:, CAP0:2 * CAP0], sig[:, j, :],
                                            ALU.mult).then_inc(s["hT_ready"], 1)
                for j, e in pair:
                    dve.wait_ge(s["down_ready"], done(e))
                    dve.wait_ge(s["add_done"], reusable(e))
                    nc.vector.tensor_scalar(y[:, j, :], down(j)[0:CAP0, 0:D], c.slot_weight[:, bass.ds(e, 1)], None,
                                            ALU.mult).then_inc(s["y_ready"], 1)

            last = E0 // L - 1
            indices(pairs(0)[0])
            with dve.Fori(0, last) as i:
                indices(pairs(i)[1])
                compute(pairs(i)[0])
                indices(pairs(i + 1)[0])
                compute(pairs(i)[1])
            indices(pairs(last)[1])
            compute(pairs(last)[0])
            compute(pairs(last)[1])


def stage_add_experts(nc, c):
    with ExitStack() as ctx:
        rows = ctx.enter_context(nc.sbuf_tensor("moe_in", [P, NT, D], F32))
        CH = 4
        s = open_sems(nc, ctx, "m_chain " + " ".join(f"m_loaded{n}" for n in range(CH)))
        block = ctx.enter_context(nc.Block())
        src = c.moe[0:N, :].rearrange("(n p) d -> p n d", p=P)
        W = NT // CH

        @block.sync
        def _(sp):
            for n in range(CH):
                sp.dma_start(rows[:, W * n:W * n + W, :], src[:, W * n:W * n + W, :]).then_inc(s[f"m_loaded{n}"], 16)

        @block.vector
        def _(dve):
            for n in range(CH):
                dve.wait_ge(s[f"m_loaded{n}"], 16)
                with dve.Fori(W * n, W * n + W) as t:
                    ch = Chain(dve, s["m_chain"], t)
                    ch.link(nc.vector.tensor_tensor(at_tile(c.x, t), at_tile(c.x, t), at_tile(rows, t), ALU.add))
                    nc.vector.bn_stats(at_tile(c.bn, t), at_tile(c.x, t))


def stage_l1_scores(nc, c):
    with ExitStack() as ctx:
        sb = lambda n, sh, dt=F32: ctx.enter_context(nc.sbuf_tensor(n, sh, dt))
        wg = sb("wg_c", [P, DK, D]); xn = sb("xn_c", [P, WIDE, D]); xT = sb("xT_c", [P, WIDE, DK, P])
        zeros = sb("zeros_c", [P, P]); padded = sb("padded", [S, H1, 3 * S])
        s = open_sems(nc, ctx, "c_weights c_zero xn_ready feat_ready feat_copied gate_ready gate_copied used_ready "
                      "sum_done c_chain padded_ready mixT_ready")
        block = ctx.enter_context(nc.Block())
        total = c.bank[7][0:S, 0:H1 * S]

        def feat(j): return c.bank[j][:, 0:D]
        def gate(j): return c.bank[j][:, D:2 * D]

        @block.sync
        def _(sp):
            sp.dma_start(wg[:, :, :], c.d["wg"].rearrange("(k p) n -> p k n", p=P)).then_inc(s["c_weights"], 16)

        @block.gpsimd
        def _(pool):
            give_credit(pool, s, "xn_ready feat_ready feat_copied gate_ready gate_copied used_ready", WIDE // CREDIT)
            nc.gpsimd.memset(zeros[:, :], 0.0).then_inc(s["c_zero"], 1)
            nc.gpsimd.memset(padded[:, :, :], 0.0).then_inc(s["c_zero"], 1)

        @block.tensor
        def _(pe):
            pe.wait_ge(s["c_weights"], 16)
            pe.wait_ge(s["c_zero"], 2)
            nc.tensor.matmul(total, zeros[:, 0:S], zeros[:, :], start=True, stop=False, skip_group_check=True)
            with pe.Fori(0, NT // WIDE) as i:
                for j, t in token_loop(i, WIDE):
                    pe.wait_ge(s["xn_ready"], ready(t, WIDE))
                    pe.wait_ge(s["gate_copied"], freed(t))
                    transpose_tile(nc, c, feat(j), xn[:, j, :]).then_inc(s["feat_ready"], 1)
                for j, t in token_loop(i, WIDE):
                    pe.wait_ge(s["feat_copied"], ready(t, WIDE))
                    for k in range(DK):
                        last = nc.tensor.matmul(gate(j)[:, 0:D], xT[:, j, k, :], wg[:, k, :],
                                                start=(k == 0), stop=(k == DK - 1))
                    last.then_inc(s["gate_ready"], 1)
                    for h in range(H1):
                        for b in range(2):
                            last = nc.tensor.matmul(total[:, h * S:(h + 1) * S], xT[:, j, h, 64 * b:64 * b + 64],
                                                    c.gramT[:, h, bass.ds(t * P + 64 * b, S)],
                                                    start=False, stop=False, skip_group_check=True)
                    last.then_inc(s["used_ready"], 1)
            nc.tensor.matmul(total, zeros[:, 0:S], zeros[:, :], start=False, stop=True,
                             skip_group_check=True).then_inc(s["sum_done"], 1)
            pe.wait_ge(s["padded_ready"], 1)
            pe.wait_ge(s["gate_copied"], NT + WIDE)
            for h in range(H1):
                for b in range(2):
                    last = nc.tensor.transpose(c.bank[0][:, h * P + 64 * b:h * P + 64 * b + 64],
                                               padded[:, h, S * (1 - b):S * (1 - b) + P], c.ident[0:S, 0:S])
            last.then_inc(s["mixT_ready"], 1)

        @block.scalar
        def _(act):
            with act.Fori(0, NT // WIDE) as i:
                for j, t in token_loop(i, WIDE):
                    act.wait_ge(s["feat_ready"], ready(t, WIDE))
                    act.wait_ge(s["used_ready"], freed(t))
                    act.copy(xT[:, j, :, :].rearrange("p k n -> p (k n)"), feat(j)[:, 0:D]).then_inc(s["feat_copied"], 1)
                for j, t in token_loop(i, WIDE):
                    act.wait_ge(s["gate_ready"], ready(t, WIDE))
                    nc.scalar.activation(at_tile(c.gate1, t), gate(j)[:, 0:D], ACT.Relu).then_inc(s["gate_copied"], 1)
            act.wait_ge(s["mixT_ready"], 1)
            act.copy(c.mixT[:, :, :].rearrange("p h n -> p (h n)"), c.bank[0][:, 0:H1 * P])

        @block.vector
        def _(dve):
            with dve.Fori(0, NT // WIDE) as i:
                for j, t in token_loop(i, WIDE):
                    dve.wait_ge(s["feat_ready"], freed(t))
                    normalize(nc, c, xn[:, j, :], t).then_inc(s["xn_ready"], 1)
            ch = Chain(dve, s["c_chain"])
            dve.wait_ge(s["sum_done"], 1)
            mid = padded[:, :, S:2 * S]
            ch.link(nc.vector.tensor_tensor(mid, total.rearrange("p (h n) -> p h n", h=H1),
                                            c.decay[0:S, :].rearrange("p (h n) -> p h n", h=H1), ALU.mult))
            ch.link(nc.vector.scalar_tensor_tensor(out=mid, in0=mid, scalar=-1.0, in1=mid, op0=ALU.mult, op1=ALU.max))
            nc.vector.tensor_scalar(mid, mid, 1.0, None, ALU.max).then_inc(s["padded_ready"], 1)


def stage_l1_mix(nc, c):
    with ExitStack() as ctx:
        sb = lambda n, sh, dt=F32: ctx.enter_context(nc.sbuf_tensor(n, sh, dt))
        wo = sb("wo_m", [P, DK, D]); gamma = sb("gn_gamma", [P, D]); beta = sb("gn_beta", [P, D])
        bn = sb("bn_m", [P, WIDE, 6]); mv = sb("mv_m", [P, WIDE, 2]); ve = sb("ve_m", [P, WIDE]); rs = sb("rs_m", [P, WIDE])
        y = sb("y_m", [P, WIDE, D]); yT = sb("yT_m", [P, WIDE, D])
        s = open_sems(nc, ctx, "m_weights mixed_ready var_ready rstd_ready y_ready yT_ready yT_copied out_ready "
                      "x_done mix_chain dve_passed")
        block = ctx.enter_context(nc.Block())
        LINKS = 6

        def mixed(j): return c.bank[2 * j]
        def turned(j): return c.bank[2 * j + 1][:, 0:D]
        def out(j): return c.bank[2 * j + 1][:, D:2 * D]

        @block.sync
        def _(sp):
            sp.dma_start(wo[:, :, :], c.d["wo"].rearrange("(k p) n -> p k n", p=P)).then_inc(s["m_weights"], 16)
            sp.dma_start(gamma[:, :], c.d["gng"].broadcast_to([P, D])).then_inc(s["m_weights"], 16)
            sp.dma_start(beta[:, :], c.d["gnb"].broadcast_to([P, D])).then_inc(s["m_weights"], 16)

        @block.gpsimd
        def _(pool):
            give_credit(pool, s, "mixed_ready var_ready rstd_ready y_ready yT_ready yT_copied out_ready x_done", WIDE // CREDIT)
            with pool.Fori(0, NT // WIDE) as i:
                for j, t in token_loop(i, WIDE):
                    pool.wait_ge(s["var_ready"], ready(t, WIDE))
                    nc.gpsimd.tensor_tensor(rs[:, j:j + 1], ve[:, j:j + 1], c.minus_half[:, 0:1],
                                            ALU.pow).then_inc(s["rstd_ready"], 1)

        @block.tensor
        def _(pe):
            pe.wait_ge(s["m_weights"], 48)
            with pe.Fori(0, NT // WIDE) as i:
                for j, t in token_loop(i, WIDE):
                    pe.wait_ge(s["y_ready"], freed(t))
                    for h in range(H1):
                        last = nc.tensor.matmul(mixed(j)[:, h * P:(h + 1) * P], c.mixT[:, h, :],
                                                at_tile(c.v, t)[:, h * P:(h + 1) * P], start=True, stop=True)
                    last.then_inc(s["mixed_ready"], 1)
                for j, t in token_loop(i, WIDE):
                    pe.wait_ge(s["y_ready"], ready(t, WIDE))
                    pe.wait_ge(s["x_done"], freed(t))
                    transpose_tile(nc, c, turned(j), y[:, j, :]).then_inc(s["yT_ready"], 1)
                for j, t in token_loop(i, WIDE):
                    pe.wait_ge(s["yT_copied"], ready(t, WIDE))
                    for k in range(DK):
                        last = nc.tensor.matmul(out(j)[:, 0:D], yT[:, j, k * P:(k + 1) * P], wo[:, k, :],
                                                start=(k == 0), stop=(k == DK - 1))
                    last.then_inc(s["out_ready"], 1)

        @block.scalar
        def _(act):
            with act.Fori(0, NT // WIDE) as i:
                for j, t in token_loop(i, WIDE):
                    act.wait_ge(s["yT_ready"], ready(t, WIDE))
                    act.wait_ge(s["out_ready"], freed(t))
                    act.copy(yT[:, j, :], turned(j)[:, 0:D]).then_inc(s["yT_copied"], 1)

        @block.vector
        def _(dve):
            dve.wait_ge(s["m_weights"], 48)
            with dve.Fori(0, NT // WIDE) as i:
                ch = Chain(dve, s["mix_chain"], i * LINKS)
                tiles = token_loop(i, WIDE)
                for j, t in tiles:
                    dve.wait_ge(s["mixed_ready"], ready(t, WIDE))
                    last = nc.vector.bn_stats(bn[:, j, :], mixed(j)[:, 0:D])
                ch.link(last)
                settle(dve, s["dve_passed"])
                for j, t in tiles:
                    last = nc.vector.bn_aggr(mv[:, j, :], bn[:, j, :])
                ch.link(last)
                for j, t in tiles:
                    nc.vector.tensor_scalar(ve[:, j:j + 1], mv[:, j, 1:2], GN_EPS, None, ALU.add).then_inc(s["var_ready"], 1)
                for j, t in tiles:
                    dve.wait_ge(s["yT_ready"], freed(t))
                    last = nc.vector.scalar_tensor_tensor(out=y[:, j, :], in0=mixed(j)[:, 0:D], scalar=mv[:, j, 0:1],
                                                          in1=gamma[:, :], op0=ALU.subtract, op1=ALU.mult)
                ch.link(last)
                for j, t in tiles:
                    dve.wait_ge(s["rstd_ready"], ready(t, WIDE))
                    last = nc.vector.scalar_tensor_tensor(out=y[:, j, :], in0=y[:, j, :], scalar=rs[:, j:j + 1],
                                                          in1=beta[:, :], op0=ALU.mult, op1=ALU.add)
                ch.link(last)
                for j, t in tiles:
                    nc.vector.tensor_tensor(y[:, j, :], y[:, j, :], at_tile(c.gate1, t), ALU.mult).then_inc(s["y_ready"], 1)
                for j, t in tiles:
                    dve.wait_ge(s["out_ready"], ready(t, WIDE))
                    last = nc.vector.tensor_tensor(at_tile(c.x, t), out(j)[:, 0:D], at_tile(c.x, t), ALU.add)
                ch.link(last)
                for j, t in tiles:
                    last = nc.vector.bn_stats(at_tile(c.bn, t), at_tile(c.x, t))
                ch.link(last)
                dve.sem_inc(s["x_done"], WIDE)
                assert ch.n == LINKS, ch.n


def stage_l1_think(nc, c):
    with ExitStack() as ctx:
        sb = lambda n, sh, dt=F32: ctx.enter_context(nc.sbuf_tensor(n, sh, dt))
        M = B
        FT = HID1 // P
        agg = sb("agg_w", [P, DK, D]); d1 = sb("d1_w", [P, DK, HID1]); d2 = sb("d2_w", [P, FT, D]); bcw = sb("bc_w", [P, DK, D])
        row = {n: sb("r_" + n, [M, D]) for n in ("in_gamma", "in_beta", "agg_b", "pn_gamma", "pn_beta", "d2_b", "bc_b")}
        d1b = sb("d1_b", [P, FT])
        last_x = sb("last_x", [M, D]); n1 = sb("n1", [M, D]); th = sb("thought", [M, D])
        bn = sb("bn_t", [M, 6]); mv = sb("mv_t", [M, 2]); ve = sb("ve_t", [M, 1]); rs = sb("rs_t", [M, 1])
        nT = sb("nT", [P, DK * M]); hT = sb("hT_t", [P, FT, M])
        s = open_sems(nc, ctx, "t_loaded t_last t_stored t_chain t_var t_rstd t_normed t_turned t_turn_copied t_up t_gelu "
                      "t_down t_added")
        block = ctx.enter_context(nc.Block())
        NORMS = 2 + STEPS1

        @block.sync
        def _(sp):
            n = 0
            for b in range(2):
                sp.dma_start(last_x[32 * b:32 * b + 32, :], c.x[64 * b + 63:64 * b + 64, :, :]).then_inc(s["t_last"], 16)
            for dst, name in ((agg, "agg_w"), (d1, "d1_w"), (d2, "d2_w"), (bcw, "bc_w")):
                sp.dma_start(dst[:, :, :], c.d["f1_" + name].rearrange("(k p) n -> p k n", p=P)).then_inc(s["t_loaded"], 16)
            for name, dst in row.items():
                sp.dma_start(dst[:, :], c.d["f1_" + name].broadcast_to([M, D])).then_inc(s["t_loaded"], 16)
            sp.dma_start(d1b[:, :], c.d["f1_d1_b"]).then_inc(s["t_loaded"], 16)
            sp.wait_ge(s["t_added"], 2 + STEPS1)
            sp.dma_start(c.think_rows[:, :], n1[:, :]).then_inc(s["t_stored"], 16)
            sp.wait_ge(s["t_stored"], 16)

        @block.gpsimd
        def _(pool):
            for n in range(NORMS):
                pool.wait_ge(s["t_var"], n + 1)
                nc.gpsimd.tensor_tensor(rs[:, :], ve[:, :], c.minus_half[0:M, 0:1], ALU.pow).then_inc(s["t_rstd"], 1)

        @block.tensor
        def _(pe):
            pe.wait_ge(s["t_loaded"], 16 * (5 + len(row)))
            for n in range(2 + STEPS1):
                pe.wait_ge(s["t_normed"], n + 1)
                for k in range(DK):
                    last = nc.tensor.transpose(c.bank[0][:, k * M:(k + 1) * M],
                                               (th if n == 1 + STEPS1 else n1)[:, k * P:(k + 1) * P], c.ident[0:M, 0:M])
                last.then_inc(s["t_turned"], 1)
                pe.wait_ge(s["t_turn_copied"], n + 1)
                if n in (0, 1 + STEPS1):
                    for k in range(DK):
                        last = nc.tensor.matmul(c.bank[1][0:M, 0:D], nT[:, k * M:(k + 1) * M],
                                                (bcw if n else agg)[:, k, :], start=(k == 0), stop=(k == DK - 1))
                    last.then_inc(s["t_down"], 1)
                    continue
                for f in range(FT):
                    for k in range(DK):
                        last = nc.tensor.matmul(c.bank[2][:, f * M:(f + 1) * M], d1[:, k, f * P:(f + 1) * P],
                                                nT[:, k * M:(k + 1) * M], start=(k == 0), stop=(k == DK - 1))
                last.then_inc(s["t_up"], 1)
                pe.wait_ge(s["t_gelu"], n)
                for f in range(FT):
                    last = nc.tensor.matmul(c.bank[1][0:M, 0:D], hT[:, f, :], d2[:, f, :],
                                            start=(f == 0), stop=(f == FT - 1))
                last.then_inc(s["t_down"], 1)

        @block.scalar
        def _(act):
            act.wait_ge(s["t_loaded"], 16 * (5 + len(row)))
            for n in range(2 + STEPS1):
                act.wait_ge(s["t_turned"], n + 1)
                act.copy(nT[:, :], c.bank[0][:, 0:DK * M]).then_inc(s["t_turn_copied"], 1)
                if 1 <= n <= STEPS1:
                    act.wait_ge(s["t_up"], n)
                    for f in range(FT):
                        last = nc.scalar.activation(hT[:, f, :], c.bank[2][:, f * M:(f + 1) * M], ACT.Gelu,
                                                    bias=d1b[:, f:f + 1])
                    last.then_inc(s["t_gelu"], 1)

        @block.vector
        def _(dve):
            ch = Chain(dve, s["t_chain"])
            v = nc.vector

            def norm(n, src, eps, gamma=None, beta=None):
                ch.link(v.bn_stats(bn[:, :], src[:, :]))
                ch.link(v.bn_aggr(mv[:, :], bn[:, :]))
                v.tensor_scalar(ve[:, :], mv[:, 1:2], eps, None, ALU.add).then_inc(s["t_var"], 1)
                dve.wait_ge(s["t_rstd"], n + 1)
                if gamma is None:
                    ch.link(v.tensor_scalar(n1[:, :], src[:, :], mv[:, 0:1], rs[:, :], ALU.subtract, ALU.mult))
                    return
                ch.link(v.scalar_tensor_tensor(out=n1[:, :], in0=src[:, :], scalar=mv[:, 0:1], in1=gamma[:, :],
                                               op0=ALU.subtract, op1=ALU.mult))
                v.scalar_tensor_tensor(out=n1[:, :], in0=n1[:, :], scalar=rs[:, :], in1=beta[:, :],
                                       op0=ALU.mult, op1=ALU.add).then_inc(s["t_normed"], 1)

            dve.wait_ge(s["t_last"], 32)
            dve.wait_ge(s["t_loaded"], 16 * (5 + len(row)))
            norm(0, last_x, LN_EPS)
            norm(1, n1, EPS1, row["in_gamma"], row["in_beta"])
            dve.wait_ge(s["t_down"], 1)
            v.tensor_tensor(th[:, :], c.bank[1][0:M, 0:D], row["agg_b"][:, :], ALU.add).then_inc(s["t_added"], 1)
            for n in range(1, 1 + STEPS1):
                dve.wait_ge(s["t_added"], n)
                norm(1 + n, th, EPS1, row["pn_gamma"], row["pn_beta"])
                dve.wait_ge(s["t_down"], 1 + n)
                ch.link(v.tensor_tensor(th[:, :], c.bank[1][0:M, 0:D], th[:, :], ALU.add))
                v.tensor_tensor(th[:, :], th[:, :], row["d2_b"][:, :], ALU.add).then_inc(s["t_added"], 1)
            dve.wait_ge(s["t_added"], 1 + STEPS1)
            dve.sem_inc(s["t_normed"], 1)
            dve.wait_ge(s["t_down"], 2 + STEPS1)
            v.tensor_tensor(n1[:, :], c.bank[1][0:M, 0:D], row["bc_b"][:, :], ALU.add).then_inc(s["t_added"], 1)


def stage_l1_broadcast(nc, c):
    with ExitStack() as ctx:
        sb = lambda n, sh, dt=F32: ctx.enter_context(nc.sbuf_tensor(n, sh, dt))
        gw = sb("gw_g", [P, DK, D]); row = {n: sb("g_" + n, [P, D]) for n in ("gate_b", "out_gamma", "out_beta")}
        xn = sb("xn_g", [P, WIDE, D]); xT = sb("xT_g", [P, WIDE, D]); think = sb("think", [P, WIDE, D])
        pre = sb("pre_g", [P, WIDE, D]); gate = sb("gate_g", [P, WIDE, D])
        bn = sb("bn_g", [P, WIDE, 6]); mv = sb("mv_g", [P, WIDE, 2]); ve = sb("ve_g", [P, WIDE]); rs = sb("rs_g", [P, WIDE])
        s = open_sems(nc, ctx, "g_weights xn_ready feat_ready feat_copied pre_ready "
                      "biased_ready gate_ready mixed_ready var_ready rstd_ready x_done g_chain dve_passed "
                      + " ".join(f"think_loaded{j}" for j in range(WIDE)))
        block = ctx.enter_context(nc.Block())
        LINKS = 8

        def feat(j): return c.bank[2 * j]
        def lin(j): return c.bank[2 * j + 1]

        @block.sync
        def _(sp):
            sp.dma_start(gw[:, :, :], c.d["f1_gate_w"].rearrange("(k p) n -> p k n", p=P)).then_inc(s["g_weights"], 16)
            for name, dst in row.items():
                sp.dma_start(dst[:, :], c.d["f1_" + name].broadcast_to([P, D])).then_inc(s["g_weights"], 16)
            with sp.Fori(0, NT // WIDE) as i:
                for j, t in token_loop(i, WIDE):
                    sp.wait_ge(s["mixed_ready"], freed(t))
                    for b in range(2):
                        sp.dma_start(think[64 * b:64 * b + 64, j, :],
                                     c.think_rows[bass.ds(t + NT * b, 1), :].broadcast_to([S, D])
                                     ).then_inc(s[f"think_loaded{j}"], 16)

        @block.gpsimd
        def _(pool):
            give_credit(pool, s, "xn_ready feat_ready feat_copied pre_ready biased_ready gate_ready mixed_ready "
                        "var_ready rstd_ready x_done", WIDE // CREDIT)
            with pool.Fori(0, NT // WIDE) as i:
                for j, t in token_loop(i, WIDE):
                    pool.wait_ge(s["var_ready"], ready(t, WIDE))
                    nc.gpsimd.tensor_tensor(rs[:, j:j + 1], ve[:, j:j + 1], c.minus_half[:, 0:1],
                                            ALU.pow).then_inc(s["rstd_ready"], 1)

        @block.tensor
        def _(pe):
            pe.wait_ge(s["g_weights"], 64)
            with pe.Fori(0, NT // WIDE) as i:
                for j, t in token_loop(i, WIDE):
                    pe.wait_ge(s["xn_ready"], ready(t, WIDE))
                    pe.wait_ge(s["feat_copied"], freed(t))
                    transpose_tile(nc, c, feat(j), xn[:, j, :]).then_inc(s["feat_ready"], 1)
                for j, t in token_loop(i, WIDE):
                    pe.wait_ge(s["feat_copied"], ready(t, WIDE))
                    pe.wait_ge(s["biased_ready"], freed(t))
                    for k in range(DK):
                        last = nc.tensor.matmul(lin(j)[:, 0:D], xT[:, j, k * P:(k + 1) * P], gw[:, k, :],
                                                start=(k == 0), stop=(k == DK - 1))
                    last.then_inc(s["pre_ready"], 1)

        @block.scalar
        def _(act):
            with act.Fori(0, NT // WIDE) as i:
                for j, t in token_loop(i, WIDE):
                    act.wait_ge(s["feat_ready"], ready(t, WIDE))
                    act.wait_ge(s["pre_ready"], freed(t))
                    act.copy(xT[:, j, :], feat(j)[:, 0:D]).then_inc(s["feat_copied"], 1)
                for j, t in token_loop(i, WIDE):
                    act.wait_ge(s["biased_ready"], ready(t, WIDE))
                    act.wait_ge(s["x_done"], freed(t))
                    nc.scalar.activation(gate[:, j, :], pre[:, j, :], ACT.Sigmoid).then_inc(s["gate_ready"], 1)

        @block.vector
        def _(dve):
            dve.wait_ge(s["g_weights"], 64)
            v = nc.vector
            with dve.Fori(0, NT // WIDE) as i:
                ch = Chain(dve, s["g_chain"], i * LINKS)
                for j, t in token_loop(i, WIDE):
                    dve.wait_ge(s["feat_ready"], freed(t))
                    normalize(nc, c, xn[:, j, :], t).then_inc(s["xn_ready"], 1)
                for j, t in token_loop(i, WIDE):
                    dve.wait_ge(s["pre_ready"], ready(t, WIDE))
                    dve.wait_ge(s["gate_ready"], freed(t))
                    v.tensor_tensor(pre[:, j, :], lin(j)[:, 0:D], row["gate_b"][:, :], ALU.add).then_inc(s["biased_ready"], 1)
                tiles = token_loop(i, WIDE)
                for j, t in tiles:
                    dve.wait_ge(s["gate_ready"], ready(t, WIDE))
                    dve.wait_ge(s[f"think_loaded{j}"], 32 * i + 32)
                    last = v.tensor_tensor(gate[:, j, :], gate[:, j, :], think[:, j, :], ALU.mult)
                ch.link(last)
                for j, t in tiles:
                    last = v.tensor_tensor(gate[:, j, :], gate[:, j, :], xn[:, j, :], ALU.add)
                ch.link(last)
                dve.sem_inc(s["mixed_ready"], WIDE)
                for j, t in tiles:
                    last = v.bn_stats(bn[:, j, :], gate[:, j, :])
                ch.link(last)
                settle(dve, s["dve_passed"])
                for j, t in tiles:
                    last = v.bn_aggr(mv[:, j, :], bn[:, j, :])
                ch.link(last)
                for j, t in tiles:
                    v.tensor_scalar(ve[:, j:j + 1], mv[:, j, 1:2], EPS1, None, ALU.add).then_inc(s["var_ready"], 1)
                for j, t in tiles:
                    last = v.scalar_tensor_tensor(out=gate[:, j, :], in0=gate[:, j, :], scalar=mv[:, j, 0:1],
                                                  in1=row["out_gamma"][:, :], op0=ALU.subtract, op1=ALU.mult)
                ch.link(last)
                for j, t in tiles:
                    dve.wait_ge(s["rstd_ready"], ready(t, WIDE))
                    last = v.scalar_tensor_tensor(out=gate[:, j, :], in0=gate[:, j, :], scalar=rs[:, j:j + 1],
                                                  in1=row["out_beta"][:, :], op0=ALU.mult, op1=ALU.add)
                ch.link(last)
                for j, t in tiles:
                    last = v.tensor_tensor(at_tile(c.x, t), gate[:, j, :], at_tile(c.x, t), ALU.add)
                ch.link(last)
                for j, t in tiles:
                    last = v.bn_stats(at_tile(c.bn, t), at_tile(c.x, t))
                ch.link(last)
                dve.sem_inc(s["x_done"], WIDE)
                assert ch.n == LINKS, ch.n


def stage_l2_attention(nc, c):
    with ExitStack() as ctx:
        sb = lambda n, sh, dt=F32: ctx.enter_context(nc.sbuf_tensor(n, sh, dt))
        HP = H2 // 2
        SC = H2 * S
        wdq = sb("wdq", [P, DK, QC]); wq = sb("wq_abs", [QC, H2, P]); wvo = sb("wvo", [P, HP, D])
        seg_i = sb("seg_i", [P, NT], I32); seg = sb("seg", [P, NT]); seg_lo = sb("seg_lo", [P, NT])
        xn = sb("xn_l", [P, LANES, D]); xT = sb("xT_l", [P, LANES, D]); qcT = sb("qcT", [QC, LANES, P])
        q = sb("q_l", [P, LANES, H2, P]); rot = sb("rot_l", [P, LANES, H2, P])
        key = sb("key_l", [P, LANES, P]); kv2 = sb("kv2", [P, LANES, 2, P])
        drop = sb("drop_l", [P, LANES, S]); sc = sb("sc_l", [P, LANES, H2, S]); scT = sb("scT_l", [P, LANES, HP, P])
        mx = sb("mx_l", [P, LANES, H2]); sm = sb("sm_l", [P, LANES, H2])
        rd = sb("rd_l", [P, LANES, HP, P])
        s = open_sems(nc, ctx, "l_weights l_zero l_pre l_folded l_seg xn_ready feat_ready feat_copied qc_ready qc_copied q_ready "
                      "nope_copied rope_done rope_added kv_ready key_ready scores_ready max_ready shifted_ready exp_ready sum_ready prob_ready turned_ready "
                      "turned_copied read_ready read_copied out_ready x_done drop_chain masked summed add_chain seg_chain")
        scale = float(np.float32(1.0) / np.sqrt(np.float32(HD2 + R2)))

        def bank(j, n): return c.bank[4 * j + n]

        with ExitStack() as pre:
            wt = lambda n, sh: pre.enter_context(nc.sbuf_tensor(n, sh, F32))
            wuqT = wt("wuqT", [P, H2, QC]); wukT = wt("wukT", [P, H2, KVC]); wuvT = wt("wuvT", [P, H2, KVC])
            wqr = wt("wqr", [QC, H2, R2]); wo = wt("wo_l", [P, H2, D])
            block = pre.enter_context(nc.Block())

            @block.sync
            def _(sp):
                for dst, src in ((wdq[:, :, :], c.d["wdq"].rearrange("(k p) n -> p k n", p=P)), (wuqT[:, :, :], c.d["wuqT"]),
                                 (wukT[:, :, :], c.d["wukT"]), (wuvT[:, :, :], c.d["wuvT"]), (wqr[:, :, :], c.d["wqr"]),
                                 (wo[:, :, :], c.d["wo2"]), (seg_i[:, :], c.d["seg"])):
                    sp.dma_start(dst, src).then_inc(s["l_weights"], 16)
                sp.wait_ge(s["l_weights"], 112)

            @block.tensor
            def _(pe):
                pe.wait_ge(s["l_weights"], 112)
                for h in range(H2):
                    last = nc.tensor.matmul(c.bank[h // 8][0:QC, (h % 8) * KVC:(h % 8 + 1) * KVC], wuqT[:, h, :],
                                            wukT[:, h, :], start=True, stop=True)
                for h in range(H2):
                    r = slice(64 * (h % 2), 64 * (h % 2) + 64)
                    hp = h // 2
                    last = nc.tensor.matmul(c.bank[2 + hp // 2][r, (hp % 2) * D:(hp % 2 + 1) * D], wuvT[:, h, :],
                                            wo[:, h, :], start=True, stop=True)
                last.then_inc(s["l_pre"], 1)

            @block.scalar
            def _(act):
                act.wait_ge(s["l_weights"], 112)
                act.mul(wq[:, :, KVC:P], wqr[:, :, :], scale)
                act.wait_ge(s["l_pre"], 1)
                for n in range(2):
                    act.mul(wq[:, 8 * n:8 * n + 8, 0:KVC],
                            c.bank[n][0:QC, :].rearrange("p (h n) -> p h n", h=8), scale)
                for n in range(4):
                    act.copy(wvo[:, 2 * n:2 * n + 2, :].rearrange("p h n -> p (h n)"), c.bank[2 + n][:, :])

            @block.vector
            def _(dve):
                ch = Chain(dve, s["seg_chain"])
                dve.wait_ge(s["l_weights"], 112)
                ch.link(nc.vector.tensor_copy(seg[:, :], seg_i[:, :]))
                nc.vector.tensor_scalar(seg_lo[:, :], seg[:, :], float(LOOKBACK), None, ALU.subtract)

        block = ctx.enter_context(nc.Block())

        def run(eng, ahead, behind, after=lambda t, j: None):
            ahead(0, 0)
            after(0, 0)
            with eng.Fori(0, NT // 2 - 1) as i:
                for j in range(2):
                    ahead(2 * i + j + 1, 1 - j)
                    behind(2 * i + j, j)
                    after(2 * i + j + 1, 1 - j)
            ahead(NT - 1, 1)
            behind(NT - 2, 0)
            after(NT - 1, 1)
            behind(NT - 1, 1)

        def halves(t, n):
            return 2 * t + n + 1 + 2 * CREDIT

        def heads(n):
            return slice(n * HP, n * HP + HP)

        @block.gpsimd
        def _(pool):
            give_credit(pool, s, "xn_ready feat_ready feat_copied qc_ready qc_copied q_ready nope_copied "
                        "kv_ready key_ready read_ready read_copied out_ready x_done")
            give_credit(pool, s, "rope_done rope_added scores_ready max_ready shifted_ready exp_ready sum_ready prob_ready "
                        "turned_ready turned_copied", 2)
            nc.gpsimd.memset(kv2[:, :, :, :], 0.0).then_inc(s["l_zero"], 1)
            flat = lambda ap: ap.rearrange("p h n -> p (h n)")

            def key_copy(t, j):
                pool.wait_ge(s["rope_added"], halves(t - 1, 1))
                pool.wait_ge(s["scores_ready"], halves(t - LANES, 1))
                nc.gpsimd.tensor_copy(key[:, j, :], c.keysT[:, bass.ds(t * P, P)]).then_inc(s["key_ready"], 1)

            def softmax(t, j):
                pool.wait_ge(s["rope_added"], halves(t, 1))
                for n in range(2):
                    pool.wait_ge(s["max_ready"], halves(t, n))
                    nc.gpsimd.tensor_tensor(sc[:, j, heads(n), :], sc[:, j, heads(n), :],
                                            mx[:, j, heads(n)].unsqueeze(2).broadcast_to([P, HP, S]),
                                            ALU.subtract).then_inc(s["shifted_ready"], 1)
                for n in range(2):
                    pool.wait_ge(s["sum_ready"], halves(t, n))
                    nc.gpsimd.tensor_tensor(sc[:, j, heads(n), :], sc[:, j, heads(n), :],
                                            sm[:, j, heads(n)].unsqueeze(2).broadcast_to([P, HP, S]),
                                            ALU.mult).then_inc(s["prob_ready"], 1)

            def rope_add(t, j):
                pool.wait_ge(s["key_ready"], ready(t))
                pool.wait_ge(s["prob_ready"], halves(t - 1, 1))
                for n in range(2):
                    pool.wait_ge(s["rope_done"], halves(t, n))
                    hs = slice(8 * n, 8 * n + 8)
                    nc.gpsimd.tensor_tensor(q[64:P, j, hs, :], q[64:P, j, hs, :], rot[64:P, j, hs, :],
                                            ALU.add).then_inc(s["rope_added"], 1)

            run(pool, key_copy, softmax, rope_add)

        @block.tensor
        def _(pe):
            def front(t, j):
                pe.wait_ge(s["xn_ready"], ready(t))
                pe.wait_ge(s["read_copied"], freed(t))
                transpose_tile(nc, c, bank(j, 0), xn[:, j, :]).then_inc(s["feat_ready"], 1)
                pe.wait_ge(s["feat_copied"], ready(t))
                for k in range(DK):
                    last = nc.tensor.matmul(bank(j, 1)[0:QC, 0:P], wdq[:, k, :], xT[:, j, k * P:(k + 1) * P],
                                            start=(k == 0), stop=(k == DK - 1))
                last.then_inc(s["qc_ready"], 1)
                pe.wait_ge(s["qc_copied"], ready(t))
                pe.wait_ge(s["x_done"], freed(t))
                for h in range(H2):
                    last = nc.tensor.matmul(bank(j, h // 4)[:, (h % 4) * P:(h % 4 + 1) * P], wq[:, h, :],
                                            qcT[:, j, :], start=True, stop=True)
                last.then_inc(s["q_ready"], 1)

            def back(t, j):
                for n in range(2):
                    pe.wait_ge(s["prob_ready"], halves(t, n))
                    for m in range(4):
                        hp = 4 * n + m
                        last = nc.tensor.transpose(bank(j, 2 + n)[:, m * P:(m + 1) * P],
                                                   sc[:, j, 2 * hp:2 * hp + 2, :].rearrange("p h n -> p (h n)"), c.ident)
                    last.then_inc(s["turned_ready"], 1)
                pe.wait_ge(s["kv_ready"], ready(t))
                for n in range(2):
                    pe.wait_ge(s["turned_copied"], halves(t, n))
                    hps = slice(4 * n, 4 * n + 4)
                    for b in range(2):
                        last = nc.tensor.matmul(bank(j, b)[:, :].rearrange("p (h q) -> p h q", h=HP)[:, hps, :],
                                                kv2[:, j, b, :], scT[:, j, hps, 64 * b:64 * b + 64], start=True, stop=True)
                last.then_inc(s["read_ready"], 1)
                pe.wait_ge(s["read_copied"], ready(t))
                for hp in range(HP):
                    last = nc.tensor.matmul(bank(j, 2)[:, 0:D], rd[:, j, hp, :], wvo[:, hp, :],
                                            start=(hp == 0), stop=(hp == HP - 1))
                last.then_inc(s["out_ready"], 1)

            def scores(t, j):
                pe.wait_ge(s["nope_copied"], ready(t))
                pe.wait_ge(s["rope_done"], halves(t, 1))
                pe.wait_ge(s["key_ready"], ready(t))
                for h in range(H2):
                    if h % 8 == 0:
                        pe.wait_ge(s["rope_added"], halves(t, h // 8))
                    for b in range(2):
                        r = slice(64 * b, 64 * b + 64)
                        last = nc.tensor.matmul(bank(j, h // 8)[r, (h % 8) * S:(h % 8 + 1) * S],
                                                q[:, j, h, r], key[:, j, r], start=True, stop=True)
                    if h % 8 == 7:
                        last.then_inc(s["scores_ready"], 1)

            run(pe, front, back, scores)

        @block.scalar
        def _(act):
            def front(t, j):
                act.wait_ge(s["feat_ready"], ready(t))
                act.wait_ge(s["qc_ready"], freed(t))
                act.copy(xT[:, j, :], bank(j, 0)[:, 0:D]).then_inc(s["feat_copied"], 1)
                act.wait_ge(s["qc_ready"], ready(t))
                act.wait_ge(s["q_ready"], freed(t))
                act.copy(qcT[:, j, :], bank(j, 1)[0:QC, 0:P]).then_inc(s["qc_copied"], 1)

            def exponent(t, j):
                for n in range(2):
                    act.wait_ge(s["shifted_ready"], halves(t, n))
                    nc.scalar.activation(sc[:, j, heads(n), :], sc[:, j, heads(n), :], ACT.Exp).then_inc(s["exp_ready"], 1)

            def nope(t, j):
                act.wait_ge(s["q_ready"], ready(t))
                act.wait_ge(s["scores_ready"], halves(t - LANES, 1))
                for n in range(4):
                    last = act.copy(q[0:64, j, 4 * n:4 * n + 4, :].rearrange("p h n -> p (h n)"), bank(j, n)[0:64, :])
                last.then_inc(s["nope_copied"], 1)
                act.wait_ge(s["read_ready"], freed(t))
                for b in range(2):
                    for r in range(2):
                        last = act.copy(kv2[64 * r:64 * r + 64, j, b, 64 * r:64 * r + 64],
                                        at_tile(c.kvc, t)[64 * b:64 * b + 64, :])
                last.then_inc(s["kv_ready"], 1)

            def back(t, j):
                act.wait_ge(s["read_ready"], freed(t))
                for n in range(2):
                    act.wait_ge(s["turned_ready"], halves(t, n))
                    act.copy(scT[:, j, 4 * n:4 * n + 4, :].rearrange("p h n -> p (h n)"),
                             bank(j, 2 + n)[:, :]).then_inc(s["turned_copied"], 1)
                act.wait_ge(s["read_ready"], ready(t))
                act.wait_ge(s["out_ready"], freed(t))
                for b in range(2):
                    last = act.copy(rd[:, j, :, 64 * b:64 * b + 64],
                                    bank(j, b)[:, :].rearrange("p (h q) -> p h q", h=HP))
                last.then_inc(s["read_copied"], 1)

            act.wait_ge(s["l_zero"], 1)
            front(0, 0)
            nope(0, 0)
            with act.Fori(0, NT // 2 - 1) as i:
                for j in range(2):
                    front(2 * i + j + 1, 1 - j)
                    exponent(2 * i + j, j)
                    back(2 * i + j, j)
                    nope(2 * i + j + 1, 1 - j)
            front(NT - 1, 1)
            exponent(NT - 2, 0)
            back(NT - 2, 0)
            nope(NT - 1, 1)
            exponent(NT - 1, 1)
            back(NT - 1, 1)

        @block.vector
        def _(dve):
            v = nc.vector

            def front(t, j):
                ch = Chain(dve, s["drop_chain"], 3 * t)
                dve.wait_ge(s["feat_ready"], freed(t))
                normalize(nc, c, xn[:, j, :], t).then_inc(s["xn_ready"], 1)
                ch.link(v.tensor_scalar(drop[:, j, :], c.iota, seg[:, bass.ds(t, 1)], None, ALU.is_le))
                ch.link(v.scalar_tensor_tensor(out=drop[:, j, :], in0=c.iota, scalar=seg_lo[:, bass.ds(t, 1)],
                                               in1=drop[:, j, :], op0=ALU.is_ge, op1=ALU.mult))
                ch.link(v.tensor_scalar(drop[:, j, :], drop[:, j, :], 1.0, -NEG, ALU.subtract, ALU.mult))

            def rope(t, j, n):
                if n == 0:
                    dve.wait_ge(s["q_ready"], ready(t))
                    dve.wait_ge(s["scores_ready"], halves(t - LANES, 1))
                for m in (2 * n, 2 * n + 1):
                    hs = slice(4 * m, 4 * m + 4)
                    raw = bank(j, m)[:, :].rearrange("p (h n) -> p h n", h=4)
                    tab = lambda ap, a, b: ap[a:b, :].unsqueeze(1).broadcast_to([b - a, 4, P])
                    v.tensor_tensor(q[64:P, j, hs, :], raw[64:P], tab(c.cos, 64, P), ALU.mult)
                    v.tensor_tensor(rot[96:P, j, hs, :], raw[64:96], tab(c.sin, 64, 96), ALU.mult)
                    last = v.tensor_tensor(rot[64:96, j, hs, :], raw[96:P], tab(c.sin, 96, P), ALU.mult)
                last.then_inc(s["rope_done"], 1)

            def maxima(t, j, n):
                ch = Chain(dve, s["masked"], 2 * t + n)
                dve.wait_ge(s["scores_ready"], halves(t, n))
                dve.wait_ge(s["turned_ready"], halves(t - LANES, n))
                ch.link(v.tensor_tensor(sc[:, j, heads(n), :], bank(j, n)[:, :].rearrange("p (h n) -> p h n", h=HP),
                                        drop[:, j, :].unsqueeze(1).broadcast_to([P, HP, S]), ALU.add))
                v.tensor_reduce(mx[:, j, heads(n)], sc[:, j, heads(n), :], AX.X, ALU.max).then_inc(s["max_ready"], 1)

            def sums(t, j, n):
                ch = Chain(dve, s["summed"], 2 * t + n)
                dve.wait_ge(s["exp_ready"], halves(t, n))
                ch.link(v.tensor_reduce(sm[:, j, heads(n)], sc[:, j, heads(n), :], AX.X, ALU.add))
                v.reciprocal(sm[:, j, heads(n)], sm[:, j, heads(n)]).then_inc(s["sum_ready"], 1)

            def back(t, j):
                dve.wait_ge(s["out_ready"], ready(t))
                add_and_stats(nc, c, Chain(dve, s["add_chain"], 2 * t), t, bank(j, 2)[:, 0:D], 1.0, s["x_done"])

            def step(t, j):
                front(t + 1, 1 - j)
                for n in range(2):
                    maxima(t, j, n)
                for n in range(2):
                    sums(t, j, n)
                for n in range(2):
                    rope(t + 1, 1 - j, n)
                back(t, j)

            front(0, 0)
            rope(0, 0, 0)
            rope(0, 0, 1)
            with dve.Fori(0, NT // 2 - 1) as i:
                step(2 * i, 0)
                step(2 * i + 1, 1)
            step(NT - 2, 0)
            for n in range(2):
                maxima(NT - 1, 1, n)
            for n in range(2):
                sums(NT - 1, 1, n)
            back(NT - 1, 1)


FT2 = -(-HID2 // P)


def stage_l2_ternary(nc, c):
    with ExitStack() as ctx:
        sb = lambda n, sh, dt=F32: ctx.enter_context(nc.sbuf_tensor(n, sh, dt))
        HW = FT2 * P
        w12 = sb("w12", [P, DK, 2, HW], BF16); w3 = sb("w3q", [P, FT2, D], BF16)
        xn = sb("xn_t", [P, LANES, D]); xT = sb("xT_t", [P, LANES, D]); rest = sb("rest_t", [P, LANES, D])
        low = sb("low_t", [P, LANES, D], BF16); sig = sb("sig_t", [P, LANES, HID2]); hT = sb("hT_tern", [P, LANES, HW])
        hrest = sb("hrest_t", [P, LANES, HW]); hlow = sb("hlow_t", [P, LANES, HW], BF16)
        s = open_sems(nc, ctx, "q_loaded q_zero q_sums q_total q_chain pad_set xn_ready feat_ready feat_copied rest_ready "
                      "low_ready up_ready sig_ready h_ready turned_ready hT_ready hrest_ready hlow_ready down_ready "
                      "x_done add_chain")
        with ExitStack() as pre:
            wt = lambda n, sh: pre.enter_context(nc.sbuf_tensor(n, sh, F32))
            raw12 = wt("raw12", [P, DK, 2, HW]); raw3 = wt("raw3", [P, FT2, D]); tmp = wt("tmp_q", [P, DK * 2 * HW])
            ab = wt("abs_sums", [P, 3]); ones = wt("ones_q", [P, P]); inv = wt("inv_q", [P, 3])
            block = pre.enter_context(nc.Block())

            @block.sync
            def _(sp):
                sp.wait_ge(s["q_zero"], 3)
                for n, name in enumerate(("t1", "t2")):
                    sp.dma_start(raw12[:, :, n, 0:HID2], c.d[name].rearrange("(k p) n -> p k n", p=P)).then_inc(s["q_loaded"], 16)
                full = HID2 // P
                sp.dma_start(raw3[:, 0:full, :], c.d["t3"][0:full * P, :].rearrange("(k p) n -> p k n", p=P)).then_inc(s["q_loaded"], 16)
                sp.dma_start(raw3[0:HID2 - full * P, full, :], c.d["t3"][full * P:HID2, :]).then_inc(s["q_loaded"], 16)

            @block.gpsimd
            def _(pool):
                nc.gpsimd.memset(raw12[:, :, :, HID2:HW], 0.0).then_inc(s["q_zero"], 1)
                nc.gpsimd.memset(raw3[:, FT2 - 1, :], 0.0).then_inc(s["q_zero"], 1)
                nc.gpsimd.memset(ones[:, :], 1.0).then_inc(s["q_zero"], 1)

            @block.tensor
            def _(pe):
                pe.wait_ge(s["q_zero"], 3)
                pe.wait_ge(s["q_sums"], 3)
                nc.tensor.matmul(c.bank[0][:, 0:3], ones[:, :], ab[:, :], start=True, stop=True).then_inc(s["q_total"], 1)

            @block.vector
            def _(dve):
                v = nc.vector
                ch = Chain(dve, s["q_chain"])
                dve.wait_ge(s["q_loaded"], 64)
                for n in range(2):
                    v.tensor_reduce(ab[:, n:n + 1], raw12[:, :, n, :], AX.XY, ALU.add,
                                    apply_absolute_value=True).then_inc(s["q_sums"], 1)
                v.tensor_reduce(ab[:, 2:3], raw3[:, :, :], AX.XY, ALU.add,
                                apply_absolute_value=True).then_inc(s["q_sums"], 1)
                dve.wait_ge(s["q_total"], 1)
                ch.link(v.tensor_scalar(inv[:, :], c.bank[0][:, 0:3], 1.0 / (HID2 * D), EPS2, ALU.mult, ALU.add))
                ch.link(v.reciprocal(inv[:, :], inv[:, :]))
                for n in range(3):
                    src = raw12[:, :, n, :] if n < 2 else raw3[:, :, :]
                    dst = w12[:, :, n, :] if n < 2 else w3[:, :, :]
                    a, b = (DK, HW) if n < 2 else (FT2, D)
                    t3 = tmp[:, 0:a * b].rearrange("p (a b) -> p a b", a=a)
                    ch.link(v.tensor_scalar(t3, src, inv[:, n:n + 1], -0.5, ALU.mult, ALU.is_lt))
                    ch.link(v.tensor_scalar(src, src, inv[:, n:n + 1], 0.5, ALU.mult, ALU.is_gt))
                    ch.link(v.tensor_tensor(dst, src, t3, ALU.subtract))

        block = ctx.enter_context(nc.Block())

        def feat(j): return c.bank[4 * j]

        def up_chunks(j):
            rest_of = HID2 - 512
            mixed = c.bank[4 * j + 2]
            return [(0, slice(0, 512), c.bank[4 * j + 1][:, :]), (0, slice(512, HID2), mixed[:, 0:rest_of]),
                    (1, slice(0, 512), c.bank[4 * j + 3][:, :]), (1, slice(512, HID2), mixed[:, rest_of:2 * rest_of])]

        def turned(j, f):
            bank = c.bank[4 * j + (1 if f < 4 else 3)]
            return bank[0:min(P, HID2 - f * P), (f % 4) * P:(f % 4 + 1) * P]

        def out(j):
            return c.bank[4 * j + 2][:, 0:D]

        def run(eng, before, step, step_before_last, last_step):
            before()
            with eng.Fori(0, NT // 2 - 1) as i:
                for j in range(2):
                    step(2 * i + j, j)
            step_before_last(NT - 2, 0)
            last_step(NT - 1, 1)

        @block.gpsimd
        def _(pool):
            give_credit(pool, s, "xn_ready feat_ready feat_copied rest_ready low_ready up_ready sig_ready h_ready "
                        "turned_ready hT_ready hrest_ready hlow_ready down_ready x_done")
            nc.gpsimd.memset(hT[:, :, :], 0.0).then_inc(s["pad_set"], 1)

            def x_low(t, j):
                pool.wait_ge(s["rest_ready"], ready(t))
                pool.wait_ge(s["up_ready"], freed(t))
                nc.gpsimd.tensor_tensor(low[:, j, :], rest[:, j, :], upper(rest[:, j, :]),
                                        ALU.subtract).then_inc(s["low_ready"], 1)

            def hidden_low(t, j):
                pool.wait_ge(s["hrest_ready"], ready(t))
                pool.wait_ge(s["down_ready"], freed(t))
                nc.gpsimd.tensor_tensor(hlow[:, j, :], hrest[:, j, :], upper(hrest[:, j, :]),
                                        ALU.subtract).then_inc(s["hlow_ready"], 1)

            def before():
                x_low(0, 0)
                x_low(1, 1)

            def step(t, j):
                hidden_low(t, j)
                x_low(t + 2, j)

            run(pool, before, step, hidden_low, hidden_low)

        @block.tensor
        def _(pe):
            def features(t, j):
                pe.wait_ge(s["xn_ready"], ready(t))
                pe.wait_ge(s["feat_copied"], freed(t))
                transpose_tile(nc, c, feat(j), xn[:, j, :]).then_inc(s["feat_ready"], 1)

            def upward(t, j):
                pe.wait_ge(s["low_ready"], ready(t))
                pe.wait_ge(s["x_done"], freed(t))
                for n, hidden, dst in up_chunks(j):
                    for k in range(DK):
                        cols = slice(k * P, (k + 1) * P)
                        for part, lhsT in enumerate((upper(xT[:, j, cols]), upper(rest[:, j, cols]), low[:, j, cols])):
                            last = nc.tensor.matmul(dst, lhsT, w12[:, k, n, hidden], start=(k == 0 and part == 0),
                                                    stop=(k == DK - 1 and part == 2))
                last.then_inc(s["up_ready"], 1)

            def turn(t, j):
                pe.wait_ge(s["h_ready"], ready(t))
                for f in range(FT2):
                    last = nc.tensor.transpose(turned(j, f), sig[:, j, f * P:min(HID2, f * P + P)], c.ident)
                last.then_inc(s["turned_ready"], 1)

            def downward(t, j):
                pe.wait_ge(s["hlow_ready"], ready(t))
                for f in range(FT2):
                    cols = slice(f * P, (f + 1) * P)
                    for part, lhsT in enumerate((upper(hT[:, j, cols]), upper(hrest[:, j, cols]), hlow[:, j, cols])):
                        last = nc.tensor.matmul(out(j), lhsT, w3[:, f, :], start=(part == 0 and f == 0),
                                                stop=(part == 2 and f == FT2 - 1))
                last.then_inc(s["down_ready"], 1)

            def before():
                features(0, 0)
                features(1, 1)
                upward(0, 0)

            def step(t, j):
                turn(t, j)
                upward(t + 1, 1 - j)
                features(t + 2, j)
                downward(t, j)

            def step_before_last(t, j):
                turn(t, j)
                upward(t + 1, 1 - j)
                downward(t, j)

            def last_step(t, j):
                turn(t, j)
                downward(t, j)

            run(pe, before, step, step_before_last, last_step)

        @block.scalar
        def _(act):
            def feat_copy(t, j):
                act.wait_ge(s["feat_ready"], ready(t))
                act.wait_ge(s["up_ready"], freed(t))
                act.copy(xT[:, j, :], feat(j)[:, 0:D]).then_inc(s["feat_copied"], 1)

            def sigmoid(t, j):
                act.wait_ge(s["up_ready"], ready(t))
                act.wait_ge(s["turned_ready"], freed(t))
                for n, hidden, src in up_chunks(j)[0:2]:
                    last = nc.scalar.activation(sig[:, j, hidden], src, ACT.Sigmoid)
                last.then_inc(s["sig_ready"], 1)

            def turned_copy(t, j):
                act.wait_ge(s["turned_ready"], ready(t))
                act.wait_ge(s["down_ready"], freed(t))
                act.copy(hT[:, j, 0:4 * P], c.bank[4 * j + 1][:, :])
                act.copy(hT[:, j, 4 * P:5 * P], turned(j, 4))
                act.copy(hT[0:HID2 - 5 * P, j, 5 * P:6 * P], turned(j, 5)).then_inc(s["hT_ready"], 1)

            def before():
                act.wait_ge(s["pad_set"], 1)
                feat_copy(0, 0)
                feat_copy(1, 1)
                sigmoid(0, 0)

            def step(t, j):
                turned_copy(t, j)
                sigmoid(t + 1, 1 - j)
                feat_copy(t + 2, j)

            def step_before_last(t, j):
                turned_copy(t, j)
                sigmoid(t + 1, 1 - j)

            run(act, before, step, step_before_last, turned_copy)

        @block.vector
        def _(dve):
            v = nc.vector

            def norm(t, j):
                dve.wait_ge(s["feat_ready"], freed(t))
                normalize(nc, c, xn[:, j, :], t).then_inc(s["xn_ready"], 1)

            def x_rest(t, j):
                dve.wait_ge(s["feat_copied"], ready(t))
                dve.wait_ge(s["low_ready"], freed(t))
                dve.wait_ge(s["up_ready"], freed(t))
                v.tensor_tensor(rest[:, j, :], xT[:, j, :], upper(xT[:, j, :]), ALU.subtract).then_inc(s["rest_ready"], 1)

            def hidden(t, j):
                dve.wait_ge(s["sig_ready"], ready(t))
                for n, cols, src in up_chunks(j)[2:4]:
                    last = v.tensor_tensor(sig[:, j, cols], src, sig[:, j, cols], ALU.mult)
                last.then_inc(s["h_ready"], 1)

            def hidden_rest(t, j):
                dve.wait_ge(s["hT_ready"], ready(t))
                dve.wait_ge(s["down_ready"], freed(t))
                v.tensor_tensor(hrest[:, j, :], hT[:, j, :], upper(hT[:, j, :]), ALU.subtract).then_inc(s["hrest_ready"], 1)

            def add(t, j):
                dve.wait_ge(s["down_ready"], ready(t))
                add_and_stats(nc, c, Chain(dve, s["add_chain"], 2 * t), t, out(j), 1.0, s["x_done"])

            def before():
                norm(0, 0)
                norm(1, 1)
                x_rest(0, 0)
                x_rest(1, 1)
                hidden(0, 0)

            def step(t, j):
                norm(t + 2, j)
                hidden_rest(t, j)
                hidden(t + 1, 1 - j)
                x_rest(t + 2, j)
                add(t, j)

            def step_before_last(t, j):
                hidden_rest(t, j)
                hidden(t + 1, 1 - j)
                add(t, j)

            def last_step(t, j):
                hidden_rest(t, j)
                add(t, j)

            run(dve, before, step, step_before_last, last_step)


def stage_l3_split(nc, c):
    with ExitStack() as ctx:
        sb = lambda n, sh, dt=F32: ctx.enter_context(nc.sbuf_tensor(n, sh, dt))
        L = 4
        src = sb("src_s", [P, L, 2 * D]); rest = sb("rest_s", [P, L, 2 * D])
        parts = sb("parts_s", [P, L, 3, 2 * D], BF16)
        ctx_loaded = [f"ctx_loaded{j}" for j in range(L)]
        stored = [f"stored{j}" for j in range(L)]
        s = open_sems(nc, ctx, "scaled xn_ready high_ready rest_ready mid_ready low_ready turned_ready turned_copied "
                      + " ".join(ctx_loaded + stored))
        block = ctx.enter_context(nc.Block())

        def done(t):
            return t + 1 + L

        def before(t):
            return t + 1

        def lanes(i):
            return [(j, i * L + j) for j in range(L)]

        @block.sync
        def _(sp):
            def load(t, j):
                sp.dma_start(src[:, j, D:2 * D], c.d["ctx"][bass.ds(t * P, P), :]).then_inc(s[ctx_loaded[j]], 16)

            def step(i, last=False):
                for j, t in lanes(i):
                    sp.wait_ge(s["mid_ready"], done(t))
                    sp.wait_ge(s["low_ready"], done(t))
                    if not last:
                        sp.wait_ge(s["turned_ready"], done(t))
                        load(t + L, j)
                    for n, dst in enumerate((c.q_parts, c.k_parts)):
                        for a in range(3):
                            sp.dma_start(dst[a, :, bass.ds(t * 2 * H3, 2 * H3), :].rearrange("c h l -> h c l"),
                                         parts[:, j, a, n * D:(n + 1) * D]).then_inc(s[stored[j]], 16)

            for j in range(L):
                load(j, j)
            with sp.Fori(0, NT // L - 1) as i:
                step(i)
            step(NT // L - 1, last=True)
            for j in range(L):
                sp.wait_ge(s[stored[j]], 96 * (NT // L) + 96)

        @block.gpsimd
        def _(pool):
            for name in ("xn_ready", "high_ready", "rest_ready", "mid_ready", "low_ready", "turned_ready", "turned_copied"):
                pool.sem_inc(s[name], L)
            for name in stored:
                pool.sem_inc(s[name], 96)
            with pool.Fori(0, NT // L) as i:
                for j, t in lanes(i):
                    pool.wait_ge(s["rest_ready"], done(t))
                    pool.wait_ge(s[stored[j]], 96 * i + 96)
                    nc.gpsimd.tensor_tensor(parts[:, j, 2, :], rest[:, j, :], upper(rest[:, j, :]),
                                            ALU.subtract).then_inc(s["low_ready"], 1)

        @block.tensor
        def _(pe):
            with pe.Fori(0, NT // L) as i:
                for j, t in lanes(i):
                    pe.wait_ge(s[ctx_loaded[j]], loaded(i))
                    pe.wait_ge(s["turned_copied"], before(t))
                    transpose_tile(nc, c, c.bank[j], src[:, j, D:2 * D]).then_inc(s["turned_ready"], 1)

        @block.scalar
        def _(act):
            with act.Fori(0, NT // L) as i:
                for j, t in lanes(i):
                    act.wait_ge(s["turned_ready"], done(t))
                    act.copy(c.vT[:, :, bass.ds(t * P, P)], half(c.bank[j][:, 0:D])).then_inc(s["turned_copied"], 1)
                    act.wait_ge(s["xn_ready"], done(t))
                    act.wait_ge(s[ctx_loaded[j]], loaded(i))
                    act.wait_ge(s[stored[j]], 96 * i + 96)
                    act.copy(parts[:, j, 0, :], upper(src[:, j, :])).then_inc(s["high_ready"], 1)
                for j, t in lanes(i):
                    act.wait_ge(s["rest_ready"], done(t))
                    act.copy(parts[:, j, 1, :], upper(rest[:, j, :])).then_inc(s["mid_ready"], 1)

        @block.vector
        def _(dve):
            v = nc.vector
            v.tensor_scalar(c.rstd[:, :], c.rstd[:, :], float(np.float32(DQ3) ** np.float32(-0.5)), None,
                            ALU.mult).then_inc(s["scaled"], 1)
            dve.wait_ge(s["scaled"], 1)
            with dve.Fori(0, NT // L) as i:
                for j, t in lanes(i):
                    dve.wait_ge(s["high_ready"], before(t))
                    dve.wait_ge(s["rest_ready"], before(t))
                    normalize(nc, c, src[:, j, 0:D], t).then_inc(s["xn_ready"], 1)
                for j, t in lanes(i):
                    dve.wait_ge(s["xn_ready"], done(t))
                    dve.wait_ge(s[ctx_loaded[j]], loaded(i))
                    dve.wait_ge(s["mid_ready"], before(t))
                    dve.wait_ge(s["low_ready"], before(t))
                    v.tensor_tensor(rest[:, j, :], src[:, j, :], upper(src[:, j, :]),
                                    ALU.subtract).then_inc(s["rest_ready"], 1)


def stage_l3_attention(nc, c):
    with ExitStack() as ctx:
        sb = lambda n, sh, dt=F32: ctx.enter_context(nc.sbuf_tensor(n, sh, dt))
        R = 9 * DQ3
        AH = DQ3 + 1
        BUF = 4
        LEAD = 2
        LAG = 4
        NS, NT_, NE = 2, 2, 8
        UC = NE
        q = sb("q_3", [R + 2, BUF, H3 * D], BF16); k = sb("k_3", [R + 2, BUF, H3 * D], BF16)
        val = sb("val_3", [P, BUF, DK, H3, 3, AH], BF16); vrest = sb("vrest_3", [P, 2, DK, H3, DQ3])
        nmax = sb("nmax_3", [P, BUF, 2 * H3])
        rows = sb("rows_3", [2 * H3, BUF, 2, P], BF16)
        eT = sb("eT_3", [P, NE, DK, D]); rest = sb("rest_3", [P, NE, DK, D]); low = sb("low_3", [P, NE, DK, D], BF16)
        total = sb("total_r3", [P, 2, 2 * H3, AH])
        rec = sb("rec_3", [P, 2, 2 * H3]); on = sb("on_3", [P, 2, 2, S]); gam = sb("gam_3", [P, 1])
        qk_loaded = [f"qk_loaded{b}" for b in range(BUF)]
        rows_loaded = [f"rows_loaded{b}" for b in range(BUF)]
        s = open_sems(nc, ctx, "gamma_loaded ones_set row_ones_set val_copied scores_ready max_ready max_turned max_split turned_ready "
                      "exp_ready rest_ready low_ready val_rest val_low used_ready batch_read tile_turned x_done split_chain norm_chain add_chain " + " ".join(qk_loaded + rows_loaded))
        block = ctx.enter_context(nc.Block())
        scores = lambda h: c.bank[h % NS]
        scoresT = lambda h: c.bank[NS + h % NT_]
        readout = lambda b: c.bank[NS + NT_ + b % 2][:, 0:2 * H3 * 3 * AH]
        final = c.bank[6][:, 0:D]
        max_rows = c.bank[7][0:2 * H3, 0:P]

        def unit_ready(g, b, h):
            return (g * BUF + b) * H3 + h + 1 + UC

        def batch_ready(g, b):
            return ready(g * BUF + b)

        def at(g, b, ahead=0):
            return g + (b + ahead) // BUF, (b + ahead) % BUF

        def exists(g, b, ahead=0):
            return not isinstance(g, int) or 0 <= g * BUF + b + ahead < B

        def run(eng, batch):
            for b in range(BUF):
                batch(0, b)
            with eng.Fori(1, B // BUF - 1) as g:
                for b in range(BUF):
                    batch(g, b)
            for b in range(BUF):
                batch(B // BUF - 1, b)

        @block.sync
        def _(sp):
            sp.dma_start(gam[:, :], c.d["gamma3"].broadcast_to([P, 1])).then_inc(s["gamma_loaded"], 16)
            sp.wait_ge(s["row_ones_set"], 1)

            def load(g, b):
                cols = bass.ds((g * BUF + b) * H3, H3)
                k_rows = c.k_parts[:, :, cols, :].rearrange("a c h l -> (a c) (h l)")
                for i in range(3):
                    part = slice(3 * DQ3 * i, 3 * DQ3 * (i + 1))
                    q_rows = c.q_parts[i, :, cols, :].rearrange("c h l -> c (h l)").unsqueeze(0)
                    sp.dma_start(q[part, b, :], q_rows.broadcast_to([3, DQ3, H3 * D])).then_inc(s[qk_loaded[b]], 16)
                    sp.dma_start(k[part, b, :], k_rows).then_inc(s[qk_loaded[b]], 16)

            def lay_rows(g, b):
                sp.wait_ge(s["max_split"], batch_ready(g, b))
                for a in range(2):
                    sp.dma_start(q[R + a:R + a + 1, b, :], rows[:, b, a, :]).then_inc(s[rows_loaded[b]], 16)

            def batch(g, b):
                if exists(g, b, 3):
                    if exists(g, b, -1):
                        sp.wait_ge(s["turned_ready"], unit_ready(*at(g, b, -1), H3 - 1))
                    load(*at(g, b, 3))
                if exists(g, b, 1):
                    lay_rows(*at(g, b, 1))

            for b in range(3):
                load(0, b)
            lay_rows(0, 0)
            run(sp, batch)

        @block.gpsimd
        def _(pool):
            nc.gpsimd.memset(val[:, :, :, :, :, :], 0.0).then_inc(s["ones_set"], 1)
            pool.wait_ge(s["ones_set"], 1)
            nc.gpsimd.memset(val[:, :, :, :, 0, DQ3:AH], 1.0).then_inc(s["ones_set"], 1)
            pool.wait_ge(s["ones_set"], 2)
            give_credit(pool, s, "val_copied val_low max_turned max_split batch_read tile_turned x_done")
            for name in ("scores_ready", "max_ready", "turned_ready", "exp_ready", "rest_ready", "low_ready", "used_ready"):
                pool.sem_inc(s[name], UC)

            def values(g, b):
                if exists(g, b, -BUF):
                    pool.wait_ge(s["used_ready"], unit_ready(g - 1, b, H3 - 1))
                n = g * BUF + b
                for lt in range(DK):
                    src = c.vT[:, lt, bass.ds(n * S, S)]
                    last = nc.gpsimd.tensor_tensor(vrest[:, b % 2, lt, :, :], src.rearrange("p (h c) -> p h c", h=H3),
                                                   upper(src).rearrange("p (h c) -> p h c", h=H3), ALU.subtract)
                last.then_inc(s["val_rest"], 1)
                pool.wait_ge(s["val_rest"], n + 1)
                rest_all = vrest[:, b % 2, :, :, :].rearrange("p k h c -> p (k h c)")
                hi = upper(rest_all).rearrange("p (n c) -> p n c", c=DQ3)
                flat = val[:, b, :, :, :, :].rearrange("p k h n a -> p (k h) n a")
                nc.gpsimd.tensor_tensor(flat[:, :, 2, 0:DQ3], rest_all.rearrange("p (n c) -> p n c", c=DQ3), hi,
                                        ALU.subtract).then_inc(s["val_low"], 1)

            def batch(g, b):
                for h in range(H3):
                    pool.wait_ge(s["rest_ready"], unit_ready(g, b, h))
                    r2 = rest[:, h, :, :].rearrange("p k n -> p (k n)")
                    nc.gpsimd.tensor_tensor(low[:, h, :, :].rearrange("p k n -> p (k n)"), r2, upper(r2),
                                            ALU.subtract).then_inc(s["low_ready"], 1)
                    if h == 3 and exists(g, b, 1):
                        values(*at(g, b, 1))

            values(0, 0)
            run(pool, batch)

        @block.tensor
        def _(pe):
            def score(g, b, h):
                if h == 0:
                    pe.wait_ge(s[qk_loaded[b]], 96 * g + 96)
                pe.wait_ge(s["max_ready"], unit_ready(g, b, h) - NS)
                for qt in range(2):
                    last = nc.tensor.matmul(scores(h)[:, qt * D:(qt + 1) * D],
                                            q[0:R, b, h * D + qt * P:h * D + qt * P + P],
                                            k[0:R, b, h * D:(h + 1) * D], start=True, stop=True)
                last.then_inc(s["scores_ready"], 1)

            def turn_max(g, b):
                pe.wait_ge(s["max_ready"], unit_ready(g, b, H3 - 1))
                pe.wait_ge(s["max_split"], batch_ready(g, b) - 1)
                nc.tensor.transpose(max_rows, nmax[:, b, :], c.ident).then_inc(s["max_turned"], 1)

            def score_turned(g, b, h):
                if h == 0:
                    pe.wait_ge(s[rows_loaded[b]], 32 * g + 32)
                pe.wait_ge(s["exp_ready"], unit_ready(g, b, h) - NT_)
                for lt in range(DK):
                    last = nc.tensor.matmul(scoresT(h)[:, lt * D:(lt + 1) * D],
                                            k[:, b, h * D + lt * P:h * D + lt * P + P],
                                            q[:, b, h * D:(h + 1) * D], start=True, stop=True)
                last.then_inc(s["turned_ready"], 1)

            def read(g, b, h):
                pe.wait_ge(s["low_ready"], unit_ready(g, b, h))
                if h == 0:
                    pe.wait_ge(s["val_copied"], batch_ready(g, b))
                    pe.wait_ge(s["val_low"], batch_ready(g, b))
                    pe.wait_ge(s["batch_read"], batch_ready(g, b) - 2)
                for qt in range(2):
                    out = readout(b)[:, (qt * H3 + h) * 3 * AH:(qt * H3 + h + 1) * 3 * AH]
                    for n, part in enumerate((lambda ap: upper(ap), lambda ap: upper(ap), lambda ap: ap)):
                        src = (eT, rest, low)[n]
                        for lt in range(DK):
                            last = nc.tensor.matmul(out, part(src[:, h % NE, lt, qt * P:(qt + 1) * P]),
                                                    val[:, b, lt, h, :, :].rearrange("p n a -> p (n a)"),
                                                    start=(n == 0 and lt == 0), stop=(n == 2 and lt == DK - 1))
                last.then_inc(s["used_ready"], 1)

            def finish(g, b):
                pe.wait_ge(s["batch_read"], batch_ready(g, b))
                pe.wait_ge(s["x_done"], ready(2 * g + b // 2) - 1)
                for qt in range(2):
                    last = nc.tensor.transpose(final[:, qt * P:(qt + 1) * P],
                                               on[:, qt, :, :].rearrange("p b n -> p (b n)"), c.ident)
                last.then_inc(s["tile_turned"], 1)

            def batch(g, b):
                for h in range(H3):
                    if exists(g, b, LEAD):
                        score(*at(g, b, LEAD), h)
                    if h == 1 and exists(g, b, 1):
                        turn_max(*at(g, b, 1))
                    score_turned(g, b, h)
                    if h >= LAG:
                        read(g, b, h - LAG)
                    elif exists(g, b, -1):
                        read(*at(g, b, -1), H3 + h - LAG)
                    if h == 7 and b % 2 == 0 and exists(g, b, -1):
                        finish(*at(g, b, -1))

            for h in range(H3):
                score(0, 0, h)
            turn_max(0, 0)
            for h in range(H3):
                score(0, 1, h)
            run(pe, batch)
            for h in range(H3 - LAG, H3):
                read(B // BUF - 1, BUF - 1, h)
            finish(B // BUF - 1, BUF - 1)

        @block.scalar
        def _(act):
            def values(g, b):
                if exists(g, b, -BUF):
                    act.wait_ge(s["used_ready"], unit_ready(g - 1, b, H3 - 1))
                for lt in range(DK):
                    act.copy(val[:, b, lt, :, 0, 0:DQ3], upper(c.vT[:, lt, bass.ds((g * BUF + b) * S, S)]).rearrange(
                        "p (h c) -> p h c", h=H3))
                act.wait_ge(s["val_rest"], g * BUF + b + 1)
                flat = val[:, b, :, :, :, :].rearrange("p k h n a -> p (k h) n a")
                act.copy(flat[:, :, 1, 0:DQ3], upper(vrest[:, b % 2, :, :, :].rearrange("p k h c -> p (k h c)")).rearrange(
                    "p (n c) -> p n c", c=DQ3)).then_inc(s["val_copied"], 1)

            def batch(g, b):
                for h in range(H3):
                    act.wait_ge(s["turned_ready"], unit_ready(g, b, h))
                    act.wait_ge(s["used_ready"], unit_ready(g, b, h) - NE)
                    nc.scalar.activation(eT[:, h % NE, :, :].rearrange("p k n -> p (k n)"), scoresT(h)[:, :],
                                         ACT.Exp).then_inc(s["exp_ready"], 1)
                    if h == 4 and exists(g, b, 1):
                        values(*at(g, b, 1))

            act.wait_ge(s["ones_set"], 2)
            values(0, 0)
            run(act, batch)

        @block.vector
        def _(dve):
            v = nc.vector

            def maxima(g, b, h):
                dve.wait_ge(s["scores_ready"], unit_ready(g, b, h))
                v.tensor_reduce(nmax[:, b, 2 * h:2 * h + 2], scores(h)[:, :].rearrange("p (a n) -> p a n", a=2), AX.X,
                                ALU.max, negate=True).then_inc(s["max_ready"], 1)

            def split_max(g, b):
                ch = Chain(dve, s["split_chain"], g * BUF + b)
                dve.wait_ge(s["max_turned"], batch_ready(g, b))
                ch.link(v.tensor_scalar(rows[:, b, 0, :], max_rows, 1.0, None, ALU.mult))
                v.tensor_tensor(rows[:, b, 1, :], max_rows, rows[:, b, 0, :], ALU.subtract).then_inc(s["max_split"], 1)

            def normalized(g, b):
                ch = Chain(dve, s["norm_chain"], (g * BUF + b) * 3)
                dve.wait_ge(s["used_ready"], unit_ready(g, b, H3 - 1))
                if b % 2 == 0:
                    dve.wait_ge(s["tile_turned"], ready(2 * g + b // 2) - 1)
                r3 = total[:, b % 2, :, :]
                ch.link(v.tensor_reduce(r3, readout(b).rearrange("p (n i a) -> p n a i", i=3, a=AH), AX.X, ALU.add))
                ch.link(v.reciprocal(rec[:, b % 2, :], r3[:, :, DQ3]))
                ch.link(v.tensor_scalar(rec[:, b % 2, :], rec[:, b % 2, :], gam[:, 0:1], None, ALU.mult))
                for qt in range(2):
                    last = v.tensor_tensor(on[:, qt, b % 2, :].rearrange("p (h c) -> p h c", h=H3),
                                           r3[:, qt * H3:(qt + 1) * H3, 0:DQ3],
                                           rec[:, b % 2, qt * H3:(qt + 1) * H3].unsqueeze(2).broadcast_to([P, H3, DQ3]), ALU.mult)
                last.then_inc(s["batch_read"], 1)

            def finish(g, b):
                t = 2 * g + b // 2
                dve.wait_ge(s["tile_turned"], ready(t))
                add_and_stats(nc, c, Chain(dve, s["add_chain"], 2 * t), t, final, 1.0, s["x_done"])

            def remainder(g, b, h):
                dve.wait_ge(s["exp_ready"], unit_ready(g, b, h))
                e2 = eT[:, h, :, :].rearrange("p k n -> p (k n)")
                v.tensor_tensor(rest[:, h, :, :].rearrange("p k n -> p (k n)"), e2, upper(e2),
                                ALU.subtract).then_inc(s["rest_ready"], 1)

            def batch(g, b):
                for h in range(H3):
                    if exists(g, b, LEAD):
                        maxima(*at(g, b, LEAD), h)
                    if h > 0:
                        remainder(g, b, h - 1)
                    elif exists(g, b, -1):
                        remainder(*at(g, b, -1), H3 - 1)
                    if h == 2 and exists(g, b, 1):
                        split_max(*at(g, b, 1))
                    if h == 5 and exists(g, b, -1):
                        normalized(*at(g, b, -1))
                    if h == 1 and b % 2 == 1 and exists(g, b, -2):
                        finish(*at(g, b, -2))

            v.memset(k[64:R + 2, :, :], 1.0).then_inc(s["row_ones_set"], 1)
            dve.wait_ge(s["gamma_loaded"], 16)
            for h in range(H3):
                maxima(0, 0, h)
            split_max(0, 0)
            for h in range(H3):
                maxima(0, 1, h)
            run(dve, batch)
            remainder(B // BUF - 1, BUF - 1, H3 - 1)
            normalized(B // BUF - 1, BUF - 1)
            finish(B // BUF - 1, BUF - 1)


def stage_l3_gate(nc, c):
    with ExitStack() as ctx:
        sb = lambda n, sh, dt=F32: ctx.enter_context(nc.sbuf_tensor(n, sh, dt))
        wg = sb("wg_3", [P, DK, E3]); xn = sb("xn_g3", [P, WIDE, D]); xT = sb("xT_g3", [P, WIDE, D])
        s = open_sems(nc, ctx, "g3_loaded xn_ready feat_ready feat_copied logit_ready logit_copied")
        block = ctx.enter_context(nc.Block())

        @block.sync
        def _(sp):
            sp.dma_start(wg[:, :, :], c.d["g3w"].rearrange("(k p) n -> p k n", p=P)).then_inc(s["g3_loaded"], 16)

        @block.gpsimd
        def _(pool):
            give_credit(pool, s, "xn_ready feat_ready feat_copied logit_ready logit_copied", WIDE // CREDIT)

        @block.tensor
        def _(pe):
            pe.wait_ge(s["g3_loaded"], 16)
            with pe.Fori(0, NT // WIDE) as i:
                for j, t in token_loop(i, WIDE):
                    pe.wait_ge(s["xn_ready"], ready(t, WIDE))
                    pe.wait_ge(s["feat_copied"], freed(t))
                    transpose_tile(nc, c, c.bank[j], xn[:, j, :]).then_inc(s["feat_ready"], 1)
                for j, t in token_loop(i, WIDE):
                    pe.wait_ge(s["feat_copied"], ready(t, WIDE))
                    pe.wait_ge(s["logit_copied"], freed(t))
                    for k in range(DK):
                        last = nc.tensor.matmul(c.bank[WIDE + j][:, 0:E3], xT[:, j, k * P:(k + 1) * P], wg[:, k, :],
                                                start=(k == 0), stop=(k == DK - 1))
                    last.then_inc(s["logit_ready"], 1)

        @block.scalar
        def _(act):
            with act.Fori(0, NT // WIDE) as i:
                for j, t in token_loop(i, WIDE):
                    act.wait_ge(s["logit_ready"], ready(t, WIDE))
                    nc.scalar.activation(at_tile(c.score3, t), c.bank[WIDE + j][:, 0:E3],
                                         ACT.Sigmoid).then_inc(s["logit_copied"], 1)

        @block.vector
        def _(dve):
            with dve.Fori(0, NT // WIDE) as i:
                for j, t in token_loop(i, WIDE):
                    dve.wait_ge(s["feat_ready"], freed(t))
                    normalize(nc, c, xn[:, j, :], t).then_inc(s["xn_ready"], 1)
                for j, t in token_loop(i, WIDE):
                    dve.wait_ge(s["feat_ready"], ready(t, WIDE))
                    dve.wait_ge(s["logit_ready"], freed(t))
                    nc.vector.tensor_copy(xT[:, j, :], c.bank[j][:, 0:D]).then_inc(s["feat_copied"], 1)


def stage_l3_route(nc, c):
    with ExitStack() as ctx:
        sb = lambda n, sh, dt=F32: ctx.enter_context(nc.sbuf_tensor(n, sh, dt))
        pad = 8 - TOP3
        cand = sb("cand_3", [P, NT, E3 + pad]); left = sb("left_3", [P, NT, E3 + pad]); top = sb("top_3", [P, NT, 8])
        total = sb("total_3", [P, NT])
        s = open_sems(nc, ctx, "r3_chain")
        block = ctx.enter_context(nc.Block())

        @block.vector
        def _(dve):
            ch = Chain(dve, s["r3_chain"])
            v = nc.vector
            v.memset(cand[:, :, E3:E3 + pad], BIG)
            ch.link(v.tensor_copy(cand[:, :, 0:E3], c.score3[:, :, :]))
            for t in range(NT):
                last = v.max(top[:, t, :], cand[:, t, 0:E3])
            ch.link(last)
            ch.link(v.memset(top[:, :, TOP3:8], BIG))
            for t in range(NT):
                last = v.match_replace(out=left[:, t, :], in_to_replace=top[:, t, :], in_values=cand[:, t, :],
                                       imm_value=-BIG)
            ch.link(last)
            ch.link(v.tensor_tensor(left[:, :, 0:E3], left[:, :, 0:E3], cand[:, :, 0:E3], ALU.not_equal))
            ch.link(v.tensor_tensor(left[:, :, 0:E3], left[:, :, 0:E3], cand[:, :, 0:E3], ALU.mult))
            ch.link(v.tensor_reduce(total[:, :], left[:, :, 0:E3], AX.X, ALU.add))
            ch.link(v.tensor_scalar(total[:, :], total[:, :], 1e-20, None, ALU.add))
            ch.link(v.reciprocal(total[:, :], total[:, :]))
            comb = c.comb[:, :].rearrange("p (t e) -> p t e", e=E3 + 1)
            v.memset(comb[:, :, E3:E3 + 1], 1.0)
            ch.link(v.scalar_tensor_tensor(out=comb[:, :, 0:E3], in0=left[:, :, 0:E3], scalar=SCALE3,
                                           in1=total[:, :].unsqueeze(2).broadcast_to([P, NT, E3]),
                                           op0=ALU.mult, op1=ALU.mult))


def stage_l3_experts(nc, c):
    with ExitStack() as ctx:
        sb = lambda n, sh, dt=F32: ctx.enter_context(nc.sbuf_tensor(n, sh, dt))
        U = E3 + 1
        HW = U * HID3
        CH = -(-HW // P)
        NA, NB, NG = 3, 2, 4
        groups = [range(0, 4), range(4, 7), range(7, 10), range(10, CH)]
        w13 = sb("w13_3", [P, DK, U * 2 * HID3]); w2 = sb("w2_3", [P, CH, D])
        xn = sb("xn_3", [P, D]); xT = sb("xT_3", [P, 2, D]); sig = sb("sig_3", [P, NA, HID3])
        hid = sb("hid_3", [P, 2, HW]); hT = sb("hT_3", [P, CH, P])
        s = open_sems(nc, ctx, "w_loaded xn_ready feat_ready xT_ready hid_ready sig_ready prod_ready turned_ready "
                      "hT_ready down_ready x_done e3_chain")
        LINKS = U
        block = ctx.enter_context(nc.Block())
        feat = c.bank[0][:, 0:D]
        gates = lambda e: c.bank[1 + e % NA]
        turned = lambda g: c.bank[1 + NA + g % NB]
        out = lambda j: c.bank[1 + NA + NB + j][:, 0:D]
        width = lambda ch: min(P, HW - ch * P)

        def unit_ready(t, e):
            return t * U + e + 1 + NA

        def group_ready(t, g):
            return t * NG + g + 1 + NG

        @block.sync
        def _(sp):
            loads = []
            for k in range(DK):
                rows = slice(k * P, (k + 1) * P)
                view = w13[:, k, :].rearrange("p (e n) -> p e n", e=U)
                for n, (routed, shared) in enumerate((("e3w1", "s3w1"), ("e3w3", "s3w3"))):
                    cols = slice(n * HID3, (n + 1) * HID3)
                    loads.append((view[:, 0:E3, cols], c.d[routed][:, rows, :].rearrange("e p n -> p e n")))
                    loads.append((view[:, E3, cols], c.d[shared][rows, :]))
            full = E3 * HID3 // P
            loads.append((w2[:, 0:full, :], c.d["e3w2"].rearrange("e h n -> (e h) n").rearrange("(c p) n -> p c n", p=P)))
            loads.append((w2[:, full, :], c.d["s3w2"][0:P, :]))
            loads.append((w2[0:HID3 - P, full + 1, :], c.d["s3w2"][P:HID3, :]))
            assert len(loads) == 11
            for dst, src in loads:
                sp.dma_start(dst, src).then_inc(s["w_loaded"], 16)

        @block.gpsimd
        def _(pool):
            for names, credit in (("hid_ready sig_ready prod_ready", NA), ("turned_ready hT_ready down_ready", NG),
                                  ("xn_ready feat_ready xT_ready x_done", CREDIT)):
                for n in names.split():
                    pool.sem_inc(s[n], credit)

        def schedule(first, last, hidden, hidden_turn, down, features):
            for e in range(U):
                hidden(0, e)
                if not first and e in (0, 1):
                    hidden_turn(-1, 2 + e)
                if e == 3:
                    hidden_turn(0, 0)
                if e == 7:
                    hidden_turn(0, 1)
                if not first and e in (2, 3):
                    down(-1, e)
                if e == 5:
                    down(0, 0)
                if e == 8:
                    down(0, 1)
                if e == 6 and not last:
                    features(1)
            if last:
                for g in (2, 3):
                    hidden_turn(0, g)
                for g in (2, 3):
                    down(0, g)

        @block.tensor
        def _(pe):
            def features(t):
                pe.wait_ge(s["xn_ready"], ready(t))
                transpose_tile(nc, c, feat, xn[:, :]).then_inc(s["feat_ready"], 1)

            def tile(t, j, first=False, last=False):
                def hidden(dt, e):
                    if e == 0:
                        pe.wait_ge(s["xT_ready"], ready(t))
                    pe.wait_ge(s["prod_ready"], unit_ready(t, e) - NA)
                    for k in range(DK):
                        op = nc.tensor.matmul(gates(e)[:, 0:2 * HID3], xT[:, j, k * P:(k + 1) * P],
                                              w13[:, k, e * 2 * HID3:(e + 1) * 2 * HID3], start=(k == 0), stop=(k == DK - 1))
                    op.then_inc(s["hid_ready"], 1)

                def turn(dt, g):
                    upto = groups[g][-1] * P + width(groups[g][-1])
                    pe.wait_ge(s["prod_ready"], unit_ready(t + dt, (upto - 1) // HID3))
                    pe.wait_ge(s["hT_ready"], group_ready(t + dt, g) - NB)
                    for n, ck in enumerate(groups[g]):
                        w = width(ck)
                        op = nc.tensor.transpose(turned(g)[0:w, n * P:(n + 1) * P],
                                                 hid[:, (j + dt) % 2, ck * P:ck * P + w], c.ident)
                    op.then_inc(s["turned_ready"], 1)

                def down(dt, g):
                    pe.wait_ge(s["hT_ready"], group_ready(t + dt, g))
                    if g == 0:
                        pe.wait_ge(s["x_done"], freed(t))
                    for ck in groups[g]:
                        w = width(ck)
                        op = nc.tensor.matmul(out((j + dt) % 2), hT[0:w, ck, :], w2[0:w, ck, :],
                                              start=(ck == 0), stop=(ck == CH - 1))
                    op.then_inc(s["down_ready"], 1)

                schedule(first, last, hidden, turn, down, lambda dt: features(t + dt))

            pe.wait_ge(s["w_loaded"], 176)
            features(0)
            tile(0, 0, first=True)
            with pe.Fori(0, (NT - 2) // 2) as i:
                tile(2 * i + 1, 1)
                tile(2 * i + 2, 0)
            tile(NT - 1, 1, last=True)

        @block.scalar
        def _(act):
            def features(t, j):
                act.wait_ge(s["feat_ready"], ready(t))
                act.copy(xT[:, j, :], feat).then_inc(s["xT_ready"], 1)

            def tile(t, j, first=False, last=False):
                def hidden(dt, e):
                    act.wait_ge(s["hid_ready"], unit_ready(t, e))
                    act.wait_ge(s["prod_ready"], unit_ready(t, e) - NA)
                    nc.scalar.activation(sig[:, e % NA, :], gates(e)[:, 0:HID3], ACT.Sigmoid).then_inc(s["sig_ready"], 1)

                def copy(dt, g):
                    act.wait_ge(s["turned_ready"], group_ready(t + dt, g))
                    act.wait_ge(s["down_ready"], group_ready(t + dt, g) - NG)
                    n, at = len(groups[g]), groups[g][0]
                    full = n if width(at + n - 1) == P else n - 1
                    op = act.copy(hT[:, at:at + full, :].rearrange("p c n -> p (c n)"), turned(g)[:, 0:full * P])
                    if full < n:
                        w = width(at + n - 1)
                        op = act.copy(hT[0:w, at + full, :], turned(g)[0:w, full * P:n * P])
                    op.then_inc(s["hT_ready"], 1)

                schedule(first, last, hidden, copy, lambda dt, g: None, lambda dt: features(t + dt, (j + dt) % 2))

            features(0, 0)
            tile(0, 0, first=True)
            with act.Fori(0, (NT - 2) // 2) as i:
                tile(2 * i + 1, 1)
                tile(2 * i + 2, 0)
            tile(NT - 1, 1, last=True)

        @block.vector
        def _(dve):
            v = nc.vector

            def features(t):
                dve.wait_ge(s["feat_ready"], t + CREDIT)
                normalize(nc, c, xn[:, :], t).then_inc(s["xn_ready"], 1)

            def add(t, j):
                dve.wait_ge(s["down_ready"], group_ready(t, NG - 1))
                v.tensor_tensor(at_tile(c.x, t), out(j), at_tile(c.x, t), ALU.add).then_inc(s["x_done"], 1)

            def tile(t, j, first=False, last=False):
                ch = Chain(dve, s["e3_chain"], t * LINKS)
                for e in range(U):
                    dve.wait_ge(s["sig_ready"], unit_ready(t, e))
                    ch.link(v.tensor_tensor(sig[:, e % NA, :], gates(e)[:, 0:HID3], sig[:, e % NA, :], ALU.mult))
                    v.scalar_tensor_tensor(out=hid[:, j, e * HID3:(e + 1) * HID3], in0=gates(e)[:, HID3:2 * HID3],
                                           scalar=c.comb[:, bass.ds(t * U + e, 1)], in1=sig[:, e % NA, :],
                                           op0=ALU.mult, op1=ALU.mult).then_inc(s["prod_ready"], 1)
                    if e == 3 and not last:
                        features(t + 1)
                    if e == 5 and not first:
                        add(t - 1, 1 - j)
                if last:
                    add(t, j)
                assert ch.n == LINKS, ch.n

            features(0)
            tile(0, 0, first=True)
            with dve.Fori(0, (NT - 2) // 2) as i:
                tile(2 * i + 1, 1)
                tile(2 * i + 2, 0)
            tile(NT - 1, 1, last=True)


def layers(nc, c):
    with ExitStack() as keys:
        c.keysT = keys.enter_context(nc.sbuf_tensor("keysT", [P, N], F32))
        c.kvc = keys.enter_context(nc.sbuf_tensor("kvc", [P, NT, KVC], F32))
        with ExitStack() as kv:
            res = lambda n, sh, dt=F32: kv.enter_context(nc.sbuf_tensor(n, sh, dt))
            c.v = res("v_all", [P, NT, D])
            c.gramT = res("gramT", [P, H1, N])
            finish_stats(nc, c, "st0")
            stage_l0_attention(nc, c)
            finish_stats(nc, c, "st1")
            with ExitStack() as moe:
                l0 = lambda n, sh, dt=F32: moe.enter_context(nc.sbuf_tensor(n, sh, dt))
                c.score0 = l0("score0", [P, NT, E0]); c.row_col = l0("row_col", [P, 1])
                c.slot_token = l0("slot_token", [CAP0, E0], I32); c.slot_weight = l0("slot_weight", [CAP0, E0])
                c.place = l0("place", [P, NT, E0], BF16)
                stage_l0_shared(nc, c)
                with ExitStack() as sl:
                    c.slot_cols = sl.enter_context(nc.sbuf_tensor("slot_cols", [P, NT, E0, 6], BF16))
                    stage_l0_route(nc, c)
                    stage_l0_slots(nc, c)
                stage_l0_experts(nc, c)
            stage_add_experts(nc, c)
            recycle(nc)
            c.gate1 = res("gate1", [P, NT, D])
            c.mixT = res("mixT", [P, H1, P])
            finish_stats(nc, c, "st2")
            stage_l1_scores(nc, c)
            stage_l1_mix(nc, c)
        finish_stats(nc, c, "st3")
        stage_l1_think(nc, c)
        stage_l1_broadcast(nc, c)
        recycle(nc)
        finish_stats(nc, c, "st4")
        stage_l2_attention(nc, c)
    finish_stats(nc, c, "st5")
    stage_l2_ternary(nc, c)
    recycle(nc)
    finish_stats(nc, c, "st6")
    with ExitStack() as l3:
        c.vT = l3.enter_context(nc.sbuf_tensor("vT", [P, DK, N], F32))
        stage_l3_split(nc, c)
        stage_l3_attention(nc, c)
    finish_stats(nc, c, "st7")
    with ExitStack() as moe:
        l3 = lambda n, sh, dt=F32: moe.enter_context(nc.sbuf_tensor(n, sh, dt))
        c.score3 = l3("score3", [P, NT, E3]); c.comb = l3("comb", [P, NT * (E3 + 1)])
        stage_l3_gate(nc, c)
        stage_l3_route(nc, c)
        stage_l3_experts(nc, c)



def build_program(nc, d):
    c = Core()
    HELD.clear()
    OPENED.clear()
    c.d = d
    with ExitStack() as ctx:
        sb = lambda n, sh, dt=F32: ctx.enter_context(nc.sbuf_tensor(n, sh, dt))
        c.bank = [ctx.enter_context(nc.psum_tensor(f"bank{k}", [P, 512], F32)) for k in range(8)]
        c.x = sb("x_all", [P, NT, D])
        c.bn = sb("bn_all", [P, NT, 6])
        c.mean = sb("mean_all", [P, NT])
        c.rstd = sb("rstd_all", [P, NT])
        c.small = sb("small", [P, 5, NT])
        c.minus_half = sb("minus_half", [P, NT])
        c.const = sb("const_sb", [P, CONST_W])
        part = lambda n: c.const[:, CONSTS[n][0]:CONSTS[n][1]]
        c.ident, c.cos, c.sin, c.before, c.iota = (part(n) for n in ("ident", "cos", "sin", "before", "iota"))
        c.moe = nc.dram_tensor("moe_rows", (NX, D), F32, kind="Internal").ap()
        c.think_rows = nc.dram_tensor("think_rows", (B, D), F32, kind="Internal").ap()
        c.xn_rows = nc.dram_tensor("xn_rows", (NX, D), F32, kind="Internal").ap()
        c.q_parts, c.k_parts = (nc.dram_tensor(n, (3, DQ3, B * H3, D), BF16, kind="Internal").ap()
                                for n in ("q_parts", "k_parts"))
        c.decay, c.lower = part("decay"), part("lower")
        c.cos_one = part("one")
        stage_first(nc, c)
        layers(nc, c)
        stage_last(nc, c)


def lay_out(inputs):
    f = {k: np.asarray(v) for k, v in inputs.items()}
    a = {
        "x": f["x"].reshape(N, D),
        "ctx": f["ctx_2048"].reshape(N, D),
        "mask": f["mask_BxS2_bk0"].view(np.int32),
        "seg": f["itok_BxS_0_1023"].reshape(NT, P).T,
        "const": constants(),
        "wh": f["L1_xattn_Wh"],
        "whT": f["L1_xattn_Wh"].transpose(0, 2, 1),
        "wkvc": f["L2_xattn_W_kvc"],
        "wkvcT": f["L2_xattn_W_kvc"].T,
        "wkr": f["L2_xattn_W_kr"],
        "g0w": f["L0_ffn_gate_w"].T,
        "g0b": f["L0_ffn_gate_bias"].reshape(1, E0),
        "e0w1": f["L0_ffn_w1"], "e0w2": f["L0_ffn_w2"], "e0w3": f["L0_ffn_w3"],
        "s0g": f["L0_ffn_shared_gate"], "s0u": f["L0_ffn_shared_up"], "s0d": f["L0_ffn_shared_down"],
        "wg": f["L1_xattn_wg_w"], "wo": f["L1_xattn_wo_w"],
        "gng": f["L1_xattn_gn_gamma"].reshape(1, D), "gnb": f["L1_xattn_gn_beta"].reshape(1, D),
    }
    for n in ("in_gamma", "in_beta", "agg_b", "pn_gamma", "pn_beta", "d1_b", "d2_b", "bc_b", "gate_b",
              "out_gamma", "out_beta"):
        a["f1_" + n] = f["L1_ffn_" + n].reshape(1, -1)
    a["f1_d1_b"] = f["L1_ffn_d1_b"].reshape(HID1 // P, P).T
    for n in ("agg_w", "d1_w", "d2_w", "bc_w", "gate_w"):
        a["f1_" + n] = f["L1_ffn_" + n]
    a.update({
        "wdq": f["L2_xattn_W_dq"],
        "wuqT": f["L2_xattn_W_uq"].reshape(QC, H2, HD2).transpose(2, 1, 0),
        "wukT": f["L2_xattn_W_uk"].reshape(KVC, H2, HD2).transpose(2, 1, 0),
        "wuvT": f["L2_xattn_W_uv"].reshape(KVC, H2, HD2).transpose(2, 1, 0),
        "wqr": f["L2_xattn_W_qr"].reshape(QC, H2, R2),
        "wo2": f["L2_xattn_W_o"].reshape(H2, HD2, D).transpose(1, 0, 2),
        "t1": f["L2_ffn_w1"].T, "t2": f["L2_ffn_w2"].T, "t3": f["L2_ffn_w3"].T,
        "gamma3": f["L3_xattn_gamma"].reshape(1, 1),
        "g3w": f["L3_ffn_gate_w"].T,
        "e3w1": f["L3_ffn_w1"], "e3w2": f["L3_ffn_w2"], "e3w3": f["L3_ffn_w3"],
        "s3w1": f["L3_ffn_sw1"], "s3w2": f["L3_ffn_sw2"], "s3w3": f["L3_ffn_sw3"],
    })
    return {k: np.ascontiguousarray(v) for k, v in a.items()}


def kernel(**inputs):
    import concourse.bacc as bacc
    from concourse.bass_utils import run_bass_kernel_spmd

    nc = bacc.Bacc("TRN2", target_bir_lowering=False, num_devices=1)
    arrays = {"in_" + k: v for k, v in lay_out(inputs).items()}
    d = {k[3:]: nc.dram_tensor(k, v.shape, mybir.dt.from_np(v.dtype), kind="ExternalInput").ap()
         for k, v in arrays.items()}
    d["out"] = nc.dram_tensor("out_x", (N, D), F32, kind="ExternalOutput").ap()
    build_program(nc, d)
    r = run_bass_kernel_spmd(nc, [arrays], core_ids=[0])
    return r.results[0]["out_x"].reshape(B, S, D)
```
